# Optimizing a Trainium2 kernel written in Bass

```python
import numpy as np
import jax
import jax.numpy as jnp

def _softmax(x, axis=-1):
    return jax.nn.softmax(x, axis=axis)

def _gelu(x):
    return jax.nn.gelu(x, approximate=True)

def _silu(x):
    return jax.nn.silu(x)

def _sigmoid(x):
    return jax.nn.sigmoid(x)

def _layernorm(x, axis=-1, eps=1e-05):
    m = jnp.mean(x, axis=axis, keepdims=True)
    v = jnp.var(x, axis=axis, keepdims=True)
    return (x - m) / jnp.sqrt(v + eps)

def _scatter_add(tgt, idx, src, axis=0):
    return tgt.at[idx].add(src)

def _segment_sum(src, seg, n):
    return jax.ops.segment_sum(src, seg, n)
kernel_name = 'mk_xattn_ffn_d4_seqx_r8_f832e8'

def setup_inputs(seed: int=0):
    np.random.seed(seed)
    _w = jnp.asarray

    def _rec_inputs():
        import jax
        import jax.numpy as jnp
        _rk = jax.random.key(seed)
        x = -0.0002928 + 1 * jax.random.normal(jax.random.fold_in(_rk, 1), (8, 256, 128), jnp.float32)
        _lenS = 256 - jax.random.randint(jax.random.fold_in(_rk, 7), (8,), 0, max(1, 256 // 4) + 1, jnp.int32)
        _lenS2 = 512 - jax.random.randint(jax.random.fold_in(_rk, 8), (8,), 0, max(1, 512 // 4) + 1, jnp.int32)
        _ctx_768P = jax.random.normal(jax.random.fold_in(_rk, 11), (8, 16, 96), jnp.float32)
        _ctx_768c = jax.random.dirichlet(jax.random.fold_in(_rk, 511), 0.3 * jnp.ones((16,), jnp.float32), (8, 512))
        _ctx_768t = jnp.einsum('bsk,bkd->bsd', _ctx_768c, _ctx_768P)
        _ctx_768t = _ctx_768t * jax.lax.rsqrt(jnp.mean(jnp.square(_ctx_768t)) + 1e-12) * 0.953939
        ctx_768 = 2.09791e-05 + 1.00001 * (_ctx_768t + 0.3 * jax.random.normal(jax.random.fold_in(_rk, 611), (8, 512, 96), jnp.float32))
        return (x, ctx_768)
    x, ctx_768 = _rec_inputs()

    def _L0_xattn_setup():
        import jax, jax.numpy as jnp
        import numpy as np
        QUERY_DIM, KV_DIM, EMBED_DIM, NUM_HEADS = (128, 96, 128, 16)
        HEAD_DIM = EMBED_DIM // NUM_HEADS
        SCALE = HEAD_DIM ** (-0.5)
        LN_EPS = 1e-05

        def _l2norm(x, eps=1e-12):
            n = jnp.sqrt(jnp.sum(x * x, axis=-1, keepdims=True))
            return x / jnp.maximum(n, eps)
        key = jax.random.key(seed)
        ks = jax.random.split(key, 12)
        B, Nq, Nk = (2, 256, 256)
        s = lambda d: 1.0 / np.sqrt(d)
        return {'query': jax.random.normal(ks[0], (B, Nq, QUERY_DIM), jnp.float32), 'key': jax.random.normal(ks[1], (B, Nk, KV_DIM), jnp.float32), 'value': jax.random.normal(ks[2], (B, Nk, KV_DIM), jnp.float32), 'Wq': jax.random.normal(ks[3], (QUERY_DIM, EMBED_DIM), jnp.float32) * s(QUERY_DIM), 'bq': jnp.zeros((EMBED_DIM,), jnp.float32), 'Wk': jax.random.normal(ks[4], (KV_DIM, EMBED_DIM), jnp.float32) * s(KV_DIM), 'bk': jnp.zeros((EMBED_DIM,), jnp.float32), 'Wv': jax.random.normal(ks[5], (KV_DIM, EMBED_DIM), jnp.float32) * s(KV_DIM), 'bv': jnp.zeros((EMBED_DIM,), jnp.float32), 'Wo': jax.random.normal(ks[6], (EMBED_DIM, EMBED_DIM), jnp.float32) * s(EMBED_DIM), 'bo': jnp.zeros((EMBED_DIM,), jnp.float32), 'ln_gamma': jnp.ones((EMBED_DIM,), jnp.float32), 'ln_beta': jnp.zeros((EMBED_DIM,), jnp.float32)}
    _L0_xattn_all = _L0_xattn_setup()
    _L0_xattn_in = {k: v for k, v in _L0_xattn_all.items() if k in ('Wq', 'bq', 'Wk', 'bk', 'Wv', 'bv', 'Wo', 'bo', 'ln_gamma', 'ln_beta')}
    del _L0_xattn_all

    def _L0_ffn_setup():
        import jax, jax.numpy as jnp
        import numpy as np
        E = 8
        TOP_K = 2
        LN_EPS = 1e-05

        def _layernorm(x, g, b):
            mu = jnp.mean(x, axis=-1, keepdims=True)
            var = jnp.var(x, axis=-1, keepdims=True)
            return (x - mu) * jax.lax.rsqrt(var + LN_EPS) * g + b
        key = jax.random.key(seed)
        ks = jax.random.split(key, 4)
        B, T, H, HF = (4, 256, 128, 256)
        s_in = 1.0 / np.sqrt(H)
        s_hid = 1.0 / np.sqrt(HF)
        return {'x': jax.random.normal(ks[0], (B, T, H), dtype=jnp.float32), 'ln_g': jnp.ones((H,), dtype=jnp.float32), 'ln_b': jnp.zeros((H,), dtype=jnp.float32), 'rW': jax.random.normal(ks[1], (H, E), dtype=jnp.float32) * s_in, 'rb': jnp.zeros((E,), dtype=jnp.float32), 'W1': jax.random.normal(ks[2], (E, H, HF), dtype=jnp.float32) * s_in, 'b1': jnp.zeros((E, HF), dtype=jnp.float32), 'W2': jax.random.normal(ks[3], (E, HF, H), dtype=jnp.float32) * s_hid, 'b2': jnp.zeros((E, H), dtype=jnp.float32)}
    _L0_ffn_all = _L0_ffn_setup()
    _L0_ffn_in = {k: v for k, v in _L0_ffn_all.items() if k in ('ln_g', 'ln_b', 'rW', 'rb', 'W1', 'b1', 'W2', 'b2')}
    del _L0_ffn_all

    def _L1_xattn_setup():
        import jax, jax.numpy as jnp
        import numpy as np
        import math
        E = 128
        EV = 128
        FFN = 512
        DINO = 96
        B, S, P = (64, 64, 32)

        def bitnet_linear(x, W, b):
            w_scale = jnp.maximum(jnp.mean(jnp.abs(W)), 1e-05)
            qW = jnp.sign(W) * (jnp.abs(W) > 0.5 * w_scale).astype(W.dtype)
            i_scale = jnp.maximum(jnp.max(jnp.abs(x)), 1e-08) / 127.0
            qx = jnp.clip(jnp.round(x / i_scale), -128.0, 127.0)
            out = jnp.einsum('...i,oi->...o', qx, qW) * (w_scale * i_scale)
            return out + b
        key = jax.random.key(seed)
        ks = iter(jax.random.split(key, 32))

        def lin_w(fin, fout):
            return jax.random.normal(next(ks), (fout, fin), jnp.float32) * math.sqrt(2.0 / fin)
        return {'text_embeddings': jax.random.normal(next(ks), (B, S, E), jnp.float32), 'dinov2_features': jax.random.normal(next(ks), (B, P, DINO), jnp.float32), 'W_d2v': lin_w(DINO, EV), 'b_d2v': jnp.zeros((EV,), jnp.float32), 'W_img': lin_w(EV, E), 'b_img': jnp.zeros((E,), jnp.float32), 'W_txt': lin_w(E, E), 'b_txt': jnp.zeros((E,), jnp.float32), 'W_att0': lin_w(E, E // 2), 'b_att0': jnp.zeros((E // 2,), jnp.float32), 'W_att1': lin_w(E, E // 2), 'b_att1': jnp.zeros((E // 2,), jnp.float32), 'W_f1': lin_w(2 * E, FFN), 'b_f1': jnp.zeros((FFN,), jnp.float32), 'W_f2': lin_w(FFN, E), 'b_f2': jnp.zeros((E,), jnp.float32)}
    _L1_xattn_all = _L1_xattn_setup()
    _L1_xattn_in = {k: v for k, v in _L1_xattn_all.items() if k in ('W_d2v', 'b_d2v', 'W_img', 'b_img', 'W_txt', 'b_txt', 'W_att0', 'b_att0', 'W_att1', 'b_att1', 'W_f1', 'b_f1', 'W_f2', 'b_f2')}
    del _L1_xattn_all

    def _L1_ffn_setup():
        import jax, jax.numpy as jnp
        import numpy as np
        MICRO_BATCHES = 2
        TOP_K = 2
        LN_EPS = 1e-05
        B, S, D = (4, 512, 128)
        E = 8
        DFF = 4 * D

        def _layernorm(x, g, b):
            mu = jnp.mean(x, axis=-1, keepdims=True)
            var = jnp.mean(jnp.square(x - mu), axis=-1, keepdims=True)
            return (x - mu) * jax.lax.rsqrt(var + LN_EPS) * g + b
        key = jax.random.key(seed)
        ks = jax.random.split(key, 12)
        sd = 1.0 / np.sqrt(D)
        sf = 1.0 / np.sqrt(DFF)
        return {'x': jax.random.normal(ks[0], (B, S, D), dtype=jnp.float32), 'ln_g': jnp.ones((D,), jnp.float32), 'ln_b': jnp.zeros((D,), jnp.float32), 'attn_w': jax.random.normal(ks[1], (D, D), jnp.float32) * sd, 'attn_b': jnp.zeros((D,), jnp.float32), 'gate_w': jax.random.normal(ks[2], (D, E), jnp.float32) * sd, 'w1': jax.random.normal(ks[3], (E, D, DFF), jnp.float32) * sd, 'b1': jnp.zeros((E, DFF), jnp.float32), 'w2': jax.random.normal(ks[4], (E, DFF, D), jnp.float32) * sf, 'b2': jnp.zeros((E, D), jnp.float32), 'next_w': jax.random.normal(ks[5], (D, D), jnp.float32) * sd, 'next_b': jnp.zeros((D,), jnp.float32)}
    _L1_ffn_all = _L1_ffn_setup()
    _L1_ffn_in = {k: v for k, v in _L1_ffn_all.items() if k in ('ln_g', 'ln_b', 'attn_w', 'attn_b', 'gate_w', 'w1', 'b1', 'w2', 'b2', 'next_w', 'next_b')}
    del _L1_ffn_all

    def _L2_xattn_setup():
        import jax, jax.numpy as jnp
        import numpy as np
        HEADS = 8
        DIM_HEAD = 64
        SCALE = DIM_HEAD ** (-0.5)
        key = jax.random.key(seed)
        ks = jax.random.split(key, 7)
        B, Nq, Nc = (4, 256, 256)
        Dq, Dc = (128, 96)
        inner = HEADS * DIM_HEAD
        x = jax.random.normal(ks[0], (B, Nq, Dq), dtype=jnp.float32)
        context = jax.random.normal(ks[1], (B, Nc, Dc), dtype=jnp.float32)
        Wq = jax.random.normal(ks[2], (Dq, inner), dtype=jnp.float32) * Dq ** (-0.5)
        Wk = jax.random.normal(ks[3], (Dc, inner), dtype=jnp.float32) * Dc ** (-0.5)
        Wv = jax.random.normal(ks[4], (Dc, inner), dtype=jnp.float32) * Dc ** (-0.5)
        Wo = jax.random.normal(ks[5], (inner, Dq), dtype=jnp.float32) * inner ** (-0.5)
        bo = jax.random.normal(ks[6], (Dq,), dtype=jnp.float32) * 0.01
        return {'x': x, 'context': context, 'Wq': Wq, 'Wk': Wk, 'Wv': Wv, 'Wo': Wo, 'bo': bo}
    _L2_xattn_all = _L2_xattn_setup()
    _L2_xattn_in = {k: v for k, v in _L2_xattn_all.items() if k in ('Wq', 'Wk', 'Wv', 'Wo', 'bo')}
    del _L2_xattn_all

    def _L2_ffn_setup():
        import jax, jax.numpy as jnp
        import numpy as np
        B, T, D, R, KEXP = (4, 512, 128, 64, 8)
        RH = max(D, 32)
        SCALE = 0.02

        def _fused_branch(Q_side, K_side, V, W, U, b, router_w1, router_b1, router_w2, router_b2, expert_bias):
            xV = jnp.einsum('btd,kdr->btkr', Q_side, V)
            yW = jnp.einsum('btd,kdr->btkr', K_side, W)
            cum_yW = jnp.cumsum(yW, axis=1)
            prod = xV * cum_yW
            h = jax.nn.gelu(Q_side @ router_w1.T + router_b1, approximate=False)
            logits = h @ router_w2.T + router_b2 + expert_bias
            weights = jax.nn.softmax(logits, axis=-1)
            out = jnp.einsum('btkr,kdr->btd', prod * weights[..., None], U)
            out = out + weights @ b
            n_valid = jnp.arange(1, Q_side.shape[1] + 1, dtype=Q_side.dtype)
            return out / n_valid[None, :, None]
        key = jax.random.key(seed)
        ks = jax.random.split(key, 20)
        x = jax.random.normal(ks[0], (B, T, D), dtype=jnp.float32)
        W_Q = jax.random.normal(ks[1], (D, D), dtype=jnp.float32) * (1.0 / np.sqrt(D))
        W_K = jax.random.normal(ks[2], (D, D), dtype=jnp.float32) * (1.0 / np.sqrt(D))
        W_O = jax.random.normal(ks[3], (D, D), dtype=jnp.float32) * (1.0 / np.sqrt(D))
        W_inv = jnp.eye(D, dtype=jnp.float32) + 0.01 * jax.random.normal(ks[4], (D, D), dtype=jnp.float32)
        V_fwd = jax.random.normal(ks[5], (KEXP, D, R), dtype=jnp.float32) * SCALE
        W_fwd = jax.random.normal(ks[6], (KEXP, D, R), dtype=jnp.float32) * SCALE
        U_fwd = jax.random.normal(ks[7], (KEXP, D, R), dtype=jnp.float32) * SCALE
        b_fwd = jnp.zeros((KEXP, D), dtype=jnp.float32)
        V_inv = jax.random.normal(ks[8], (KEXP, D, R), dtype=jnp.float32) * SCALE
        W_inv_exp = jax.random.normal(ks[9], (KEXP, D, R), dtype=jnp.float32) * SCALE
        U_inv = jax.random.normal(ks[10], (KEXP, D, R), dtype=jnp.float32) * SCALE
        b_inv = jnp.zeros((KEXP, D), dtype=jnp.float32)
        router_w1 = jax.random.normal(ks[11], (RH, D), dtype=jnp.float32) * (1.0 / np.sqrt(D))
        router_b1 = jnp.zeros((RH,), dtype=jnp.float32)
        router_w2 = jax.random.normal(ks[12], (KEXP, RH), dtype=jnp.float32) * (1.0 / np.sqrt(RH))
        router_b2 = jnp.zeros((KEXP,), dtype=jnp.float32)
        alpha_bi = jnp.asarray(0.5, dtype=jnp.float32)
        expert_bias = jnp.zeros((KEXP,), dtype=jnp.float32)
        return dict(x=x, W_Q=W_Q, W_K=W_K, W_O=W_O, W_inv=W_inv, V_fwd=V_fwd, W_fwd=W_fwd, U_fwd=U_fwd, b_fwd=b_fwd, V_inv=V_inv, W_inv_exp=W_inv_exp, U_inv=U_inv, b_inv=b_inv, router_w1=router_w1, router_b1=router_b1, router_w2=router_w2, router_b2=router_b2, alpha_bi=alpha_bi, expert_bias=expert_bias)
    _L2_ffn_all = _L2_ffn_setup()
    _L2_ffn_in = {k: v for k, v in _L2_ffn_all.items() if k in ('W_Q', 'W_K', 'W_O', 'W_inv', 'V_fwd', 'W_fwd', 'U_fwd', 'b_fwd', 'V_inv', 'W_inv_exp', 'U_inv', 'b_inv', 'router_w1', 'router_b1', 'router_w2', 'router_b2', 'alpha_bi', 'expert_bias')}
    del _L2_ffn_all

    def _L3_xattn_setup():
        import jax, jax.numpy as jnp
        import numpy as np
        HEADS = 16
        DIM_HEAD = 64
        key = jax.random.key(seed)
        ks = jax.random.split(key, 8)
        B, S, D = (16, 512, 128)
        K, DE = (77, 96)
        inner = HEADS * DIM_HEAD
        hidden_states = jax.random.normal(ks[0], (B, S, D), dtype=jnp.float32)
        encoder_hidden_states = jax.random.normal(ks[1], (B, K, DE), dtype=jnp.float32)
        sc_q = 1.0 / np.sqrt(D)
        sc_kv = 1.0 / np.sqrt(DE)
        sc_o = 1.0 / np.sqrt(inner)
        Wq = jax.random.normal(ks[2], (D, inner), dtype=jnp.float32) * sc_q
        Wk = jax.random.normal(ks[3], (DE, inner), dtype=jnp.float32) * sc_kv
        Wv = jax.random.normal(ks[4], (DE, inner), dtype=jnp.float32) * sc_kv
        Wo = jax.random.normal(ks[5], (inner, D), dtype=jnp.float32) * sc_o
        bo = jax.random.normal(ks[6], (D,), dtype=jnp.float32) * 0.01
        return {'hidden_states': hidden_states, 'encoder_hidden_states': encoder_hidden_states, 'Wq': Wq, 'Wk': Wk, 'Wv': Wv, 'Wo': Wo, 'bo': bo}
    _L3_xattn_all = _L3_xattn_setup()
    _L3_xattn_in = {k: v for k, v in _L3_xattn_all.items() if k in ('Wq', 'Wk', 'Wv', 'Wo', 'bo')}
    del _L3_xattn_all

    def _L3_ffn_setup():
        import jax, jax.numpy as jnp
        import numpy as np
        TOP_K = 2
        key = jax.random.key(seed)
        ks = jax.random.split(key, 6)
        B, S, D, E = (8, 512, 128, 8)
        s = 1.0 / np.sqrt(D)
        return {'x': jax.random.normal(ks[0], (B, S, D), dtype=jnp.float32), 'Wr': jax.random.normal(ks[1], (D, E), dtype=jnp.float32) * s, 'br': jnp.zeros((E,), dtype=jnp.float32), 'W1': jax.random.normal(ks[2], (E, D, D), dtype=jnp.float32) * s, 'b1': jnp.zeros((E, D), dtype=jnp.float32), 'W2': jax.random.normal(ks[3], (E, D, D), dtype=jnp.float32) * s, 'b2': jnp.zeros((E, D), dtype=jnp.float32)}
    _L3_ffn_all = _L3_ffn_setup()
    _L3_ffn_in = {k: v for k, v in _L3_ffn_all.items() if k in ('Wr', 'br', 'W1', 'b1', 'W2', 'b2')}
    del _L3_ffn_all
    return {'x': x, 'ctx_768': ctx_768, 'L0_xattn_Wq': _L0_xattn_in['Wq'], 'L0_xattn_bq': _L0_xattn_in['bq'], 'L0_xattn_Wk': _L0_xattn_in['Wk'], 'L0_xattn_bk': _L0_xattn_in['bk'], 'L0_xattn_Wv': _L0_xattn_in['Wv'], 'L0_xattn_bv': _L0_xattn_in['bv'], 'L0_xattn_Wo': _L0_xattn_in['Wo'], 'L0_xattn_bo': _L0_xattn_in['bo'], 'L0_xattn_ln_gamma': _L0_xattn_in['ln_gamma'], 'L0_xattn_ln_beta': _L0_xattn_in['ln_beta'], 'L0_ffn_ln_g': _L0_ffn_in['ln_g'], 'L0_ffn_ln_b': _L0_ffn_in['ln_b'], 'L0_ffn_rW': _L0_ffn_in['rW'], 'L0_ffn_rb': _L0_ffn_in['rb'], 'L0_ffn_W1': _L0_ffn_in['W1'], 'L0_ffn_b1': _L0_ffn_in['b1'], 'L0_ffn_W2': _L0_ffn_in['W2'], 'L0_ffn_b2': _L0_ffn_in['b2'], 'L1_xattn_W_d2v': _L1_xattn_in['W_d2v'], 'L1_xattn_b_d2v': _L1_xattn_in['b_d2v'], 'L1_xattn_W_img': _L1_xattn_in['W_img'], 'L1_xattn_b_img': _L1_xattn_in['b_img'], 'L1_xattn_W_txt': _L1_xattn_in['W_txt'], 'L1_xattn_b_txt': _L1_xattn_in['b_txt'], 'L1_xattn_W_att0': _L1_xattn_in['W_att0'], 'L1_xattn_b_att0': _L1_xattn_in['b_att0'], 'L1_xattn_W_att1': _L1_xattn_in['W_att1'], 'L1_xattn_b_att1': _L1_xattn_in['b_att1'], 'L1_xattn_W_f1': _L1_xattn_in['W_f1'], 'L1_xattn_b_f1': _L1_xattn_in['b_f1'], 'L1_xattn_W_f2': _L1_xattn_in['W_f2'], 'L1_xattn_b_f2': _L1_xattn_in['b_f2'], 'L1_ffn_ln_g': _L1_ffn_in['ln_g'], 'L1_ffn_ln_b': _L1_ffn_in['ln_b'], 'L1_ffn_attn_w': _L1_ffn_in['attn_w'], 'L1_ffn_attn_b': _L1_ffn_in['attn_b'], 'L1_ffn_gate_w': _L1_ffn_in['gate_w'], 'L1_ffn_w1': _L1_ffn_in['w1'], 'L1_ffn_b1': _L1_ffn_in['b1'], 'L1_ffn_w2': _L1_ffn_in['w2'], 'L1_ffn_b2': _L1_ffn_in['b2'], 'L1_ffn_next_w': _L1_ffn_in['next_w'], 'L1_ffn_next_b': _L1_ffn_in['next_b'], 'L2_xattn_Wq': _L2_xattn_in['Wq'], 'L2_xattn_Wk': _L2_xattn_in['Wk'], 'L2_xattn_Wv': _L2_xattn_in['Wv'], 'L2_xattn_Wo': _L2_xattn_in['Wo'], 'L2_xattn_bo': _L2_xattn_in['bo'], 'L2_ffn_W_Q': _L2_ffn_in['W_Q'], 'L2_ffn_W_K': _L2_ffn_in['W_K'], 'L2_ffn_W_O': _L2_ffn_in['W_O'], 'L2_ffn_W_inv': _L2_ffn_in['W_inv'], 'L2_ffn_V_fwd': _L2_ffn_in['V_fwd'], 'L2_ffn_W_fwd': _L2_ffn_in['W_fwd'], 'L2_ffn_U_fwd': _L2_ffn_in['U_fwd'], 'L2_ffn_b_fwd': _L2_ffn_in['b_fwd'], 'L2_ffn_V_inv': _L2_ffn_in['V_inv'], 'L2_ffn_W_inv_exp': _L2_ffn_in['W_inv_exp'], 'L2_ffn_U_inv': _L2_ffn_in['U_inv'], 'L2_ffn_b_inv': _L2_ffn_in['b_inv'], 'L2_ffn_router_w1': _L2_ffn_in['router_w1'], 'L2_ffn_router_b1': _L2_ffn_in['router_b1'], 'L2_ffn_router_w2': _L2_ffn_in['router_w2'], 'L2_ffn_router_b2': _L2_ffn_in['router_b2'], 'L2_ffn_alpha_bi': _L2_ffn_in['alpha_bi'], 'L2_ffn_expert_bias': _L2_ffn_in['expert_bias'], 'L3_xattn_Wq': _L3_xattn_in['Wq'], 'L3_xattn_Wk': _L3_xattn_in['Wk'], 'L3_xattn_Wv': _L3_xattn_in['Wv'], 'L3_xattn_Wo': _L3_xattn_in['Wo'], 'L3_xattn_bo': _L3_xattn_in['bo'], 'L3_ffn_Wr': _L3_ffn_in['Wr'], 'L3_ffn_br': _L3_ffn_in['br'], 'L3_ffn_W1': _L3_ffn_in['W1'], 'L3_ffn_b1': _L3_ffn_in['b1'], 'L3_ffn_W2': _L3_ffn_in['W2'], 'L3_ffn_b2': _L3_ffn_in['b2']}

def reference(x, ctx_768, L0_xattn_Wq, L0_xattn_bq, L0_xattn_Wk, L0_xattn_bk, L0_xattn_Wv, L0_xattn_bv, L0_xattn_Wo, L0_xattn_bo, L0_xattn_ln_gamma, L0_xattn_ln_beta, L0_ffn_ln_g, L0_ffn_ln_b, L0_ffn_rW, L0_ffn_rb, L0_ffn_W1, L0_ffn_b1, L0_ffn_W2, L0_ffn_b2, L1_xattn_W_d2v, L1_xattn_b_d2v, L1_xattn_W_img, L1_xattn_b_img, L1_xattn_W_txt, L1_xattn_b_txt, L1_xattn_W_att0, L1_xattn_b_att0, L1_xattn_W_att1, L1_xattn_b_att1, L1_xattn_W_f1, L1_xattn_b_f1, L1_xattn_W_f2, L1_xattn_b_f2, L1_ffn_ln_g, L1_ffn_ln_b, L1_ffn_attn_w, L1_ffn_attn_b, L1_ffn_gate_w, L1_ffn_w1, L1_ffn_b1, L1_ffn_w2, L1_ffn_b2, L1_ffn_next_w, L1_ffn_next_b, L2_xattn_Wq, L2_xattn_Wk, L2_xattn_Wv, L2_xattn_Wo, L2_xattn_bo, L2_ffn_W_Q, L2_ffn_W_K, L2_ffn_W_O, L2_ffn_W_inv, L2_ffn_V_fwd, L2_ffn_W_fwd, L2_ffn_U_fwd, L2_ffn_b_fwd, L2_ffn_V_inv, L2_ffn_W_inv_exp, L2_ffn_U_inv, L2_ffn_b_inv, L2_ffn_router_w1, L2_ffn_router_b1, L2_ffn_router_w2, L2_ffn_router_b2, L2_ffn_alpha_bi, L2_ffn_expert_bias, L3_xattn_Wq, L3_xattn_Wk, L3_xattn_Wv, L3_xattn_Wo, L3_xattn_bo, L3_ffn_Wr, L3_ffn_br, L3_ffn_W1, L3_ffn_b1, L3_ffn_W2, L3_ffn_b2):
    import jax
    import jax.numpy as jnp

    def _L0_xattn_ref(query, key, value, Wq, bq, Wk, bk, Wv, bv, Wo, bo, ln_gamma, ln_beta):
        import jax, jax.numpy as jnp
        import numpy as np
        QUERY_DIM, KV_DIM, EMBED_DIM, NUM_HEADS = (128, 96, 128, 16)
        HEAD_DIM = EMBED_DIM // NUM_HEADS
        SCALE = HEAD_DIM ** (-0.5)
        LN_EPS = 1e-05

        def _l2norm(x, eps=1e-12):
            n = jnp.sqrt(jnp.sum(x * x, axis=-1, keepdims=True))
            return x / jnp.maximum(n, eps)
        B, Nq, _ = query.shape
        Nk = key.shape[1]
        Qp = query @ Wq + bq
        K = _l2norm(key @ Wk + bk)
        V = value @ Wv + bv
        Q = _l2norm(Qp)
        Q = Q.reshape(B, Nq, NUM_HEADS, HEAD_DIM).transpose(0, 2, 1, 3)
        K = K.reshape(B, Nk, NUM_HEADS, HEAD_DIM).transpose(0, 2, 1, 3)
        V = V.reshape(B, Nk, NUM_HEADS, HEAD_DIM).transpose(0, 2, 1, 3)
        scores = jnp.einsum('bhqd,bhkd->bhqk', Q, K) * SCALE
        attn = jax.nn.softmax(scores, axis=-1)
        out = jnp.einsum('bhqk,bhkd->bhqd', attn, V)
        out = out.transpose(0, 2, 1, 3).reshape(B, Nq, EMBED_DIM)
        out = out @ Wo + bo
        x = out + Qp
        mu = jnp.mean(x, axis=-1, keepdims=True)
        var = jnp.mean((x - mu) ** 2, axis=-1, keepdims=True)
        return (x - mu) / jnp.sqrt(var + LN_EPS) * ln_gamma + ln_beta

    def _L0_ffn_ref(x, ln_g, ln_b, rW, rb, W1, b1, W2, b2):
        import jax, jax.numpy as jnp
        import numpy as np
        E = 8
        TOP_K = 2
        LN_EPS = 1e-05

        def _layernorm(x, g, b):
            mu = jnp.mean(x, axis=-1, keepdims=True)
            var = jnp.var(x, axis=-1, keepdims=True)
            return (x - mu) * jax.lax.rsqrt(var + LN_EPS) * g + b
        z = _layernorm(x, ln_g, ln_b)
        logits = jnp.einsum('bth,he->bte', z, rW) + rb
        probs = jax.nn.softmax(logits, axis=-1)
        topv, topi = jax.lax.top_k(probs, TOP_K)
        mask = jnp.sum(jax.nn.one_hot(topi, E, dtype=probs.dtype) * topv[..., None], axis=-2)
        denom = jnp.maximum(jnp.sum(mask, axis=-1, keepdims=True), 1e-08)
        w = mask / denom
        hid = jax.nn.gelu(jnp.einsum('bth,ehf->btef', z, W1) + b1, approximate=False)
        outs = jnp.einsum('btef,efh->bteh', hid, W2) + b2
        mixed = jnp.sum(outs * w[..., None], axis=2)
        return x + mixed

    def _L1_xattn_ref(text_embeddings, dinov2_features, W_d2v, b_d2v, W_img, b_img, W_txt, b_txt, W_att0, b_att0, W_att1, b_att1, W_f1, b_f1, W_f2, b_f2):
        import jax, jax.numpy as jnp
        import numpy as np
        import math
        E = 128
        EV = 128
        FFN = 512
        DINO = 96
        B, S, P = (64, 64, 32)

        def bitnet_linear(x, W, b):
            w_scale = jnp.maximum(jnp.mean(jnp.abs(W)), 1e-05)
            qW = jnp.sign(W) * (jnp.abs(W) > 0.5 * w_scale).astype(W.dtype)
            i_scale = jnp.maximum(jnp.max(jnp.abs(x)), 1e-08) / 127.0
            qx = jnp.clip(jnp.round(x / i_scale), -128.0, 127.0)
            out = jnp.einsum('...i,oi->...o', qx, qW) * (w_scale * i_scale)
            return out + b
        b, s, e = text_embeddings.shape
        vis = bitnet_linear(dinov2_features, W_d2v, b_d2v)
        image_embeds = bitnet_linear(vis, W_img, b_img)
        fused = bitnet_linear(text_embeddings, W_txt, b_txt)
        inv_sqrt_e = 1.0 / math.sqrt(e)
        for Wa, ba in ((W_att0, b_att0), (W_att1, b_att1)):
            kv = bitnet_linear(image_embeds, Wa, ba)
            k = jnp.concatenate([kv, kv], axis=-1)
            scores = jnp.einsum('bse,bpe->bsp', fused, k) * inv_sqrt_e
            attn = jax.nn.softmax(scores, axis=-1)
            fused = fused + 0.1 * jnp.einsum('bsp,bpe->bse', attn, k)
        avg_img = jnp.mean(image_embeds, axis=1, keepdims=True)
        concatenated = jnp.concatenate([fused, jnp.broadcast_to(avg_img, (b, s, e))], axis=-1)
        h = jax.nn.relu(bitnet_linear(concatenated, W_f1, b_f1))
        return bitnet_linear(h, W_f2, b_f2)

    def _L1_ffn_ref(x, ln_g, ln_b, attn_w, attn_b, gate_w, w1, b1, w2, b2, next_w, next_b):
        import jax, jax.numpy as jnp
        import numpy as np
        MICRO_BATCHES = 2
        TOP_K = 2
        LN_EPS = 1e-05
        B, S, D = (4, 512, 128)
        E = 8
        DFF = 4 * D

        def _layernorm(x, g, b):
            mu = jnp.mean(x, axis=-1, keepdims=True)
            var = jnp.mean(jnp.square(x - mu), axis=-1, keepdims=True)
            return (x - mu) * jax.lax.rsqrt(var + LN_EPS) * g + b
        Bx, Sx, Dx = x.shape
        N = Bx * Sx
        x_flat = x.reshape(N, Dx)
        x_attn = _layernorm(x_flat, ln_g, ln_b) @ attn_w + attn_b + x_flat
        logits = x_attn @ gate_w
        _ = jax.lax.top_k(logits, TOP_K)
        tpe = N // (MICRO_BATCHES * E)
        g = x_attn.reshape(MICRO_BATCHES, E, tpe, Dx)
        h = jax.nn.gelu(jnp.einsum('metd,edf->metf', g, w1) + b1[None, :, None, :], approximate=False)
        y = jnp.einsum('metf,efd->metd', h, w2) + b2[None, :, None, :]
        out = jax.nn.gelu(y @ next_w + next_b, approximate=False)
        return out.reshape(Bx, Sx, Dx)

    def _L2_xattn_ref(x, context, Wq, Wk, Wv, Wo, bo):
        import jax, jax.numpy as jnp
        import numpy as np
        HEADS = 8
        DIM_HEAD = 64
        SCALE = DIM_HEAD ** (-0.5)
        B, Nq, _ = x.shape
        q = (x @ Wq).reshape(B, Nq, HEADS, DIM_HEAD)
        k = (context @ Wk).reshape(B, context.shape[1], HEADS, DIM_HEAD)
        v = (context @ Wv).reshape(B, context.shape[1], HEADS, DIM_HEAD)
        sim = jnp.einsum('bihd,bjhd->bhij', q, k) * SCALE
        attn = jax.nn.softmax(sim, axis=-1)
        out = jnp.einsum('bhij,bjhd->bihd', attn, v)
        out = out.reshape(B, Nq, HEADS * DIM_HEAD)
        return out @ Wo + bo

    def _L2_ffn_ref(x, W_Q, W_K, W_O, W_inv, V_fwd, W_fwd, U_fwd, b_fwd, V_inv, W_inv_exp, U_inv, b_inv, router_w1, router_b1, router_w2, router_b2, alpha_bi, expert_bias):
        import jax, jax.numpy as jnp
        import numpy as np
        B, T, D, R, KEXP = (4, 512, 128, 64, 8)
        RH = max(D, 32)
        SCALE = 0.02

        def _fused_branch(Q_side, K_side, V, W, U, b, router_w1, router_b1, router_w2, router_b2, expert_bias):
            xV = jnp.einsum('btd,kdr->btkr', Q_side, V)
            yW = jnp.einsum('btd,kdr->btkr', K_side, W)
            cum_yW = jnp.cumsum(yW, axis=1)
            prod = xV * cum_yW
            h = jax.nn.gelu(Q_side @ router_w1.T + router_b1, approximate=False)
            logits = h @ router_w2.T + router_b2 + expert_bias
            weights = jax.nn.softmax(logits, axis=-1)
            out = jnp.einsum('btkr,kdr->btd', prod * weights[..., None], U)
            out = out + weights @ b
            n_valid = jnp.arange(1, Q_side.shape[1] + 1, dtype=Q_side.dtype)
            return out / n_valid[None, :, None]
        Q = x @ W_Q.T
        K = x @ W_K.T
        invQ = Q @ W_inv.T
        invK = K @ W_inv.T
        fwd = _fused_branch(Q, K, V_fwd, W_fwd, U_fwd, b_fwd, router_w1, router_b1, router_w2, router_b2, expert_bias)
        inv = _fused_branch(invQ, invK, W_inv_exp, V_inv, U_inv, b_inv, router_w1, router_b1, router_w2, router_b2, expert_bias)
        out = fwd + alpha_bi * inv
        return out @ W_O.T

    def _L3_xattn_ref(hidden_states, encoder_hidden_states, Wq, Wk, Wv, Wo, bo):
        import jax, jax.numpy as jnp
        import numpy as np
        HEADS = 16
        DIM_HEAD = 64
        B, S, D = hidden_states.shape
        K = encoder_hidden_states.shape[1]
        H, Dh = (HEADS, DIM_HEAD)
        scale = 1.0 / np.sqrt(Dh)
        q = hidden_states @ Wq
        k = encoder_hidden_states @ Wk
        v = encoder_hidden_states @ Wv
        q = q.reshape(B, S, H, Dh).transpose(0, 2, 1, 3)
        k = k.reshape(B, K, H, Dh).transpose(0, 2, 1, 3)
        v = v.reshape(B, K, H, Dh).transpose(0, 2, 1, 3)
        scores = jnp.einsum('bhsd,bhkd->bhsk', q, k) * scale
        probs = jax.nn.softmax(scores, axis=-1)
        out = jnp.einsum('bhsk,bhkd->bhsd', probs, v)
        out = out.transpose(0, 2, 1, 3).reshape(B, S, H * Dh)
        out = out @ Wo + bo
        return out

    def _L3_ffn_ref(x, Wr, br, W1, b1, W2, b2):
        import jax, jax.numpy as jnp
        import numpy as np
        TOP_K = 2
        k = TOP_K
        scores0 = x[:, 0, :] @ Wr + br
        _, idx = jax.lax.top_k(scores0, k)
        W1g, b1g = (W1[idx], b1[idx])
        W2g, b2g = (W2[idx], b2[idx])
        h = jnp.einsum('bsd,bkde->bkse', x, W1g) + b1g[:, :, None, :]
        h = jax.nn.gelu(h, approximate=False)
        o = jnp.einsum('bkse,bkef->bksf', h, W2g) + b2g[:, :, None, :]
        return jnp.sum(o, axis=1) / k
    x = x + _L0_xattn_ref(_layernorm(x, axis=-1), ctx_768, ctx_768, L0_xattn_Wq, L0_xattn_bq, L0_xattn_Wk, L0_xattn_bk, L0_xattn_Wv, L0_xattn_bv, L0_xattn_Wo, L0_xattn_bo, L0_xattn_ln_gamma, L0_xattn_ln_beta)
    x = x + _L0_ffn_ref(_layernorm(x, axis=-1), L0_ffn_ln_g, L0_ffn_ln_b, L0_ffn_rW, L0_ffn_rb, L0_ffn_W1, L0_ffn_b1, L0_ffn_W2, L0_ffn_b2)
    x = x + _L1_xattn_ref(_layernorm(x, axis=-1), ctx_768, L1_xattn_W_d2v, L1_xattn_b_d2v, L1_xattn_W_img, L1_xattn_b_img, L1_xattn_W_txt, L1_xattn_b_txt, L1_xattn_W_att0, L1_xattn_b_att0, L1_xattn_W_att1, L1_xattn_b_att1, L1_xattn_W_f1, L1_xattn_b_f1, L1_xattn_W_f2, L1_xattn_b_f2)
    x = x + _L1_ffn_ref(_layernorm(x, axis=-1), L1_ffn_ln_g, L1_ffn_ln_b, L1_ffn_attn_w, L1_ffn_attn_b, L1_ffn_gate_w, L1_ffn_w1, L1_ffn_b1, L1_ffn_w2, L1_ffn_b2, L1_ffn_next_w, L1_ffn_next_b)
    x = x + _L2_xattn_ref(_layernorm(x, axis=-1), ctx_768, L2_xattn_Wq, L2_xattn_Wk, L2_xattn_Wv, L2_xattn_Wo, L2_xattn_bo)
    x = x + _L2_ffn_ref(_layernorm(x, axis=-1), L2_ffn_W_Q, L2_ffn_W_K, L2_ffn_W_O, L2_ffn_W_inv, L2_ffn_V_fwd, L2_ffn_W_fwd, L2_ffn_U_fwd, L2_ffn_b_fwd, L2_ffn_V_inv, L2_ffn_W_inv_exp, L2_ffn_U_inv, L2_ffn_b_inv, L2_ffn_router_w1, L2_ffn_router_b1, L2_ffn_router_w2, L2_ffn_router_b2, L2_ffn_alpha_bi, L2_ffn_expert_bias)
    x = x + _L3_xattn_ref(_layernorm(x, axis=-1), ctx_768, L3_xattn_Wq, L3_xattn_Wk, L3_xattn_Wv, L3_xattn_Wo, L3_xattn_bo)
    x = x + _L3_ffn_ref(_layernorm(x, axis=-1), L3_ffn_Wr, L3_ffn_br, L3_ffn_W1, L3_ffn_b1, L3_ffn_W2, L3_ffn_b2)
    return x

_drawn_inputs = setup_inputs


def setup_inputs(seed=0):
    import zlib

    import numpy as np

    out = dict(_drawn_inputs(seed))
    spreads = {'L0_xattn_bq': (0.0, 0.1),
     'L0_xattn_bk': (0.0, 0.1),
     'L0_xattn_bv': (0.0, 0.1),
     'L0_xattn_bo': (0.0, 0.1),
     'L0_xattn_ln_gamma': (1.0, 0.2),
     'L0_xattn_ln_beta': (0.0, 0.1),
     'L0_ffn_ln_g': (1.0, 0.2),
     'L0_ffn_ln_b': (0.0, 0.1),
     'L0_ffn_rb': (0.0, 0.1),
     'L0_ffn_b1': (0.0, 0.1),
     'L0_ffn_b2': (0.0, 0.1),
     'L1_xattn_b_d2v': (0.0, 0.1),
     'L1_xattn_b_img': (0.0, 0.1),
     'L1_xattn_b_txt': (0.0, 0.1),
     'L1_xattn_b_att0': (0.0, 0.1),
     'L1_xattn_b_att1': (0.0, 0.1),
     'L1_xattn_b_f1': (0.0, 0.1),
     'L1_xattn_b_f2': (0.0, 0.1),
     'L1_ffn_ln_g': (1.0, 0.2),
     'L1_ffn_ln_b': (0.0, 0.1),
     'L1_ffn_attn_b': (0.0, 0.1),
     'L1_ffn_b1': (0.0, 0.1),
     'L1_ffn_b2': (0.0, 0.1),
     'L1_ffn_next_b': (0.0, 0.1),
     'L2_ffn_b_fwd': (0.0, 0.1),
     'L2_ffn_b_inv': (0.0, 0.1),
     'L2_ffn_router_b1': (0.0, 0.1),
     'L2_ffn_router_b2': (0.0, 0.1),
     'L2_ffn_expert_bias': (0.0, 0.1),
     'L3_ffn_br': (0.0, 0.1),
     'L3_ffn_b1': (0.0, 0.1),
     'L3_ffn_b2': (0.0, 0.1)}
    factors = {}
    for name, (base, spread) in spreads.items():
        noise = np.random.default_rng([zlib.crc32(name.encode()), seed]).standard_normal(out[name].shape)
        drawn = base * np.exp(spread * noise) if base else spread * noise
        out[name] = jnp.asarray(drawn.astype(out[name].dtype))
    for name, factor in factors.items():
        out[name] = (out[name] * factor).astype(out[name].dtype)
    return out
```

```python
from collections import namedtuple
from contextlib import ExitStack

import concourse.bass as bass
import numpy as np
from concourse import mybir

F32 = mybir.dt.float32
BF16 = mybir.dt.bfloat16
I32 = mybir.dt.int32
ALU = mybir.AluOpType
ACT = mybir.ActivationFunctionType
AX = mybir.AxisListType

P = 128
B, T, D = 8, 256, 128
S, DC = 512, 96
N = B * T
TILES = N // P
TPB = T // P
KT = S // P
EPS = 1e-5
E = 8
MAGIC = 12582912.0

C_ID = 0
C_HEAD = C_ID + P
C_REV = C_HEAD + 16
C_INVN = C_REV + E
C_SEL = C_INVN + TPB
C_ALL = C_SEL + 4 * P



def shape_constants():
    c = np.zeros((P, C_ALL), np.float32)
    c[:, C_ID:C_ID + P] = np.eye(P)
    for p in range(P):
        c[p, C_HEAD + p // 8] = 1
        for i in range(TPB):
            c[p, C_INVN + i] = 1.0 / (i * P + p + 1)
    c[:, C_REV:C_REV + E] = E - np.arange(E)
    for k in range(E):
        lo = C_SEL + (k // 2) * P + (k % 2) * 64
        c[k, lo:lo + 64] = 1
    return c


class Steps:

    def __init__(self, engine, sem, per_turn=0):
        self.engine, self.sem, self.per_turn = engine, sem, per_turn
        self.turn, self.done = 0, 0

    def begin(self, turn):
        self.turn, self.done = turn, 0

    def add(self, instruction):
        instruction.then_inc(self.sem, 1)
        self.done += 1

    def settle(self):
        self.engine.wait_ge(self.sem, self.turn * self.per_turn + self.done)

    def end(self):
        assert self.done == self.per_turn, (self.done, self.per_turn)


class Scope:

    to_clear = []

    def __init__(self, nc, ctx, name):
        self.nc, self.ctx, self.name = nc, ctx, name

    def sb(self, name, shape, dtype=F32):
        return self.ctx.enter_context(self.nc.sbuf_tensor(f"{self.name}_{name}", shape, dtype))

    def ps(self, name, shape=(P, 512), dtype=F32):
        return self.ctx.enter_context(self.nc.psum_tensor(f"{self.name}_{name}_ps", list(shape), dtype))

    def sem(self, name):
        sem = self.ctx.enter_context(self.nc.semaphore(f"{self.name}_{name}"))
        Scope.to_clear.append(sem.num)
        return sem

    def sems(self, names):
        return namedtuple("Semaphores", names)(*[self.sem(n) for n in names])

    def block(self):
        return self.ctx.enter_context(self.nc.Block())


def clear_semaphores(nc):
    nums = sorted(set(Scope.to_clear))
    Scope.to_clear.clear()
    runs = []
    for n in nums:
        if runs and runs[-1][1] == n:
            runs[-1][1] = n + 1
        else:
            runs.append([n, n + 1])
    with nc.Block() as block:
        @block.gpsimd
        def _(e):
            for first, end in runs:
                e.sem_clear(range(first, end))


class Shared:
    pass


def bcast(ap, shape):
    return ap.to_broadcast(shape)



class Front:

    def __init__(self, s, g, tile=None, tiles=TPB, twice=False):
        self.g, self.tiles, self.twice = g, tiles, twice
        self.tile = tile or (lambda b, i: g.x[:, TPB * b + i, :])
        norms = 2 if twice else 1
        self.steps = 2 * tiles * norms
        self.stats = s.sb("ln_stats", [P, tiles, 6])
        self.mv = s.sb("ln_mean_var", [P, tiles, 2])
        self.held = s.sb("ln_held", [P, 1])
        self.var = s.sb("ln_var_eps", [P, tiles])
        self.rstd = s.sb("ln_rstd", [P, tiles])
        self.outer = s.sb("ln_outer", [P, tiles, D]) if twice else None
        self.z = s.sb("ln_z", [P, tiles, D])
        self.norms = norms
        self.var_ready = s.sem("var_ready")
        self.rstd_ready = s.sem("rstd_ready")
        self.outer_ready = s.sem("outer_ready") if twice else None
        self.z_ready = s.sem("z_ready")
        self.z_turned = s.sem("z_turned")

    def _norm(self, e, b, steps, turn, source, out, ready):
        for i in range(self.tiles):
            steps.add(e.bn_stats(self.stats[:, i, :], source(i)))
        steps.settle()
        e.memset(self.held[:, :], 0.0)
        for i in range(self.tiles):
            steps.add(e.bn_aggr(self.mv[:, i, :], self.stats[:, i, :]))
        steps.settle()
        e.tensor_scalar(self.var[:, :], self.mv[:, :, 1], EPS, None, ALU.add).then_inc(self.var_ready, 1)
        e.wait_ge(self.rstd_ready, self.norms * b + turn + 1)
        for i in range(self.tiles):
            e.tensor_scalar(out[:, i, :], source(i), self.mv[:, i, 0:1], self.rstd[:, i:i + 1],
                            ALU.subtract, ALU.mult).then_inc(ready, 1)

    def vector(self, e, b, steps):
        if self.twice:
            self._norm(e, b, steps, 0, lambda i: self.tile(b, i), self.outer, self.outer_ready)
            e.wait_ge(self.outer_ready, self.tiles * (b + 1))
            self._norm(e, b, steps, 1, lambda i: self.outer[:, i, :], self.z, self.z_ready)
        else:
            self._norm(e, b, steps, 0, lambda i: self.tile(b, i), self.z, self.z_ready)

    def gpsimd(self, e, b):
        for n in range(self.norms):
            e.wait_ge(self.var_ready, self.norms * b + n + 1)
            e.tensor_tensor(self.rstd[:, :], self.var[:, :], self.g.neg_half[:, 0:self.tiles],
                            ALU.pow).then_inc(self.rstd_ready, 1)

    def tensor(self, e, b, out):
        e.wait_ge(self.z_ready, self.tiles * (b + 1))
        for i in range(self.tiles):
            last = e.transpose(out[:, i * P:(i + 1) * P], self.z[:, i, :], self.g.ident)
        last.then_inc(self.z_turned, 1)



def load_stage(nc, g, a):
    with ExitStack() as ctx:
        s = Scope(nc, ctx, "load")
        rows = s.sb("ctx_rows", [P, B * KT, DC])
        turned = [s.ps(f"turned{i}") for i in range(2)]
        ctx_loaded = s.sem("ctx_loaded")
        const_loaded = s.sem("const_loaded")
        ctx_turned = s.sem("ctx_turned")
        ctx_kept = s.sem("ctx_kept")
        filled = s.sem("filled")
        block = s.block()

        @block.sync
        def _(sp):
            sp.dma_start(g.const[:, :], a["constants"]).then_inc(const_loaded, 16)
            sp.dma_start(rows[:, :, :].rearrange("p (b t) d -> p b (t d)", t=KT),
                         a["ctx_768"].rearrange("b (p t) d -> p b (t d)", t=KT)).then_inc(ctx_loaded, 16)
            sp.dma_start(g.x[:, :, :], a["x"].rearrange("b (i p) d -> p (b i) d", p=P)).then_inc(const_loaded, 16)
            for dst, src in g.loads_first:
                sp.dma_start(dst, src).then_inc(const_loaded, 16)
            for dst, src in g.loads:
                sp.dma_start(dst, src).then_inc(g.weights_loaded, 16)
            sp.wait_ge(const_loaded, 16 * (2 + len(g.loads_first)))

        @block.gpsimd
        def _(e):
            e.memset(g.neg_half[:, :], -0.5).then_inc(filled, 1)
            e.memset(g.ones[:, :], 1.0).then_inc(filled, 1)
            e.memset(g.magic[:, :], MAGIC).then_inc(filled, 1)
            e.wait_ge(filled, 3)
            e.memset(g.ctxT[DC:DC + 1, :], 1.0).then_inc(filled, 1)
            e.wait_ge(filled, 4)

        @block.tensor
        def _(e):
            e.wait_ge(const_loaded, 16 * (2 + len(g.loads_first)))
            e.wait_ge(ctx_loaded, 16)
            for b in range(B):
                if b >= 2:
                    e.wait_ge(ctx_kept, b - 1)
                for t in range(KT):
                    last = e.transpose(turned[b % 2][0:DC, t * P:(t + 1) * P], rows[:, KT * b + t, :], g.ident)
                last.then_inc(ctx_turned, 1)
            e.wait_ge(ctx_kept, B - 1)
            e.transpose(turned[0][:, 0:g.vectors_used], g.vector_rows[0:g.vectors_used, :],
                        g.ident[0:g.vectors_used, 0:g.vectors_used]).then_inc(ctx_turned, 1)

        @block.scalar
        def _(e):
            for b in range(B):
                e.wait_ge(ctx_turned, b + 1)
                e.activation(g.ctxT[0:DC, b * S:(b + 1) * S], turned[b % 2][0:DC, :], ACT.Copy).then_inc(ctx_kept, 1)
            e.wait_ge(ctx_turned, B + 1)
            e.activation(g.vectors[:, 0:g.vectors_used], turned[0][:, 0:g.vectors_used], ACT.Copy).then_inc(ctx_kept, 1)
            e.wait_ge(ctx_kept, B + 1)



def l0_attention(nc, g, a):
    HEADS, HD = 16, 8
    SCALE = HD ** -0.5
    GROUPS, GH = 4, 4
    STEPS = GROUPS * KT
    with ExitStack() as ctx:
        s = Scope(nc, ctx, "l0a")
        front = Front(s, g)
        zT = s.sb("zT", [P, T])
        cT = s.sb("cT", [DC + 1, S])
        square = s.sb("square", [P, KT + TPB, D])
        sumsq = s.sb("sumsq", [P, KT + TPB])
        clamped = s.sb("clamped", [P, KT + TPB])
        rnorm = s.sb("rnorm", [P, KT + TPB])
        qp = s.sb("qp", [P, TPB, D])
        kn = s.sb("kn", [P, KT, D])
        qn = s.sb("qn", [P, TPB, D])
        kT = s.sb("kT", [P, S])
        qT = s.sb("qT", [P, T])
        qm = s.sb("qm", [P, HEADS, T])
        v = s.sb("v", [P, KT, HEADS, 32])
        prob = [s.sb(f"prob{i}", [P, GH * T]) for i in range(2)]
        pv = s.sb("pv", [P, T])
        rsum = s.sb("rsum", [P, TPB, GH])
        o = s.sb("o", [P, TPB, D])
        oT = s.sb("oT", [P, T])
        y = s.sb("y", [P, TPB, D])
        stats = s.sb("y_stats", [P, TPB, 6])
        mv = s.sb("y_mean_var", [P, TPB, 2])
        yvar = s.sb("y_var", [P, TPB])
        yrstd = s.sb("y_rstd", [P, TPB])
        turn = s.ps("turn")
        kps = s.ps("kps")
        qps = s.ps("qps")
        vps = s.ps("vps")
        sc = [s.ps(f"scores{i}", (P, 2 * 512)) for i in range(2)]
        pvps = [kps, vps]

        names = ["v_padded", "c_fixed", "zT_ready", "kqv_projected", "qp_ready", "v_ready", "sumsq_ready",
                 "sumsq_clamped", "norm_ready", "kn_ready", "qn_ready", "kn_turned", "kT_ready", "qn_turned", "qT_ready",
                 "qm_ready", "scores_ready", "prob_ready", "pv_ready", "pv_kept", "pv_turned", "o_ready",
                 "o_turned", "oT_ready", "out_ready", "y_kept", "yvar_ready", "yrstd_ready", "x_updated", "steps"]
        m = s.sems(names)
        block = s.block()

        @block.gpsimd
        def _(e):
            e.memset(v[:, :, :, :], 0.0).then_inc(m.v_padded, 1)
            e.wait_ge(m.v_padded, 1)
            e.memset(v[:, :, :, HD:HD + 1], 1.0).then_inc(m.v_padded, 1)
            with e.Fori(0, B) as b:
                e.wait_ge(m.v_ready, b)
                e.tensor_copy(cT[:, :], g.ctxT[:, bass.ds(b * S, S)]).then_inc(m.c_fixed, 1)
                front.gpsimd(e, b)
                e.wait_ge(m.sumsq_clamped, b + 1)
                e.tensor_tensor(rnorm[:, :], clamped[:, :], g.neg_half[:, 0:KT + TPB], ALU.pow).then_inc(m.norm_ready, 1)
                e.wait_ge(m.yvar_ready, b + 1)
                e.tensor_tensor(yrstd[:, :], yvar[:, :], g.neg_half[:, 0:TPB], ALU.pow).then_inc(m.yrstd_ready, 1)

        @block.tensor
        def _(e):
            with e.Fori(0, B) as b:
                e.wait_ge(m.c_fixed, b + 1)
                e.wait_ge(m.pv_kept, GROUPS * b)
                for t in range(KT):
                    last = e.matmul(kps[:, t * P:(t + 1) * P], cT[:, t * P:(t + 1) * P], g.l0_wk[:, :], start=True, stop=True)
                last.then_inc(m.kqv_projected, 1)
                for t in range(KT):
                    last = e.matmul(vps[:, t * P:(t + 1) * P], cT[:, t * P:(t + 1) * P], g.l0_wv[:, :], start=True, stop=True)
                last.then_inc(m.kqv_projected, 1)
                e.wait_ge(m.o_ready, GROUPS * b)
                front.tensor(e, b, turn)
                e.wait_ge(m.zT_ready, b + 1)
                e.wait_ge(m.y_kept, b)
                for i in range(TPB):
                    e.matmul(qps[:, i * P:(i + 1) * P], zT[:, i * P:(i + 1) * P], g.l0_wq[:, :], start=True, stop=False)
                    last = e.matmul(qps[:, i * P:(i + 1) * P], g.ones[0:1, 0:P], g.l0_bq[:, :], start=False, stop=True)
                last.then_inc(m.kqv_projected, 1)
                e.wait_ge(m.kn_ready, b + 1)
                for t in range(KT):
                    last = e.transpose(turn[:, t * P:(t + 1) * P], kn[:, t, :], g.ident)
                last.then_inc(m.kn_turned, 1)
                e.wait_ge(m.kT_ready, b + 1)
                e.wait_ge(m.qn_ready, b + 1)
                for i in range(TPB):
                    last = e.transpose(turn[:, i * P:(i + 1) * P], qn[:, i, :], g.ident)
                last.then_inc(m.qn_turned, 1)
                e.wait_ge(m.qm_ready, HEADS * b + HEADS)
                e.wait_ge(m.v_ready, b + 1)
                e.wait_ge(m.v_padded, 2)

                def scores(n):
                    grp, t = divmod(n, KT)
                    if n >= 2:
                        e.wait_ge(m.prob_ready, STEPS * b + n - 1)
                    for half in range(2):
                        last = e.matmul(sc[n % 2][:, half * 512:half * 512 + 512], kT[:, t * P:(t + 1) * P],
                                        qm[:, GH * grp + 2 * half:GH * grp + 2 * half + 2, :], start=True, stop=True)
                    last.then_inc(m.scores_ready, 1)

                def weighted(n):
                    grp, t = divmod(n, KT)
                    e.wait_ge(m.prob_ready, STEPS * b + n + 1)
                    if t == 0 and grp >= 2:
                        e.wait_ge(m.pv_kept, GROUPS * b + grp - 1)
                    for j in range(GH):
                        last = e.matmul(pvps[grp % 2][32 * j:32 * j + 32, 0:T], v[:, t, GH * grp + j, :],
                                        prob[n % 2][:, j * T:(j + 1) * T], start=t == 0, stop=t == KT - 1,
                                        tile_position=(0, 32 * j))
                    last.then_inc(m.pv_ready, 1)
                    if t == KT - 1:
                        e.wait_ge(m.pv_kept, GROUPS * b + grp + 1)
                        e.wait_ge(m.o_ready, GROUPS * b + grp)
                        for i in range(TPB):
                            last = e.transpose(turn[:, i * P:(i + 1) * P], pv[:, i * P:(i + 1) * P], g.ident)
                        last.then_inc(m.pv_turned, 1)

                scores(0)
                for n in range(STEPS):
                    if n + 1 < STEPS:
                        scores(n + 1)
                    weighted(n)
                e.wait_ge(m.o_ready, GROUPS * b + GROUPS)
                for i in range(TPB):
                    last = e.transpose(turn[:, i * P:(i + 1) * P], o[:, i, :], g.ident)
                last.then_inc(m.o_turned, 1)
                e.wait_ge(m.oT_ready, b + 1)
                for i in range(TPB):
                    e.matmul(qps[:, i * P:(i + 1) * P], oT[:, i * P:(i + 1) * P], g.l0_wo[:, :], start=True, stop=False)
                    last = e.matmul(qps[:, i * P:(i + 1) * P], g.ones[0:1, 0:P], g.l0_bo[:, :], start=False, stop=True)
                last.then_inc(m.out_ready, 1)

        @block.scalar
        def _(e):
            with e.Fori(0, B) as b:
                e.wait_ge(m.kqv_projected, 3 * b + 1)
                for t in range(KT):
                    if t == 0:
                        e.wait_ge(m.sumsq_clamped, b)
                    e.activation(square[:, t, :], kps[:, t * P:(t + 1) * P], ACT.Square,
                                 accum_out=sumsq[:, t:t + 1]).then_inc(m.sumsq_ready, 1)
                e.wait_ge(m.kqv_projected, 3 * b + 2)
                e.wait_ge(m.pv_ready, STEPS * b)
                e.activation(v[:, :, :, 0:HD], vps[:, :].rearrange("p (t h d) -> p t h d", t=KT, d=HD),
                             ACT.Copy).then_inc(m.v_ready, 1)
                e.wait_ge(front.z_turned, b + 1)
                e.activation(zT[:, :], turn[:, 0:T], ACT.Copy).then_inc(m.zT_ready, 1)
                e.wait_ge(m.kqv_projected, 3 * b + 3)
                e.activation(qp[:, :, :], qps[:, 0:T].rearrange("p (i d) -> p i d", d=D), ACT.Copy).then_inc(m.qp_ready, 1)
                for i in range(TPB):
                    e.activation(square[:, KT + i, :], qps[:, i * P:(i + 1) * P], ACT.Square,
                                 accum_out=sumsq[:, KT + i:KT + i + 1]).then_inc(m.sumsq_ready, 1)
                e.wait_ge(m.kn_turned, b + 1)
                e.activation(kT[:, :], turn[:, :], ACT.Copy).then_inc(m.kT_ready, 1)
                for n in range(STEPS):
                    e.wait_ge(m.scores_ready, STEPS * b + n + 1)
                    if n >= 2:
                        e.wait_ge(m.pv_ready, STEPS * b + n - 1)
                    e.activation(prob[n % 2][:, :], sc[n % 2][:, :], ACT.Exp, scale=SCALE).then_inc(m.prob_ready, 1)
                e.wait_ge(m.o_turned, b + 1)
                e.activation(oT[:, :], turn[:, 0:T], ACT.Copy).then_inc(m.oT_ready, 1)

        @block.vector
        def _(e):
            PER = front.steps + GROUPS + 2 * TPB + 3 * TPB
            steps = Steps(e, m.steps, PER)
            with e.Fori(0, B) as b:
                steps.begin(b)
                front.vector(e, b, steps)
                e.wait_ge(m.sumsq_ready, (KT + TPB) * b + KT + TPB)
                e.tensor_scalar(clamped[:, :], sumsq[:, :], 1e-24, None, ALU.max).then_inc(m.sumsq_clamped, 1)
                e.wait_ge(m.norm_ready, b + 1)
                e.tensor_tensor(kn[:, :, :], kps[:, :].rearrange("p (t d) -> p t d", d=D),
                                bcast(rnorm[:, 0:KT].unsqueeze(2), [P, KT, D]), ALU.mult).then_inc(m.kn_ready, 1)
                e.tensor_tensor(qn[:, :, :], qps[:, 0:T].rearrange("p (t d) -> p t d", d=D),
                                bcast(rnorm[:, KT:KT + TPB].unsqueeze(2), [P, TPB, D]), ALU.mult).then_inc(m.qn_ready, 1)
                e.wait_ge(m.qn_turned, b + 1)
                e.tensor_copy(qT[:, :], turn[:, 0:T]).then_inc(m.qT_ready, 1)
                e.wait_ge(m.qT_ready, b + 1)
                for h in range(HEADS):
                    e.tensor_scalar(qm[:, h, :], qT[:, :], g.const[:, C_HEAD + h:C_HEAD + h + 1], None,
                                    ALU.mult).then_inc(m.qm_ready, 1)
                for grp in range(GROUPS):
                    e.wait_ge(m.pv_ready, STEPS * b + KT * (grp + 1))
                    e.wait_ge(m.pv_turned, GROUPS * b + grp)
                    e.tensor_copy(pv[:, :], pvps[grp % 2][:, 0:T]).then_inc(m.pv_kept, 1)
                    e.wait_ge(m.pv_turned, GROUPS * b + grp + 1)
                    heads = turn[:, 0:T].rearrange("p (i j d) -> p i j d", i=TPB, d=32)
                    steps.add(e.reciprocal(rsum[:, :, :], heads[:, :, :, HD]))
                    steps.settle()
                    e.tensor_tensor(o[:, :, 32 * grp:32 * grp + 32].rearrange("p i (j d) -> p i j d", d=HD),
                                    heads[:, :, :, 0:HD], bcast(rsum[:, :, :].unsqueeze(3), [P, TPB, GH, HD]),
                                    ALU.mult).then_inc(m.o_ready, 1)
                e.wait_ge(m.out_ready, b + 1)
                e.wait_ge(m.qp_ready, b + 1)
                e.tensor_tensor(y[:, :, :], qps[:, 0:T].rearrange("p (i d) -> p i d", d=D), qp[:, :, :],
                                ALU.add).then_inc(m.y_kept, 1)
                e.wait_ge(m.y_kept, b + 1)
                for i in range(TPB):
                    steps.add(e.bn_stats(stats[:, i, :], y[:, i, :]))
                steps.settle()
                e.memset(front.held[:, :], 0.0)
                for i in range(TPB):
                    steps.add(e.bn_aggr(mv[:, i, :], stats[:, i, :]))
                steps.settle()
                e.tensor_scalar(yvar[:, :], mv[:, :, 1], EPS, None, ALU.add).then_inc(m.yvar_ready, 1)
                e.wait_ge(m.yrstd_ready, b + 1)
                for i in range(TPB):
                    steps.add(e.tensor_scalar(y[:, i, :], y[:, i, :], mv[:, i, 0:1], yrstd[:, i:i + 1],
                                              ALU.subtract, ALU.mult))
                steps.settle()
                for i in range(TPB):
                    steps.add(e.tensor_tensor(y[:, i, :], y[:, i, :], g.l0_gamma[:, :], ALU.mult))
                steps.settle()
                for i in range(TPB):
                    steps.add(e.tensor_tensor(y[:, i, :], y[:, i, :], g.l0_beta[:, :], ALU.add))
                steps.settle()
                for i in range(TPB):
                    e.tensor_tensor(g.x[:, TPB * b + i, :], g.x[:, TPB * b + i, :], y[:, i, :],
                                    ALU.add).then_inc(m.x_updated, 1)
                steps.end()
                e.wait_ge(m.x_updated, TPB * b + TPB)



def l0_ffn(nc, g, a):
    HF = 256
    FT = HF // P
    CT = 4
    CHUNKS = TILES // CT
    with ExitStack() as outer:
        so = Scope(nc, outer, "l0f")
        zT = so.sb("zT", [P, N])
        logits = so.sb("logits", [P, TILES, E])
        gate = so.sb("gate", [P, TILES, E])
        gateT = so.sb("gateT", [E, N])

        with ExitStack() as ctx:
            s = Scope(nc, ctx, "l0f_norm")
            front = Front(s, g, twice=True)
            zb = s.sb("zb", [P, T])
            turn = s.ps("turn")
            lps = s.ps("logits")
            m = s.sems(["x_updated", "zb_ready", "z_stored", "logits_ready", "logits_kept", "steps"])
            block = s.block()

            @block.vector
            def _(e):
                steps = Steps(e, m.steps, front.steps)
                with e.Fori(0, B) as b:
                    steps.begin(b)
                    front.vector(e, b, steps)
                    e.tensor_tensor(g.x[:, bass.ds(TPB * b, TPB), :], g.x[:, bass.ds(TPB * b, TPB), :],
                                    front.outer[:, :, :], ALU.add).then_inc(m.x_updated, 1)
                    steps.end()
                    e.wait_ge(m.x_updated, b + 1)
                    e.wait_ge(front.z_turned, b + 1)

            @block.gpsimd
            def _(e):
                with e.Fori(0, B) as b:
                    front.gpsimd(e, b)
                    e.wait_ge(m.zb_ready, b + 1)
                    e.tensor_copy(zT[:, bass.ds(b * T, T)], zb[:, :]).then_inc(m.z_stored, 1)

            @block.tensor
            def _(e):
                with e.Fori(0, B) as b:
                    e.wait_ge(m.zb_ready, b)
                    front.tensor(e, b, turn)
                    e.wait_ge(m.zb_ready, b + 1)
                    e.wait_ge(m.logits_kept, b)
                    for i in range(TPB):
                        e.matmul(lps[:, i * E:(i + 1) * E], zb[:, i * P:(i + 1) * P], g.l0_rw[:, :], start=True, stop=False)
                        last = e.matmul(lps[:, i * E:(i + 1) * E], g.ones[0:1, 0:P], g.l0_rb[:, :], start=False, stop=True)
                    last.then_inc(m.logits_ready, 1)

            @block.scalar
            def _(e):
                with e.Fori(0, B) as b:
                    e.wait_ge(front.z_turned, b + 1)
                    e.wait_ge(m.z_stored, b)
                    e.wait_ge(m.logits_ready, b)
                    e.activation(zb[:, :], turn[:, 0:T], ACT.Identity, scale=g.l0_lng[:, 0:1],
                                 bias=g.l0_lnb[:, 0:1]).then_inc(m.zb_ready, 1)
                    e.wait_ge(m.logits_ready, b + 1)
                    e.activation(logits[:, bass.ds(b * TPB, TPB), :], lps[:, 0:TPB * E].rearrange("p (i e) -> p i e", e=E),
                                 ACT.Copy).then_inc(m.logits_kept, 1)

        with ExitStack() as ctx:
            s = Scope(nc, ctx, "l0f_route")
            full = [P, TILES, E]
            red = s.sb("red", [P, 8, TILES])
            w = [s.sb(f"w{i}", full) for i in range(8)]
            turn = s.ps("turn", (P, 4 * 512))
            m = s.sems(["shifted", "exped", "gate_ready", "gate_turned", "steps", "gateT_ready"])
            block = s.block()

            @block.vector
            def _(e):
                steps = Steps(e, m.steps)

                def then(instruction):
                    steps.add(instruction)
                    steps.settle()

                def over(i):
                    return bcast(red[:, i, :].unsqueeze(2), full)

                rev = bcast(g.const[:, C_REV:C_REV + E].unsqueeze(1), full)
                then(e.tensor_reduce(red[:, 0, :], logits[:, :, :], AX.X, ALU.max))
                e.tensor_tensor(w[0][:, :, :], logits[:, :, :], over(0), ALU.subtract).then_inc(m.shifted, 1)
                e.wait_ge(m.exped, 1)
                then(e.tensor_reduce(red[:, 1, :], w[1][:, :, :], AX.X, ALU.add))
                then(e.reciprocal(red[:, 2, :], red[:, 1, :]))
                then(e.tensor_tensor(w[2][:, :, :], w[1][:, :, :], over(2), ALU.mult))
                then(e.tensor_reduce(red[:, 3, :], w[2][:, :, :], AX.X, ALU.max))
                then(e.tensor_tensor(w[3][:, :, :], w[2][:, :, :], over(3), ALU.is_equal))
                then(e.tensor_tensor(w[4][:, :, :], w[3][:, :, :], rev, ALU.mult))
                then(e.tensor_reduce(red[:, 4, :], w[4][:, :, :], AX.X, ALU.max))
                then(e.tensor_tensor(w[5][:, :, :], rev, over(4), ALU.is_equal))
                then(e.scalar_tensor_tensor(out=w[6][:, :, :].rearrange("p t e -> p (t e)"),
                                            in0=w[5][:, :, :].rearrange("p t e -> p (t e)"), scalar=-4.0,
                                            in1=w[2][:, :, :].rearrange("p t e -> p (t e)"), op0=ALU.mult, op1=ALU.add))
                then(e.tensor_reduce(red[:, 5, :], w[6][:, :, :], AX.X, ALU.max))
                then(e.tensor_tensor(w[3][:, :, :], w[6][:, :, :], over(5), ALU.is_equal))
                then(e.tensor_tensor(w[4][:, :, :], w[3][:, :, :], rev, ALU.mult))
                then(e.tensor_reduce(red[:, 6, :], w[4][:, :, :], AX.X, ALU.max))
                then(e.tensor_tensor(w[7][:, :, :], rev, over(6), ALU.is_equal))
                then(e.tensor_tensor(w[3][:, :, :], w[5][:, :, :], w[7][:, :, :], ALU.add))
                then(e.tensor_tensor(w[4][:, :, :], w[3][:, :, :], w[2][:, :, :], ALU.mult))
                then(e.tensor_reduce(red[:, 7, :], w[4][:, :, :], AX.X, ALU.add))
                then(e.tensor_scalar(red[:, 0, :], red[:, 7, :], 1e-8, None, ALU.max))
                then(e.reciprocal(red[:, 1, :], red[:, 0, :]))
                e.tensor_tensor(gate[:, :, :], w[4][:, :, :], over(1), ALU.mult).then_inc(m.gate_ready, 1)

            @block.scalar
            def _(e):
                e.wait_ge(m.shifted, 1)
                e.activation(w[1][:, :, :], w[0][:, :, :], ACT.Exp).then_inc(m.exped, 1)
                e.wait_ge(m.gate_turned, 1)
                e.activation(gateT[:, :], turn[0:E, :], ACT.Copy).then_inc(m.gateT_ready, 1)

            @block.tensor
            def _(e):
                e.wait_ge(m.gate_ready, 1)
                for t in range(TILES):
                    last = e.transpose(turn[0:E, t * P:(t + 1) * P], gate[:, t, :], g.ident)
                last.then_inc(m.gate_turned, 1)

        with ExitStack() as ctx:
            s = Scope(nc, ctx, "l0f_experts")
            gT = s.sb("gateT_chunk", [E, CT * P])
            gc = s.sb("gate_chunk", [P, CT, E])
            h = [s.sb(f"hidden{i}", [P, FT, CT * P]) for i in range(2)]
            acc = s.sb("acc", [P, CT, D])
            hps = [s.ps(f"hidden{i}") for i in range(2 * FT)]
            yps = [s.ps(f"y{i}") for i in range(2)]
            bps = s.ps("gated_bias")
            m = s.sems(["gate_fixed", "hidden_ready", "act_ready", "y_ready", "y_added", "bias_ready", "acc_started",
                        "x_updated"])
            block = s.block()

            @block.gpsimd
            def _(e):
                with e.Fori(0, CHUNKS) as c:
                    e.wait_ge(m.bias_ready, c)
                    e.wait_ge(m.y_added, E * CT * c)
                    e.tensor_copy(gT[:, :], gateT[:, bass.ds(c * CT * P, CT * P)]).then_inc(m.gate_fixed, 1)
                    e.tensor_copy(gc[:, :, :], gate[:, bass.ds(c * CT, CT), :]).then_inc(m.gate_fixed, 1)

            @block.tensor
            def _(e):
                with e.Fori(0, CHUNKS) as c:
                    def hidden(x):
                        for f in range(FT):
                            n = FT * x + f
                            if n >= 2 * FT:
                                e.wait_ge(m.act_ready, E * FT * c + n - 2 * FT + 1)
                            e.matmul(hps[n % (2 * FT)][:, :], g.l0_w1[:, x, f * P:(f + 1) * P],
                                     zT[:, bass.ds(c * CT * P, CT * P)], start=True, stop=True).then_inc(m.hidden_ready, 1)

                    def second(x):
                        e.wait_ge(m.act_ready, E * FT * c + FT * x + FT)
                        if x >= 2:
                            e.wait_ge(m.y_added, CT * (E * c + x - 1))
                        for t in range(CT):
                            for f in range(FT):
                                last = e.matmul(yps[x % 2][:, t * P:(t + 1) * P], h[x % 2][:, f, t * P:(t + 1) * P],
                                                g.l0_w2[:, x, f, :], start=f == 0, stop=f == FT - 1)
                        last.then_inc(m.y_ready, 1)

                    e.wait_ge(m.act_ready, E * FT * c)
                    hidden(0)
                    e.wait_ge(m.gate_fixed, 2 * c + 2)
                    e.wait_ge(m.acc_started, c)
                    for t in range(CT):
                        last = e.matmul(bps[:, t * P:(t + 1) * P], gT[:, t * P:(t + 1) * P], g.l0_b2[:, :], start=True, stop=True)
                    last.then_inc(m.bias_ready, 1)
                    e.wait_ge(m.y_added, CT * E * c)
                    for x in range(E):
                        if x + 1 < E:
                            hidden(x + 1)
                        second(x)

            @block.scalar
            def _(e):
                with e.Fori(0, CHUNKS) as c:
                    for x in range(E):
                        for f in range(FT):
                            e.wait_ge(m.hidden_ready, E * FT * c + FT * x + f + 1)
                            if f == 0:
                                if x >= 2:
                                    e.wait_ge(m.y_ready, E * c + x - 1)
                                else:
                                    e.wait_ge(m.y_ready, E * c)
                            e.activation(h[x % 2][:, f, :], hps[(FT * x + f) % (2 * FT)][:, :], ACT.Gelu,
                                         bias=g.l0_b1[:, FT * x + f:FT * x + f + 1]).then_inc(m.act_ready, 1)

            @block.vector
            def _(e):
                with e.Fori(0, CHUNKS) as c:
                    e.wait_ge(m.bias_ready, c + 1)
                    e.wait_ge(m.x_updated, c)
                    e.tensor_copy(acc[:, :, :], bps[:, :].rearrange("p (t d) -> p t d", d=D)).then_inc(m.acc_started, 1)
                    e.wait_ge(m.acc_started, c + 1)
                    for x in range(E):
                        e.wait_ge(m.y_ready, E * c + x + 1)
                        e.wait_ge(m.y_added, CT * (E * c + x))
                        for t in range(CT):
                            e.scalar_tensor_tensor(out=acc[:, t, :], in0=yps[x % 2][:, t * P:(t + 1) * P],
                                                   scalar=gc[:, t, x:x + 1], in1=acc[:, t, :], op0=ALU.mult,
                                                   op1=ALU.add).then_inc(m.y_added, 1)
                    e.wait_ge(m.y_added, CT * E * (c + 1))
                    e.tensor_tensor(g.x[:, bass.ds(c * CT, CT), :], g.x[:, bass.ds(c * CT, CT), :], acc[:, :, :],
                                    ALU.add).then_inc(m.x_updated, 1)



def wide_attention(nc, g, name, HEADS, wq, wk, wv, wo, bo):
    HD = 64
    SCALE = HD ** -0.5
    C = HEADS // 2
    UNITS = HEADS * TPB
    VW = HEADS * HD // 512
    NS, NP_, AHEAD = 3, 4, 3
    LAG = 3
    with ExitStack() as ctx:
        s = Scope(nc, ctx, name)
        front = Front(s, g)
        zT = s.sb("zT", [P, T])
        cT = s.sb("cT", [DC, S])
        kT = s.sb("kT", [P, C, S])
        v = s.sb("v", [P, KT, HEADS * HD])
        q = s.sb("q", [P, HEADS, T])
        nmax = s.sb("nmax", [P, UNITS])
        rsum = s.sb("rsum", [P, UNITS])
        rinv = s.sb("rinv", [P, UNITS])
        prob = [s.sb(f"prob{i}", [P, S]) for i in range(NP_)]
        pT = [s.sb(f"probT{i}", [P, 2, KT, T]) for i in range(2)]
        oT = s.sb("oT", [P, C, T])
        sps = [s.ps(f"scores{i}") for i in range(NS)]
        tps = [s.ps(f"turned{i}") for i in range(2)]
        ops = s.ps("o")
        jps = [s.ps(f"proj{i}") for i in range(2)]
        m = s.sems(["q_zeroed", "c_fixed", "zT_ready", "k_projected", "k_ready", "v_projected", "v_ready",
                    "q_projected", "q_even_ready", "q_odd_ready", "scores_ready", "max_ready", "exp_ready",
                    "rinv_ready", "prob_ready", "prob_turned", "pT_even_kept", "pT_odd_kept", "o_projected",
                    "o_kept", "out_ready", "x_updated", "steps"])
        block = s.block()

        @block.gpsimd
        def _(e):
            for h in range(HEADS):
                lo = 64 * (1 - h % 2)
                e.memset(q[lo:lo + 64, h, :], 0.0).then_inc(m.q_zeroed, 1)
            e.wait_ge(m.q_zeroed, HEADS)
            with e.Fori(0, B) as b:
                e.wait_ge(m.v_projected, KT * VW * b)
                e.tensor_copy(cT[:, :], g.ctxT[0:DC, bass.ds(b * S, S)]).then_inc(m.c_fixed, 1)
                front.gpsimd(e, b)
                for n in range(UNITS):
                    e.wait_ge(m.rinv_ready, UNITS * b + n + 1)
                    e.tensor_tensor(prob[n % NP_][:, :], prob[n % NP_][:, :], bcast(rinv[:, n:n + 1], [P, S]),
                                    ALU.mult).then_inc(m.prob_ready, 1)

        @block.tensor
        def _(e):
            e.wait_ge(m.q_zeroed, HEADS)
            with e.Fori(0, B) as b:
                J = 0
                for c in range(C):
                    if c >= 2:
                        e.wait_ge(m.k_ready, C * b + c - 1)
                    elif c == 0:
                        e.wait_ge(m.x_updated, b)
                    e.matmul(jps[c % 2][:, :], wk[0:DC, c * P:(c + 1) * P], g.ctxT[0:DC, bass.ds(b * S, S)],
                             start=True, stop=True).then_inc(m.k_projected, 1)
                e.wait_ge(m.c_fixed, b + 1)
                e.wait_ge(m.k_ready, C * b + C)
                for n in range(KT * VW):
                    t, w = divmod(n, VW)
                    if n >= 2:
                        e.wait_ge(m.v_ready, KT * VW * b + n - 1)
                    e.matmul(jps[n % 2][:, :], cT[:, t * P:(t + 1) * P], wv[0:DC, w * 512:(w + 1) * 512],
                             start=True, stop=True).then_inc(m.v_projected, 1)
                e.wait_ge(m.pT_even_kept, UNITS // 2 * b)
                front.tensor(e, b, tps[0])
                e.wait_ge(m.zT_ready, b + 1)
                e.wait_ge(m.v_ready, KT * VW * (b + 1))
                for c in range(C):
                    if c >= 2:
                        e.wait_ge(m.q_even_ready, C * b + c - 1)
                        e.wait_ge(m.q_odd_ready, C * b + c - 1)
                    e.matmul(jps[c % 2][:, 0:T], wq[:, c * P:(c + 1) * P], zT[:, :],
                             start=True, stop=True).then_inc(m.q_projected, 1)

                def scores(n):
                    h, i = divmod(n, TPB)
                    if n >= NS:
                        e.wait_ge(m.exp_ready, UNITS * b + n - NS + 1)
                    if i == 0:
                        done = m.q_even_ready if h % 2 == 0 else m.q_odd_ready
                        e.wait_ge(done, C * b + h // 2 + 1)
                    e.matmul(sps[n % NS][:, :], q[:, h, i * P:(i + 1) * P], kT[:, h // 2, :],
                             start=True, stop=True).then_inc(m.scores_ready, 1)

                def turn(n):
                    if n >= 2:
                        e.wait_ge(m.pT_odd_kept if n % 2 else m.pT_even_kept, UNITS // 2 * b + n // 2)
                    e.wait_ge(m.prob_ready, UNITS * b + n + 1)
                    for t in range(KT):
                        last = e.transpose(tps[n % 2][:, t * P:(t + 1) * P], prob[n % NP_][:, t * P:(t + 1) * P], g.ident)
                    last.then_inc(m.prob_turned, 1)

                def weighted(c):
                    e.wait_ge(m.pT_even_kept, UNITS // 2 * b + 2 * c + 2)
                    e.wait_ge(m.pT_odd_kept, UNITS // 2 * b + 2 * c + 2)
                    e.wait_ge(m.o_kept, C * b + c)
                    for t in range(KT):
                        for j in range(2):
                            h = 2 * c + j
                            last = e.matmul(ops[64 * j:64 * j + 64, 0:T], v[:, t, h * HD:(h + 1) * HD],
                                            pT[c % 2][:, j, t, :], start=t == 0, stop=t == KT - 1,
                                            tile_position=(0, 64 * j))
                    last.then_inc(m.o_projected, 1)

                for n in range(AHEAD):
                    scores(n)
                for n in range(UNITS):
                    turn(n)
                    if n + AHEAD < UNITS:
                        scores(n + AHEAD)
                    if n % 4 == 3 and n > 4:
                        weighted(n // 4 - 1)
                weighted(C - 1)
                e.wait_ge(m.o_kept, C * b + C)
                for i in range(TPB):
                    for c in range(C):
                        e.matmul(jps[0][:, i * P:(i + 1) * P], oT[:, c, i * P:(i + 1) * P], wo[:, c, :],
                                 start=c == 0, stop=False)
                    last = e.matmul(jps[0][:, i * P:(i + 1) * P], g.ones[0:1, 0:P], bo[:, :], start=False, stop=True)
                last.then_inc(m.out_ready, 1)

        @block.scalar
        def _(e):
            with e.Fori(0, B) as b:
                for c in range(C):
                    e.wait_ge(m.k_projected, C * b + c + 1)
                    e.activation(kT[:, c, :], jps[c % 2][:, :], ACT.Copy).then_inc(m.k_ready, 1)
                e.wait_ge(front.z_turned, b + 1)
                e.activation(zT[:, :], tps[0][:, 0:T], ACT.Copy).then_inc(m.zT_ready, 1)
                for c in range(C):
                    e.wait_ge(m.q_projected, C * b + c + 1)
                    e.activation(q[0:64, 2 * c, :], jps[c % 2][0:64, 0:T], ACT.Copy, scale=SCALE).then_inc(m.q_even_ready, 1)
                for n in range(UNITS + LAG):
                    if n < UNITS:
                        e.wait_ge(m.max_ready, UNITS * b + n + 1)
                        if n >= NP_:
                            e.wait_ge(m.prob_turned, UNITS * b + n - NP_ + 1)
                        e.activation(prob[n % NP_][:, :], sps[n % NS][:, :], ACT.Exp, bias=nmax[:, n:n + 1],
                                     accum_out=rsum[:, n:n + 1]).then_inc(m.exp_ready, 1)
                    k = n - LAG
                    if k >= 0 and k % 2 == 1:
                        e.wait_ge(m.prob_turned, UNITS * b + k + 1)
                        if k // 4 >= 2:
                            e.wait_ge(m.o_projected, C * b + k // 4 - 1)
                        e.activation(pT[k // 4 % 2][:, k // 2 % 2, :, P:T],
                                     tps[1][:, :].rearrange("p (t q) -> p t q", q=P), ACT.Copy).then_inc(m.pT_odd_kept, 1)

        @block.vector
        def _(e):
            steps = Steps(e, m.steps, front.steps)
            with e.Fori(0, B) as b:
                steps.begin(b)
                front.vector(e, b, steps)
                for n in range(KT * VW):
                    t, w = divmod(n, VW)
                    e.wait_ge(m.v_projected, KT * VW * b + n + 1)
                    e.tensor_copy(v[:, t, w * 512:(w + 1) * 512], jps[n % 2][:, :]).then_inc(m.v_ready, 1)
                for c in range(C):
                    e.wait_ge(m.q_even_ready, C * b + c + 1)
                    e.tensor_scalar(q[64:P, 2 * c + 1, :], jps[c % 2][64:P, 0:T], SCALE, None,
                                    ALU.mult).then_inc(m.q_odd_ready, 1)

                def keep_pair(c):
                    e.wait_ge(m.o_projected, C * b + c + 1)
                    e.tensor_copy(oT[:, c, :], ops[:, 0:T]).then_inc(m.o_kept, 1)

                for n in range(UNITS + LAG):
                    if n < UNITS:
                        e.wait_ge(m.scores_ready, UNITS * b + n + 1)
                        e.tensor_reduce(nmax[:, n:n + 1], sps[n % NS][:, :], AX.X, ALU.max, negate=True).then_inc(m.max_ready, 1)
                    if 1 <= n <= UNITS:
                        e.wait_ge(m.exp_ready, UNITS * b + n)
                        e.reciprocal(rinv[:, n - 1:n], rsum[:, n - 1:n]).then_inc(m.rinv_ready, 1)
                    k = n - LAG
                    if k >= 0 and k % 2 == 0:
                        e.wait_ge(m.prob_turned, UNITS * b + k + 1)
                        if k // 4 >= 2:
                            e.wait_ge(m.o_projected, C * b + k // 4 - 1)
                        e.tensor_copy(pT[k // 4 % 2][:, k // 2 % 2, :, 0:P],
                                      tps[0][:, :].rearrange("p (t q) -> p t q", q=P)).then_inc(m.pT_even_kept, 1)
                    if k >= 6 and k % 4 == 2:
                        keep_pair(k // 4 - 1)
                keep_pair(C - 1)
                e.wait_ge(m.out_ready, b + 1)
                e.tensor_tensor(g.x[:, bass.ds(TPB * b, TPB), :], jps[0][:, 0:T].rearrange("p (i d) -> p i d", d=D),
                                g.x[:, bass.ds(TPB * b, TPB), :], ALU.add).then_inc(m.x_updated, 1)
                steps.end()
                e.wait_ge(m.x_updated, b + 1)


def l2_attention(nc, g, a):
    wide_attention(nc, g, "l2a", 8, g.l2_wq, g.l2_wk, g.l2_wv, g.l2_wo, g.l2_bo)


def l3_attention(nc, g, a):
    wide_attention(nc, g, "l3a", 16, g.l3_wq, g.l3_wk, g.l3_wv, g.l3_wo, g.l3_bo)






def l1_ffn(nc, g, a):
    FF = 512
    FT = FF // P
    MB = TILES // E
    PAIR = 2
    NT = PAIR * MB
    TURNS = E // PAIR
    W = MB * P
    with ExitStack() as ctx:
        s = Scope(nc, ctx, "l1f")
        x_e = g.x[:, :, :].rearrange("p (m e) d -> p e m d", e=E)

        def tile(u, i):
            return g.x[:, PAIR * u + (i % MB) * E + i // MB, :]

        front = Front(s, g, tile=tile, tiles=NT, twice=True)
        w1 = s.sb("w1", [P, PAIR, FF])
        w2 = s.sb("w2", [P, PAIR, FT, D])
        zT = s.sb("zT", [P, NT * P])
        xaT = s.sb("xaT", [P, NT * P])
        h = s.sb("h", [P, PAIR, FT, W])
        yT = s.sb("yT", [P, NT * P])
        og = s.sb("og", [P, NT, D])
        turn = s.ps("turn")
        xps = s.ps("xa")
        hps = [s.ps(f"h{i}") for i in range(4)]
        yps = s.ps("y")
        ops = s.ps("o")
        m = s.sems(["w_loaded", "zT_ready", "xa_ready", "xaT_ready", "h_ready", "h_kept", "y_ready", "yT_ready",
                    "o_ready", "og_ready", "x_updated", "steps"])
        block = s.block()

        @block.sync
        def _(sp):
            with sp.Fori(0, TURNS) as u:
                sp.wait_ge(m.y_ready, PAIR * u)
                sp.dma_start(w1[:, :, :], a["L1_ffn_w1"].rearrange("e d f -> d e f")[:, bass.ds(PAIR * u, PAIR), :]
                             ).then_inc(m.w_loaded, 16)
                sp.dma_start(w2[:, :, :, :], a["L1_ffn_w2"].rearrange("e (f p) d -> p e f d", p=P)[:, bass.ds(PAIR * u, PAIR), :, :]
                             ).then_inc(m.w_loaded, 16)

        @block.gpsimd
        def _(e):
            with e.Fori(0, TURNS) as u:
                front.gpsimd(e, u)

        @block.vector
        def _(e):
            steps = Steps(e, m.steps, front.steps)
            with e.Fori(0, TURNS) as u:
                steps.begin(u)
                e.wait_ge(m.xa_ready, u)
                front.vector(e, u, steps)
                for j in range(PAIR):
                    e.wait_ge(m.y_ready, PAIR * u + j + 1)
                    e.tensor_scalar(yT[:, j * W:(j + 1) * W], yps[:, j * W:(j + 1) * W],
                                    g.l1_b2[:, bass.ds(PAIR * u + j, 1)], None, ALU.add).then_inc(m.yT_ready, 1)
                for j in range(PAIR):
                    e.wait_ge(m.og_ready, u + 1)
                    xs = x_e[:, bass.ds(PAIR * u + j, 1), :, :].squeeze(1)
                    e.tensor_tensor(xs, xs, og[:, j * MB:(j + 1) * MB, :], ALU.add).then_inc(m.x_updated, 1)
                steps.end()
                e.wait_ge(m.x_updated, PAIR * (u + 1))

        @block.tensor
        def _(e):
            with e.Fori(0, TURNS) as u:
                e.wait_ge(m.zT_ready, u)
                front.tensor(e, u, turn)
                e.wait_ge(m.zT_ready, u + 1)
                e.wait_ge(m.xaT_ready, u)
                e.matmul(xps[:, :], g.l1_attn_w[:, :], zT[:, :], start=True, stop=False)
                for i in range(NT):
                    last = e.matmul(xps[:, i * P:(i + 1) * P], front.outer[:, i, :], g.ident, start=False, stop=i == NT - 1)
                last.then_inc(m.xa_ready, 1)
                e.wait_ge(m.xaT_ready, u + 1)
                e.wait_ge(m.w_loaded, 32 * (u + 1))
                for j in range(PAIR):
                    for f in range(0, FT, 2):
                        n = (j * FT + f) // 2
                        for k in range(2):
                            last = e.matmul(hps[n][:, k * W:(k + 1) * W], w1[:, j, (f + k) * P:(f + k + 1) * P],
                                            xaT[:, j * W:(j + 1) * W], start=True, stop=True)
                        last.then_inc(m.h_ready, 1)
                for j in range(PAIR):
                    e.wait_ge(m.h_kept, PAIR * FT * u + FT * (j + 1))
                    for f in range(FT):
                        last = e.matmul(yps[:, j * W:(j + 1) * W], w2[:, j, f, :], h[:, j, f, :], start=f == 0, stop=f == FT - 1)
                    last.then_inc(m.y_ready, 1)
                    if j == 0:
                        e.wait_ge(m.yT_ready, PAIR * u + 1)
                e.wait_ge(m.yT_ready, PAIR * u + PAIR)
                for i in range(NT):
                    e.matmul(ops[:, i * P:(i + 1) * P], yT[:, i * P:(i + 1) * P], g.l1_next_w[:, :], start=True, stop=False)
                    last = e.matmul(ops[:, i * P:(i + 1) * P], g.ones[0:1, 0:P], g.l1_next_b[:, :], start=False, stop=True)
                last.then_inc(m.o_ready, 1)

        @block.scalar
        def _(e):
            with e.Fori(0, TURNS) as u:
                e.wait_ge(front.z_turned, u + 1)
                e.activation(zT[:, :], turn[:, :], ACT.Identity, scale=g.l1_lng[:, 0:1], bias=g.l1_lnb[:, 0:1]
                             ).then_inc(m.zT_ready, 1)
                e.wait_ge(m.xa_ready, u + 1)
                e.activation(xaT[:, :], xps[:, :], ACT.Identity, bias=g.l1_attn_b[:, 0:1]).then_inc(m.xaT_ready, 1)
                for j in range(PAIR):
                    for f in range(FT):
                        n = j * FT + f
                        e.wait_ge(m.h_ready, PAIR * FT // 2 * u + n // 2 + 1)
                        e.activation(h[:, j, f, :], hps[n // 2][:, (n % 2) * W:(n % 2 + 1) * W], ACT.Gelu,
                                     bias=g.l1_b1[:, bass.ds((PAIR * u + j) * FT + f, 1)]).then_inc(m.h_kept, 1)
                e.wait_ge(m.o_ready, u + 1)
                e.wait_ge(m.x_updated, PAIR * u)
                e.activation(og[:, :, :], ops[:, :].rearrange("p (i d) -> p i d", d=D), ACT.Gelu).then_inc(m.og_ready, 1)



def l2_ffn(nc, g, a):
    NB = 2
    NT = NB * TPB
    W = NT * P
    TURNS = B // NB
    C = 4
    with ExitStack() as ctx:
        s = Scope(nc, ctx, "l2f")
        front = Front(s, g, tile=lambda u, i: g.x[:, NT * u + i, :], tiles=NT)
        scale = s.sb("scale", [P, 2, NT])
        zT = s.sb("zT", [P, W])
        ones = s.sb("ones", [P, T])
        qT = [s.sb(f"qT{i}", [P, W]) for i in range(2)]
        cum = [s.sb(f"cum{i}", [P, W]) for i in range(2)]
        hT = [s.sb(f"hT{i}", [P, W]) for i in range(2)]
        red = s.sb("red", [P, 4, 2 * NT])
        shifted = s.sb("shifted", [P, 2 * NT, E])
        ex = s.sb("ex", [P, 2 * NT, E])
        w = s.sb("w", [P, 2 * NT, E])
        wT = s.sb("wT", [E, 2, W])
        xv = [s.sb(f"xv{i}", [P, W]) for i in range(2)]
        xy = [s.sb(f"xy{i}", [P, W]) for i in range(2)]
        prod = [s.sb(f"prod{i}", [P, W]) for i in range(2)]
        oT = s.sb("oT", [P, W])
        bank = [s.ps(f"bank{i}") for i in range(2)]
        xps = [s.ps(f"xv{i}") for i in range(2)]
        yps = [s.ps(f"yw{i}") for i in range(2)]
        wps = s.ps("weights")
        ops = s.ps("out")
        m = s.sems(["scale_ready", "ones_ready", "zT_ready", "q_projected", "q_kept", "k_projected", "cum_kept",
                    "h_projected", "h_kept", "logits_ready", "shifted_ready", "ex_ready", "w_ready", "w_turned",
                    "wT_kept", "xv_ready", "xv_kept", "yw_ready", "xy_kept", "wb_ready", "prod_ready", "prod_used",
                    "o_ready", "oT_kept", "y_ready", "x_updated", "steps"])
        block = s.block()

        @block.gpsimd
        def _(e):
            e.memset(ones[:, :], 1.0).then_inc(m.ones_ready, 1)
            with e.Fori(0, TURNS) as u:
                front.gpsimd(e, u)

        @block.tensor
        def _(e):
            with e.Fori(0, TURNS) as u:
                e.wait_ge(m.x_updated, u)
                front.tensor(e, u, bank[0])
                e.wait_ge(m.zT_ready, u + 1)
                e.matmul(bank[1][:, :], g.l2_wqT[:, :], zT[:, :], start=True, stop=True).then_inc(m.q_projected, 1)
                e.matmul(xps[0][:, :], g.l2_wkT[:, :], zT[:, :], start=True, stop=True).then_inc(m.k_projected, 1)
                e.wait_ge(m.q_kept, 2 * u + 1)
                e.matmul(xps[1][:, :], g.l2_winvT[:, :], qT[0][:, :], start=True, stop=True).then_inc(m.q_projected, 1)
                e.matmul(yps[0][:, :], g.l2_rw1T[:, :], qT[0][:, :], start=True, stop=True).then_inc(m.h_projected, 1)
                e.wait_ge(m.q_kept, 2 * u + 2)
                e.matmul(yps[1][:, :], g.l2_rw1T[:, :], qT[1][:, :], start=True, stop=True).then_inc(m.h_projected, 1)
                e.wait_ge(m.cum_kept, 3 * u + 2)
                e.matmul(xps[0][:, :], g.l2_winvT[:, :], cum[0][:, :], start=True, stop=True).then_inc(m.k_projected, 1)
                for r in range(2):
                    e.wait_ge(m.h_kept, 2 * u + r + 1)
                    for i in range(NT):
                        at = (r * NT + i) * E
                        e.matmul(wps[:, at:at + E], hT[r][:, i * P:(i + 1) * P], g.l2_rw2T[:, :], start=True, stop=False)
                        e.matmul(wps[:, at:at + E], g.ones[0:1, 0:P], g.l2_rb2[:, :], start=False, stop=False)
                        last = e.matmul(wps[:, at:at + E], g.ones[0:1, 0:P], g.l2_eb[:, :], start=False, stop=True)
                last.then_inc(m.logits_ready, 1)
                e.wait_ge(m.w_ready, u + 1)
                for r in range(2):
                    for i in range(NT):
                        last = e.transpose(bank[r][0:E, i * P:(i + 1) * P], w[:, r * NT + i, :], g.ident)
                last.then_inc(m.w_turned, 1)
                e.wait_ge(m.cum_kept, 3 * u + 3)
                e.wait_ge(m.wT_kept, 2 * u + 2)

                def front_products(n):
                    r, c = divmod(n, C)
                    if n >= 2:
                        e.wait_ge(m.xv_kept, 2 * C * u + n - 1)
                        e.wait_ge(m.xy_kept, 2 * C * u + n - 1)
                    e.matmul(xps[n % 2][:, :], g.l2_v[r][:, 2 * c:2 * c + 2, :], qT[r][:, :], start=True, stop=True).then_inc(m.xv_ready, 1)
                    e.matmul(yps[n % 2][:, :], g.l2_w[r][:, 2 * c:2 * c + 2, :], cum[r][:, :], start=True, stop=True).then_inc(m.yw_ready, 1)
                    if n >= 1:
                        e.wait_ge(m.prod_ready, 2 * C * u + n)
                    e.matmul(wps[:, :], g.const[0:E, C_SEL + c * P:C_SEL + (c + 1) * P], wT[:, r, :], start=True,
                             stop=True).then_inc(m.wb_ready, 1)

                front_products(0)
                for n in range(2 * C):
                    if n + 1 < 2 * C:
                        front_products(n + 1)
                    e.wait_ge(m.prod_ready, 2 * C * u + n + 1)
                    r, c = divmod(n, C)
                    e.matmul(ops[:, :], g.l2_uT[r][:, c, :], prod[n % 2][:, :], start=n == 0, stop=False).then_inc(m.prod_used, 1)
                for r in range(2):
                    last = e.matmul(ops[:, :], g.l2_b[r][:, :], wT[:, r, :], start=False, stop=r == 1)
                last.then_inc(m.o_ready, 1)
                e.wait_ge(m.oT_kept, u + 1)
                for i in range(NT):
                    last = e.matmul(bank[0][:, i * P:(i + 1) * P], oT[:, i * P:(i + 1) * P], g.l2_woT[:, :], start=True, stop=True)
                last.then_inc(m.y_ready, 1)

        @block.scalar
        def _(e):
            with e.Fori(0, TURNS) as u:
                e.wait_ge(front.z_turned, u + 1)
                e.activation(zT[:, :], bank[0][:, :], ACT.Copy).then_inc(m.zT_ready, 1)
                e.wait_ge(m.q_projected, 2 * u + 1)
                e.activation(qT[0][:, :], bank[1][:, :], ACT.Copy).then_inc(m.q_kept, 1)
                e.wait_ge(m.q_projected, 2 * u + 2)
                e.activation(qT[1][:, :], xps[1][:, :], ACT.Copy).then_inc(m.q_kept, 1)
                for r in range(2):
                    e.wait_ge(m.h_projected, 2 * u + r + 1)
                    e.activation(hT[r][:, :], yps[r][:, :], ACT.Gelu, bias=g.l2_rb1[:, 0:1]).then_inc(m.h_kept, 1)
                e.wait_ge(m.shifted_ready, u + 1)
                e.activation(ex[:, :, :], shifted[:, :, :], ACT.Exp).then_inc(m.ex_ready, 1)
                e.wait_ge(m.w_turned, u + 1)
                for r in range(2):
                    e.activation(wT[:, r, :], bank[r][0:E, :], ACT.Copy).then_inc(m.wT_kept, 1)
                for n in range(2 * C):
                    e.wait_ge(m.xv_ready, 2 * C * u + n + 1)
                    if n >= 2:
                        e.wait_ge(m.xy_kept, 2 * C * u + n - 1)
                    e.activation(xv[n % 2][:, :], xps[n % 2][:, :], ACT.Copy).then_inc(m.xv_kept, 1)
                e.wait_ge(m.o_ready, u + 1)
                e.activation(oT[:, :], ops[:, :], ACT.Copy).then_inc(m.oT_kept, 1)

        @block.vector
        def _(e):
            steps = Steps(e, m.steps, front.steps + 4)
            for r in range(2):
                for i in range(NT):
                    at = C_INVN + i % TPB
                    if r == 0:
                        e.tensor_copy(scale[:, r, i:i + 1], g.const[:, at:at + 1]).then_inc(m.scale_ready, 1)
                    else:
                        e.tensor_tensor(scale[:, r, i:i + 1], g.const[:, at:at + 1], g.l2_alpha[:, :],
                                        ALU.mult).then_inc(m.scale_ready, 1)
            e.wait_ge(m.scale_ready, 2 * NT)
            e.wait_ge(m.ones_ready, 1)
            with e.Fori(0, TURNS) as u:
                steps.begin(u)
                front.vector(e, u, steps)
                e.wait_ge(m.k_projected, 2 * u + 1)
                for n in range(NB):
                    e.tensor_tensor_scan(cum[0][:, n * T:(n + 1) * T], ones[:, :], xps[0][:, n * T:(n + 1) * T], 0.0,
                                         ALU.mult, ALU.add).then_inc(m.cum_kept, 1)
                e.wait_ge(m.k_projected, 2 * u + 2)
                e.tensor_copy(cum[1][:, :], xps[0][:, :]).then_inc(m.cum_kept, 1)
                e.wait_ge(m.logits_ready, u + 1)
                logits = wps[:, 0:2 * NT * E].rearrange("p (i e) -> p i e", e=E)
                full = [P, 2 * NT, E]
                steps.add(e.tensor_reduce(red[:, 0, :], logits, AX.X, ALU.max))
                steps.settle()
                e.tensor_tensor(shifted[:, :, :], logits, bcast(red[:, 0, :].unsqueeze(2), full),
                                ALU.subtract).then_inc(m.shifted_ready, 1)
                e.wait_ge(m.ex_ready, u + 1)
                steps.add(e.tensor_reduce(red[:, 1, :], ex[:, :, :], AX.X, ALU.add))
                steps.settle()
                steps.add(e.reciprocal(red[:, 2, :], red[:, 1, :]))
                steps.settle()
                steps.add(e.tensor_tensor(red[:, 3, :], red[:, 2, :], scale[:, :, :].rearrange("p r i -> p (r i)"), ALU.mult))
                steps.settle()
                e.tensor_tensor(w[:, :, :], ex[:, :, :], bcast(red[:, 3, :].unsqueeze(2), full), ALU.mult).then_inc(m.w_ready, 1)
                for n in range(2 * C):
                    e.wait_ge(m.xv_kept, 2 * C * u + n + 1)
                    e.wait_ge(m.yw_ready, 2 * C * u + n + 1)
                    e.tensor_tensor(xy[n % 2][:, :], xv[n % 2][:, :], yps[n % 2][:, :], ALU.mult).then_inc(m.xy_kept, 1)
                    e.wait_ge(m.wb_ready, 2 * C * u + n + 1)
                    e.wait_ge(m.xy_kept, 2 * C * u + n + 1)
                    if n >= 2:
                        e.wait_ge(m.prod_used, 2 * C * u + n - 1)
                    e.tensor_tensor(prod[n % 2][:, :], xy[n % 2][:, :], wps[:, :], ALU.mult).then_inc(m.prod_ready, 1)
                e.wait_ge(m.y_ready, u + 1)
                e.tensor_tensor(g.x[:, bass.ds(NT * u, NT), :], bank[0][:, :].rearrange("p (i d) -> p i d", d=D),
                                g.x[:, bass.ds(NT * u, NT), :], ALU.add).then_inc(m.x_updated, 1)
                steps.end()
                e.wait_ge(m.x_updated, u + 1)



def l3_ffn(nc, g, a):
    K = 2
    with ExitStack() as outer:
        so = Scope(nc, outer, "l3f")
        zT = so.sb("zT", [P, N])
        zT0 = so.sb("zT_first", [P, B])
        index = so.sb("index", [K, B], I32)

        with ExitStack() as ctx:
            s = Scope(nc, ctx, "l3f_norm")
            front = Front(s, g)
            red = s.sb("red", [B, 4])
            w = [s.sb(f"w{i}", [B, E]) for i in range(6)]
            pick = s.sb("pick", [B, K])
            turn = s.ps("turn")
            sps = s.ps("scores")
            m = s.sems(["zT_kept", "scores_ready", "pick_ready", "pick_turned", "index_ready", "steps", "steps2"])
            block = s.block()

            @block.gpsimd
            def _(e):
                with e.Fori(0, B) as b:
                    front.gpsimd(e, b)

            @block.tensor
            def _(e):
                with e.Fori(0, B) as b:
                    e.wait_ge(m.zT_kept, 2 * b)
                    front.tensor(e, b, turn)
                e.wait_ge(m.zT_kept, 2 * B)
                e.matmul(sps[0:B, 0:E], zT0[:, :], g.l3_wr[:, :], start=True, stop=False)
                e.matmul(sps[0:B, 0:E], g.ones[0:1, 0:B], g.l3_br[:, :], start=False, stop=True).then_inc(m.scores_ready, 1)
                e.wait_ge(m.pick_ready, K)
                e.transpose(turn[0:K, 0:B], pick[:, :], g.ident[0:B, 0:B]).then_inc(m.pick_turned, 1)

            @block.scalar
            def _(e):
                with e.Fori(0, B) as b:
                    e.wait_ge(front.z_turned, b + 1)
                    e.activation(zT[:, bass.ds(b * T, T)], turn[:, 0:T], ACT.Copy).then_inc(m.zT_kept, 1)
                    e.activation(zT0[:, bass.ds(b, 1)], turn[:, 0:1], ACT.Copy).then_inc(m.zT_kept, 1)

            @block.vector
            def _(e):
                steps = Steps(e, m.steps, front.steps)
                with e.Fori(0, B) as b:
                    steps.begin(b)
                    e.wait_ge(front.z_turned, b)
                    front.vector(e, b, steps)
                    steps.end()
                steps = Steps(e, m.steps2)

                def then(instruction):
                    steps.add(instruction)
                    steps.settle()

                rev = g.const[0:B, C_REV:C_REV + E]

                def first_of_largest(source, at, k):
                    then(e.tensor_reduce(red[:, at:at + 1], source, AX.X, ALU.max))
                    then(e.tensor_scalar(w[0][:, :], source, red[:, at:at + 1], None, ALU.is_equal))
                    then(e.tensor_tensor(w[1][:, :], w[0][:, :], rev, ALU.mult))
                    then(e.tensor_reduce(red[:, at + 1:at + 2], w[1][:, :], AX.X, ALU.max))
                    e.tensor_scalar(pick[:, k:k + 1], red[:, at + 1:at + 2], -1.0, float(E), ALU.mult,
                                    ALU.add).then_inc(m.pick_ready, 1)

                e.wait_ge(m.scores_ready, 1)
                then(e.tensor_copy(w[2][:, :], sps[0:B, 0:E]))
                first_of_largest(w[2][:, :], 0, 0)
                then(e.tensor_scalar(w[3][:, :], rev, red[:, 1:2], None, ALU.is_equal))
                then(e.tensor_scalar(w[4][:, :], w[3][:, :], -3.0e38, None, ALU.mult))
                then(e.tensor_tensor(w[5][:, :], w[2][:, :], w[4][:, :], ALU.add))
                first_of_largest(w[5][:, :], 2, 1)
                e.wait_ge(m.pick_turned, 1)
                e.tensor_copy(index[:, :], turn[0:K, 0:B]).then_inc(m.index_ready, 1)
                e.wait_ge(m.index_ready, 1)

        with ExitStack() as ctx:
            s = Scope(nc, ctx, "l3f_experts")
            U = 2
            w1 = [s.sb(f"w1_{p}", [P, K, D]) for p in range(U)]
            w2 = [s.sb(f"w2_{p}", [P, K, D]) for p in range(U)]
            b1 = [s.sb(f"b1_{p}", [1, K, D]) for p in range(U)]
            b2 = [s.sb(f"b2_{p}", [1, K, D]) for p in range(U)]
            ones = s.sb("ones", [1, T])
            h = [s.sb(f"h{p}", [P, K, T]) for p in range(U)]
            hps = [s.ps(f"h{p}") for p in range(U)]
            ops = [s.ps(f"o{p}") for p in range(U)]
            m = s.sems(["ones_ready", "loaded_even", "loaded_odd", "h_projected", "h_kept", "o_ready", "x_updated"])
            loaded = [m.loaded_even, m.loaded_odd]
            block = s.block()

            @block.sync
            def _(sp):
                with sp.Fori(0, B // U) as u:
                    for p in range(U):
                        sp.wait_ge(m.o_ready, U * u)
                        for k in range(K):
                            x = sp.value_load(index[k:k + 1, bass.ds(U * u + p, 1)], min_val=0, max_val=E - 1)
                            for dst, src in ((w1[p][:, k, :], a["L3_ffn_W1"][bass.ds(x, 1), :, :].squeeze(0)),
                                             (w2[p][:, k, :], a["L3_ffn_W2"][bass.ds(x, 1), :, :].squeeze(0)),
                                             (b1[p][:, k, :], a["L3_ffn_b1"][bass.ds(x, 1), :]),
                                             (b2[p][:, k, :], a["L3_ffn_b2"][bass.ds(x, 1), :])):
                                sp.dma_start(dst, src).then_inc(loaded[p], 16)

            @block.gpsimd
            def _(e):
                e.memset(ones[:, :], 1.0).then_inc(m.ones_ready, 1)

            @block.tensor
            def _(e):
                e.wait_ge(m.ones_ready, 1)
                with e.Fori(0, B // U) as u:
                    for p in range(U):
                        e.wait_ge(loaded[p], 16 * 4 * K * (u + 1))
                        e.wait_ge(m.h_kept, U * u)
                        for k in range(K):
                            e.matmul(hps[p][:, k * T:(k + 1) * T], w1[p][:, k, :], zT[:, bass.ds((U * u + p) * T, T)], start=True, stop=False)
                            last = e.matmul(hps[p][:, k * T:(k + 1) * T], b1[p][:, k, :], ones[:, :], start=False, stop=True)
                        last.then_inc(m.h_projected, 1)
                    for p in range(U):
                        e.wait_ge(m.h_kept, U * u + p + 1)
                        e.wait_ge(m.x_updated, U * u)
                        for i in range(TPB):
                            for k in range(K):
                                e.matmul(ops[p][:, i * P:(i + 1) * P], h[p][:, k, i * P:(i + 1) * P], w2[p][:, k, :], start=k == 0, stop=False)
                                last = e.matmul(ops[p][:, i * P:(i + 1) * P], g.ones[0:1, 0:P], b2[p][:, k, :], start=False, stop=k == K - 1)
                        last.then_inc(m.o_ready, 1)

            @block.scalar
            def _(e):
                with e.Fori(0, B // U) as u:
                    for p in range(U):
                        e.wait_ge(m.h_projected, U * u + p + 1)
                        e.wait_ge(m.o_ready, U * u)
                        e.activation(h[p][:, :, :], hps[p][:, :].rearrange("p (k t) -> p k t", k=K), ACT.Gelu).then_inc(m.h_kept, 1)

            @block.vector
            def _(e):
                with e.Fori(0, B // U) as u:
                    for p in range(U):
                        e.wait_ge(m.o_ready, U * u + p + 1)
                        xs = g.x[:, bass.ds(TPB * (U * u + p), TPB), :]
                        e.scalar_tensor_tensor(out=xs, in0=ops[p][:, 0:T].rearrange("p (i d) -> p i d", d=D), scalar=1.0 / K,
                                               in1=xs, op0=ALU.mult, op1=ALU.add).then_inc(m.x_updated, 1)




QW = ["d2v", "img", "txt", "att0", "att1", "f1", "f2"]


def quantise_weights(nc, g, a, q, wscale):
    FT = 4
    shape = {"d2v": (P, DC), "img": (P, D), "txt": (P, D), "att0": (D // 2, D), "att1": (D // 2, D)}
    with ExitStack() as ctx:
        s = Scope(nc, ctx, "l1q")
        raw = {n: s.sb("raw_" + n, list(shape[n])) for n in shape}
        raw["f1"] = s.sb("raw_f1", [P, FT, 2 * D])
        raw["f2"] = s.sb("raw_f2", [P, FT, D])
        low = {n: s.sb("low_" + n, list(raw[n].shape)) for n in QW}
        absum = s.sb("absum", [P, len(QW)])
        thr = s.sb("threshold", [P, len(QW)])
        nthr = s.sb("neg_threshold", [P, len(QW)])
        total = s.ps("total")
        turned = [s.ps(f"turned{i}") for i in range(4)]
        m = s.sems(["loaded", "zeroed", "summed", "total_ready", "scale_ready", "thr_ready", "low_ready", "q_ready",
                    "turned", "kept"])
        moves = [(raw["d2v"][:, :], [q["d2v"][:, :]]), (raw["img"][:, :], [q["img"][:, :]]),
                 (raw["txt"][:, :], [q["txt"][:, :]])]
        for n in ("att0", "att1"):
            moves.append((raw[n][:, :], [q[n][:, 0:D // 2], q[n][:, D // 2:D]]))
        for f in range(FT):
            for half in range(2):
                moves.append((raw["f1"][:, f, half * D:(half + 1) * D], [q["f1"][:, half, f * P:(f + 1) * P]]))
        for f in range(FT):
            moves.append((raw["f2"][:, f, :], [q["f2"][:, f, :]]))
        block = s.block()

        @block.sync
        def _(sp):
            for n in ("d2v", "img", "txt", "att0", "att1"):
                sp.dma_start(raw[n][:, :], a["L1_xattn_W_" + n]).then_inc(m.loaded, 16)
            sp.dma_start(raw["f1"][:, :, :], a["L1_xattn_W_f1"].rearrange("(f p) i -> p f i", p=P)).then_inc(m.loaded, 16)
            sp.dma_start(raw["f2"][:, :, :], a["L1_xattn_W_f2"].rearrange("o (f i) -> o f i", i=D)).then_inc(m.loaded, 16)

        @block.vector
        def _(e):
            e.memset(absum[:, :], 0.0).then_inc(m.zeroed, 1)
            e.wait_ge(m.zeroed, 1)
            e.wait_ge(m.loaded, 16 * len(QW))
            size = {}
            for i, n in enumerate(QW):
                t = raw[n]
                rows = t.shape[0]
                size[n] = int(np.prod(t.shape))
                flat = t[:, :, :].rearrange("p f i -> p (f i)") if len(t.shape) == 3 else t[:, :]
                e.tensor_reduce(absum[0:rows, i:i + 1], flat, AX.X, ALU.add, apply_absolute_value=True).then_inc(m.summed, 1)
            e.wait_ge(m.total_ready, 1)
            for i, n in enumerate(QW):
                e.tensor_scalar(wscale[:, i:i + 1], total[:, i:i + 1], 1.0 / size[n], 1e-5, ALU.mult, ALU.max
                                ).then_inc(m.scale_ready, 1)
            e.wait_ge(m.scale_ready, len(QW))
            e.tensor_scalar(thr[:, :], wscale[:, :], 0.5, None, ALU.mult).then_inc(m.thr_ready, 1)
            e.tensor_scalar(nthr[:, :], wscale[:, :], -0.5, None, ALU.mult).then_inc(m.thr_ready, 1)
            e.wait_ge(m.thr_ready, 2)
            for i, n in enumerate(QW):
                rows = raw[n].shape[0]
                whole = tuple(slice(None) for _ in raw[n].shape)
                e.tensor_scalar(low[n][whole], raw[n][whole], nthr[0:rows, i:i + 1], None, ALU.is_lt).then_inc(m.low_ready, 1)
            for i, n in enumerate(QW):
                rows = raw[n].shape[0]
                whole = tuple(slice(None) for _ in raw[n].shape)
                e.wait_ge(m.low_ready, i + 1)
                e.scalar_tensor_tensor(out=raw[n][whole], in0=raw[n][whole], scalar=thr[0:rows, i:i + 1],
                                       in1=low[n][whole], op0=ALU.is_gt, op1=ALU.subtract).then_inc(m.q_ready, 1)

        @block.tensor
        def _(e):
            e.wait_ge(m.summed, len(QW))
            e.matmul(total[:, 0:len(QW)], g.ones[:, 0:P], absum[:, :], start=True, stop=True).then_inc(m.total_ready, 1)
            e.wait_ge(m.q_ready, len(QW))
            for n, (src, _dst) in enumerate(moves):
                if n >= 4:
                    e.wait_ge(m.kept, n - 3)
                rows, cols = src.shape
                e.transpose(turned[n % 4][0:cols, 0:rows], src, g.ident[0:rows, 0:rows]).then_inc(m.turned, 1)

        @block.scalar
        def _(e):
            for n, (src, dsts) in enumerate(moves):
                rows, cols = src.shape
                e.wait_ge(m.turned, n + 1)
                for k, dst in enumerate(dsts):
                    last = e.activation(dst, turned[n % 4][0:cols, 0:rows], ACT.Copy)
                last.then_inc(m.kept, 1)
            e.wait_ge(m.kept, len(moves))


def activation_scales(nc, g, name, groups, scales):
    G = len(groups)
    with ExitStack() as ctx:
        s = Scope(nc, ctx, name)
        part = s.sb("part", [P, G])
        top = s.sb("top", [1, G])
        step = s.sb("step", [1, G])
        turned = s.ps("turned")
        spread = s.ps("spread")
        m = s.sems(["zeroed", "part_ready", "turned", "top_ready", "step_ready", "spread", "scale_ready"])
        block = s.block()

        @block.vector
        def _(e):
            e.memset(part[:, :], 0.0).then_inc(m.zeroed, 1)
            e.wait_ge(m.zeroed, 1)
            for i, x in enumerate(groups):
                e.tensor_reduce(part[0:x.shape[0], i:i + 1], x, AX.X, ALU.max).then_inc(m.part_ready, 1)
            e.wait_ge(m.turned, 1)
            e.tensor_reduce(top[:, :], turned[0:1, 0:G * P].rearrange("p (g n) -> p g n", n=P), AX.X, ALU.max).then_inc(m.top_ready, 1)
            e.wait_ge(m.top_ready, 1)
            e.tensor_scalar(step[:, :], top[:, :], 1e-8, 1.0 / 127.0, ALU.max, ALU.mult).then_inc(m.step_ready, 1)
            e.wait_ge(m.spread, 1)
            for i, (step_all, inverse) in enumerate(scales):
                e.tensor_copy(step_all, spread[:, i:i + 1]).then_inc(m.scale_ready, 1)
                e.reciprocal(inverse, spread[:, i:i + 1]).then_inc(m.scale_ready, 1)
            e.wait_ge(m.scale_ready, 2 * G)

        @block.tensor
        def _(e):
            e.wait_ge(m.part_ready, G)
            for i in range(G):
                last = e.transpose(turned[0:1, i * P:(i + 1) * P], part[:, i:i + 1], g.ident)
            last.then_inc(m.turned, 1)
            e.wait_ge(m.step_ready, 1)
            e.matmul(spread[:, 0:G], g.ones[0:1, 0:P], step[:, :], start=True, stop=True).then_inc(m.spread, 1)


def quantised_projection(nc, g, name, src, rows, weight, dst, top, step, inverse, wstep, bias, mean=None):
    with ExitStack() as ctx:
        s = Scope(nc, ctx, name)
        out_scale = s.sb("out_scale", [P, 1])
        shifted = [s.sb(f"shifted{i}", [rows, S]) for i in range(2)]
        qx = [s.sb(f"qx{i}", [rows, S], BF16) for i in range(2)]
        ps = [s.ps(f"y{i}") for i in range(2)]
        m = s.sems(["scale_ready", "shifted_ready", "qx_ready", "y_ready", "y_kept", "top_ready", "mean_ready"])
        U = 2
        block = s.block()

        @block.vector
        def _(e):
            e.tensor_tensor(out_scale[:, :], step, wstep, ALU.mult).then_inc(m.scale_ready, 1)
            with e.Fori(0, B // U) as u:
                for p in range(U):
                    e.wait_ge(m.shifted_ready, U * u + p + 1)
                    e.wait_ge(m.y_ready, U * u)
                    e.tensor_scalar(qx[p][:, :], shifted[p][:, :], MAGIC, None, ALU.subtract).then_inc(m.qx_ready, 1)
                for p in range(U):
                    e.wait_ge(m.y_kept, U * u + p + 1)
                    at = U * u + p
                    e.tensor_reduce(top[:, bass.ds(at, 1)], dst[:, bass.ds(at * S, S)], AX.X, ALU.max,
                                    apply_absolute_value=True).then_inc(m.top_ready, 1)
                    if mean is not None:
                        e.tensor_reduce(mean[:, bass.ds(at, 1)], dst[:, bass.ds(at * S, S)], AX.X, ALU.add).then_inc(m.mean_ready, 1)

        @block.scalar
        def _(e):
            e.wait_ge(m.scale_ready, 1)
            with e.Fori(0, B // U) as u:
                for p in range(U):
                    e.wait_ge(m.qx_ready, U * u)
                    e.activation(shifted[p][:, :], src[0:rows, bass.ds((U * u + p) * S, S)], ACT.Identity,
                                 scale=inverse[0:rows, :], bias=g.magic[0:rows, :]).then_inc(m.shifted_ready, 1)
                for p in range(U):
                    e.wait_ge(m.y_ready, U * u + p + 1)
                    e.activation(dst[:, bass.ds((U * u + p) * S, S)], ps[p][:, :], ACT.Identity, scale=out_scale[:, :],
                                 bias=bias).then_inc(m.y_kept, 1)

        @block.tensor
        def _(e):
            with e.Fori(0, B // U) as u:
                for p in range(U):
                    e.wait_ge(m.y_kept, U * u)
                    e.wait_ge(m.qx_ready, U * u + p + 1)
                    e.matmul(ps[p][:, :], weight, qx[p][:, :], start=True, stop=True).then_inc(m.y_ready, 1)


def l1_attention(nc, g, a):
    FT = 4
    INV_SQRT = 1.0 / np.sqrt(D)
    with ExitStack() as outer:
        so = Scope(nc, outer, "l1a")
        q = {"d2v": so.sb("q_d2v", [DC, D], BF16), "img": so.sb("q_img", [D, D], BF16), "txt": so.sb("q_txt", [D, D], BF16),
             "att0": so.sb("q_att0", [D, D], BF16), "att1": so.sb("q_att1", [D, D], BF16),
             "f1": so.sb("q_f1", [D, 2, FT * P], BF16), "f2": so.sb("q_f2", [P, FT, D], BF16)}
        wscale = so.sb("wscale", [P, len(QW)])
        step = so.sb("step", [P, 8])
        inverse = so.sb("inverse", [P, 8])
        CTX, Z, VIS, IMG, FUSED, HID = range(6)
        big = so.sb("big", [P, 2 * B * S])
        vis, img = big[:, 0:B * S], big[:, B * S:2 * B * S]
        hid = big[:, :].rearrange("p (f n) -> p f n", f=FT)
        zT = so.sb("zT", [P, N])
        top = so.sb("top", [P, 2 * B])
        ctx_top = so.sb("ctx_top", [DC, 1])
        avg = so.sb("avg", [P, B])
        f1_bias = so.sb("f1_bias", [P, FT, B])

        def scales(i):
            return step[:, i:i + 1], inverse[:, i:i + 1]

        def w(n):
            return wscale[:, QW.index(n):QW.index(n) + 1]

        quantise_weights(nc, g, a, q, wscale)

        with ExitStack() as ctx:
            s = Scope(nc, ctx, "l1a_norm")
            front = Front(s, g)
            turn = s.ps("turn")
            m = s.sems(["z_kept", "top_ready", "ctx_top_ready", "steps"])
            block = s.block()

            @block.gpsimd
            def _(e):
                with e.Fori(0, B) as b:
                    front.gpsimd(e, b)

            @block.tensor
            def _(e):
                with e.Fori(0, B) as b:
                    e.wait_ge(m.z_kept, b)
                    front.tensor(e, b, turn)

            @block.scalar
            def _(e):
                with e.Fori(0, B) as b:
                    e.wait_ge(front.z_turned, b + 1)
                    e.activation(zT[:, bass.ds(b * T, T)], turn[:, 0:T], ACT.Copy).then_inc(m.z_kept, 1)

            @block.vector
            def _(e):
                steps = Steps(e, m.steps, front.steps)
                e.tensor_reduce(ctx_top[:, :], g.ctxT[0:DC, :], AX.X, ALU.max, apply_absolute_value=True).then_inc(m.ctx_top_ready, 1)
                with e.Fori(0, B) as b:
                    steps.begin(b)
                    front.vector(e, b, steps)
                    e.wait_ge(m.z_kept, b + 1)
                    e.tensor_reduce(top[:, bass.ds(b, 1)], zT[:, bass.ds(b * T, T)], AX.X, ALU.max,
                                    apply_absolute_value=True).then_inc(m.top_ready, 1)
                    steps.end()

        activation_scales(nc, g, "l1s_in", [ctx_top[:, :], top[:, 0:B]], [scales(CTX), scales(Z)])
        quantised_projection(nc, g, "l1p_vis", g.ctxT, DC, q["d2v"][:, :], vis, top, step[:, CTX:CTX + 1],
                             inverse[:, CTX:CTX + 1], w("d2v"), g.l1_bd2v[:, 0:1])
        activation_scales(nc, g, "l1s_vis", [top[:, 0:B]], [scales(VIS)])
        quantised_projection(nc, g, "l1p_img", vis, P, q["img"][:, :], img, top, step[:, VIS:VIS + 1],
                             inverse[:, VIS:VIS + 1], w("img"), g.l1_bimg[:, 0:1], mean=avg)
        activation_scales(nc, g, "l1s_img", [top[:, 0:B]], [scales(IMG)])

        with ExitStack() as ctx:
            s = Scope(nc, ctx, "l1a_att")
            sc = s.sb("out_scales", [P, 3])
            shift_i = s.sb("shifted_img", [P, S])
            shift_z = s.sb("shifted_z", [P, T])
            qi = s.sb("q_img_chunk", [P, S], BF16)
            qz = s.sb("q_z_chunk", [P, T], BF16)
            kT = [s.sb(f"kT{i}", [P, S]) for i in range(2)]
            kt = [s.sb(f"k_rows{i}", [P, KT, D]) for i in range(2)]
            f = s.sb("fused", [P, T])
            rmax = s.sb("rmax", [P, 2 * TPB])
            nmax = s.sb("nmax", [P, 2 * TPB])
            rsum = s.sb("rsum", [P, 2 * TPB])
            rinv = s.sb("rinv", [P, 2 * TPB])
            prob = [s.sb(f"prob{i}", [P, S]) for i in range(TPB)]
            pT = s.sb("probT", [P, KT, T])
            kps = [s.ps(f"k{i}") for i in range(2)]
            fps = s.ps("f")
            sps = [s.ps(f"scores{i}") for i in range(TPB)]
            tps = [s.ps(f"turned{i}") for i in range(TPB)]
            ops = s.ps("o")
            m = s.sems(["scales_ready", "shifted", "quantised", "kT_projected", "kT_kept", "kr_projected", "kr_kept",
                        "f_projected", "f_kept", "scores_ready", "max_ready", "nmax_ready", "exp_ready", "rinv_ready",
                        "prob_ready", "turned", "pT_kept", "o_ready", "f_updated", "f_stored", "top_ready", "avg_scaled"])
            R = 2
            block = s.block()

            @block.vector
            def _(e):
                e.tensor_tensor(sc[:, 0:1], step[:, IMG:IMG + 1], w("att0"), ALU.mult).then_inc(m.scales_ready, 1)
                e.tensor_tensor(sc[:, 1:2], step[:, IMG:IMG + 1], w("att1"), ALU.mult).then_inc(m.scales_ready, 1)
                e.tensor_tensor(sc[:, 2:3], step[:, Z:Z + 1], w("txt"), ALU.mult).then_inc(m.scales_ready, 1)
                e.tensor_scalar(avg[:, :], avg[:, :], 1.0 / S, None, ALU.mult).then_inc(m.avg_scaled, 1)
                e.wait_ge(m.scales_ready, 3)
                with e.Fori(0, B) as b:
                    e.wait_ge(m.shifted, 2 * b + 1)
                    e.tensor_scalar(qi[:, :], shift_i[:, :], MAGIC, None, ALU.subtract).then_inc(m.quantised, 1)
                    e.wait_ge(m.shifted, 2 * b + 2)
                    e.tensor_scalar(qz[:, :], shift_z[:, :], MAGIC, None, ALU.subtract).then_inc(m.quantised, 1)
                    for r in range(R):
                        e.wait_ge(m.kr_projected, R * b + r + 1)
                        e.scalar_tensor_tensor(out=kt[r][:, :, :], in0=ops[:, :].rearrange("p (t d) -> p t d", d=D),
                                               scalar=sc[:, r:r + 1], in1=bcast(g.l1_batt_rows[r][:, :].unsqueeze(1), [P, KT, D]),
                                               op0=ALU.mult, op1=ALU.add).then_inc(m.kr_kept, 1)
                    for r in range(R):
                        for i in range(TPB):
                            n = r * TPB + i
                            e.wait_ge(m.scores_ready, R * TPB * b + n + 1)
                            e.tensor_reduce(rmax[:, n:n + 1], sps[i][:, :], AX.X, ALU.max, negate=True).then_inc(m.max_ready, 1)
                            e.wait_ge(m.max_ready, R * TPB * b + n + 1)
                            e.tensor_scalar(nmax[:, n:n + 1], rmax[:, n:n + 1], INV_SQRT, None, ALU.mult).then_inc(m.nmax_ready, 1)
                        for i in range(TPB):
                            n = r * TPB + i
                            e.wait_ge(m.exp_ready, R * TPB * b + n + 1)
                            e.reciprocal(rinv[:, n:n + 1], rsum[:, n:n + 1]).then_inc(m.rinv_ready, 1)
                            e.wait_ge(m.rinv_ready, R * TPB * b + n + 1)
                            e.tensor_scalar(prob[i][:, :], prob[i][:, :], rinv[:, n:n + 1], None, ALU.mult).then_inc(m.prob_ready, 1)
                        e.wait_ge(m.o_ready, R * b + r + 1)
                        e.wait_ge(m.f_kept, b + 1)
                        if r:
                            e.wait_ge(m.f_updated, R * b + r)
                        e.scalar_tensor_tensor(out=f[:, :], in0=ops[:, 0:T], scalar=0.1, in1=f[:, :], op0=ALU.mult,
                                               op1=ALU.add).then_inc(m.f_updated, 1)
                    e.wait_ge(m.f_updated, R * b + R)
                    e.tensor_copy(zT[:, bass.ds(b * T, T)], f[:, :]).then_inc(m.f_stored, 1)
                    e.tensor_reduce(top[:, bass.ds(b, 1)], f[:, :], AX.X, ALU.max, apply_absolute_value=True).then_inc(m.top_ready, 1)
                e.wait_ge(m.avg_scaled, 1)
                e.tensor_reduce(top[:, B:B + 1], avg[:, :], AX.X, ALU.max, apply_absolute_value=True).then_inc(m.top_ready, 1)

            @block.scalar
            def _(e):
                e.wait_ge(m.scales_ready, 3)
                with e.Fori(0, B) as b:
                    e.wait_ge(m.top_ready, b)
                    e.activation(shift_i[:, :], img[:, bass.ds(b * S, S)], ACT.Identity, scale=inverse[:, IMG:IMG + 1],
                                 bias=g.magic[:, :]).then_inc(m.shifted, 1)
                    e.activation(shift_z[:, :], zT[:, bass.ds(b * T, T)], ACT.Identity, scale=inverse[:, Z:Z + 1],
                                 bias=g.magic[:, :]).then_inc(m.shifted, 1)
                    for r in range(R):
                        e.wait_ge(m.kT_projected, R * b + r + 1)
                        e.activation(kT[r][:, :], kps[r][:, :], ACT.Identity, scale=sc[:, r:r + 1],
                                     bias=g.l1_batt[r][:, 0:1]).then_inc(m.kT_kept, 1)
                    e.wait_ge(m.f_projected, b + 1)
                    e.activation(f[:, :], fps[:, 0:T], ACT.Identity, scale=sc[:, 2:3], bias=g.l1_btxt[:, 0:1]).then_inc(m.f_kept, 1)
                    for r in range(R):
                        for i in range(TPB):
                            n = r * TPB + i
                            e.wait_ge(m.nmax_ready, R * TPB * b + n + 1)
                            e.activation(prob[i][:, :], sps[i][:, :], ACT.Exp, scale=INV_SQRT, bias=nmax[:, n:n + 1],
                                         accum_out=rsum[:, n:n + 1]).then_inc(m.exp_ready, 1)
                        for i in range(TPB):
                            n = r * TPB + i
                            e.wait_ge(m.turned, R * TPB * b + n + 1)
                            e.activation(pT[:, :, i * P:(i + 1) * P], tps[i][:, :].rearrange("p (t q) -> p t q", q=P),
                                         ACT.Copy).then_inc(m.pT_kept, 1)

            @block.tensor
            def _(e):
                with e.Fori(0, B) as b:
                    e.wait_ge(m.quantised, 2 * b + 1)
                    for r, n in enumerate(("att0", "att1")):
                        e.matmul(kps[r][:, :], q[n][:, :], qi[:, :], start=True, stop=True).then_inc(m.kT_projected, 1)
                    e.wait_ge(m.quantised, 2 * b + 2)
                    e.matmul(fps[:, 0:T], q["txt"][:, :], qz[:, :], start=True, stop=True).then_inc(m.f_projected, 1)
                    for r, n in enumerate(("att0", "att1")):
                        e.wait_ge(m.f_updated, R * b)
                        e.wait_ge(m.kr_kept, R * b + r)
                        for t in range(KT):
                            last = e.matmul(ops[:, t * P:(t + 1) * P], qi[:, t * P:(t + 1) * P], q[n][:, :], start=True, stop=True)
                        last.then_inc(m.kr_projected, 1)
                    e.wait_ge(m.kr_kept, R * b + R)
                    for r in range(R):
                        e.wait_ge(m.kT_kept, R * b + r + 1)
                        e.wait_ge(m.f_kept, b + 1)
                        e.wait_ge(m.f_updated, R * b + r)
                        for i in range(TPB):
                            e.matmul(sps[i][:, :], f[:, i * P:(i + 1) * P], kT[r][:, :], start=True, stop=True).then_inc(m.scores_ready, 1)
                        for i in range(TPB):
                            e.wait_ge(m.prob_ready, R * TPB * b + r * TPB + i + 1)
                            for t in range(KT):
                                last = e.transpose(tps[i][:, t * P:(t + 1) * P], prob[i][:, t * P:(t + 1) * P], g.ident)
                            last.then_inc(m.turned, 1)
                        e.wait_ge(m.pT_kept, R * TPB * b + r * TPB + TPB)
                        for t in range(KT):
                            last = e.matmul(ops[:, 0:T], kt[r][:, t, :], pT[:, t, :], start=t == 0, stop=t == KT - 1)
                        last.then_inc(m.o_ready, 1)

        activation_scales(nc, g, "l1s_fused", [top[:, 0:B + 1]], [scales(FUSED)])

        with ExitStack() as ctx:
            s = Scope(nc, ctx, "l1a_f1")
            sc = s.sb("out_scale", [P, 1])
            shift_a = s.sb("shifted_avg", [P, B])
            qa = s.sb("q_avg", [P, B], BF16)
            shift = [s.sb(f"shifted{i}", [P, T]) for i in range(2)]
            qx = [s.sb(f"qx{i}", [P, T], BF16) for i in range(2)]
            aps = s.ps("avg")
            hps = [s.ps(f"h{i}", (P, 2 * 512)) for i in range(2)]
            U = 2
            m = s.sems(["scale_ready", "avg_shifted", "avg_quantised", "avg_projected", "bias_ready", "shifted",
                        "quantised", "h_ready", "h_kept", "top_ready"])
            block = s.block()

            @block.scalar
            def _(e):
                e.activation(shift_a[:, :], avg[:, :], ACT.Identity, scale=inverse[:, FUSED:FUSED + 1], bias=g.magic[:, :]).then_inc(m.avg_shifted, 1)
                e.wait_ge(m.bias_ready, FT)
                with e.Fori(0, B // U) as u:
                    for p in range(U):
                        e.wait_ge(m.quantised, U * u)
                        e.activation(shift[p][:, :], zT[:, bass.ds((U * u + p) * T, T)], ACT.Identity,
                                     scale=inverse[:, FUSED:FUSED + 1], bias=g.magic[:, :]).then_inc(m.shifted, 1)
                    for p in range(U):
                        for k in range(FT):
                            e.wait_ge(m.h_ready, U * u + p + 1)
                            e.activation(hid[:, k, bass.ds((U * u + p) * T, T)], hps[p][:, k * T:(k + 1) * T], ACT.Relu,
                                         scale=sc[:, :], bias=f1_bias[:, k, bass.ds(U * u + p, 1)]).then_inc(m.h_kept, 1)

            @block.vector
            def _(e):
                e.tensor_tensor(sc[:, :], step[:, FUSED:FUSED + 1], w("f1"), ALU.mult).then_inc(m.scale_ready, 1)
                e.wait_ge(m.avg_shifted, 1)
                e.tensor_scalar(qa[:, :], shift_a[:, :], MAGIC, None, ALU.subtract).then_inc(m.avg_quantised, 1)
                e.wait_ge(m.avg_projected, 1)
                e.wait_ge(m.scale_ready, 1)
                for k in range(FT):
                    e.tensor_scalar(f1_bias[:, k, :], aps[:, k * B:(k + 1) * B], sc[:, :], g.l1_bf1[:, k:k + 1], ALU.mult,
                                    ALU.add).then_inc(m.bias_ready, 1)
                with e.Fori(0, B // U) as u:
                    for p in range(U):
                        e.wait_ge(m.shifted, U * u + p + 1)
                        e.wait_ge(m.h_ready, U * u)
                        e.tensor_scalar(qx[p][:, :], shift[p][:, :], MAGIC, None, ALU.subtract).then_inc(m.quantised, 1)
                    for p in range(U):
                        e.wait_ge(m.h_kept, FT * (U * u + p + 1))
                        e.tensor_reduce(top[:, bass.ds(U * u + p, 1)], hid[:, :, bass.ds((U * u + p) * T, T)], AX.XY,
                                        ALU.max).then_inc(m.top_ready, 1)

            @block.tensor
            def _(e):
                e.wait_ge(m.avg_quantised, 1)
                for k in range(FT):
                    last = e.matmul(aps[:, k * B:(k + 1) * B], q["f1"][:, 1, k * P:(k + 1) * P], qa[:, :], start=True, stop=True)
                last.then_inc(m.avg_projected, 1)
                with e.Fori(0, B // U) as u:
                    for p in range(U):
                        e.wait_ge(m.quantised, U * u + p + 1)
                        e.wait_ge(m.h_kept, FT * U * u)
                        for k in range(FT):
                            last = e.matmul(hps[p][:, k * T:(k + 1) * T], q["f1"][:, 0, k * P:(k + 1) * P], qx[p][:, :], start=True, stop=True)
                        last.then_inc(m.h_ready, 1)

        activation_scales(nc, g, "l1s_hid", [top[:, 0:B]], [scales(HID)])

        with ExitStack() as ctx:
            s = Scope(nc, ctx, "l1a_f2")
            sc = s.sb("out_scale", [P, 1])
            shift = [s.sb(f"shifted{i}", [P, FT, T]) for i in range(2)]
            qx = [s.sb(f"qx{i}", [P, FT, T], BF16) for i in range(2)]
            yps = [s.ps(f"y{i}") for i in range(2)]
            U = 2
            m = s.sems(["scale_ready", "shifted", "quantised", "y_ready", "x_biased", "x_updated"])
            block = s.block()

            @block.scalar
            def _(e):
                with e.Fori(0, B // U) as u:
                    for p in range(U):
                        e.wait_ge(m.quantised, U * u)
                        e.activation(shift[p][:, :, :], hid[:, :, bass.ds((U * u + p) * T, T)], ACT.Identity,
                                     scale=inverse[:, HID:HID + 1], bias=g.magic[:, :]).then_inc(m.shifted, 1)

            @block.vector
            def _(e):
                e.tensor_tensor(sc[:, :], step[:, HID:HID + 1], w("f2"), ALU.mult).then_inc(m.scale_ready, 1)
                e.wait_ge(m.scale_ready, 1)
                with e.Fori(0, B // U) as u:
                    for p in range(U):
                        e.wait_ge(m.shifted, U * u + p + 1)
                        e.wait_ge(m.y_ready, U * u)
                        e.tensor_scalar(qx[p][:, :, :], shift[p][:, :, :], MAGIC, None, ALU.subtract).then_inc(m.quantised, 1)
                        xs = g.x[:, bass.ds(TPB * (U * u + p), TPB), :]
                        e.tensor_tensor(xs, xs, bcast(g.l1_bf2[:, :].unsqueeze(1), [P, TPB, D]), ALU.add).then_inc(m.x_biased, 1)
                    for p in range(U):
                        e.wait_ge(m.y_ready, U * u + p + 1)
                        e.wait_ge(m.x_biased, U * u + p + 1)
                        xs = g.x[:, bass.ds(TPB * (U * u + p), TPB), :]
                        e.scalar_tensor_tensor(out=xs, in0=yps[p][:, 0:T].rearrange("p (i d) -> p i d", d=D), scalar=sc[:, :],
                                               in1=xs, op0=ALU.mult, op1=ALU.add).then_inc(m.x_updated, 1)

            @block.tensor
            def _(e):
                with e.Fori(0, B // U) as u:
                    for p in range(U):
                        e.wait_ge(m.quantised, U * u + p + 1)
                        e.wait_ge(m.x_updated, U * u)
                        for i in range(TPB):
                            for k in range(FT):
                                last = e.matmul(yps[p][:, i * P:(i + 1) * P], qx[p][:, k, i * P:(i + 1) * P], q["f2"][:, k, :],
                                                start=k == 0, stop=k == FT - 1)
                        last.then_inc(m.y_ready, 1)



def weights_stage(nc, g, a):
    with ExitStack() as ctx:
        s = Scope(nc, ctx, "weights")
        ps = [s.ps(f"turned{i}") for i in range(2)]
        turned = s.sem("turned")
        kept = s.sem("kept")
        block = s.block()

        @block.tensor
        def _(e):
            e.wait_ge(g.weights_loaded, 16 * len(g.loads))
            for n, (dst, src) in enumerate(g.to_turn):
                if n >= 2:
                    e.wait_ge(kept, n - 1)
                rows, cols = src.shape
                e.transpose(ps[n % 2][0:cols, 0:rows], src, g.ident[0:rows, 0:rows]).then_inc(turned, 1)

        @block.scalar
        def _(e):
            for n, (dst, src) in enumerate(g.to_turn):
                rows, cols = src.shape
                e.wait_ge(turned, n + 1)
                e.activation(dst, ps[n % 2][0:cols, 0:rows], ACT.Copy).then_inc(kept, 1)
            e.wait_ge(kept, len(g.to_turn))


def store_stage(nc, g, a):
    with ExitStack() as ctx:
        s = Scope(nc, ctx, "store")
        stored = s.sem("stored")
        block = s.block()

        @block.sync
        def _(sp):
            sp.dma_start(a["out"].rearrange("b (i p) d -> p (b i) d", p=P), g.x[:, :, :]).then_inc(stored, 16)
            sp.wait_ge(stored, 16)


STAGES = [l0_attention, l0_ffn, l1_attention, l1_ffn, l2_attention, l2_ffn, l3_attention, l3_ffn]


def build(nc, a, stages=None):
    with ExitStack() as ctx:
        g = Shared()

        def keep(name, shape, dtype=F32):
            return ctx.enter_context(nc.sbuf_tensor(name, shape, dtype))

        def loaded(name, shape, src, first=False):
            t = keep("w_" + name, shape)
            (g.loads_first if first else g.loads).append((t[tuple(slice(None) for _ in shape)], src))
            return t

        g.loads_first, g.loads, g.to_turn = [], [], []
        g.const = keep("const", [P, C_ALL])
        g.x = keep("x_tokens", [P, TILES, D])
        g.ctxT = keep("ctxT", [DC + 1, B * S])
        g.ones = keep("ones", [P, P])
        g.neg_half = keep("neg_half", [P, TILES])
        g.magic = keep("magic", [P, 1])
        g.ident = g.const[:, C_ID:C_ID + P]
        g.vector_rows = keep("vector_rows", [P, P])
        g.vectors = keep("vectors", [P, P])
        g.vectors_used = 0
        g.weights_loaded = ctx.enter_context(nc.semaphore("weights_loaded"))

        def row(v):
            return a[v].unsqueeze(0)

        def rows(v):
            return a[v].unsqueeze(0).to_broadcast([P, a[v].shape[0]])

        def columns(*sources):
            first = g.vectors_used
            for src, at in sources:
                n, width = src.shape
                g.loads_first.append((g.vector_rows[first:first + n, at:at + width], src))
            g.vectors_used = first + n
            return g.vectors[:, first:first + n]

        def transposed(name, w):
            rows, cols = a[w].shape
            raw = loaded(name + "_raw", [rows, cols], a[w])
            t = keep("w_" + name, [cols, rows])
            g.to_turn.append((t[:, :], raw[:, :]))
            return t

        def biased(name, w, bias, width):
            t = keep("w_" + name, [DC + 1, width])
            g.loads_first.append((t[0:DC, :], a[w]))
            if bias is not None:
                g.loads_first.append((t[DC:DC + 1, :], row(bias)))
            return t

        g.l0_wk = biased("l0_wk", "L0_xattn_Wk", "L0_xattn_bk", D)
        g.l0_wv = biased("l0_wv", "L0_xattn_Wv", "L0_xattn_bv", D)
        g.l0_wq = loaded("l0_wq", [D, D], a["L0_xattn_Wq"], True)
        g.l0_bq = loaded("l0_bq", [1, D], row("L0_xattn_bq"), True)
        g.l0_wo = loaded("l0_wo", [D, D], a["L0_xattn_Wo"], True)
        g.l0_bo = loaded("l0_bo", [1, D], row("L0_xattn_bo"), True)
        g.l0_gamma = loaded("l0_gamma", [P, D], rows("L0_xattn_ln_gamma"), True)
        g.l0_beta = loaded("l0_beta", [P, D], rows("L0_xattn_ln_beta"), True)

        g.l0_lng = columns((row("L0_ffn_ln_g"), 0))
        g.l0_lnb = columns((row("L0_ffn_ln_b"), 0))
        g.l0_rw = loaded("l0_rw", [D, E], a["L0_ffn_rW"])
        g.l0_rb = loaded("l0_rb", [1, E], row("L0_ffn_rb"))
        g.l0_w1 = loaded("l0_w1", [D, E, 256], a["L0_ffn_W1"].rearrange("e d f -> d e f"))
        g.l0_b1 = columns((a["L0_ffn_b1"].rearrange("e (f p) -> (e f) p", p=P), 0))
        g.l0_w2 = loaded("l0_w2", [P, E, 2, D], a["L0_ffn_W2"].rearrange("e (f p) d -> p e f d", p=P))
        g.l0_b2 = loaded("l0_b2", [E, D], a["L0_ffn_b2"])

        for l, heads in (("2", 8), ("3", 16)):
            w = heads * 64
            wq = loaded(f"l{l}_wq", [D, w], a[f"L{l}_xattn_Wq"])
            wk = loaded(f"l{l}_wk", [DC, w], a[f"L{l}_xattn_Wk"])
            wv = loaded(f"l{l}_wv", [DC, w], a[f"L{l}_xattn_Wv"])
            wo = loaded(f"l{l}_wo", [P, heads // 2, D], a[f"L{l}_xattn_Wo"].rearrange("(c p) d -> p c d", p=P))
            bo = loaded(f"l{l}_bo", [1, D], row(f"L{l}_xattn_bo"))
            if l == "2":
                g.l2_wq, g.l2_wk, g.l2_wv, g.l2_wo, g.l2_bo = wq, wk, wv, wo, bo
            else:
                g.l3_wq, g.l3_wk, g.l3_wv, g.l3_wo, g.l3_bo = wq, wk, wv, wo, bo

        g.l1_lng = columns((row("L1_ffn_ln_g"), 0))
        g.l1_lnb = columns((row("L1_ffn_ln_b"), 0))
        g.l1_attn_b = columns((row("L1_ffn_attn_b"), 0))
        g.l1_b1 = columns((a["L1_ffn_b1"].rearrange("e (f p) -> (e f) p", p=P), 0))
        g.l1_b2 = columns((a["L1_ffn_b2"], 0))
        g.l1_attn_w = loaded("l1_attn_w", [D, D], a["L1_ffn_attn_w"])
        g.l1_next_w = loaded("l1_next_w", [D, D], a["L1_ffn_next_w"])
        g.l1_next_b = loaded("l1_next_b", [1, D], row("L1_ffn_next_b"))

        g.l2_wqT = transposed("l2_wqT", "L2_ffn_W_Q")
        g.l2_wkT = transposed("l2_wkT", "L2_ffn_W_K")
        g.l2_woT = transposed("l2_woT", "L2_ffn_W_O")
        g.l2_winvT = transposed("l2_winvT", "L2_ffn_W_inv")
        g.l2_rw1T = transposed("l2_rw1T", "L2_ffn_router_w1")
        g.l2_rw2T = transposed("l2_rw2T", "L2_ffn_router_w2")
        g.l2_rb1 = columns((row("L2_ffn_router_b1"), 0))
        g.l2_rb2 = loaded("l2_rb2", [1, E], row("L2_ffn_router_b2"))
        g.l2_eb = loaded("l2_eb", [1, E], row("L2_ffn_expert_bias"))
        g.l2_alpha = loaded("l2_alpha", [P, 1], a["L2_ffn_alpha_bi"].unsqueeze(0).to_broadcast([P, 1]))
        g.l2_v = [loaded(f"l2_v{i}", [D, E, 64], a[w].rearrange("k d r -> d k r")) for i, w in
                  enumerate(("L2_ffn_V_fwd", "L2_ffn_W_inv_exp"))]
        g.l2_w = [loaded(f"l2_w{i}", [D, E, 64], a[w].rearrange("k d r -> d k r")) for i, w in
                  enumerate(("L2_ffn_W_fwd", "L2_ffn_V_inv"))]
        g.l2_uT = []
        for i, w in enumerate(("L2_ffn_U_fwd", "L2_ffn_U_inv")):
            raw = loaded(f"l2_u{i}", [D, E, 64], a[w].rearrange("k d r -> d k r"))
            uT = keep(f"l2_uT{i}", [P, 4, D])
            for c in range(4):
                g.to_turn.append((uT[:, c, :], raw[:, 2 * c:2 * c + 2, :].rearrange("p k r -> p (k r)")))
            g.l2_uT.append(uT)
        g.l2_b = [loaded(f"l2_b{i}", [E, D], a[w]) for i, w in enumerate(("L2_ffn_b_fwd", "L2_ffn_b_inv"))]

        g.l3_wr = loaded("l3_wr", [D, E], a["L3_ffn_Wr"])
        g.l3_br = loaded("l3_br", [1, E], row("L3_ffn_br"))

        g.l1_bd2v = columns((row("L1_xattn_b_d2v"), 0))
        g.l1_bimg = columns((row("L1_xattn_b_img"), 0))
        g.l1_btxt = columns((row("L1_xattn_b_txt"), 0))
        g.l1_batt = [columns((row(f"L1_xattn_b_att{i}"), 0), (row(f"L1_xattn_b_att{i}"), D // 2)) for i in range(2)]
        g.l1_batt_rows = []
        for i in range(2):
            t = keep(f"w_l1_batt_rows{i}", [P, D])
            for half in range(2):
                g.loads.append((t[:, half * D // 2:(half + 1) * D // 2], rows(f"L1_xattn_b_att{i}")))
            g.l1_batt_rows.append(t)
        g.l1_bf1 = columns((a["L1_xattn_b_f1"].rearrange("(f p) -> f p", p=P), 0))
        g.l1_bf2 = loaded("l1_bf2", [P, D], rows("L1_xattn_b_f2"))
        load_stage(nc, g, a)
        weights_stage(nc, g, a)
        for stage in (STAGES if stages is None else stages):
            stage(nc, g, a)
            clear_semaphores(nc)
        store_stage(nc, g, a)


def kernel(**inputs):
    import concourse.bacc as bacc
    from concourse.bass_utils import run_bass_kernel_spmd

    nc = bacc.Bacc("TRN2", target_bir_lowering=False, num_devices=1)
    arrays, args = {}, {}
    for name, value in {**inputs, "constants": shape_constants()}.items():
        v = np.ascontiguousarray(value)
        v = v.reshape(v.shape or (1,))
        arrays["in_" + name] = v
        args[name] = nc.dram_tensor("in_" + name, v.shape, mybir.dt.from_np(v.dtype), kind="ExternalInput").ap()
    args["out"] = nc.dram_tensor("out_x", (B, T, D), F32, kind="ExternalOutput").ap()
    build(nc, args)
    return run_bass_kernel_spmd(nc, [arrays], core_ids=[0]).results[0]["out_x"]
```

```python
from collections import namedtuple
from contextlib import ExitStack

import concourse.bass as bass
import numpy as np
from concourse import mybir

F32 = mybir.dt.float32
F32R = mybir.dt.float32r
BF16 = mybir.dt.bfloat16
I32 = mybir.dt.int32
ALU = mybir.AluOpType
ACT = mybir.ActivationFunctionType
AX = mybir.AxisListType

P = 128
B, T, D = 8, 256, 128
S, DC = 512, 96
N = B * T
TILES = N // P
TPB = T // P
KT = S // P
EPS = 1e-5
E = 8
MAGIC = 12582912.0

C_ID = 0
C_HEAD = C_ID + P
C_REV = C_HEAD + 16
C_INVN = C_REV + E
C_SEL = C_INVN + TPB
C_ALL = C_SEL + 4 * P



def shape_constants():
    c = np.zeros((P, C_ALL), np.float32)
    c[:, C_ID:C_ID + P] = np.eye(P)
    for p in range(P):
        c[p, C_HEAD + p // 8] = 1
        for i in range(TPB):
            c[p, C_INVN + i] = 1.0 / (i * P + p + 1)
    c[:, C_REV:C_REV + E] = E - np.arange(E)
    for k in range(E):
        lo = C_SEL + (k // 2) * P + (k % 2) * 64
        c[k, lo:lo + 64] = 1
    return c


class Steps:

    def __init__(self, engine, sem, per_turn=0):
        self.engine, self.sem, self.per_turn = engine, sem, per_turn
        self.turn, self.done = 0, 0

    def begin(self, turn):
        self.turn, self.done = turn, 0

    def add(self, instruction):
        instruction.then_inc(self.sem, 1)
        self.done += 1

    def settle(self):
        self.engine.wait_ge(self.sem, self.turn * self.per_turn + self.done)

    def end(self):
        assert self.done == self.per_turn, (self.done, self.per_turn)


class Scope:

    to_clear = []

    def __init__(self, nc, ctx, name):
        self.nc, self.ctx, self.name = nc, ctx, name

    def sb(self, name, shape, dtype=F32):
        return self.ctx.enter_context(self.nc.sbuf_tensor(f"{self.name}_{name}", shape, dtype))

    def ps(self, name, shape=(P, 512), dtype=F32):
        return self.ctx.enter_context(self.nc.psum_tensor(f"{self.name}_{name}_ps", list(shape), dtype))

    def sem(self, name):
        sem = self.ctx.enter_context(self.nc.semaphore(f"{self.name}_{name}"))
        Scope.to_clear.append(sem.num)
        return sem

    def sems(self, names):
        return namedtuple("Semaphores", names)(*[self.sem(n) for n in names])

    def block(self):
        return self.ctx.enter_context(self.nc.Block())


def clear_semaphores(nc):
    nums = sorted(set(Scope.to_clear))
    Scope.to_clear.clear()
    runs = []
    for n in nums:
        if runs and runs[-1][1] == n:
            runs[-1][1] = n + 1
        else:
            runs.append([n, n + 1])
    with nc.Block() as block:
        @block.gpsimd
        def _(e):
            for first, end in runs:
                e.sem_clear(range(first, end))


def wait(e, sem, count):
    if not isinstance(count, int) or count > 0:
        e.wait_ge(sem, count)


class Shared:
    pass


def bcast(ap, shape):
    return ap.to_broadcast(shape)



class Front:

    def __init__(self, s, g, tile=None, tiles=TPB, twice=False):
        self.g, self.tiles, self.twice = g, tiles, twice
        self.tile = tile or (lambda b, i: g.x[:, TPB * b + i, :])
        norms = 2 if twice else 1
        self.steps = 2 * tiles * norms
        self.stats = s.sb("ln_stats", [P, tiles, 6])
        self.mv = s.sb("ln_mean_var", [P, tiles, 2])
        self.held = s.sb("ln_held", [P, 1])
        self.var = s.sb("ln_var_eps", [P, tiles])
        self.rstd = s.sb("ln_rstd", [P, tiles])
        self.outer = s.sb("ln_outer", [P, tiles, D]) if twice else None
        self.z = s.sb("ln_z", [P, tiles, D])
        self.norms = norms
        self.var_ready = s.sem("var_ready")
        self.rstd_ready = s.sem("rstd_ready")
        self.outer_ready = s.sem("outer_ready") if twice else None
        self.z_ready = s.sem("z_ready")
        self.z_turned = s.sem("z_turned")

    def _norm(self, e, b, steps, turn, source, out, ready):
        for i in range(self.tiles):
            steps.add(e.bn_stats(self.stats[:, i, :], source(i)))
        steps.settle()
        e.memset(self.held[:, :], 0.0)
        for i in range(self.tiles):
            steps.add(e.bn_aggr(self.mv[:, i, :], self.stats[:, i, :]))
        steps.settle()
        e.tensor_scalar(self.var[:, :], self.mv[:, :, 1], EPS, None, ALU.add).then_inc(self.var_ready, 1)
        e.wait_ge(self.rstd_ready, self.norms * b + turn + 1)
        for i in range(self.tiles):
            e.tensor_scalar(out[:, i, :], source(i), self.mv[:, i, 0:1], self.rstd[:, i:i + 1],
                            ALU.subtract, ALU.mult).then_inc(ready, 1)

    def vector(self, e, b, steps):
        if self.twice:
            self._norm(e, b, steps, 0, lambda i: self.tile(b, i), self.outer, self.outer_ready)
            e.wait_ge(self.outer_ready, self.tiles * (b + 1))
            self._norm(e, b, steps, 1, lambda i: self.outer[:, i, :], self.z, self.z_ready)
        else:
            self._norm(e, b, steps, 0, lambda i: self.tile(b, i), self.z, self.z_ready)

    def gpsimd(self, e, b):
        for n in range(self.norms):
            e.wait_ge(self.var_ready, self.norms * b + n + 1)
            e.tensor_tensor(self.rstd[:, :], self.var[:, :], self.g.neg_half[:, 0:self.tiles],
                            ALU.pow).then_inc(self.rstd_ready, 1)

    def tensor(self, e, b, out):
        e.wait_ge(self.z_ready, self.tiles * (b + 1))
        for i in range(self.tiles):
            last = e.transpose(out[:, i * P:(i + 1) * P], self.z[:, i, :], self.g.ident)
        last.then_inc(self.z_turned, 1)



def load_stage(nc, g, a):
    with ExitStack() as ctx:
        s = Scope(nc, ctx, "load")
        rows = g.ctx_rows
        turned = [s.ps(f"turned{i}") for i in range(2)]
        ctx_loaded = s.sem("ctx_loaded")
        const_loaded = s.sem("const_loaded")
        ctx_turned = s.sem("ctx_turned")
        ctx_kept = s.sem("ctx_kept")
        filled = s.sem("filled")
        block = s.block()

        @block.sync
        def _(sp):
            sp.dma_start(g.const[:, :], a["constants"]).then_inc(const_loaded, 16)
            sp.dma_start(rows[:, :, :].rearrange("p (b t) d -> p b (t d)", t=KT),
                         a["ctx_768"].rearrange("b (p t) d -> p b (t d)", t=KT)).then_inc(ctx_loaded, 16)
            sp.dma_start(g.x[:, :, :], a["x"].rearrange("b (i p) d -> p (b i) d", p=P)).then_inc(const_loaded, 16)
            for dst, src in g.loads_first:
                sp.dma_start(dst, src).then_inc(const_loaded, 16)
            for dst, src in g.loads:
                sp.dma_start(dst, src).then_inc(g.weights_loaded, 16)
            sp.wait_ge(const_loaded, 16 * (2 + len(g.loads_first)))

        @block.gpsimd
        def _(e):
            e.memset(g.neg_half[:, :], -0.5).then_inc(filled, 1)
            e.memset(g.ones[:, :], 1.0).then_inc(filled, 1)
            e.memset(g.magic[:, :], MAGIC).then_inc(filled, 1)
            e.wait_ge(filled, 3)
            e.memset(g.ctxT[DC:DC + 1, :], 1.0).then_inc(filled, 1)
            e.wait_ge(filled, 4)

        @block.tensor
        def _(e):
            e.wait_ge(const_loaded, 16 * (2 + len(g.loads_first)))
            e.wait_ge(ctx_loaded, 16)
            for b in range(B):
                if b >= 2:
                    e.wait_ge(ctx_kept, b - 1)
                for t in range(KT):
                    last = e.transpose(turned[b % 2][0:DC, t * P:(t + 1) * P], rows[:, KT * b + t, :], g.ident)
                last.then_inc(ctx_turned, 1)
            e.wait_ge(ctx_kept, B - 1)
            e.transpose(turned[0][:, 0:g.vectors_used], g.vector_rows[0:g.vectors_used, :],
                        g.ident[0:g.vectors_used, 0:g.vectors_used]).then_inc(ctx_turned, 1)

        @block.scalar
        def _(e):
            for b in range(B):
                e.wait_ge(ctx_turned, b + 1)
                e.activation(g.ctxT[0:DC, b * S:(b + 1) * S], turned[b % 2][0:DC, :], ACT.Copy).then_inc(ctx_kept, 1)
            e.wait_ge(ctx_turned, B + 1)
            e.activation(g.vectors[:, 0:g.vectors_used], turned[0][:, 0:g.vectors_used], ACT.Copy).then_inc(ctx_kept, 1)
            e.wait_ge(ctx_kept, B + 1)



def l0_attention(nc, g, a):
    HEADS, HD = 16, 8
    GROUPS, GH = 4, 4
    STEPS = GROUPS * KT
    STACK = 4 * D
    with ExitStack() as ctx:
        s = Scope(nc, ctx, "l0a")
        front = Front(s, g)
        ident = s.sb("ident", [P, P], F32R)
        zero = s.sb("zero", [P, GH * T])
        zT = s.sb("zT", [P, T])
        cT = s.sb("cT", [DC + 1, S])
        square = s.sb("square", [P, KT + TPB, D])
        ksum = s.sb("k_sumsq", [P, KT])
        qsum = s.sb("q_sumsq", [P, TPB])
        kclamped = s.sb("k_clamped", [P, KT])
        qclamped = s.sb("q_clamped", [P, TPB])
        kscale_next = s.sb("k_scale_next", [P, KT])
        kscale = s.sb("k_scale", [P, KT])
        qnorm = s.sb("q_norm", [P, TPB])
        k_rows = s.sb("k_rows", [P, KT, D])
        v_rows = s.sb("v_rows", [P, KT, D])
        qp = s.sb("qp", [P, TILES, D])
        qn = s.sb("qn", [P, TPB, D])
        kst = s.sb("k_stacked", [P, KT, STACK], F32R)
        qst = s.sb("q_stacked", [P, TPB, STACK], F32R)
        kS = s.sb("kS", [P, GROUPS, S], F32R)
        qS = s.sb("qS", [P, GROUPS, GH, T], F32R)
        v = s.sb("v", [P, KT, HEADS, 32])
        prob = [s.sb(f"prob{i}", [P, GH * T]) for i in range(2)]
        pv = s.sb("pv", [P, T])
        rsum = s.sb("rsum", [P, TPB, GH])
        o = s.sb("o", [P, TPB, D])
        oT = s.sb("oT", [P, T])
        y = s.sb("y", [P, TPB, D])
        stats = s.sb("y_stats", [P, TPB, 6])
        mv = s.sb("y_mean_var", [P, TPB, 2])
        yvar = s.sb("y_var", [P, TPB])
        yrstd = s.sb("y_rstd", [P, TPB])
        sc = [s.ps(f"scores{i}", (P, 2 * 512)) for i in range(2)]
        pvps = [s.ps(f"pv{i}") for i in range(2)]
        work = [s.ps(f"work{i}") for i in range(2)]

        names = ["filled", "v_padded", "zeroed", "c_fixed", "zT_ready", "k_projected", "v_projected", "q_projected",
                 "k_kept", "v_kept", "qp_ready", "k_squared", "q_squared", "k_clamped", "q_clamped",
                 "k_scale_next", "k_scale_ready", "q_norm_ready", "k_hi_ready", "k_lo_ready", "qn_ready", "q_hi_ready",
                 "q_lo_ready", "k_turned", "q_turned", "kS_ready", "qS_ready_dve", "qS_ready_act", "v_low_ready",
                 "v_high_ready", "scores_ready", "prob_ready", "pv_ready", "pv_kept", "pv_turned", "rsum_ready",
                 "o_ready", "o_turned", "oT_ready", "out_ready", "y_kept", "y_stats", "yvar_ready", "yrstd_ready", "y_ready",
                 "x_updated", "steps"]
        m = s.sems(names)
        block = s.block()

        def stacked(ap, first, step):
            parts = ap.rearrange("p t (h k d) -> p (t h) k d", k=4, d=HD)
            return parts[:, :, first:first + step + 1:step, :]

        def repeated(ap):
            x = ap.rearrange("p t (h d) -> p (t h) d", d=HD)
            return bcast(x.unsqueeze(2), [P, x.shape[1], 2, HD])

        def turns(e, turn):
            turn(0)
            with e.Fori(1, B - 2) as b:
                turn(b)
            turn(B - 2)
            turn(B - 1)

        def parts(b):
            if isinstance(b, int):
                return b > 0, b + 1 < B, b + 2 < B
            return True, True, True

        @block.gpsimd
        def _(e):
            def fix_c(b):
                wait(e, m.v_projected, b)
                e.tensor_copy(cT[:, :], g.ctxT[:, bass.ds(b * S, S)]).then_inc(m.c_fixed, 1)

            def keep_v(b, low):
                done = 12 if low else 16
                wait(e, m.pv_ready, STEPS * (b - 1) + done)
                e.wait_ge(m.v_kept, b + 1)
                h = slice(0, 12) if low else slice(12, 16)
                rows = v_rows[:, :, :].rearrange("p t (h d) -> p t h d", d=HD)[:, :, h, :]
                ones = bcast(g.ones[:, 0:1].unsqueeze(2).unsqueeze(3), list(rows.shape))
                e.tensor_tensor(v[:, :, h, 0:HD], rows, ones, ALU.mult).then_inc(m.v_low_ready if low else m.v_high_ready, 1)

            def k_low(b):
                e.wait_ge(m.k_hi_ready, b + 1)
                e.tensor_tensor(stacked(kst[:, :, :], 1, 2), repeated(k_rows[:, :, :]), stacked(kst[:, :, :], 0, 2),
                                ALU.subtract).then_inc(m.k_lo_ready, 1)

            def k_scales(b):
                e.wait_ge(m.k_clamped, b + 1)
                e.tensor_tensor(kscale_next[:, :], kclamped[:, :], g.neg_half[:, 0:KT], ALU.pow).then_inc(m.k_scale_next, 1)

            def q_norms(b):
                e.wait_ge(m.q_clamped, b + 1)
                e.tensor_tensor(qnorm[:, :], qclamped[:, :], g.neg_half[:, 0:TPB], ALU.pow).then_inc(m.q_norm_ready, 1)

            def finish(b):
                e.wait_ge(m.yvar_ready, b + 1)
                e.tensor_tensor(yrstd[:, :], yvar[:, :], g.neg_half[:, 0:TPB], ALU.pow).then_inc(m.yrstd_ready, 1)

            def update(b):
                per_batch = lambda ap: bcast(ap.unsqueeze(1), [P, TPB, D])
                xs = g.x[:, bass.ds(TPB * b, TPB), :]
                e.wait_ge(m.y_ready, TPB * b + TPB)
                e.tensor_tensor(y[:, :, :], y[:, :, :], per_batch(g.l0_gamma[:, :]), ALU.mult).then_inc(m.x_updated, 1)
                e.wait_ge(m.x_updated, 3 * b + 1)
                e.tensor_tensor(y[:, :, :], y[:, :, :], per_batch(g.l0_beta[:, :]), ALU.add).then_inc(m.x_updated, 1)
                e.wait_ge(m.x_updated, 3 * b + 2)
                e.tensor_tensor(xs, xs, y[:, :, :], ALU.add).then_inc(m.x_updated, 1)

            def turn(b):
                before, after, after_that = parts(b)
                if before:
                    keep_v(b, False)
                if after:
                    front.gpsimd(e, b + 1)
                    if after_that:
                        fix_c(b + 2)
                    k_low(b + 1)
                if before:
                    finish(b - 1)
                if after:
                    k_scales(b + 1)
                if before:
                    update(b - 1)
                if after:
                    q_norms(b + 1)
                    keep_v(b + 1, True)

            e.memset(zero[:, :], 0.0).then_inc(m.filled, 1)
            e.memset(v[:, :, :, :], 0.0).then_inc(m.v_padded, 1)
            fix_c(0)
            front.gpsimd(e, 0)
            e.wait_ge(m.v_padded, 1)
            e.memset(v[:, :, :, HD:HD + 1], 1.0).then_inc(m.v_padded, 1)
            k_low(0)
            k_scales(0)
            q_norms(0)
            fix_c(1)
            keep_v(0, True)
            keep_v(0, False)
            turns(e, turn)
            finish(B - 1)
            update(B - 1)
            e.wait_ge(m.x_updated, 3 * B)

        @block.tensor
        def _(e):
            last_item = [None, None]

            def bank(n, kind, b, i=0):
                before = last_item[n % 2]
                if before is not None:
                    kept, c, j = before
                    for sem, count in {
                            "k": ((m.k_kept, c + 1),),
                            "v": ((m.v_kept, c + 1),),
                            "z": ((m.zT_ready, c + 1),),
                            "q": ((m.qp_ready, c + 1), (m.q_squared, TPB * c + TPB)),
                            "k_turned": ((m.kS_ready, GROUPS * c + j + 1),),
                            "q_turned": ((m.qS_ready_dve, 3 * (2 * c + j + 1)), (m.qS_ready_act, 2 * c + j + 1)),
                            "pv": ((m.o_ready, GROUPS * c + j + 1),),
                            "o": ((m.oT_ready, c + 1),),
                            "out": ((m.y_kept, c + 1),)}[kept]:
                        e.wait_ge(sem, count)
                last_item[n % 2] = (kind, b, i)
                return work[n % 2]

            def keys(n, b):
                w = bank(n, "k", b)
                e.wait_ge(m.c_fixed, b + 1)
                for t in range(KT):
                    last = e.matmul(w[:, t * P:(t + 1) * P], cT[:, t * P:(t + 1) * P], g.l0_wk[:, :], start=True, stop=True)
                last.then_inc(m.k_projected, 1)

            def values(n, b):
                w = bank(n, "v", b)
                for t in range(KT):
                    last = e.matmul(w[:, t * P:(t + 1) * P], cT[:, t * P:(t + 1) * P], g.l0_wv[:, :], start=True, stop=True)
                last.then_inc(m.v_projected, 1)

            def tokens(n, b):
                front.tensor(e, b, bank(n, "z", b))

            def queries(n, b):
                w = bank(n, "q", b)
                e.wait_ge(m.zT_ready, b + 1)
                for i in range(TPB):
                    e.matmul(w[:, i * P:(i + 1) * P], zT[:, i * P:(i + 1) * P], g.l0_wq[:, :], start=True, stop=False)
                    last = e.matmul(w[:, i * P:(i + 1) * P], g.ones[0:1, 0:P], g.l0_bq[:, :], start=False, stop=True)
                last.then_inc(m.q_projected, 1)

            def turn_keys(n, b, grp):
                w = bank(n, "k_turned", b, grp)
                if grp == 0:
                    e.wait_ge(m.k_lo_ready, b + 1)
                for t in range(KT):
                    last = e.transpose(w[:, t * P:(t + 1) * P].bitcast(F32R), kst[:, t, grp * P:(grp + 1) * P], ident[:, :])
                last.then_inc(m.k_turned, 1)

            def turn_queries(n, b, i):
                w = bank(n, "q_turned", b, i)
                if i == 0:
                    e.wait_ge(m.q_lo_ready, b + 1)
                for j in range(2):
                    for t in range(TPB):
                        last = e.transpose(w[:, j * T + t * P:j * T + (t + 1) * P].bitcast(F32R),
                                           qst[:, t, (2 * i + j) * P:(2 * i + j + 1) * P], ident[:, :])
                last.then_inc(m.q_turned, 1)

            def turn_pv(n, b, grp):
                w = bank(n, "pv", b, grp)
                e.wait_ge(m.pv_kept, GROUPS * b + grp + 1)
                for i in range(TPB):
                    last = e.transpose(w[:, i * P:(i + 1) * P], pv[:, i * P:(i + 1) * P], g.ident)
                last.then_inc(m.pv_turned, 1)

            def turn_o(n, b):
                w = bank(n, "o", b)
                e.wait_ge(m.o_ready, GROUPS * b + GROUPS)
                for i in range(TPB):
                    last = e.transpose(w[:, i * P:(i + 1) * P], o[:, i, :], g.ident)
                last.then_inc(m.o_turned, 1)

            def output(n, b):
                w = bank(n, "out", b)
                e.wait_ge(m.oT_ready, b + 1)
                for i in range(TPB):
                    e.matmul(w[:, i * P:(i + 1) * P], oT[:, i * P:(i + 1) * P], g.l0_wo[:, :], start=True, stop=False)
                    last = e.matmul(w[:, i * P:(i + 1) * P], g.ones[0:1, 0:P], g.l0_bo[:, :], start=False, stop=True)
                last.then_inc(m.out_ready, 1)

            def scores(b, n):
                grp, t = divmod(n, KT)
                wait(e, m.prob_ready, STEPS * b + n - 1)
                if t == 0:
                    e.wait_ge(m.kS_ready, GROUPS * b + grp + 1)
                    e.wait_ge(m.qS_ready_dve, 3 * (2 * b + grp // 2 + 1))
                    e.wait_ge(m.qS_ready_act, 2 * b + grp // 2 + 1)
                for half in range(2):
                    last = e.matmul(sc[n % 2][:, half * 512:half * 512 + 512], kS[:, grp, t * P:(t + 1) * P],
                                    qS[:, grp, 2 * half:2 * half + 2, :], start=True, stop=True)
                last.then_inc(m.scores_ready, 1)

            def weighted(b, n):
                grp, t = divmod(n % STEPS, KT)
                e.wait_ge(m.prob_ready, STEPS * b + n + 1)
                if n == 0:
                    e.wait_ge(m.v_low_ready, b + 1)
                if n == 12:
                    e.wait_ge(m.v_high_ready, b + 1)
                if t == 0:
                    wait(e, m.pv_kept, GROUPS * b + grp - 1)
                for j in range(GH):
                    last = e.matmul(pvps[grp % 2][32 * j:32 * j + 32, 0:T], v[:, t, GH * grp + j, :],
                                    prob[n % 2][:, j * T:(j + 1) * T], start=t == 0, stop=t == KT - 1,
                                    tile_position=(0, 32 * j))
                last.then_inc(m.pv_ready, 1)

            def turn(b):
                before, after, _ = parts(b)
                last_item[:] = [("k_turned", b, 3), ("q_turned", b, 1)]
                for n in range(STEPS):
                    if n + 1 < STEPS:
                        scores(b, n + 1)
                    elif after:
                        scores(b + 1, 0)
                    if n > 0 or before:
                        weighted(b, n - 1)
                    if before and n == 1:
                        turn_pv(n, b - 1, 3)
                    if before and n == 3:
                        turn_o(n, b - 1)
                    if before and n == 4:
                        output(n, b - 1)
                    if n in (6, 9, 13):
                        turn_pv(n, b, (6, 9, 13).index(n))
                    if after and n == 0:
                        keys(n, b + 1)
                    if after and n == 2:
                        values(n, b + 1)
                    if after and n == 5:
                        tokens(n, b + 1)
                    if after and n == 7:
                        queries(n, b + 1)
                    if after and n in (8, 10, 11, 14):
                        turn_keys(n, b + 1, (8, 10, 11, 14).index(n))
                    if after and n in (12, 15):
                        turn_queries(n, b + 1, (12, 15).index(n))

            e.wait_ge(m.zeroed, 1)
            e.wait_ge(m.v_padded, 2)
            keys(0, 0)
            tokens(1, 0)
            values(2, 0)
            queries(3, 0)
            turn_keys(4, 0, 0)
            turn_queries(5, 0, 0)
            turn_keys(6, 0, 1)
            turn_keys(7, 0, 2)
            turn_keys(8, 0, 3)
            turn_queries(9, 0, 1)
            scores(0, 0)
            turns(e, turn)
            weighted(B, -1)
            turn_pv(1, B - 1, 3)
            turn_o(3, B - 1)
            output(4, B - 1)

        @block.scalar
        def _(e):
            def keep_k(b):
                e.wait_ge(m.k_projected, b + 1)
                wait(e, m.k_lo_ready, b)
                e.activation(k_rows[:, :, :], work[0][:, :].rearrange("p (t d) -> p t d", d=D), ACT.Copy).then_inc(m.k_kept, 1)

            def square_k(b, t):
                if t == 0:
                    e.wait_ge(m.k_kept, b + 1)
                    wait(e, m.k_clamped, b)
                e.activation(square[:, t, :], k_rows[:, t, :], ACT.Square, accum_out=ksum[:, t:t + 1]).then_inc(m.k_squared, 1)

            def keep_v(b):
                e.wait_ge(m.v_projected, b + 1)
                wait(e, m.v_high_ready, b)
                e.activation(v_rows[:, :, :], work[0][:, :].rearrange("p (t d) -> p t d", d=D), ACT.Copy).then_inc(m.v_kept, 1)

            def keep_z(b):
                e.wait_ge(front.z_turned, b + 1)
                e.activation(zT[:, :], work[1][:, 0:T], ACT.Copy).then_inc(m.zT_ready, 1)

            def keep_q(b):
                e.wait_ge(m.q_projected, b + 1)
                e.activation(qp[:, bass.ds(TPB * b, TPB), :], work[1][:, 0:T].rearrange("p (i d) -> p i d", d=D),
                             ACT.Copy).then_inc(m.qp_ready, 1)
                wait(e, m.q_clamped, b)
                for i in range(TPB):
                    e.activation(square[:, KT + i, :], work[1][:, i * P:(i + 1) * P], ACT.Square,
                                 accum_out=qsum[:, i:i + 1]).then_inc(m.q_squared, 1)

            def keep_qS(b, i, w):
                e.wait_ge(m.q_turned, 2 * b + i + 1)
                wait(e, m.scores_ready, STEPS * (b - 1) + 8 * i + 8)
                e.activation(qS[96:128, 2 * i:2 * i + 2, 3, :], work[w][96:128, :].bitcast(F32R).rearrange("p (g q) -> p g q", q=T),
                             ACT.Copy).then_inc(m.qS_ready_act, 1)

            def keep_o(b):
                e.wait_ge(m.o_turned, b + 1)
                e.activation(oT[:, :], work[1][:, 0:T], ACT.Copy).then_inc(m.oT_ready, 1)

            def take_scales(b):
                wait(e, m.prob_ready, STEPS * b)
                e.wait_ge(m.k_scale_next, b + 1)
                e.activation(kscale[:, :], kscale_next[:, :], ACT.Copy).then_inc(m.k_scale_ready, 1)

            def exps(b, n):
                if n == 0:
                    e.wait_ge(m.k_scale_ready, b + 1)
                e.wait_ge(m.scores_ready, STEPS * b + n + 1)
                wait(e, m.pv_ready, STEPS * b + n - 1)
                e.activation(prob[n % 2][:, :], sc[n % 2][:, :], ACT.Exp, scale=kscale[:, n % KT:n % KT + 1]).then_inc(m.prob_ready, 1)

            def turn(b):
                before, after, _ = parts(b)
                for n in range(STEPS):
                    exps(b, n)
                    if n == 0 and before:
                        keep_qS(b, 1, 1)
                    if n == 1 and after:
                        keep_k(b + 1)
                    if n == 2 and after:
                        square_k(b + 1, 0)
                        square_k(b + 1, 1)
                    if n == 3 and after:
                        keep_v(b + 1)
                    if n == 4 and before:
                        keep_o(b - 1)
                    if n == 5 and after:
                        square_k(b + 1, 2)
                        square_k(b + 1, 3)
                    if n == 6 and after:
                        keep_z(b + 1)
                    if n == 8 and after:
                        keep_q(b + 1)
                    if n == 13 and after:
                        keep_qS(b + 1, 0, 0)
                    if n == 15 and after:
                        take_scales(b + 1)

            keep_k(0)
            for t in range(KT):
                square_k(0, t)
            keep_z(0)
            keep_v(0)
            keep_q(0)
            take_scales(0)
            e.wait_ge(m.zeroed, 1 + GROUPS)
            keep_qS(0, 0, 1)
            keep_qS(0, 1, 1)
            turns(e, turn)
            keep_o(B - 1)

        @block.vector
        def _(e):
            norm_steps = Steps(e, m.steps, front.steps)

            def norm(b):
                norm_steps.begin(b)
                front.vector(e, b, norm_steps)
                norm_steps.end()

            def k_high(b):
                e.wait_ge(m.k_kept, b + 1)
                wait(e, m.k_turned, GROUPS * b)
                e.tensor_copy(stacked(kst[:, :, :], 0, 2), repeated(k_rows[:, :, :])).then_inc(m.k_hi_ready, 1)

            def clamp_k(b):
                e.wait_ge(m.k_squared, KT * b + KT)
                wait(e, m.k_scale_ready, b)
                e.tensor_scalar(kclamped[:, :], ksum[:, :], 1e-24, float(HD), ALU.max, ALU.mult).then_inc(m.k_clamped, 1)

            def clamp_q(b):
                e.wait_ge(m.q_squared, TPB * b + TPB)
                e.tensor_scalar(qclamped[:, :], qsum[:, :], 1e-24, None, ALU.max).then_inc(m.q_clamped, 1)

            def split_q(b):
                e.wait_ge(m.q_norm_ready, b + 1)
                e.wait_ge(m.qp_ready, b + 1)
                wait(e, m.q_turned, 2 * b)
                for i in range(TPB):
                    e.tensor_scalar(qn[:, i, :], qp[:, TPB * b + i, :], qnorm[:, i:i + 1], None, ALU.mult).then_inc(m.qn_ready, 1)
                e.wait_ge(m.qn_ready, TPB * b + TPB)
                high = qst[:, :, :].rearrange("p t (h k d) -> p (t h) k d", k=4, d=HD)[:, :, 0:2, :]
                low = qst[:, :, :].rearrange("p t (h k d) -> p (t h) k d", k=4, d=HD)[:, :, 2:4, :]
                e.tensor_copy(high, repeated(qn[:, :, :])).then_inc(m.q_hi_ready, 1)
                e.wait_ge(m.q_hi_ready, b + 1)
                e.tensor_tensor(low, repeated(qn[:, :, :]), high, ALU.subtract).then_inc(m.q_lo_ready, 1)

            def keep_kS(b, grp, w):
                e.wait_ge(m.k_turned, GROUPS * b + grp + 1)
                wait(e, m.scores_ready, STEPS * (b - 1) + 4 * grp + 4)
                e.tensor_copy(kS[:, grp, :], work[w][:, :].bitcast(F32R)).then_inc(m.kS_ready, 1)

            def keep_qS(b, i, w):
                e.wait_ge(m.q_turned, 2 * b + i + 1)
                wait(e, m.scores_ready, STEPS * (b - 1) + 8 * i + 8)
                for j in range(3):
                    rows = slice(32 * j, 32 * j + 32)
                    e.tensor_copy(qS[rows, 2 * i:2 * i + 2, j, :],
                                  work[w][rows, :].bitcast(F32R).rearrange("p (g q) -> p g q", q=T)).then_inc(m.qS_ready_dve, 1)

            def keep_pv(b, grp):
                e.wait_ge(m.pv_ready, STEPS * b + KT * (grp + 1))
                wait(e, m.pv_turned, GROUPS * b + grp)
                e.tensor_copy(pv[:, :], pvps[grp % 2][:, 0:T]).then_inc(m.pv_kept, 1)

            def divide(b, grp, w):
                e.wait_ge(m.pv_turned, GROUPS * b + grp + 1)
                heads = work[w][:, 0:T].rearrange("p (i j d) -> p i j d", i=TPB, d=32)
                e.reciprocal(rsum[:, :, :], heads[:, :, :, HD]).then_inc(m.rsum_ready, 1)
                e.wait_ge(m.rsum_ready, GROUPS * b + grp + 1)
                if grp == 0:
                    wait(e, m.o_turned, b)
                e.tensor_tensor(o[:, :, 32 * grp:32 * grp + 32].rearrange("p i (j d) -> p i j d", d=HD),
                                heads[:, :, :, 0:HD], bcast(rsum[:, :, :].unsqueeze(3), [P, TPB, GH, HD]),
                                ALU.mult).then_inc(m.o_ready, 1)

            def add_qp(b):
                e.wait_ge(m.out_ready, b + 1)
                wait(e, m.x_updated, 3 * b)
                e.tensor_tensor(y[:, :, :], work[0][:, 0:T].rearrange("p (i d) -> p i d", d=D),
                                qp[:, bass.ds(TPB * b, TPB), :], ALU.add).then_inc(m.y_kept, 1)
                e.wait_ge(m.y_kept, b + 1)
                for i in range(TPB):
                    e.bn_stats(stats[:, i, :], y[:, i, :]).then_inc(m.y_stats, 1)
                e.wait_ge(m.y_stats, 2 * TPB * b + TPB)
                e.memset(front.held[:, :], 0.0)
                for i in range(TPB):
                    e.bn_aggr(mv[:, i, :], stats[:, i, :]).then_inc(m.y_stats, 1)
                e.wait_ge(m.y_stats, 2 * TPB * b + 2 * TPB)
                e.tensor_scalar(yvar[:, :], mv[:, :, 1], EPS, None, ALU.add).then_inc(m.yvar_ready, 1)

            def norm_y(b):
                e.wait_ge(m.yrstd_ready, b + 1)
                for i in range(TPB):
                    e.tensor_scalar(y[:, i, :], y[:, i, :], mv[:, i, 0:1], yrstd[:, i:i + 1],
                                    ALU.subtract, ALU.mult).then_inc(m.y_ready, 1)

            def turn(b):
                before, after, _ = parts(b)
                for n in range(STEPS):
                    if n == 0 and before:
                        keep_qS(b, 1, 1)
                    if n == 1 and before:
                        keep_pv(b - 1, 3)
                    if n == 2 and before:
                        divide(b - 1, 3, 1)
                    if n == 3 and after:
                        k_high(b + 1)
                        norm(b + 1)
                    if n == 5:
                        keep_pv(b, 0)
                        if before:
                            add_qp(b - 1)
                    if n == 6:
                        if before:
                            norm_y(b - 1)
                        if after:
                            clamp_k(b + 1)
                    if n == 7:
                        divide(b, 0, 0)
                    if n == 9:
                        keep_pv(b, 1)
                        if after:
                            keep_kS(b + 1, 0, 0)
                            clamp_q(b + 1)
                    if n == 10:
                        divide(b, 1, 1)
                        if after:
                            split_q(b + 1)
                    if n == 11 and after:
                        keep_kS(b + 1, 1, 0)
                    if n == 12 and after:
                        keep_kS(b + 1, 2, 1)
                    if n == 13:
                        keep_pv(b, 2)
                        if after:
                            keep_qS(b + 1, 0, 0)
                    if n == 14:
                        divide(b, 2, 1)
                    if n == 15 and after:
                        keep_kS(b + 1, 3, 0)

            e.tensor_copy(ident[:, :], g.ident).then_inc(m.zeroed, 1)
            norm(0)
            k_high(0)
            clamp_k(0)
            e.wait_ge(m.filled, 1)
            for grp in range(GROUPS):
                e.tensor_copy(qS[:, grp, :, :].rearrange("p j q -> p (j q)"), zero[:, :]).then_inc(m.zeroed, 1)
            clamp_q(0)
            split_q(0)
            e.wait_ge(m.zeroed, 1 + GROUPS)
            keep_kS(0, 0, 0)
            keep_qS(0, 0, 1)
            keep_kS(0, 1, 0)
            keep_kS(0, 2, 1)
            keep_kS(0, 3, 0)
            keep_qS(0, 1, 1)
            turns(e, turn)
            keep_pv(B - 1, 3)
            divide(B - 1, 3, 1)
            add_qp(B - 1)
            norm_y(B - 1)



def l0_ffn(nc, g, a):
    HF = 256
    FT = HF // P
    CT = 4
    CHUNKS = TILES // CT
    with ExitStack() as outer:
        so = Scope(nc, outer, "l0f")
        zT = so.sb("zT", [P, N])
        logits = so.sb("logits", [P, TILES, E])
        gate = so.sb("gate", [P, TILES, E])
        gateT = so.sb("gateT", [E, N])

        with ExitStack() as ctx:
            s = Scope(nc, ctx, "l0f_norm")
            front = Front(s, g, twice=True)
            zb = s.sb("zb", [P, T])
            turn = s.ps("turn")
            lps = s.ps("logits")
            m = s.sems(["x_updated", "zb_ready", "z_stored", "logits_ready", "logits_kept", "steps"])
            block = s.block()

            @block.vector
            def _(e):
                steps = Steps(e, m.steps, front.steps)
                with e.Fori(0, B) as b:
                    steps.begin(b)
                    front.vector(e, b, steps)
                    e.tensor_tensor(g.x[:, bass.ds(TPB * b, TPB), :], g.x[:, bass.ds(TPB * b, TPB), :],
                                    front.outer[:, :, :], ALU.add).then_inc(m.x_updated, 1)
                    steps.end()
                    e.wait_ge(m.x_updated, b + 1)
                    e.wait_ge(front.z_turned, b + 1)

            @block.gpsimd
            def _(e):
                with e.Fori(0, B) as b:
                    front.gpsimd(e, b)
                    e.wait_ge(m.zb_ready, b + 1)
                    e.tensor_copy(zT[:, bass.ds(b * T, T)], zb[:, :]).then_inc(m.z_stored, 1)

            @block.tensor
            def _(e):
                with e.Fori(0, B) as b:
                    e.wait_ge(m.zb_ready, b)
                    front.tensor(e, b, turn)
                    e.wait_ge(m.zb_ready, b + 1)
                    e.wait_ge(m.logits_kept, b)
                    for i in range(TPB):
                        e.matmul(lps[:, i * E:(i + 1) * E], zb[:, i * P:(i + 1) * P], g.l0_rw[:, :], start=True, stop=False)
                        last = e.matmul(lps[:, i * E:(i + 1) * E], g.ones[0:1, 0:P], g.l0_rb[:, :], start=False, stop=True)
                    last.then_inc(m.logits_ready, 1)

            @block.scalar
            def _(e):
                with e.Fori(0, B) as b:
                    e.wait_ge(front.z_turned, b + 1)
                    e.wait_ge(m.z_stored, b)
                    e.wait_ge(m.logits_ready, b)
                    e.activation(zb[:, :], turn[:, 0:T], ACT.Identity, scale=g.l0_lng[:, 0:1],
                                 bias=g.l0_lnb[:, 0:1]).then_inc(m.zb_ready, 1)
                    e.wait_ge(m.logits_ready, b + 1)
                    e.activation(logits[:, bass.ds(b * TPB, TPB), :], lps[:, 0:TPB * E].rearrange("p (i e) -> p i e", e=E),
                                 ACT.Copy).then_inc(m.logits_kept, 1)

        with ExitStack() as ctx:
            s = Scope(nc, ctx, "l0f_route")
            full = [P, TILES, E]
            red = s.sb("red", [P, 8, TILES])
            w = [s.sb(f"w{i}", full) for i in range(8)]
            turn = s.ps("turn", (P, 4 * 512))
            m = s.sems(["shifted", "exped", "gate_ready", "gate_turned", "steps", "gateT_ready"])
            block = s.block()

            @block.vector
            def _(e):
                steps = Steps(e, m.steps)

                def then(instruction):
                    steps.add(instruction)
                    steps.settle()

                def over(i):
                    return bcast(red[:, i, :].unsqueeze(2), full)

                rev = bcast(g.const[:, C_REV:C_REV + E].unsqueeze(1), full)
                then(e.tensor_reduce(red[:, 0, :], logits[:, :, :], AX.X, ALU.max))
                e.tensor_tensor(w[0][:, :, :], logits[:, :, :], over(0), ALU.subtract).then_inc(m.shifted, 1)
                e.wait_ge(m.exped, 1)
                then(e.tensor_reduce(red[:, 1, :], w[1][:, :, :], AX.X, ALU.add))
                then(e.reciprocal(red[:, 2, :], red[:, 1, :]))
                then(e.tensor_tensor(w[2][:, :, :], w[1][:, :, :], over(2), ALU.mult))
                then(e.tensor_reduce(red[:, 3, :], w[2][:, :, :], AX.X, ALU.max))
                then(e.tensor_tensor(w[3][:, :, :], w[2][:, :, :], over(3), ALU.is_equal))
                then(e.tensor_tensor(w[4][:, :, :], w[3][:, :, :], rev, ALU.mult))
                then(e.tensor_reduce(red[:, 4, :], w[4][:, :, :], AX.X, ALU.max))
                then(e.tensor_tensor(w[5][:, :, :], rev, over(4), ALU.is_equal))
                then(e.scalar_tensor_tensor(out=w[6][:, :, :].rearrange("p t e -> p (t e)"),
                                            in0=w[5][:, :, :].rearrange("p t e -> p (t e)"), scalar=-4.0,
                                            in1=w[2][:, :, :].rearrange("p t e -> p (t e)"), op0=ALU.mult, op1=ALU.add))
                then(e.tensor_reduce(red[:, 5, :], w[6][:, :, :], AX.X, ALU.max))
                then(e.tensor_tensor(w[3][:, :, :], w[6][:, :, :], over(5), ALU.is_equal))
                then(e.tensor_tensor(w[4][:, :, :], w[3][:, :, :], rev, ALU.mult))
                then(e.tensor_reduce(red[:, 6, :], w[4][:, :, :], AX.X, ALU.max))
                then(e.tensor_tensor(w[7][:, :, :], rev, over(6), ALU.is_equal))
                then(e.tensor_tensor(w[3][:, :, :], w[5][:, :, :], w[7][:, :, :], ALU.add))
                then(e.tensor_tensor(w[4][:, :, :], w[3][:, :, :], w[2][:, :, :], ALU.mult))
                then(e.tensor_reduce(red[:, 7, :], w[4][:, :, :], AX.X, ALU.add))
                then(e.tensor_scalar(red[:, 0, :], red[:, 7, :], 1e-8, None, ALU.max))
                then(e.reciprocal(red[:, 1, :], red[:, 0, :]))
                e.tensor_tensor(gate[:, :, :], w[4][:, :, :], over(1), ALU.mult).then_inc(m.gate_ready, 1)

            @block.scalar
            def _(e):
                e.wait_ge(m.shifted, 1)
                e.activation(w[1][:, :, :], w[0][:, :, :], ACT.Exp).then_inc(m.exped, 1)
                e.wait_ge(m.gate_turned, 1)
                e.activation(gateT[:, :], turn[0:E, :], ACT.Copy).then_inc(m.gateT_ready, 1)

            @block.tensor
            def _(e):
                e.wait_ge(m.gate_ready, 1)
                for t in range(TILES):
                    last = e.transpose(turn[0:E, t * P:(t + 1) * P], gate[:, t, :], g.ident)
                last.then_inc(m.gate_turned, 1)

        with ExitStack() as ctx:
            s = Scope(nc, ctx, "l0f_experts")
            gT = s.sb("gateT_chunk", [E, CT * P])
            gc = s.sb("gate_chunk", [P, CT, E])
            h = [s.sb(f"hidden{i}", [P, FT, CT * P]) for i in range(2)]
            acc = s.sb("acc", [P, CT, D])
            hps = [s.ps(f"hidden{i}") for i in range(2 * FT)]
            yps = [s.ps(f"y{i}") for i in range(2)]
            bps = s.ps("gated_bias")
            m = s.sems(["gate_fixed", "hidden_ready", "act_ready", "y_ready", "y_added", "bias_ready", "acc_started",
                        "x_updated"])
            block = s.block()

            @block.gpsimd
            def _(e):
                with e.Fori(0, CHUNKS) as c:
                    e.wait_ge(m.bias_ready, c)
                    e.wait_ge(m.y_added, E * CT * c)
                    e.tensor_copy(gT[:, :], gateT[:, bass.ds(c * CT * P, CT * P)]).then_inc(m.gate_fixed, 1)
                    e.tensor_copy(gc[:, :, :], gate[:, bass.ds(c * CT, CT), :]).then_inc(m.gate_fixed, 1)

            @block.tensor
            def _(e):
                with e.Fori(0, CHUNKS) as c:
                    def hidden(x):
                        for f in range(FT):
                            n = FT * x + f
                            if n >= 2 * FT:
                                e.wait_ge(m.act_ready, E * FT * c + n - 2 * FT + 1)
                            e.matmul(hps[n % (2 * FT)][:, :], g.l0_w1[:, x, f * P:(f + 1) * P],
                                     zT[:, bass.ds(c * CT * P, CT * P)], start=True, stop=True).then_inc(m.hidden_ready, 1)

                    def second(x):
                        e.wait_ge(m.act_ready, E * FT * c + FT * x + FT)
                        if x >= 2:
                            e.wait_ge(m.y_added, CT * (E * c + x - 1))
                        for t in range(CT):
                            for f in range(FT):
                                last = e.matmul(yps[x % 2][:, t * P:(t + 1) * P], h[x % 2][:, f, t * P:(t + 1) * P],
                                                g.l0_w2[:, x, f, :], start=f == 0, stop=f == FT - 1)
                        last.then_inc(m.y_ready, 1)

                    e.wait_ge(m.act_ready, E * FT * c)
                    hidden(0)
                    e.wait_ge(m.gate_fixed, 2 * c + 2)
                    e.wait_ge(m.acc_started, c)
                    for t in range(CT):
                        last = e.matmul(bps[:, t * P:(t + 1) * P], gT[:, t * P:(t + 1) * P], g.l0_b2[:, :], start=True, stop=True)
                    last.then_inc(m.bias_ready, 1)
                    e.wait_ge(m.y_added, CT * E * c)
                    for x in range(E):
                        if x + 1 < E:
                            hidden(x + 1)
                        second(x)

            @block.scalar
            def _(e):
                with e.Fori(0, CHUNKS) as c:
                    for x in range(E):
                        for f in range(FT):
                            e.wait_ge(m.hidden_ready, E * FT * c + FT * x + f + 1)
                            if f == 0:
                                if x >= 2:
                                    e.wait_ge(m.y_ready, E * c + x - 1)
                                else:
                                    e.wait_ge(m.y_ready, E * c)
                            e.activation(h[x % 2][:, f, :], hps[(FT * x + f) % (2 * FT)][:, :], ACT.Gelu,
                                         bias=g.l0_b1[:, FT * x + f:FT * x + f + 1]).then_inc(m.act_ready, 1)

            @block.vector
            def _(e):
                with e.Fori(0, CHUNKS) as c:
                    e.wait_ge(m.bias_ready, c + 1)
                    e.wait_ge(m.x_updated, c)
                    e.tensor_copy(acc[:, :, :], bps[:, :].rearrange("p (t d) -> p t d", d=D)).then_inc(m.acc_started, 1)
                    e.wait_ge(m.acc_started, c + 1)
                    for x in range(E):
                        e.wait_ge(m.y_ready, E * c + x + 1)
                        e.wait_ge(m.y_added, CT * (E * c + x))
                        for t in range(CT):
                            e.scalar_tensor_tensor(out=acc[:, t, :], in0=yps[x % 2][:, t * P:(t + 1) * P],
                                                   scalar=gc[:, t, x:x + 1], in1=acc[:, t, :], op0=ALU.mult,
                                                   op1=ALU.add).then_inc(m.y_added, 1)
                    e.wait_ge(m.y_added, CT * E * (c + 1))
                    e.tensor_tensor(g.x[:, bass.ds(c * CT, CT), :], g.x[:, bass.ds(c * CT, CT), :], acc[:, :, :],
                                    ALU.add).then_inc(m.x_updated, 1)



def prepare(nc, g, name, HEADS, wq, wk, wv, wo, A, G, zT):
    HD = 64
    SCALE = HD ** -0.5
    C = HEADS // 2
    with ExitStack() as ctx:
        s = Scope(nc, ctx, name)
        turned = s.sb("turned", [P, 3, C, P])
        stats = s.sb("ln_stats", [P, TILES, 6])
        mv = s.sb("ln_mean_var", [P, TILES, 2])
        var = s.sb("ln_var_eps", [P, TILES])
        rstd = s.sb("ln_rstd", [P, TILES])
        z = s.sb("ln_z", [P, TILES, D])
        tps = [s.ps(f"turned{i}") for i in range(4)]
        pps = [s.ps(f"product{i}") for i in range(4)]
        m = s.sems(["turned", "turned_kept", "products", "A_kept", "G_kept", "stats_ready", "var_ready",
                    "rstd_ready", "z_ready", "z_turned", "zT_kept"])
        jobs = [(i, c, w[:, c * P:(c + 1) * P]) for i, w in enumerate((wq, wk, wv)) for c in range(C)]
        block = s.block()

        @block.tensor
        def _(e):
            for n, (i, c, src) in enumerate(jobs):
                if n >= 4:
                    e.wait_ge(m.turned_kept, n - 3)
                rows = src.shape[0]
                e.transpose(tps[n % 4][:, 0:rows], src, g.ident[0:rows, 0:rows]).then_inc(m.turned, 1)
            e.wait_ge(m.turned_kept, len(jobs))
            for h in range(HEADS):
                c, lo = h // 2, 64 * (h % 2)
                half = slice(lo, lo + HD)
                if h >= 2:
                    e.wait_ge(m.A_kept, h - 1)
                    e.wait_ge(m.G_kept, h - 1)
                e.matmul(pps[2 * (h % 2)][:, 0:DC], turned[half, 0, c, :], turned[half, 1, c, 0:DC], start=True,
                         stop=True, tile_position=(lo, 0)).then_inc(m.products, 1)
                e.matmul(pps[2 * (h % 2) + 1][0:DC, 0:D], turned[half, 2, c, 0:DC], wo[half, c, :], start=True,
                         stop=True, tile_position=(lo, 0)).then_inc(m.products, 1)
            e.wait_ge(m.z_ready, TILES)
            for n in range(TILES // 4):
                for i in range(4):
                    last = e.transpose(tps[n][:, i * P:(i + 1) * P], z[:, 4 * n + i, :], g.ident)
                last.then_inc(m.z_turned, 1)

        @block.gpsimd
        def _(e):
            e.wait_ge(m.var_ready, 1)
            e.tensor_tensor(rstd[:, :], var[:, :], g.neg_half[:, 0:TILES], ALU.pow).then_inc(m.rstd_ready, 1)

        @block.scalar
        def _(e):
            for n, (i, c, src) in enumerate(jobs):
                rows = src.shape[0]
                e.wait_ge(m.turned, n + 1)
                e.activation(turned[:, i, c, 0:rows], tps[n % 4][:, 0:rows], ACT.Copy).then_inc(m.turned_kept, 1)
            for h in range(HEADS):
                e.wait_ge(m.products, 2 * h + 1)
                e.activation(A[:, h, :], pps[2 * (h % 2)][:, 0:DC], ACT.Copy, scale=SCALE).then_inc(m.A_kept, 1)
            for n in range(TILES // 4):
                e.wait_ge(m.z_turned, n + 1)
                e.activation(zT[:, 4 * n * P:4 * (n + 1) * P], tps[n][:, :], ACT.Copy).then_inc(m.zT_kept, 1)
            e.wait_ge(m.zT_kept, TILES // 4)

        @block.vector
        def _(e):
            for i in range(TILES):
                e.bn_stats(stats[:, i, :], g.x[:, i, :]).then_inc(m.stats_ready, 1)
            for i in range(TILES):
                e.wait_ge(m.stats_ready, i + 1)
                e.bn_aggr(mv[:, i, :], stats[:, i, :]).then_inc(m.stats_ready, 1)
            e.wait_ge(m.stats_ready, 2 * TILES)
            e.tensor_scalar(var[:, :], mv[:, :, 1], EPS, None, ALU.add).then_inc(m.var_ready, 1)
            e.wait_ge(m.rstd_ready, 1)
            for i in range(TILES):
                e.tensor_scalar(z[:, i, :], g.x[:, i, :], mv[:, i, 0:1], rstd[:, i:i + 1],
                                ALU.subtract, ALU.mult).then_inc(m.z_ready, 1)
            for h in range(HEADS):
                e.wait_ge(m.products, 2 * h + 2)
                e.tensor_copy(G[:, h, :], pps[2 * (h % 2) + 1][0:DC, 0:D]).then_inc(m.G_kept, 1)
            e.wait_ge(m.G_kept, HEADS)


def wide_attention(nc, g, name, HEADS, A, G, zT, bo):
    C = HEADS // 2
    UNITS = HEADS * TPB
    NS = NP_ = AHEAD = 4
    LAG = 3
    with ExitStack() as ctx:
        s = Scope(nc, ctx, name)
        tT = s.sb("tT", [DC, HEADS, T])
        rows = s.sb("ctx_rows", [P, KT, DC])
        nmax = s.sb("nmax", [P, UNITS])
        rsum = s.sb("rsum", [P, UNITS])
        rinv = s.sb("rinv", [P, UNITS])
        prob = [s.sb(f"prob{i}", [P, S]) for i in range(NP_)]
        pT = [s.sb(f"probT{i}", [P, KT, 2, T]) for i in range(2)]
        uT = s.sb("uT", [DC, 2, T])
        sps = [s.ps(f"scores{i}") for i in range(NS)]
        tps = [s.ps(f"turned{i}") for i in range(2)]
        jps = s.ps("u_and_t")
        yps = s.ps("y")
        m = s.sems(["rows_fixed", "t_projected", "t_ready", "scores_ready", "max_ready", "exp_ready",
                    "rinv_ready", "prob_ready", "prob_turned", "pT_even_kept", "pT_odd_kept", "u_projected",
                    "u_kept", "u_used", "y_ready", "x_updated"])
        block = s.block()

        def turns(e, turn):
            turn(0, True)
            with e.Fori(1, B - 1) as b:
                turn(b, True)
            turn(B - 1, False)

        @block.gpsimd
        def _(e):
            def fix_rows(b):
                wait(e, m.u_projected, C * b)
                e.tensor_copy(rows[:, :, :], g.ctx_rows[:, bass.ds(b * KT, KT), :]).then_inc(m.rows_fixed, 1)

            def turn(b, more):
                for n in range(UNITS):
                    if n == 6:
                        fix_rows(b)
                    e.wait_ge(m.rinv_ready, UNITS * b + n + 1)
                    e.tensor_tensor(prob[n % NP_][:, :], prob[n % NP_][:, :], bcast(rinv[:, n:n + 1], [P, S]),
                                    ALU.mult).then_inc(m.prob_ready, 1)

            turns(e, turn)

        @block.tensor
        def _(e):
            def project(b, c):
                wait(e, m.t_ready, C * b + c)
                for j in range(2):
                    last = e.matmul(jps[0:DC, j * T:(j + 1) * T], A[:, 2 * c + j, :], zT[:, bass.ds(b * T, T)],
                                    start=True, stop=True)
                last.then_inc(m.t_projected, 1)

            def scores(b, n):
                h, i = divmod(n, TPB)
                wait(e, m.exp_ready, UNITS * b + n - NS + 1)
                if n % 4 == 0:
                    e.wait_ge(m.t_ready, C * b + h // 2 + 1)
                e.matmul(sps[n % NS][:, :], tT[:, h, i * P:(i + 1) * P],
                         g.ctxT[0:DC, bass.ds(b * S, S)], start=True, stop=True).then_inc(m.scores_ready, 1)

            def turned(b, n):
                wait(e, m.pT_odd_kept if n % 2 else m.pT_even_kept, UNITS // 2 * b + n // 2)
                e.wait_ge(m.prob_ready, UNITS * b + n + 1)
                for t in range(KT):
                    last = e.transpose(tps[n % 2][:, t * P:(t + 1) * P], prob[n % NP_][:, t * P:(t + 1) * P], g.ident)
                last.then_inc(m.prob_turned, 1)

            def weighted(b, c):
                e.wait_ge(m.pT_even_kept, UNITS // 2 * b + 2 * c + 2)
                e.wait_ge(m.pT_odd_kept, UNITS // 2 * b + 2 * c + 2)
                wait(e, m.u_kept, C * b + c)
                if c == 0:
                    e.wait_ge(m.rows_fixed, b + 1)
                for t in range(KT):
                    last = e.matmul(jps[0:DC, :], rows[:, t, :], pT[c % 2][:, t, :, :], start=t == 0, stop=t == KT - 1)
                last.then_inc(m.u_projected, 1)

            def joined(b, c):
                e.wait_ge(m.u_kept, C * b + c + 1)
                if c == 0:
                    wait(e, m.x_updated, b)
                for j in range(2):
                    for i in range(TPB):
                        last = e.matmul(yps[:, i * P:(i + 1) * P], uT[:, j, i * P:(i + 1) * P], G[:, (2 * c + j) % HEADS, :],
                                        start=c == 0 and j == 0 and i == 0, stop=False, skip_group_check=True)
                last.then_inc(m.u_used, 1)
                if c % C == C - 1:
                    for i in range(TPB):
                        last = e.matmul(yps[:, i * P:(i + 1) * P], g.ones[0:1, 0:P], bo[:, :], start=False, stop=True,
                                        skip_group_check=True)
                    last.then_inc(m.y_ready, 1)

            def turn(b, more):
                first = isinstance(b, int) and b == 0
                for n in range(UNITS):
                    turned(b, n)
                    if n + AHEAD < UNITS:
                        scores(b, n + AHEAD)
                    elif more:
                        scores(b + 1, n + AHEAD - UNITS)
                    if n % 4 == 1 and more:
                        wait(e, m.u_kept, C * b + n // 4 - 1)
                        project(b + 1, n // 4)
                    if n % 4 == 3 and (n > 4 or not first):
                        if more:
                            e.wait_ge(m.t_ready, C * (b + 1) + n // 4 + 1)
                        weighted(b, n // 4 - 1)
                    if n % 4 == 2 and (n > 8 or not first):
                        joined(b, n // 4 - 2)

            for c in range(C):
                project(0, c)
            for n in range(AHEAD):
                scores(0, n)
            turns(e, turn)
            joined(B, -2)
            weighted(B, -1)
            joined(B, -1)

        @block.scalar
        def _(e):
            def keep_t(b, c):
                e.wait_ge(m.t_projected, C * b + c + 1)
                wait(e, m.scores_ready, UNITS * (b - 1) + 4 * c + 4)
                e.activation(tT[:, 2 * c:2 * c + 2, :], jps[0:DC, :].rearrange("p (h t) -> p h t", h=2),
                             ACT.Copy).then_inc(m.t_ready, 1)

            def exps(b, n):
                e.wait_ge(m.max_ready, UNITS * b + n + 1)
                wait(e, m.prob_turned, UNITS * b + n - NP_ + 1)
                e.activation(prob[n % NP_][:, :], sps[n % NS][:, :], ACT.Exp, bias=nmax[:, n:n + 1],
                             accum_out=rsum[:, n:n + 1]).then_inc(m.exp_ready, 1)

            def keep_odd(b, k):
                e.wait_ge(m.prob_turned, UNITS * b + k + 1)
                wait(e, m.u_projected, C * b + k // 4 - 1)
                e.activation(pT[k // 4 % 2][:, :, k // 2 % 2, P:T], tps[1][:, :].rearrange("p (t q) -> p t q", q=P),
                             ACT.Copy).then_inc(m.pT_odd_kept, 1)

            def turn(b, more):
                first = isinstance(b, int) and b == 0
                for n in range(UNITS):
                    exps(b, n)
                    k = n - LAG
                    if k % 2 == 1 and (k >= 0 or not first):
                        keep_odd(b, k)
                    if n == 0 and not first:
                        keep_t(b, C - 1)
                    if n > 0 and n % 4 == 0 and more:
                        keep_t(b + 1, n // 4 - 1)

            for c in range(C):
                keep_t(0, c)
            turns(e, turn)
            for k in range(-LAG, 0):
                if k % 2 == 1:
                    keep_odd(B, k)

        @block.vector
        def _(e):
            def maxima(b, n):
                e.wait_ge(m.scores_ready, UNITS * b + n + 1)
                e.tensor_reduce(nmax[:, n:n + 1], sps[n % NS][:, :], AX.X, ALU.max, negate=True).then_inc(m.max_ready, 1)

            def invert(b, k):
                e.wait_ge(m.exp_ready, UNITS * b + k + 1)
                k %= UNITS
                e.reciprocal(rinv[:, k:k + 1], rsum[:, k:k + 1]).then_inc(m.rinv_ready, 1)

            def keep_even(b, k):
                e.wait_ge(m.prob_turned, UNITS * b + k + 1)
                wait(e, m.u_projected, C * b + k // 4 - 1)
                e.tensor_copy(pT[k // 4 % 2][:, :, k // 2 % 2, 0:P],
                              tps[0][:, :].rearrange("p (t q) -> p t q", q=P)).then_inc(m.pT_even_kept, 1)

            def keep_u(b, c):
                e.wait_ge(m.u_projected, C * b + c + 1)
                wait(e, m.u_used, C * b + c)
                e.tensor_copy(uT[:, :, :], jps[0:DC, :].rearrange("p (h t) -> p h t", h=2)).then_inc(m.u_kept, 1)

            def update(b):
                e.wait_ge(m.y_ready, b)
                xs = g.x[:, bass.ds(TPB * (b - 1), TPB), :]
                e.tensor_tensor(xs, yps[:, 0:T].rearrange("p (i d) -> p i d", d=D), xs, ALU.add).then_inc(m.x_updated, 1)

            def turn(b, more):
                first = isinstance(b, int) and b == 0
                for n in range(UNITS):
                    if n > 0 or not first:
                        invert(b, n - 1)
                    maxima(b, n)
                    k = n - LAG
                    if k % 2 == 0 and (k >= 0 or not first):
                        keep_even(b, k)
                    if n % 4 == 2 and (n > 8 or not first):
                        keep_u(b, n // 4 - 2)
                    if n == 9 and not first:
                        update(b)

            turns(e, turn)
            invert(B, -1)
            for k in range(-LAG, 0):
                if k % 2 == 0:
                    keep_even(B, k)
            keep_u(B, -2)
            keep_u(B, -1)
            update(B)



def l2_attention(nc, g, a):
    HEADS = 8
    with ExitStack() as ctx:
        s = Scope(nc, ctx, "l2h")
        A, G, zT = s.sb("A", [P, HEADS, DC]), s.sb("G", [DC, HEADS, D]), s.sb("zT", [P, N])
        prepare(nc, g, "l2w", HEADS, g.l2_wq, g.l2_wk, g.l2_wv, g.l2_wo, A, G, zT)
        wide_attention(nc, g, "l2a", HEADS, A, G, zT, g.l2_bo)


def l3_attention(nc, g, a):
    HEADS = 16
    with ExitStack() as ctx:
        s = Scope(nc, ctx, "l3h")
        A, G, zT = s.sb("A", [P, HEADS, DC]), s.sb("G", [DC, HEADS, D]), s.sb("zT", [P, N])
        prepare(nc, g, "l3w", HEADS, g.l3_wq, g.l3_wk, g.l3_wv, g.l3_wo, A, G, zT)
        wide_attention(nc, g, "l3a", HEADS, A, G, zT, g.l3_bo)




def l1_ffn(nc, g, a):
    FF = 512
    FT = FF // P
    MB = TILES // E
    PAIR = 2
    NT = PAIR * MB
    TURNS = E // PAIR
    W = MB * P
    with ExitStack() as ctx:
        s = Scope(nc, ctx, "l1f")
        x_e = g.x[:, :, :].rearrange("p (m e) d -> p e m d", e=E)

        def tile(u, i):
            return g.x[:, PAIR * u + (i % MB) * E + i // MB, :]

        front = Front(s, g, tile=tile, tiles=NT, twice=True)
        w1 = s.sb("w1", [P, PAIR, FF])
        w2 = s.sb("w2", [P, PAIR, FT, D])
        zT = s.sb("zT", [P, NT * P])
        xaT = s.sb("xaT", [P, NT * P])
        h = s.sb("h", [P, PAIR, FT, W])
        yT = s.sb("yT", [P, NT * P])
        og = s.sb("og", [P, NT, D])
        turn = s.ps("turn")
        xps = s.ps("xa")
        hps = [s.ps(f"h{i}") for i in range(4)]
        yps = s.ps("y")
        ops = s.ps("o")
        m = s.sems(["w_loaded", "zT_ready", "xa_ready", "xaT_ready", "h_ready", "h_kept", "y_ready", "yT_ready",
                    "o_ready", "og_ready", "x_updated", "steps"])
        block = s.block()

        @block.sync
        def _(sp):
            with sp.Fori(0, TURNS) as u:
                sp.wait_ge(m.y_ready, PAIR * u)
                sp.dma_start(w1[:, :, :], a["L1_ffn_w1"].rearrange("e d f -> d e f")[:, bass.ds(PAIR * u, PAIR), :]
                             ).then_inc(m.w_loaded, 16)
                sp.dma_start(w2[:, :, :, :], a["L1_ffn_w2"].rearrange("e (f p) d -> p e f d", p=P)[:, bass.ds(PAIR * u, PAIR), :, :]
                             ).then_inc(m.w_loaded, 16)

        @block.gpsimd
        def _(e):
            with e.Fori(0, TURNS) as u:
                front.gpsimd(e, u)

        @block.vector
        def _(e):
            steps = Steps(e, m.steps, front.steps)
            with e.Fori(0, TURNS) as u:
                steps.begin(u)
                e.wait_ge(m.xa_ready, u)
                front.vector(e, u, steps)
                for j in range(PAIR):
                    e.wait_ge(m.y_ready, PAIR * u + j + 1)
                    e.tensor_scalar(yT[:, j * W:(j + 1) * W], yps[:, j * W:(j + 1) * W],
                                    g.l1_b2[:, bass.ds(PAIR * u + j, 1)], None, ALU.add).then_inc(m.yT_ready, 1)
                for j in range(PAIR):
                    e.wait_ge(m.og_ready, u + 1)
                    xs = x_e[:, bass.ds(PAIR * u + j, 1), :, :].squeeze(1)
                    e.tensor_tensor(xs, xs, og[:, j * MB:(j + 1) * MB, :], ALU.add).then_inc(m.x_updated, 1)
                steps.end()
                e.wait_ge(m.x_updated, PAIR * (u + 1))

        @block.tensor
        def _(e):
            with e.Fori(0, TURNS) as u:
                e.wait_ge(m.zT_ready, u)
                front.tensor(e, u, turn)
                e.wait_ge(m.zT_ready, u + 1)
                e.wait_ge(m.xaT_ready, u)
                e.matmul(xps[:, :], g.l1_attn_w[:, :], zT[:, :], start=True, stop=False)
                for i in range(NT):
                    last = e.matmul(xps[:, i * P:(i + 1) * P], front.outer[:, i, :], g.ident, start=False, stop=i == NT - 1)
                last.then_inc(m.xa_ready, 1)
                e.wait_ge(m.xaT_ready, u + 1)
                e.wait_ge(m.w_loaded, 32 * (u + 1))
                for j in range(PAIR):
                    for f in range(0, FT, 2):
                        n = (j * FT + f) // 2
                        for k in range(2):
                            last = e.matmul(hps[n][:, k * W:(k + 1) * W], w1[:, j, (f + k) * P:(f + k + 1) * P],
                                            xaT[:, j * W:(j + 1) * W], start=True, stop=True)
                        last.then_inc(m.h_ready, 1)
                for j in range(PAIR):
                    e.wait_ge(m.h_kept, PAIR * FT * u + FT * (j + 1))
                    for f in range(FT):
                        last = e.matmul(yps[:, j * W:(j + 1) * W], w2[:, j, f, :], h[:, j, f, :], start=f == 0, stop=f == FT - 1)
                    last.then_inc(m.y_ready, 1)
                    if j == 0:
                        e.wait_ge(m.yT_ready, PAIR * u + 1)
                e.wait_ge(m.yT_ready, PAIR * u + PAIR)
                for i in range(NT):
                    e.matmul(ops[:, i * P:(i + 1) * P], yT[:, i * P:(i + 1) * P], g.l1_next_w[:, :], start=True, stop=False)
                    last = e.matmul(ops[:, i * P:(i + 1) * P], g.ones[0:1, 0:P], g.l1_next_b[:, :], start=False, stop=True)
                last.then_inc(m.o_ready, 1)

        @block.scalar
        def _(e):
            with e.Fori(0, TURNS) as u:
                e.wait_ge(front.z_turned, u + 1)
                e.activation(zT[:, :], turn[:, :], ACT.Identity, scale=g.l1_lng[:, 0:1], bias=g.l1_lnb[:, 0:1]
                             ).then_inc(m.zT_ready, 1)
                e.wait_ge(m.xa_ready, u + 1)
                e.activation(xaT[:, :], xps[:, :], ACT.Identity, bias=g.l1_attn_b[:, 0:1]).then_inc(m.xaT_ready, 1)
                for j in range(PAIR):
                    for f in range(FT):
                        n = j * FT + f
                        e.wait_ge(m.h_ready, PAIR * FT // 2 * u + n // 2 + 1)
                        e.activation(h[:, j, f, :], hps[n // 2][:, (n % 2) * W:(n % 2 + 1) * W], ACT.Gelu,
                                     bias=g.l1_b1[:, bass.ds((PAIR * u + j) * FT + f, 1)]).then_inc(m.h_kept, 1)
                e.wait_ge(m.o_ready, u + 1)
                e.wait_ge(m.x_updated, PAIR * u)
                e.activation(og[:, :, :], ops[:, :].rearrange("p (i d) -> p i d", d=D), ACT.Gelu).then_inc(m.og_ready, 1)



def l2_ffn(nc, g, a):
    NB = 2
    NT = NB * TPB
    W = NT * P
    TURNS = B // NB
    C = 4
    with ExitStack() as ctx:
        s = Scope(nc, ctx, "l2f")
        front = Front(s, g, tile=lambda u, i: g.x[:, NT * u + i, :], tiles=NT)
        scale = s.sb("scale", [P, 2, NT])
        zT = s.sb("zT", [P, W])
        ones = s.sb("ones", [P, T])
        qT = [s.sb(f"qT{i}", [P, W]) for i in range(2)]
        cum = [s.sb(f"cum{i}", [P, W]) for i in range(2)]
        hT = [s.sb(f"hT{i}", [P, W]) for i in range(2)]
        red = s.sb("red", [P, 4, 2 * NT])
        shifted = s.sb("shifted", [P, 2 * NT, E])
        ex = s.sb("ex", [P, 2 * NT, E])
        w = s.sb("w", [P, 2 * NT, E])
        wT = s.sb("wT", [E, 2, W])
        xv = [s.sb(f"xv{i}", [P, W]) for i in range(2)]
        xy = [s.sb(f"xy{i}", [P, W]) for i in range(2)]
        prod = [s.sb(f"prod{i}", [P, W]) for i in range(2)]
        oT = s.sb("oT", [P, W])
        bank = [s.ps(f"bank{i}") for i in range(2)]
        xps = [s.ps(f"xv{i}") for i in range(2)]
        yps = [s.ps(f"yw{i}") for i in range(2)]
        wps = s.ps("weights")
        ops = s.ps("out")
        m = s.sems(["scale_ready", "ones_ready", "zT_ready", "q_projected", "q_kept", "k_projected", "cum_kept",
                    "h_projected", "h_kept", "logits_ready", "shifted_ready", "ex_ready", "w_ready", "w_turned",
                    "wT_kept", "xv_ready", "xv_kept", "yw_ready", "xy_kept", "wb_ready", "prod_ready", "prod_used",
                    "o_ready", "oT_kept", "y_ready", "x_updated", "steps"])
        block = s.block()

        @block.gpsimd
        def _(e):
            e.memset(ones[:, :], 1.0).then_inc(m.ones_ready, 1)
            with e.Fori(0, TURNS) as u:
                front.gpsimd(e, u)

        @block.tensor
        def _(e):
            with e.Fori(0, TURNS) as u:
                e.wait_ge(m.x_updated, u)
                front.tensor(e, u, bank[0])
                e.wait_ge(m.zT_ready, u + 1)
                e.matmul(bank[1][:, :], g.l2_wqT[:, :], zT[:, :], start=True, stop=True).then_inc(m.q_projected, 1)
                e.matmul(xps[0][:, :], g.l2_wkT[:, :], zT[:, :], start=True, stop=True).then_inc(m.k_projected, 1)
                e.wait_ge(m.q_kept, 2 * u + 1)
                e.matmul(xps[1][:, :], g.l2_winvT[:, :], qT[0][:, :], start=True, stop=True).then_inc(m.q_projected, 1)
                e.matmul(yps[0][:, :], g.l2_rw1T[:, :], qT[0][:, :], start=True, stop=True).then_inc(m.h_projected, 1)
                e.wait_ge(m.q_kept, 2 * u + 2)
                e.matmul(yps[1][:, :], g.l2_rw1T[:, :], qT[1][:, :], start=True, stop=True).then_inc(m.h_projected, 1)
                e.wait_ge(m.cum_kept, 3 * u + 2)
                e.matmul(xps[0][:, :], g.l2_winvT[:, :], cum[0][:, :], start=True, stop=True).then_inc(m.k_projected, 1)
                for r in range(2):
                    e.wait_ge(m.h_kept, 2 * u + r + 1)
                    for i in range(NT):
                        at = (r * NT + i) * E
                        e.matmul(wps[:, at:at + E], hT[r][:, i * P:(i + 1) * P], g.l2_rw2T[:, :], start=True, stop=False)
                        e.matmul(wps[:, at:at + E], g.ones[0:1, 0:P], g.l2_rb2[:, :], start=False, stop=False)
                        last = e.matmul(wps[:, at:at + E], g.ones[0:1, 0:P], g.l2_eb[:, :], start=False, stop=True)
                last.then_inc(m.logits_ready, 1)
                e.wait_ge(m.w_ready, u + 1)
                for r in range(2):
                    for i in range(NT):
                        last = e.transpose(bank[r][0:E, i * P:(i + 1) * P], w[:, r * NT + i, :], g.ident)
                last.then_inc(m.w_turned, 1)
                e.wait_ge(m.cum_kept, 3 * u + 3)
                e.wait_ge(m.wT_kept, 2 * u + 2)

                def front_products(n):
                    r, c = divmod(n, C)
                    if n >= 2:
                        e.wait_ge(m.xv_kept, 2 * C * u + n - 1)
                        e.wait_ge(m.xy_kept, 2 * C * u + n - 1)
                    e.matmul(xps[n % 2][:, :], g.l2_v[r][:, 2 * c:2 * c + 2, :], qT[r][:, :], start=True, stop=True).then_inc(m.xv_ready, 1)
                    e.matmul(yps[n % 2][:, :], g.l2_w[r][:, 2 * c:2 * c + 2, :], cum[r][:, :], start=True, stop=True).then_inc(m.yw_ready, 1)
                    if n >= 1:
                        e.wait_ge(m.prod_ready, 2 * C * u + n)
                    e.matmul(wps[:, :], g.const[0:E, C_SEL + c * P:C_SEL + (c + 1) * P], wT[:, r, :], start=True,
                             stop=True).then_inc(m.wb_ready, 1)

                front_products(0)
                for n in range(2 * C):
                    if n + 1 < 2 * C:
                        front_products(n + 1)
                    e.wait_ge(m.prod_ready, 2 * C * u + n + 1)
                    r, c = divmod(n, C)
                    e.matmul(ops[:, :], g.l2_uT[r][:, c, :], prod[n % 2][:, :], start=n == 0, stop=False).then_inc(m.prod_used, 1)
                for r in range(2):
                    last = e.matmul(ops[:, :], g.l2_b[r][:, :], wT[:, r, :], start=False, stop=r == 1)
                last.then_inc(m.o_ready, 1)
                e.wait_ge(m.oT_kept, u + 1)
                for i in range(NT):
                    last = e.matmul(bank[0][:, i * P:(i + 1) * P], oT[:, i * P:(i + 1) * P], g.l2_woT[:, :], start=True, stop=True)
                last.then_inc(m.y_ready, 1)

        @block.scalar
        def _(e):
            with e.Fori(0, TURNS) as u:
                e.wait_ge(front.z_turned, u + 1)
                e.activation(zT[:, :], bank[0][:, :], ACT.Copy).then_inc(m.zT_ready, 1)
                e.wait_ge(m.q_projected, 2 * u + 1)
                e.activation(qT[0][:, :], bank[1][:, :], ACT.Copy).then_inc(m.q_kept, 1)
                e.wait_ge(m.q_projected, 2 * u + 2)
                e.activation(qT[1][:, :], xps[1][:, :], ACT.Copy).then_inc(m.q_kept, 1)
                for r in range(2):
                    e.wait_ge(m.h_projected, 2 * u + r + 1)
                    e.activation(hT[r][:, :], yps[r][:, :], ACT.Gelu, bias=g.l2_rb1[:, 0:1]).then_inc(m.h_kept, 1)
                e.wait_ge(m.shifted_ready, u + 1)
                e.activation(ex[:, :, :], shifted[:, :, :], ACT.Exp).then_inc(m.ex_ready, 1)
                e.wait_ge(m.w_turned, u + 1)
                for r in range(2):
                    e.activation(wT[:, r, :], bank[r][0:E, :], ACT.Copy).then_inc(m.wT_kept, 1)
                for n in range(2 * C):
                    e.wait_ge(m.xv_ready, 2 * C * u + n + 1)
                    if n >= 2:
                        e.wait_ge(m.xy_kept, 2 * C * u + n - 1)
                    e.activation(xv[n % 2][:, :], xps[n % 2][:, :], ACT.Copy).then_inc(m.xv_kept, 1)
                e.wait_ge(m.o_ready, u + 1)
                e.activation(oT[:, :], ops[:, :], ACT.Copy).then_inc(m.oT_kept, 1)

        @block.vector
        def _(e):
            steps = Steps(e, m.steps, front.steps + 4)
            for r in range(2):
                for i in range(NT):
                    at = C_INVN + i % TPB
                    if r == 0:
                        e.tensor_copy(scale[:, r, i:i + 1], g.const[:, at:at + 1]).then_inc(m.scale_ready, 1)
                    else:
                        e.tensor_tensor(scale[:, r, i:i + 1], g.const[:, at:at + 1], g.l2_alpha[:, :],
                                        ALU.mult).then_inc(m.scale_ready, 1)
            e.wait_ge(m.scale_ready, 2 * NT)
            e.wait_ge(m.ones_ready, 1)
            with e.Fori(0, TURNS) as u:
                steps.begin(u)
                front.vector(e, u, steps)
                e.wait_ge(m.k_projected, 2 * u + 1)
                for n in range(NB):
                    e.tensor_tensor_scan(cum[0][:, n * T:(n + 1) * T], ones[:, :], xps[0][:, n * T:(n + 1) * T], 0.0,
                                         ALU.mult, ALU.add).then_inc(m.cum_kept, 1)
                e.wait_ge(m.k_projected, 2 * u + 2)
                e.tensor_copy(cum[1][:, :], xps[0][:, :]).then_inc(m.cum_kept, 1)
                e.wait_ge(m.logits_ready, u + 1)
                logits = wps[:, 0:2 * NT * E].rearrange("p (i e) -> p i e", e=E)
                full = [P, 2 * NT, E]
                steps.add(e.tensor_reduce(red[:, 0, :], logits, AX.X, ALU.max))
                steps.settle()
                e.tensor_tensor(shifted[:, :, :], logits, bcast(red[:, 0, :].unsqueeze(2), full),
                                ALU.subtract).then_inc(m.shifted_ready, 1)
                e.wait_ge(m.ex_ready, u + 1)
                steps.add(e.tensor_reduce(red[:, 1, :], ex[:, :, :], AX.X, ALU.add))
                steps.settle()
                steps.add(e.reciprocal(red[:, 2, :], red[:, 1, :]))
                steps.settle()
                steps.add(e.tensor_tensor(red[:, 3, :], red[:, 2, :], scale[:, :, :].rearrange("p r i -> p (r i)"), ALU.mult))
                steps.settle()
                e.tensor_tensor(w[:, :, :], ex[:, :, :], bcast(red[:, 3, :].unsqueeze(2), full), ALU.mult).then_inc(m.w_ready, 1)
                for n in range(2 * C):
                    e.wait_ge(m.xv_kept, 2 * C * u + n + 1)
                    e.wait_ge(m.yw_ready, 2 * C * u + n + 1)
                    e.tensor_tensor(xy[n % 2][:, :], xv[n % 2][:, :], yps[n % 2][:, :], ALU.mult).then_inc(m.xy_kept, 1)
                    e.wait_ge(m.wb_ready, 2 * C * u + n + 1)
                    e.wait_ge(m.xy_kept, 2 * C * u + n + 1)
                    if n >= 2:
                        e.wait_ge(m.prod_used, 2 * C * u + n - 1)
                    e.tensor_tensor(prod[n % 2][:, :], xy[n % 2][:, :], wps[:, :], ALU.mult).then_inc(m.prod_ready, 1)
                e.wait_ge(m.y_ready, u + 1)
                e.tensor_tensor(g.x[:, bass.ds(NT * u, NT), :], bank[0][:, :].rearrange("p (i d) -> p i d", d=D),
                                g.x[:, bass.ds(NT * u, NT), :], ALU.add).then_inc(m.x_updated, 1)
                steps.end()
                e.wait_ge(m.x_updated, u + 1)



def l3_ffn(nc, g, a):
    K = 2
    with ExitStack() as outer:
        so = Scope(nc, outer, "l3f")
        zT = so.sb("zT", [P, N])
        zT0 = so.sb("zT_first", [P, B])
        index = so.sb("index", [K, B], I32)

        with ExitStack() as ctx:
            s = Scope(nc, ctx, "l3f_norm")
            front = Front(s, g)
            red = s.sb("red", [B, 4])
            w = [s.sb(f"w{i}", [B, E]) for i in range(6)]
            pick = s.sb("pick", [B, K])
            turn = s.ps("turn")
            sps = s.ps("scores")
            m = s.sems(["zT_kept", "scores_ready", "pick_ready", "pick_turned", "index_ready", "steps", "steps2"])
            block = s.block()

            @block.gpsimd
            def _(e):
                with e.Fori(0, B) as b:
                    front.gpsimd(e, b)

            @block.tensor
            def _(e):
                with e.Fori(0, B) as b:
                    e.wait_ge(m.zT_kept, 2 * b)
                    front.tensor(e, b, turn)
                e.wait_ge(m.zT_kept, 2 * B)
                e.matmul(sps[0:B, 0:E], zT0[:, :], g.l3_wr[:, :], start=True, stop=False)
                e.matmul(sps[0:B, 0:E], g.ones[0:1, 0:B], g.l3_br[:, :], start=False, stop=True).then_inc(m.scores_ready, 1)
                e.wait_ge(m.pick_ready, K)
                e.transpose(turn[0:K, 0:B], pick[:, :], g.ident[0:B, 0:B]).then_inc(m.pick_turned, 1)

            @block.scalar
            def _(e):
                with e.Fori(0, B) as b:
                    e.wait_ge(front.z_turned, b + 1)
                    e.activation(zT[:, bass.ds(b * T, T)], turn[:, 0:T], ACT.Copy).then_inc(m.zT_kept, 1)
                    e.activation(zT0[:, bass.ds(b, 1)], turn[:, 0:1], ACT.Copy).then_inc(m.zT_kept, 1)

            @block.vector
            def _(e):
                steps = Steps(e, m.steps, front.steps)
                with e.Fori(0, B) as b:
                    steps.begin(b)
                    e.wait_ge(front.z_turned, b)
                    front.vector(e, b, steps)
                    steps.end()
                steps = Steps(e, m.steps2)

                def then(instruction):
                    steps.add(instruction)
                    steps.settle()

                rev = g.const[0:B, C_REV:C_REV + E]

                def first_of_largest(source, at, k):
                    then(e.tensor_reduce(red[:, at:at + 1], source, AX.X, ALU.max))
                    then(e.tensor_scalar(w[0][:, :], source, red[:, at:at + 1], None, ALU.is_equal))
                    then(e.tensor_tensor(w[1][:, :], w[0][:, :], rev, ALU.mult))
                    then(e.tensor_reduce(red[:, at + 1:at + 2], w[1][:, :], AX.X, ALU.max))
                    e.tensor_scalar(pick[:, k:k + 1], red[:, at + 1:at + 2], -1.0, float(E), ALU.mult,
                                    ALU.add).then_inc(m.pick_ready, 1)

                e.wait_ge(m.scores_ready, 1)
                then(e.tensor_copy(w[2][:, :], sps[0:B, 0:E]))
                first_of_largest(w[2][:, :], 0, 0)
                then(e.tensor_scalar(w[3][:, :], rev, red[:, 1:2], None, ALU.is_equal))
                then(e.tensor_scalar(w[4][:, :], w[3][:, :], -3.0e38, None, ALU.mult))
                then(e.tensor_tensor(w[5][:, :], w[2][:, :], w[4][:, :], ALU.add))
                first_of_largest(w[5][:, :], 2, 1)
                e.wait_ge(m.pick_turned, 1)
                e.tensor_copy(index[:, :], turn[0:K, 0:B]).then_inc(m.index_ready, 1)
                e.wait_ge(m.index_ready, 1)

        with ExitStack() as ctx:
            s = Scope(nc, ctx, "l3f_experts")
            U = 2
            w1 = [s.sb(f"w1_{p}", [P, K, D]) for p in range(U)]
            w2 = [s.sb(f"w2_{p}", [P, K, D]) for p in range(U)]
            b1 = [s.sb(f"b1_{p}", [1, K, D]) for p in range(U)]
            b2 = [s.sb(f"b2_{p}", [1, K, D]) for p in range(U)]
            ones = s.sb("ones", [1, T])
            h = [s.sb(f"h{p}", [P, K, T]) for p in range(U)]
            hps = [s.ps(f"h{p}") for p in range(U)]
            ops = [s.ps(f"o{p}") for p in range(U)]
            m = s.sems(["ones_ready", "loaded_even", "loaded_odd", "h_projected", "h_kept", "o_ready", "x_updated"])
            loaded = [m.loaded_even, m.loaded_odd]
            block = s.block()

            @block.sync
            def _(sp):
                with sp.Fori(0, B // U) as u:
                    for p in range(U):
                        sp.wait_ge(m.o_ready, U * u)
                        for k in range(K):
                            x = sp.value_load(index[k:k + 1, bass.ds(U * u + p, 1)], min_val=0, max_val=E - 1)
                            for dst, src in ((w1[p][:, k, :], a["L3_ffn_W1"][bass.ds(x, 1), :, :].squeeze(0)),
                                             (w2[p][:, k, :], a["L3_ffn_W2"][bass.ds(x, 1), :, :].squeeze(0)),
                                             (b1[p][:, k, :], a["L3_ffn_b1"][bass.ds(x, 1), :]),
                                             (b2[p][:, k, :], a["L3_ffn_b2"][bass.ds(x, 1), :])):
                                sp.dma_start(dst, src).then_inc(loaded[p], 16)

            @block.gpsimd
            def _(e):
                e.memset(ones[:, :], 1.0).then_inc(m.ones_ready, 1)

            @block.tensor
            def _(e):
                e.wait_ge(m.ones_ready, 1)
                with e.Fori(0, B // U) as u:
                    for p in range(U):
                        e.wait_ge(loaded[p], 16 * 4 * K * (u + 1))
                        e.wait_ge(m.h_kept, U * u)
                        for k in range(K):
                            e.matmul(hps[p][:, k * T:(k + 1) * T], w1[p][:, k, :], zT[:, bass.ds((U * u + p) * T, T)], start=True, stop=False)
                            last = e.matmul(hps[p][:, k * T:(k + 1) * T], b1[p][:, k, :], ones[:, :], start=False, stop=True)
                        last.then_inc(m.h_projected, 1)
                    for p in range(U):
                        e.wait_ge(m.h_kept, U * u + p + 1)
                        e.wait_ge(m.x_updated, U * u)
                        for i in range(TPB):
                            for k in range(K):
                                e.matmul(ops[p][:, i * P:(i + 1) * P], h[p][:, k, i * P:(i + 1) * P], w2[p][:, k, :], start=k == 0, stop=False)
                                last = e.matmul(ops[p][:, i * P:(i + 1) * P], g.ones[0:1, 0:P], b2[p][:, k, :], start=False, stop=k == K - 1)
                        last.then_inc(m.o_ready, 1)

            @block.scalar
            def _(e):
                with e.Fori(0, B // U) as u:
                    for p in range(U):
                        e.wait_ge(m.h_projected, U * u + p + 1)
                        e.wait_ge(m.o_ready, U * u)
                        e.activation(h[p][:, :, :], hps[p][:, :].rearrange("p (k t) -> p k t", k=K), ACT.Gelu).then_inc(m.h_kept, 1)

            @block.vector
            def _(e):
                with e.Fori(0, B // U) as u:
                    for p in range(U):
                        e.wait_ge(m.o_ready, U * u + p + 1)
                        xs = g.x[:, bass.ds(TPB * (U * u + p), TPB), :]
                        e.scalar_tensor_tensor(out=xs, in0=ops[p][:, 0:T].rearrange("p (i d) -> p i d", d=D), scalar=1.0 / K,
                                               in1=xs, op0=ALU.mult, op1=ALU.add).then_inc(m.x_updated, 1)




QW = ["d2v", "img", "txt", "att0", "att1", "f1", "f2"]


def quantise_weights(nc, g, a, q, wscale):
    FT = 4
    shape = {"d2v": (P, DC), "img": (P, D), "txt": (P, D), "att0": (D // 2, D), "att1": (D // 2, D)}
    with ExitStack() as ctx:
        s = Scope(nc, ctx, "l1q")
        raw = {n: s.sb("raw_" + n, list(shape[n])) for n in shape}
        raw["f1"] = s.sb("raw_f1", [P, FT, 2 * D])
        raw["f2"] = s.sb("raw_f2", [P, FT, D])
        low = {n: s.sb("low_" + n, list(raw[n].shape)) for n in QW}
        absum = s.sb("absum", [P, len(QW)])
        thr = s.sb("threshold", [P, len(QW)])
        nthr = s.sb("neg_threshold", [P, len(QW)])
        total = s.ps("total")
        turned = [s.ps(f"turned{i}") for i in range(4)]
        m = s.sems(["loaded", "zeroed", "summed", "total_ready", "scale_ready", "thr_ready", "low_ready", "q_ready",
                    "turned", "kept"])
        moves = [(raw["d2v"][:, :], [q["d2v"][:, :]]), (raw["img"][:, :], [q["img"][:, :]]),
                 (raw["txt"][:, :], [q["txt"][:, :]])]
        for n in ("att0", "att1"):
            moves.append((raw[n][:, :], [q[n][:, 0:D // 2], q[n][:, D // 2:D]]))
        for f in range(FT):
            for half in range(2):
                moves.append((raw["f1"][:, f, half * D:(half + 1) * D], [q["f1"][:, half, f * P:(f + 1) * P]]))
        for f in range(FT):
            moves.append((raw["f2"][:, f, :], [q["f2"][:, f, :]]))
        block = s.block()

        @block.sync
        def _(sp):
            for n in ("d2v", "img", "txt", "att0", "att1"):
                sp.dma_start(raw[n][:, :], a["L1_xattn_W_" + n]).then_inc(m.loaded, 16)
            sp.dma_start(raw["f1"][:, :, :], a["L1_xattn_W_f1"].rearrange("(f p) i -> p f i", p=P)).then_inc(m.loaded, 16)
            sp.dma_start(raw["f2"][:, :, :], a["L1_xattn_W_f2"].rearrange("o (f i) -> o f i", i=D)).then_inc(m.loaded, 16)

        @block.vector
        def _(e):
            e.memset(absum[:, :], 0.0).then_inc(m.zeroed, 1)
            e.wait_ge(m.zeroed, 1)
            e.wait_ge(m.loaded, 16 * len(QW))
            size = {}
            for i, n in enumerate(QW):
                t = raw[n]
                rows = t.shape[0]
                size[n] = int(np.prod(t.shape))
                flat = t[:, :, :].rearrange("p f i -> p (f i)") if len(t.shape) == 3 else t[:, :]
                e.tensor_reduce(absum[0:rows, i:i + 1], flat, AX.X, ALU.add, apply_absolute_value=True).then_inc(m.summed, 1)
            e.wait_ge(m.total_ready, 1)
            for i, n in enumerate(QW):
                e.tensor_scalar(wscale[:, i:i + 1], total[:, i:i + 1], 1.0 / size[n], 1e-5, ALU.mult, ALU.max
                                ).then_inc(m.scale_ready, 1)
            e.wait_ge(m.scale_ready, len(QW))
            e.tensor_scalar(thr[:, :], wscale[:, :], 0.5, None, ALU.mult).then_inc(m.thr_ready, 1)
            e.tensor_scalar(nthr[:, :], wscale[:, :], -0.5, None, ALU.mult).then_inc(m.thr_ready, 1)
            e.wait_ge(m.thr_ready, 2)
            for i, n in enumerate(QW):
                rows = raw[n].shape[0]
                whole = tuple(slice(None) for _ in raw[n].shape)
                e.tensor_scalar(low[n][whole], raw[n][whole], nthr[0:rows, i:i + 1], None, ALU.is_lt).then_inc(m.low_ready, 1)
            for i, n in enumerate(QW):
                rows = raw[n].shape[0]
                whole = tuple(slice(None) for _ in raw[n].shape)
                e.wait_ge(m.low_ready, i + 1)
                e.scalar_tensor_tensor(out=raw[n][whole], in0=raw[n][whole], scalar=thr[0:rows, i:i + 1],
                                       in1=low[n][whole], op0=ALU.is_gt, op1=ALU.subtract).then_inc(m.q_ready, 1)

        @block.tensor
        def _(e):
            e.wait_ge(m.summed, len(QW))
            e.matmul(total[:, 0:len(QW)], g.ones[:, 0:P], absum[:, :], start=True, stop=True).then_inc(m.total_ready, 1)
            e.wait_ge(m.q_ready, len(QW))
            for n, (src, _dst) in enumerate(moves):
                if n >= 4:
                    e.wait_ge(m.kept, n - 3)
                rows, cols = src.shape
                e.transpose(turned[n % 4][0:cols, 0:rows], src, g.ident[0:rows, 0:rows]).then_inc(m.turned, 1)

        @block.scalar
        def _(e):
            for n, (src, dsts) in enumerate(moves):
                rows, cols = src.shape
                e.wait_ge(m.turned, n + 1)
                for k, dst in enumerate(dsts):
                    last = e.activation(dst, turned[n % 4][0:cols, 0:rows], ACT.Copy)
                last.then_inc(m.kept, 1)
            e.wait_ge(m.kept, len(moves))


def activation_scales(nc, g, name, groups, scales):
    G = len(groups)
    with ExitStack() as ctx:
        s = Scope(nc, ctx, name)
        part = s.sb("part", [P, G])
        top = s.sb("top", [1, G])
        step = s.sb("step", [1, G])
        turned = s.ps("turned")
        spread = s.ps("spread")
        m = s.sems(["zeroed", "part_ready", "turned", "top_ready", "step_ready", "spread", "scale_ready"])
        block = s.block()

        @block.vector
        def _(e):
            e.memset(part[:, :], 0.0).then_inc(m.zeroed, 1)
            e.wait_ge(m.zeroed, 1)
            for i, x in enumerate(groups):
                e.tensor_reduce(part[0:x.shape[0], i:i + 1], x, AX.X, ALU.max).then_inc(m.part_ready, 1)
            e.wait_ge(m.turned, 1)
            e.tensor_reduce(top[:, :], turned[0:1, 0:G * P].rearrange("p (g n) -> p g n", n=P), AX.X, ALU.max).then_inc(m.top_ready, 1)
            e.wait_ge(m.top_ready, 1)
            e.tensor_scalar(step[:, :], top[:, :], 1e-8, 1.0 / 127.0, ALU.max, ALU.mult).then_inc(m.step_ready, 1)
            e.wait_ge(m.spread, 1)
            for i, (step_all, inverse) in enumerate(scales):
                e.tensor_copy(step_all, spread[:, i:i + 1]).then_inc(m.scale_ready, 1)
                e.reciprocal(inverse, spread[:, i:i + 1]).then_inc(m.scale_ready, 1)
            e.wait_ge(m.scale_ready, 2 * G)

        @block.tensor
        def _(e):
            e.wait_ge(m.part_ready, G)
            for i in range(G):
                last = e.transpose(turned[0:1, i * P:(i + 1) * P], part[:, i:i + 1], g.ident)
            last.then_inc(m.turned, 1)
            e.wait_ge(m.step_ready, 1)
            e.matmul(spread[:, 0:G], g.ones[0:1, 0:P], step[:, :], start=True, stop=True).then_inc(m.spread, 1)


def quantised_projection(nc, g, name, src, rows, weight, dst, top, step, inverse, wstep, bias, mean=None):
    with ExitStack() as ctx:
        s = Scope(nc, ctx, name)
        out_scale = s.sb("out_scale", [P, 1])
        shifted = [s.sb(f"shifted{i}", [rows, S]) for i in range(2)]
        qx = [s.sb(f"qx{i}", [rows, S], BF16) for i in range(2)]
        ps = [s.ps(f"y{i}") for i in range(2)]
        m = s.sems(["scale_ready", "shifted_ready", "qx_ready", "y_ready", "y_kept", "top_ready", "mean_ready"])
        U = 2
        block = s.block()

        @block.vector
        def _(e):
            e.tensor_tensor(out_scale[:, :], step, wstep, ALU.mult).then_inc(m.scale_ready, 1)
            with e.Fori(0, B // U) as u:
                for p in range(U):
                    e.wait_ge(m.shifted_ready, U * u + p + 1)
                    e.wait_ge(m.y_ready, U * u)
                    e.tensor_scalar(qx[p][:, :], shifted[p][:, :], MAGIC, None, ALU.subtract).then_inc(m.qx_ready, 1)
                for p in range(U):
                    e.wait_ge(m.y_kept, U * u + p + 1)
                    at = U * u + p
                    e.tensor_reduce(top[:, bass.ds(at, 1)], dst[:, bass.ds(at * S, S)], AX.X, ALU.max,
                                    apply_absolute_value=True).then_inc(m.top_ready, 1)
                    if mean is not None:
                        e.tensor_reduce(mean[:, bass.ds(at, 1)], dst[:, bass.ds(at * S, S)], AX.X, ALU.add).then_inc(m.mean_ready, 1)

        @block.scalar
        def _(e):
            e.wait_ge(m.scale_ready, 1)
            with e.Fori(0, B // U) as u:
                for p in range(U):
                    e.wait_ge(m.qx_ready, U * u)
                    e.activation(shifted[p][:, :], src[0:rows, bass.ds((U * u + p) * S, S)], ACT.Identity,
                                 scale=inverse[0:rows, :], bias=g.magic[0:rows, :]).then_inc(m.shifted_ready, 1)
                for p in range(U):
                    e.wait_ge(m.y_ready, U * u + p + 1)
                    e.activation(dst[:, bass.ds((U * u + p) * S, S)], ps[p][:, :], ACT.Identity, scale=out_scale[:, :],
                                 bias=bias).then_inc(m.y_kept, 1)

        @block.tensor
        def _(e):
            with e.Fori(0, B // U) as u:
                for p in range(U):
                    e.wait_ge(m.y_kept, U * u)
                    e.wait_ge(m.qx_ready, U * u + p + 1)
                    e.matmul(ps[p][:, :], weight, qx[p][:, :], start=True, stop=True).then_inc(m.y_ready, 1)


def l1_attention(nc, g, a):
    FT = 4
    INV_SQRT = 1.0 / np.sqrt(D)
    with ExitStack() as outer:
        so = Scope(nc, outer, "l1a")
        q = {"d2v": so.sb("q_d2v", [DC, D], BF16), "img": so.sb("q_img", [D, D], BF16), "txt": so.sb("q_txt", [D, D], BF16),
             "att0": so.sb("q_att0", [D, D], BF16), "att1": so.sb("q_att1", [D, D], BF16),
             "f1": so.sb("q_f1", [D, 2, FT * P], BF16), "f2": so.sb("q_f2", [P, FT, D], BF16)}
        wscale = so.sb("wscale", [P, len(QW)])
        step = so.sb("step", [P, 8])
        inverse = so.sb("inverse", [P, 8])
        CTX, Z, VIS, IMG, FUSED, HID = range(6)
        big = so.sb("big", [P, 2 * B * S])
        vis, img = big[:, 0:B * S], big[:, B * S:2 * B * S]
        hid = big[:, :].rearrange("p (f n) -> p f n", f=FT)
        zT = so.sb("zT", [P, N])
        top = so.sb("top", [P, 2 * B])
        ctx_top = so.sb("ctx_top", [DC, 1])
        avg = so.sb("avg", [P, B])
        f1_bias = so.sb("f1_bias", [P, FT, B])

        def scales(i):
            return step[:, i:i + 1], inverse[:, i:i + 1]

        def w(n):
            return wscale[:, QW.index(n):QW.index(n) + 1]

        quantise_weights(nc, g, a, q, wscale)

        with ExitStack() as ctx:
            s = Scope(nc, ctx, "l1a_norm")
            front = Front(s, g)
            turn = s.ps("turn")
            m = s.sems(["z_kept", "top_ready", "ctx_top_ready", "steps"])
            block = s.block()

            @block.gpsimd
            def _(e):
                with e.Fori(0, B) as b:
                    front.gpsimd(e, b)

            @block.tensor
            def _(e):
                with e.Fori(0, B) as b:
                    e.wait_ge(m.z_kept, b)
                    front.tensor(e, b, turn)

            @block.scalar
            def _(e):
                with e.Fori(0, B) as b:
                    e.wait_ge(front.z_turned, b + 1)
                    e.activation(zT[:, bass.ds(b * T, T)], turn[:, 0:T], ACT.Copy).then_inc(m.z_kept, 1)

            @block.vector
            def _(e):
                steps = Steps(e, m.steps, front.steps)
                e.tensor_reduce(ctx_top[:, :], g.ctxT[0:DC, :], AX.X, ALU.max, apply_absolute_value=True).then_inc(m.ctx_top_ready, 1)
                with e.Fori(0, B) as b:
                    steps.begin(b)
                    front.vector(e, b, steps)
                    e.wait_ge(m.z_kept, b + 1)
                    e.tensor_reduce(top[:, bass.ds(b, 1)], zT[:, bass.ds(b * T, T)], AX.X, ALU.max,
                                    apply_absolute_value=True).then_inc(m.top_ready, 1)
                    steps.end()

        activation_scales(nc, g, "l1s_in", [ctx_top[:, :], top[:, 0:B]], [scales(CTX), scales(Z)])
        quantised_projection(nc, g, "l1p_vis", g.ctxT, DC, q["d2v"][:, :], vis, top, step[:, CTX:CTX + 1],
                             inverse[:, CTX:CTX + 1], w("d2v"), g.l1_bd2v[:, 0:1])
        activation_scales(nc, g, "l1s_vis", [top[:, 0:B]], [scales(VIS)])
        quantised_projection(nc, g, "l1p_img", vis, P, q["img"][:, :], img, top, step[:, VIS:VIS + 1],
                             inverse[:, VIS:VIS + 1], w("img"), g.l1_bimg[:, 0:1], mean=avg)
        activation_scales(nc, g, "l1s_img", [top[:, 0:B]], [scales(IMG)])

        with ExitStack() as ctx:
            s = Scope(nc, ctx, "l1a_att")
            sc = s.sb("out_scales", [P, 3])
            shift_i = s.sb("shifted_img", [P, S])
            shift_z = s.sb("shifted_z", [P, T])
            qi = s.sb("q_img_chunk", [P, S], BF16)
            qz = s.sb("q_z_chunk", [P, T], BF16)
            kT = [s.sb(f"kT{i}", [P, S]) for i in range(2)]
            kt = [s.sb(f"k_rows{i}", [P, KT, D]) for i in range(2)]
            f = s.sb("fused", [P, T])
            rmax = s.sb("rmax", [P, 2 * TPB])
            nmax = s.sb("nmax", [P, 2 * TPB])
            rsum = s.sb("rsum", [P, 2 * TPB])
            rinv = s.sb("rinv", [P, 2 * TPB])
            prob = [s.sb(f"prob{i}", [P, S]) for i in range(TPB)]
            pT = s.sb("probT", [P, KT, T])
            kps = [s.ps(f"k{i}") for i in range(2)]
            fps = s.ps("f")
            sps = [s.ps(f"scores{i}") for i in range(TPB)]
            tps = [s.ps(f"turned{i}") for i in range(TPB)]
            ops = s.ps("o")
            m = s.sems(["scales_ready", "shifted", "quantised", "kT_projected", "kT_kept", "kr_projected", "kr_kept",
                        "f_projected", "f_kept", "scores_ready", "max_ready", "nmax_ready", "exp_ready", "rinv_ready",
                        "prob_ready", "turned", "pT_kept", "o_ready", "f_updated", "f_stored", "top_ready", "avg_scaled"])
            R = 2
            block = s.block()

            @block.vector
            def _(e):
                e.tensor_tensor(sc[:, 0:1], step[:, IMG:IMG + 1], w("att0"), ALU.mult).then_inc(m.scales_ready, 1)
                e.tensor_tensor(sc[:, 1:2], step[:, IMG:IMG + 1], w("att1"), ALU.mult).then_inc(m.scales_ready, 1)
                e.tensor_tensor(sc[:, 2:3], step[:, Z:Z + 1], w("txt"), ALU.mult).then_inc(m.scales_ready, 1)
                e.tensor_scalar(avg[:, :], avg[:, :], 1.0 / S, None, ALU.mult).then_inc(m.avg_scaled, 1)
                e.wait_ge(m.scales_ready, 3)
                with e.Fori(0, B) as b:
                    e.wait_ge(m.shifted, 2 * b + 1)
                    e.tensor_scalar(qi[:, :], shift_i[:, :], MAGIC, None, ALU.subtract).then_inc(m.quantised, 1)
                    e.wait_ge(m.shifted, 2 * b + 2)
                    e.tensor_scalar(qz[:, :], shift_z[:, :], MAGIC, None, ALU.subtract).then_inc(m.quantised, 1)
                    for r in range(R):
                        e.wait_ge(m.kr_projected, R * b + r + 1)
                        e.scalar_tensor_tensor(out=kt[r][:, :, :], in0=ops[:, :].rearrange("p (t d) -> p t d", d=D),
                                               scalar=sc[:, r:r + 1], in1=bcast(g.l1_batt_rows[r][:, :].unsqueeze(1), [P, KT, D]),
                                               op0=ALU.mult, op1=ALU.add).then_inc(m.kr_kept, 1)
                    for r in range(R):
                        for i in range(TPB):
                            n = r * TPB + i
                            e.wait_ge(m.scores_ready, R * TPB * b + n + 1)
                            e.tensor_reduce(rmax[:, n:n + 1], sps[i][:, :], AX.X, ALU.max, negate=True).then_inc(m.max_ready, 1)
                            e.wait_ge(m.max_ready, R * TPB * b + n + 1)
                            e.tensor_scalar(nmax[:, n:n + 1], rmax[:, n:n + 1], INV_SQRT, None, ALU.mult).then_inc(m.nmax_ready, 1)
                        for i in range(TPB):
                            n = r * TPB + i
                            e.wait_ge(m.exp_ready, R * TPB * b + n + 1)
                            e.reciprocal(rinv[:, n:n + 1], rsum[:, n:n + 1]).then_inc(m.rinv_ready, 1)
                            e.wait_ge(m.rinv_ready, R * TPB * b + n + 1)
                            e.tensor_scalar(prob[i][:, :], prob[i][:, :], rinv[:, n:n + 1], None, ALU.mult).then_inc(m.prob_ready, 1)
                        e.wait_ge(m.o_ready, R * b + r + 1)
                        e.wait_ge(m.f_kept, b + 1)
                        if r:
                            e.wait_ge(m.f_updated, R * b + r)
                        e.scalar_tensor_tensor(out=f[:, :], in0=ops[:, 0:T], scalar=0.1, in1=f[:, :], op0=ALU.mult,
                                               op1=ALU.add).then_inc(m.f_updated, 1)
                    e.wait_ge(m.f_updated, R * b + R)
                    e.tensor_copy(zT[:, bass.ds(b * T, T)], f[:, :]).then_inc(m.f_stored, 1)
                    e.tensor_reduce(top[:, bass.ds(b, 1)], f[:, :], AX.X, ALU.max, apply_absolute_value=True).then_inc(m.top_ready, 1)
                e.wait_ge(m.avg_scaled, 1)
                e.tensor_reduce(top[:, B:B + 1], avg[:, :], AX.X, ALU.max, apply_absolute_value=True).then_inc(m.top_ready, 1)

            @block.scalar
            def _(e):
                e.wait_ge(m.scales_ready, 3)
                with e.Fori(0, B) as b:
                    e.wait_ge(m.top_ready, b)
                    e.activation(shift_i[:, :], img[:, bass.ds(b * S, S)], ACT.Identity, scale=inverse[:, IMG:IMG + 1],
                                 bias=g.magic[:, :]).then_inc(m.shifted, 1)
                    e.activation(shift_z[:, :], zT[:, bass.ds(b * T, T)], ACT.Identity, scale=inverse[:, Z:Z + 1],
                                 bias=g.magic[:, :]).then_inc(m.shifted, 1)
                    for r in range(R):
                        e.wait_ge(m.kT_projected, R * b + r + 1)
                        e.activation(kT[r][:, :], kps[r][:, :], ACT.Identity, scale=sc[:, r:r + 1],
                                     bias=g.l1_batt[r][:, 0:1]).then_inc(m.kT_kept, 1)
                    e.wait_ge(m.f_projected, b + 1)
                    e.activation(f[:, :], fps[:, 0:T], ACT.Identity, scale=sc[:, 2:3], bias=g.l1_btxt[:, 0:1]).then_inc(m.f_kept, 1)
                    for r in range(R):
                        for i in range(TPB):
                            n = r * TPB + i
                            e.wait_ge(m.nmax_ready, R * TPB * b + n + 1)
                            e.activation(prob[i][:, :], sps[i][:, :], ACT.Exp, scale=INV_SQRT, bias=nmax[:, n:n + 1],
                                         accum_out=rsum[:, n:n + 1]).then_inc(m.exp_ready, 1)
                        for i in range(TPB):
                            n = r * TPB + i
                            e.wait_ge(m.turned, R * TPB * b + n + 1)
                            e.activation(pT[:, :, i * P:(i + 1) * P], tps[i][:, :].rearrange("p (t q) -> p t q", q=P),
                                         ACT.Copy).then_inc(m.pT_kept, 1)

            @block.tensor
            def _(e):
                with e.Fori(0, B) as b:
                    e.wait_ge(m.quantised, 2 * b + 1)
                    for r, n in enumerate(("att0", "att1")):
                        e.matmul(kps[r][:, :], q[n][:, :], qi[:, :], start=True, stop=True).then_inc(m.kT_projected, 1)
                    e.wait_ge(m.quantised, 2 * b + 2)
                    e.matmul(fps[:, 0:T], q["txt"][:, :], qz[:, :], start=True, stop=True).then_inc(m.f_projected, 1)
                    for r, n in enumerate(("att0", "att1")):
                        e.wait_ge(m.f_updated, R * b)
                        e.wait_ge(m.kr_kept, R * b + r)
                        for t in range(KT):
                            last = e.matmul(ops[:, t * P:(t + 1) * P], qi[:, t * P:(t + 1) * P], q[n][:, :], start=True, stop=True)
                        last.then_inc(m.kr_projected, 1)
                    e.wait_ge(m.kr_kept, R * b + R)
                    for r in range(R):
                        e.wait_ge(m.kT_kept, R * b + r + 1)
                        e.wait_ge(m.f_kept, b + 1)
                        e.wait_ge(m.f_updated, R * b + r)
                        for i in range(TPB):
                            e.matmul(sps[i][:, :], f[:, i * P:(i + 1) * P], kT[r][:, :], start=True, stop=True).then_inc(m.scores_ready, 1)
                        for i in range(TPB):
                            e.wait_ge(m.prob_ready, R * TPB * b + r * TPB + i + 1)
                            for t in range(KT):
                                last = e.transpose(tps[i][:, t * P:(t + 1) * P], prob[i][:, t * P:(t + 1) * P], g.ident)
                            last.then_inc(m.turned, 1)
                        e.wait_ge(m.pT_kept, R * TPB * b + r * TPB + TPB)
                        for t in range(KT):
                            last = e.matmul(ops[:, 0:T], kt[r][:, t, :], pT[:, t, :], start=t == 0, stop=t == KT - 1)
                        last.then_inc(m.o_ready, 1)

        activation_scales(nc, g, "l1s_fused", [top[:, 0:B + 1]], [scales(FUSED)])

        with ExitStack() as ctx:
            s = Scope(nc, ctx, "l1a_f1")
            sc = s.sb("out_scale", [P, 1])
            shift_a = s.sb("shifted_avg", [P, B])
            qa = s.sb("q_avg", [P, B], BF16)
            shift = [s.sb(f"shifted{i}", [P, T]) for i in range(2)]
            qx = [s.sb(f"qx{i}", [P, T], BF16) for i in range(2)]
            aps = s.ps("avg")
            hps = [s.ps(f"h{i}", (P, 2 * 512)) for i in range(2)]
            U = 2
            m = s.sems(["scale_ready", "avg_shifted", "avg_quantised", "avg_projected", "bias_ready", "shifted",
                        "quantised", "h_ready", "h_kept", "top_ready"])
            block = s.block()

            @block.scalar
            def _(e):
                e.activation(shift_a[:, :], avg[:, :], ACT.Identity, scale=inverse[:, FUSED:FUSED + 1], bias=g.magic[:, :]).then_inc(m.avg_shifted, 1)
                e.wait_ge(m.bias_ready, FT)
                with e.Fori(0, B // U) as u:
                    for p in range(U):
                        e.wait_ge(m.quantised, U * u)
                        e.activation(shift[p][:, :], zT[:, bass.ds((U * u + p) * T, T)], ACT.Identity,
                                     scale=inverse[:, FUSED:FUSED + 1], bias=g.magic[:, :]).then_inc(m.shifted, 1)
                    for p in range(U):
                        for k in range(FT):
                            e.wait_ge(m.h_ready, U * u + p + 1)
                            e.activation(hid[:, k, bass.ds((U * u + p) * T, T)], hps[p][:, k * T:(k + 1) * T], ACT.Relu,
                                         scale=sc[:, :], bias=f1_bias[:, k, bass.ds(U * u + p, 1)]).then_inc(m.h_kept, 1)

            @block.vector
            def _(e):
                e.tensor_tensor(sc[:, :], step[:, FUSED:FUSED + 1], w("f1"), ALU.mult).then_inc(m.scale_ready, 1)
                e.wait_ge(m.avg_shifted, 1)
                e.tensor_scalar(qa[:, :], shift_a[:, :], MAGIC, None, ALU.subtract).then_inc(m.avg_quantised, 1)
                e.wait_ge(m.avg_projected, 1)
                e.wait_ge(m.scale_ready, 1)
                for k in range(FT):
                    e.tensor_scalar(f1_bias[:, k, :], aps[:, k * B:(k + 1) * B], sc[:, :], g.l1_bf1[:, k:k + 1], ALU.mult,
                                    ALU.add).then_inc(m.bias_ready, 1)
                with e.Fori(0, B // U) as u:
                    for p in range(U):
                        e.wait_ge(m.shifted, U * u + p + 1)
                        e.wait_ge(m.h_ready, U * u)
                        e.tensor_scalar(qx[p][:, :], shift[p][:, :], MAGIC, None, ALU.subtract).then_inc(m.quantised, 1)
                    for p in range(U):
                        e.wait_ge(m.h_kept, FT * (U * u + p + 1))
                        e.tensor_reduce(top[:, bass.ds(U * u + p, 1)], hid[:, :, bass.ds((U * u + p) * T, T)], AX.XY,
                                        ALU.max).then_inc(m.top_ready, 1)

            @block.tensor
            def _(e):
                e.wait_ge(m.avg_quantised, 1)
                for k in range(FT):
                    last = e.matmul(aps[:, k * B:(k + 1) * B], q["f1"][:, 1, k * P:(k + 1) * P], qa[:, :], start=True, stop=True)
                last.then_inc(m.avg_projected, 1)
                with e.Fori(0, B // U) as u:
                    for p in range(U):
                        e.wait_ge(m.quantised, U * u + p + 1)
                        e.wait_ge(m.h_kept, FT * U * u)
                        for k in range(FT):
                            last = e.matmul(hps[p][:, k * T:(k + 1) * T], q["f1"][:, 0, k * P:(k + 1) * P], qx[p][:, :], start=True, stop=True)
                        last.then_inc(m.h_ready, 1)

        activation_scales(nc, g, "l1s_hid", [top[:, 0:B]], [scales(HID)])

        with ExitStack() as ctx:
            s = Scope(nc, ctx, "l1a_f2")
            sc = s.sb("out_scale", [P, 1])
            shift = [s.sb(f"shifted{i}", [P, FT, T]) for i in range(2)]
            qx = [s.sb(f"qx{i}", [P, FT, T], BF16) for i in range(2)]
            yps = [s.ps(f"y{i}") for i in range(2)]
            U = 2
            m = s.sems(["scale_ready", "shifted", "quantised", "y_ready", "x_biased", "x_updated"])
            block = s.block()

            @block.scalar
            def _(e):
                with e.Fori(0, B // U) as u:
                    for p in range(U):
                        e.wait_ge(m.quantised, U * u)
                        e.activation(shift[p][:, :, :], hid[:, :, bass.ds((U * u + p) * T, T)], ACT.Identity,
                                     scale=inverse[:, HID:HID + 1], bias=g.magic[:, :]).then_inc(m.shifted, 1)

            @block.vector
            def _(e):
                e.tensor_tensor(sc[:, :], step[:, HID:HID + 1], w("f2"), ALU.mult).then_inc(m.scale_ready, 1)
                e.wait_ge(m.scale_ready, 1)
                with e.Fori(0, B // U) as u:
                    for p in range(U):
                        e.wait_ge(m.shifted, U * u + p + 1)
                        e.wait_ge(m.y_ready, U * u)
                        e.tensor_scalar(qx[p][:, :, :], shift[p][:, :, :], MAGIC, None, ALU.subtract).then_inc(m.quantised, 1)
                        xs = g.x[:, bass.ds(TPB * (U * u + p), TPB), :]
                        e.tensor_tensor(xs, xs, bcast(g.l1_bf2[:, :].unsqueeze(1), [P, TPB, D]), ALU.add).then_inc(m.x_biased, 1)
                    for p in range(U):
                        e.wait_ge(m.y_ready, U * u + p + 1)
                        e.wait_ge(m.x_biased, U * u + p + 1)
                        xs = g.x[:, bass.ds(TPB * (U * u + p), TPB), :]
                        e.scalar_tensor_tensor(out=xs, in0=yps[p][:, 0:T].rearrange("p (i d) -> p i d", d=D), scalar=sc[:, :],
                                               in1=xs, op0=ALU.mult, op1=ALU.add).then_inc(m.x_updated, 1)

            @block.tensor
            def _(e):
                with e.Fori(0, B // U) as u:
                    for p in range(U):
                        e.wait_ge(m.quantised, U * u + p + 1)
                        e.wait_ge(m.x_updated, U * u)
                        for i in range(TPB):
                            for k in range(FT):
                                last = e.matmul(yps[p][:, i * P:(i + 1) * P], qx[p][:, k, i * P:(i + 1) * P], q["f2"][:, k, :],
                                                start=k == 0, stop=k == FT - 1)
                        last.then_inc(m.y_ready, 1)



def weights_stage(nc, g, a):
    with ExitStack() as ctx:
        s = Scope(nc, ctx, "weights")
        ps = [s.ps(f"turned{i}") for i in range(2)]
        turned = s.sem("turned")
        kept = s.sem("kept")
        block = s.block()

        @block.tensor
        def _(e):
            e.wait_ge(g.weights_loaded, 16 * len(g.loads))
            for n, (dst, src) in enumerate(g.to_turn):
                if n >= 2:
                    e.wait_ge(kept, n - 1)
                rows, cols = src.shape
                e.transpose(ps[n % 2][0:cols, 0:rows], src, g.ident[0:rows, 0:rows]).then_inc(turned, 1)

        @block.scalar
        def _(e):
            for n, (dst, src) in enumerate(g.to_turn):
                rows, cols = src.shape
                e.wait_ge(turned, n + 1)
                e.activation(dst, ps[n % 2][0:cols, 0:rows], ACT.Copy).then_inc(kept, 1)
            e.wait_ge(kept, len(g.to_turn))


def store_stage(nc, g, a):
    with ExitStack() as ctx:
        s = Scope(nc, ctx, "store")
        stored = s.sem("stored")
        block = s.block()

        @block.sync
        def _(sp):
            sp.dma_start(a["out"].rearrange("b (i p) d -> p (b i) d", p=P), g.x[:, :, :]).then_inc(stored, 16)
            sp.wait_ge(stored, 16)


STAGES = [l0_attention, l0_ffn, l1_attention, l1_ffn, l2_attention, l2_ffn, l3_attention, l3_ffn]


def build(nc, a, stages=None):
    with ExitStack() as ctx:
        g = Shared()

        def keep(name, shape, dtype=F32):
            return ctx.enter_context(nc.sbuf_tensor(name, shape, dtype))

        def loaded(name, shape, src, first=False):
            t = keep("w_" + name, shape)
            (g.loads_first if first else g.loads).append((t[tuple(slice(None) for _ in shape)], src))
            return t

        g.loads_first, g.loads, g.to_turn = [], [], []
        g.const = keep("const", [P, C_ALL])
        g.x = keep("x_tokens", [P, TILES, D])
        g.ctxT = keep("ctxT", [DC + 1, B * S])
        g.ctx_rows = keep("ctx_rows", [P, B * KT, DC])
        g.ones = keep("ones", [P, P])
        g.neg_half = keep("neg_half", [P, TILES])
        g.magic = keep("magic", [P, 1])
        g.ident = g.const[:, C_ID:C_ID + P]
        g.vector_rows = keep("vector_rows", [P, P])
        g.vectors = keep("vectors", [P, P])
        g.vectors_used = 0
        g.weights_loaded = ctx.enter_context(nc.semaphore("weights_loaded"))

        def row(v):
            return a[v].unsqueeze(0)

        def rows(v):
            return a[v].unsqueeze(0).to_broadcast([P, a[v].shape[0]])

        def columns(*sources):
            first = g.vectors_used
            for src, at in sources:
                n, width = src.shape
                g.loads_first.append((g.vector_rows[first:first + n, at:at + width], src))
            g.vectors_used = first + n
            return g.vectors[:, first:first + n]

        def transposed(name, w):
            rows, cols = a[w].shape
            raw = loaded(name + "_raw", [rows, cols], a[w])
            t = keep("w_" + name, [cols, rows])
            g.to_turn.append((t[:, :], raw[:, :]))
            return t

        def biased(name, w, bias, width):
            t = keep("w_" + name, [DC + 1, width])
            g.loads_first.append((t[0:DC, :], a[w]))
            if bias is not None:
                g.loads_first.append((t[DC:DC + 1, :], row(bias)))
            return t

        g.l0_wk = biased("l0_wk", "L0_xattn_Wk", "L0_xattn_bk", D)
        g.l0_wv = biased("l0_wv", "L0_xattn_Wv", "L0_xattn_bv", D)
        g.l0_wq = loaded("l0_wq", [D, D], a["L0_xattn_Wq"], True)
        g.l0_bq = loaded("l0_bq", [1, D], row("L0_xattn_bq"), True)
        g.l0_wo = loaded("l0_wo", [D, D], a["L0_xattn_Wo"], True)
        g.l0_bo = loaded("l0_bo", [1, D], row("L0_xattn_bo"), True)
        g.l0_gamma = loaded("l0_gamma", [P, D], rows("L0_xattn_ln_gamma"), True)
        g.l0_beta = loaded("l0_beta", [P, D], rows("L0_xattn_ln_beta"), True)

        g.l0_lng = columns((row("L0_ffn_ln_g"), 0))
        g.l0_lnb = columns((row("L0_ffn_ln_b"), 0))
        g.l0_rw = loaded("l0_rw", [D, E], a["L0_ffn_rW"])
        g.l0_rb = loaded("l0_rb", [1, E], row("L0_ffn_rb"))
        g.l0_w1 = loaded("l0_w1", [D, E, 256], a["L0_ffn_W1"].rearrange("e d f -> d e f"))
        g.l0_b1 = columns((a["L0_ffn_b1"].rearrange("e (f p) -> (e f) p", p=P), 0))
        g.l0_w2 = loaded("l0_w2", [P, E, 2, D], a["L0_ffn_W2"].rearrange("e (f p) d -> p e f d", p=P))
        g.l0_b2 = loaded("l0_b2", [E, D], a["L0_ffn_b2"])

        for l, heads in (("2", 8), ("3", 16)):
            w = heads * 64
            wq = loaded(f"l{l}_wq", [D, w], a[f"L{l}_xattn_Wq"])
            wk = loaded(f"l{l}_wk", [DC, w], a[f"L{l}_xattn_Wk"])
            wv = loaded(f"l{l}_wv", [DC, w], a[f"L{l}_xattn_Wv"])
            wo = loaded(f"l{l}_wo", [P, heads // 2, D], a[f"L{l}_xattn_Wo"].rearrange("(c p) d -> p c d", p=P))
            bo = loaded(f"l{l}_bo", [1, D], row(f"L{l}_xattn_bo"))
            if l == "2":
                g.l2_wq, g.l2_wk, g.l2_wv, g.l2_wo, g.l2_bo = wq, wk, wv, wo, bo
            else:
                g.l3_wq, g.l3_wk, g.l3_wv, g.l3_wo, g.l3_bo = wq, wk, wv, wo, bo

        g.l1_lng = columns((row("L1_ffn_ln_g"), 0))
        g.l1_lnb = columns((row("L1_ffn_ln_b"), 0))
        g.l1_attn_b = columns((row("L1_ffn_attn_b"), 0))
        g.l1_b1 = columns((a["L1_ffn_b1"].rearrange("e (f p) -> (e f) p", p=P), 0))
        g.l1_b2 = columns((a["L1_ffn_b2"], 0))
        g.l1_attn_w = loaded("l1_attn_w", [D, D], a["L1_ffn_attn_w"])
        g.l1_next_w = loaded("l1_next_w", [D, D], a["L1_ffn_next_w"])
        g.l1_next_b = loaded("l1_next_b", [1, D], row("L1_ffn_next_b"))

        g.l2_wqT = transposed("l2_wqT", "L2_ffn_W_Q")
        g.l2_wkT = transposed("l2_wkT", "L2_ffn_W_K")
        g.l2_woT = transposed("l2_woT", "L2_ffn_W_O")
        g.l2_winvT = transposed("l2_winvT", "L2_ffn_W_inv")
        g.l2_rw1T = transposed("l2_rw1T", "L2_ffn_router_w1")
        g.l2_rw2T = transposed("l2_rw2T", "L2_ffn_router_w2")
        g.l2_rb1 = columns((row("L2_ffn_router_b1"), 0))
        g.l2_rb2 = loaded("l2_rb2", [1, E], row("L2_ffn_router_b2"))
        g.l2_eb = loaded("l2_eb", [1, E], row("L2_ffn_expert_bias"))
        g.l2_alpha = loaded("l2_alpha", [P, 1], a["L2_ffn_alpha_bi"].unsqueeze(0).to_broadcast([P, 1]))
        g.l2_v = [loaded(f"l2_v{i}", [D, E, 64], a[w].rearrange("k d r -> d k r")) for i, w in
                  enumerate(("L2_ffn_V_fwd", "L2_ffn_W_inv_exp"))]
        g.l2_w = [loaded(f"l2_w{i}", [D, E, 64], a[w].rearrange("k d r -> d k r")) for i, w in
                  enumerate(("L2_ffn_W_fwd", "L2_ffn_V_inv"))]
        g.l2_uT = []
        for i, w in enumerate(("L2_ffn_U_fwd", "L2_ffn_U_inv")):
            raw = loaded(f"l2_u{i}", [D, E, 64], a[w].rearrange("k d r -> d k r"))
            uT = keep(f"l2_uT{i}", [P, 4, D])
            for c in range(4):
                g.to_turn.append((uT[:, c, :], raw[:, 2 * c:2 * c + 2, :].rearrange("p k r -> p (k r)")))
            g.l2_uT.append(uT)
        g.l2_b = [loaded(f"l2_b{i}", [E, D], a[w]) for i, w in enumerate(("L2_ffn_b_fwd", "L2_ffn_b_inv"))]

        g.l3_wr = loaded("l3_wr", [D, E], a["L3_ffn_Wr"])
        g.l3_br = loaded("l3_br", [1, E], row("L3_ffn_br"))

        g.l1_bd2v = columns((row("L1_xattn_b_d2v"), 0))
        g.l1_bimg = columns((row("L1_xattn_b_img"), 0))
        g.l1_btxt = columns((row("L1_xattn_b_txt"), 0))
        g.l1_batt = [columns((row(f"L1_xattn_b_att{i}"), 0), (row(f"L1_xattn_b_att{i}"), D // 2)) for i in range(2)]
        g.l1_batt_rows = []
        for i in range(2):
            t = keep(f"w_l1_batt_rows{i}", [P, D])
            for half in range(2):
                g.loads.append((t[:, half * D // 2:(half + 1) * D // 2], rows(f"L1_xattn_b_att{i}")))
            g.l1_batt_rows.append(t)
        g.l1_bf1 = columns((a["L1_xattn_b_f1"].rearrange("(f p) -> f p", p=P), 0))
        g.l1_bf2 = loaded("l1_bf2", [P, D], rows("L1_xattn_b_f2"))
        load_stage(nc, g, a)
        weights_stage(nc, g, a)
        for stage in (STAGES if stages is None else stages):
            stage(nc, g, a)
            clear_semaphores(nc)
        store_stage(nc, g, a)


def kernel(**inputs):
    import concourse.bacc as bacc
    from concourse.bass_utils import run_bass_kernel_spmd

    nc = bacc.Bacc("TRN2", target_bir_lowering=False, num_devices=1)
    arrays, args = {}, {}
    for name, value in {**inputs, "constants": shape_constants()}.items():
        v = np.ascontiguousarray(value)
        v = v.reshape(v.shape or (1,))
        arrays["in_" + name] = v
        args[name] = nc.dram_tensor("in_" + name, v.shape, mybir.dt.from_np(v.dtype), kind="ExternalInput").ap()
    args["out"] = nc.dram_tensor("out_x", (B, T, D), F32, kind="ExternalOutput").ap()
    build(nc, args)
    return run_bass_kernel_spmd(nc, [arrays], core_ids=[0]).results[0]["out_x"]
```

```python
from collections import namedtuple
from contextlib import ExitStack

import concourse.bass as bass
import numpy as np
from concourse import mybir

F32 = mybir.dt.float32
F32R = mybir.dt.float32r
BF16 = mybir.dt.bfloat16
I32 = mybir.dt.int32
ALU = mybir.AluOpType
ACT = mybir.ActivationFunctionType
AX = mybir.AxisListType

P = 128
B, T, D = 8, 256, 128
S, DC = 512, 96
N = B * T
TILES = N // P
TPB = T // P
KT = S // P
EPS = 1e-5
E = 8
MAGIC = 12582912.0

C_ID = 0
C_HEAD = C_ID + P
C_REV = C_HEAD + 16
C_INVN = C_REV + E
C_SEL = C_INVN + TPB
C_ALL = C_SEL + 4 * P



def shape_constants():
    c = np.zeros((P, C_ALL), np.float32)
    c[:, C_ID:C_ID + P] = np.eye(P)
    for p in range(P):
        c[p, C_HEAD + p // 8] = 1
        for i in range(TPB):
            c[p, C_INVN + i] = 1.0 / (i * P + p + 1)
    c[:, C_REV:C_REV + E] = E - np.arange(E)
    for k in range(E):
        lo = C_SEL + (k // 2) * P + (k % 2) * 64
        c[k, lo:lo + 64] = c[32 + k, lo:lo + 64] = 1
    return c


class Steps:

    def __init__(self, engine, sem, per_turn=0):
        self.engine, self.sem, self.per_turn = engine, sem, per_turn
        self.turn, self.done = 0, 0

    def begin(self, turn):
        self.turn, self.done = turn, 0

    def add(self, instruction):
        instruction.then_inc(self.sem, 1)
        self.done += 1

    def settle(self):
        self.engine.wait_ge(self.sem, self.turn * self.per_turn + self.done)

    def end(self):
        assert self.done == self.per_turn, (self.done, self.per_turn)


class Scope:

    to_clear = []

    def __init__(self, nc, ctx, name):
        self.nc, self.ctx, self.name = nc, ctx, name

    def sb(self, name, shape, dtype=F32):
        return self.ctx.enter_context(self.nc.sbuf_tensor(f"{self.name}_{name}", shape, dtype))

    def ps(self, name, shape=(P, 512), dtype=F32):
        return self.ctx.enter_context(self.nc.psum_tensor(f"{self.name}_{name}_ps", list(shape), dtype))

    def sem(self, name):
        sem = self.ctx.enter_context(self.nc.semaphore(f"{self.name}_{name}"))
        Scope.to_clear.append(sem.num)
        return sem

    def sems(self, names):
        return namedtuple("Semaphores", names)(*[self.sem(n) for n in names])

    def block(self):
        return self.ctx.enter_context(self.nc.Block())


def clear_semaphores(nc):
    nums = sorted(set(Scope.to_clear))
    Scope.to_clear.clear()
    runs = []
    for n in nums:
        if runs and runs[-1][1] == n:
            runs[-1][1] = n + 1
        else:
            runs.append([n, n + 1])
    with nc.Block() as block:
        @block.gpsimd
        def _(e):
            for first, end in runs:
                e.sem_clear(range(first, end))


def wait(e, sem, count):
    if not isinstance(count, int) or count > 0:
        e.wait_ge(sem, count)


def first_and_rest(e, count, turn):
    turn(0)
    with e.Fori(1, count) as n:
        turn(n)


class Shared:
    pass


def bcast(ap, shape):
    return ap.to_broadcast(shape)



class Front:

    def __init__(self, s, g, tile=None, tiles=TPB, twice=False):
        self.g, self.tiles, self.twice = g, tiles, twice
        self.tile = tile or (lambda b, i: g.x[:, TPB * b + i, :])
        norms = 2 if twice else 1
        self.steps = 2 * tiles * norms
        self.stats = s.sb("ln_stats", [P, tiles, 6])
        self.mv = s.sb("ln_mean_var", [P, tiles, 2])
        self.held = s.sb("ln_held", [P, 1])
        self.var = s.sb("ln_var_eps", [P, tiles])
        self.rstd = s.sb("ln_rstd", [P, tiles])
        self.outer = s.sb("ln_outer", [P, tiles, D]) if twice else None
        self.z = s.sb("ln_z", [P, tiles, D])
        self.norms = norms
        self.var_ready = s.sem("var_ready")
        self.rstd_ready = s.sem("rstd_ready")
        self.outer_ready = s.sem("outer_ready") if twice else None
        self.z_ready = s.sem("z_ready")
        self.z_turned = s.sem("z_turned")

    def _norm(self, e, b, steps, turn, source, out, ready):
        for i in range(self.tiles):
            steps.add(e.bn_stats(self.stats[:, i, :], source(i)))
        steps.settle()
        e.memset(self.held[:, :], 0.0)
        for i in range(self.tiles):
            steps.add(e.bn_aggr(self.mv[:, i, :], self.stats[:, i, :]))
        steps.settle()
        e.tensor_scalar(self.var[:, :], self.mv[:, :, 1], EPS, None, ALU.add).then_inc(self.var_ready, 1)
        e.wait_ge(self.rstd_ready, self.norms * b + turn + 1)
        for i in range(self.tiles):
            e.tensor_scalar(out[:, i, :], source(i), self.mv[:, i, 0:1], self.rstd[:, i:i + 1],
                            ALU.subtract, ALU.mult).then_inc(ready, 1)

    def vector(self, e, b, steps):
        if self.twice:
            self._norm(e, b, steps, 0, lambda i: self.tile(b, i), self.outer, self.outer_ready)
            e.wait_ge(self.outer_ready, self.tiles * (b + 1))
            self._norm(e, b, steps, 1, lambda i: self.outer[:, i, :], self.z, self.z_ready)
        else:
            self._norm(e, b, steps, 0, lambda i: self.tile(b, i), self.z, self.z_ready)

    def gpsimd(self, e, b):
        for n in range(self.norms):
            e.wait_ge(self.var_ready, self.norms * b + n + 1)
            e.tensor_tensor(self.rstd[:, :], self.var[:, :], self.g.neg_half[:, 0:self.tiles],
                            ALU.pow).then_inc(self.rstd_ready, 1)

    def tensor(self, e, b, out):
        e.wait_ge(self.z_ready, self.tiles * (b + 1))
        for i in range(self.tiles):
            last = e.transpose(out[:, i * P:(i + 1) * P], self.z[:, i, :], self.g.ident)
        last.then_inc(self.z_turned, 1)



class AllTiles:

    HALVES = 2
    HT = TILES // HALVES
    BANK = 4
    BANKS = TILES // BANK

    def __init__(self, s, g, order=range(TILES), twice=False):
        self.g, self.order, self.norms = g, list(order), 2 if twice else 1
        self.stats = s.sb("all_stats", [P, TILES, 6])
        self.mv = s.sb("all_mean_var", [P, TILES, 2])
        self.var = s.sb("all_var_eps", [P, TILES])
        self.rstd = s.sb("all_rstd", [P, TILES])
        self.outer = s.sb("all_outer", [P, TILES, D]) if twice else None
        self.z = s.sb("all_z", [P, TILES, D])
        self.stats_ready = s.sem("all_stats_ready")
        self.var_ready = s.sem("all_var_ready")
        self.rstd_ready = s.sem("all_rstd_ready")
        self.outer_ready = s.sem("all_outer_ready")
        self.z_ready = s.sem("all_z_ready")
        self.z_turned = s.sem("all_z_turned")

    def vector(self, e):
        done = 0

        def half_of(half):
            return range(half * self.HT, (half + 1) * self.HT)

        def source(norm, i):
            return self.outer[:, i, :] if norm else self.g.x[:, self.order[i], :]

        def statistics(norm, half):
            nonlocal done
            first = done
            for i in half_of(half):
                if norm:
                    e.wait_ge(self.outer_ready, i + 1)
                e.bn_stats(self.stats[:, i, :], source(norm, i)).then_inc(self.stats_ready, 1)
            for n, i in enumerate(half_of(half)):
                e.wait_ge(self.stats_ready, first + n + 1)
                if norm and n == 0:
                    e.wait_ge(self.rstd_ready, self.HALVES)
                e.bn_aggr(self.mv[:, i, :], self.stats[:, i, :]).then_inc(self.stats_ready, 1)
            done += 2 * self.HT
            e.wait_ge(self.stats_ready, done)
            h = half_of(half)
            e.tensor_scalar(self.var[:, h.start:h.stop], self.mv[:, h.start:h.stop, 1], EPS, None,
                            ALU.add).then_inc(self.var_ready, 1)

        def apply(norm, half):
            out, ready = (self.outer, self.outer_ready) if norm + 1 < self.norms else (self.z, self.z_ready)
            e.wait_ge(self.rstd_ready, self.HALVES * norm + half + 1)
            for i in half_of(half):
                e.tensor_scalar(out[:, i, :], source(norm, i), self.mv[:, i, 0:1], self.rstd[:, i:i + 1],
                                ALU.subtract, ALU.mult).then_inc(ready, 1)

        statistics(0, 0)
        statistics(0, 1)
        apply(0, 0)
        if self.norms == 1:
            apply(0, 1)
        else:
            apply(0, 1)
            statistics(1, 0)
            statistics(1, 1)
            apply(1, 0)
            apply(1, 1)

    def gpsimd(self, e):
        for n in range(self.HALVES * self.norms):
            tiles = slice(n % self.HALVES * self.HT, (n % self.HALVES + 1) * self.HT)
            if n >= self.HALVES:
                e.wait_ge(self.outer_ready, TILES)
            e.wait_ge(self.var_ready, n + 1)
            e.tensor_tensor(self.rstd[:, tiles], self.var[:, tiles], self.g.neg_half[:, tiles],
                            ALU.pow).then_inc(self.rstd_ready, 1)

    def tensor(self, e, n, out):
        e.wait_ge(self.z_ready, self.BANK * (n + 1))
        for i in range(self.BANK):
            last = e.transpose(out[:, i * P:(i + 1) * P], self.z[:, self.BANK * n + i, :], self.g.ident)
        last.then_inc(self.z_turned, 1)



def load_stage(nc, g, a):
    with ExitStack() as ctx:
        s = Scope(nc, ctx, "load")
        rows = g.ctx_rows
        turned = [s.ps(f"turned{i}") for i in range(2)]
        ctx_loaded = s.sem("ctx_loaded")
        const_loaded = s.sem("const_loaded")
        ctx_turned = s.sem("ctx_turned")
        ctx_kept = s.sem("ctx_kept")
        filled = s.sem("filled")
        block = s.block()

        @block.sync
        def _(sp):
            sp.dma_start(g.const[:, :], a["constants"]).then_inc(const_loaded, 16)
            sp.dma_start(rows[:, :, :].rearrange("p (b t) d -> p b (t d)", t=KT),
                         a["ctx_768"].rearrange("b (p t) d -> p b (t d)", t=KT)).then_inc(ctx_loaded, 16)
            sp.dma_start(g.x[:, :, :], a["x"].rearrange("b (i p) d -> p (b i) d", p=P)).then_inc(const_loaded, 16)
            for dst, src in g.loads_first:
                sp.dma_start(dst, src).then_inc(const_loaded, 16)
            sp.wait_ge(const_loaded, 16 * (2 + len(g.loads_first)))

        @block.gpsimd
        def _(e):
            e.memset(g.neg_half[:, :], -0.5).then_inc(filled, 1)
            e.memset(g.ones[:, :], 1.0).then_inc(filled, 1)
            e.memset(g.magic[:, :], MAGIC).then_inc(filled, 1)
            e.wait_ge(filled, 3)
            e.memset(g.ctxT[DC:DC + 1, :], 1.0).then_inc(filled, 1)
            e.wait_ge(filled, 4)

        @block.tensor
        def _(e):
            e.wait_ge(const_loaded, 16 * (2 + len(g.loads_first)))
            e.wait_ge(ctx_loaded, 16)
            for b in range(B):
                if b >= 2:
                    e.wait_ge(ctx_kept, b - 1)
                for t in range(KT):
                    last = e.transpose(turned[b % 2][0:DC, t * P:(t + 1) * P], rows[:, KT * b + t, :], g.ident)
                last.then_inc(ctx_turned, 1)
            e.wait_ge(ctx_kept, B - 1)
            e.transpose(turned[0][:, 0:g.vectors_used], g.vector_rows[0:g.vectors_used, :],
                        g.ident[0:g.vectors_used, 0:g.vectors_used]).then_inc(ctx_turned, 1)

        @block.scalar
        def _(e):
            for b in range(B):
                e.wait_ge(ctx_turned, b + 1)
                e.activation(g.ctxT[0:DC, b * S:(b + 1) * S], turned[b % 2][0:DC, :], ACT.Copy).then_inc(ctx_kept, 1)
            e.wait_ge(ctx_turned, B + 1)
            e.activation(g.vectors[:, 0:g.vectors_used], turned[0][:, 0:g.vectors_used], ACT.Copy).then_inc(ctx_kept, 1)
            e.wait_ge(ctx_kept, B + 1)



def l0_attention(nc, g, a):
    HEADS, HD = 16, 8
    GROUPS, GH = 4, 4
    STEPS = GROUPS * KT
    STACK = 4 * D
    with ExitStack() as ctx:
        s = Scope(nc, ctx, "l0a")
        front = Front(s, g)
        ident = s.sb("ident", [P, P], F32R)
        zero = s.sb("zero", [P, GH * T])
        zT = s.sb("zT", [P, T])
        cT = s.sb("cT", [DC + 1, S])
        square = s.sb("square", [P, KT + TPB, D])
        ksum = s.sb("k_sumsq", [P, KT])
        qsum = s.sb("q_sumsq", [P, TPB])
        kclamped = s.sb("k_clamped", [P, KT])
        qclamped = s.sb("q_clamped", [P, TPB])
        kscale_next = s.sb("k_scale_next", [P, KT])
        kscale = s.sb("k_scale", [P, KT])
        qnorm = s.sb("q_norm", [P, TPB])
        k_rows = s.sb("k_rows", [P, KT, D])
        v_rows = s.sb("v_rows", [P, KT, D])
        qp = s.sb("qp", [P, TILES, D])
        qn = s.sb("qn", [P, TPB, D])
        kst = s.sb("k_stacked", [P, KT, STACK], F32R)
        qst = s.sb("q_stacked", [P, TPB, STACK], F32R)
        kS = s.sb("kS", [P, GROUPS, S], F32R)
        qS = s.sb("qS", [P, GROUPS, GH, T], F32R)
        v = s.sb("v", [P, KT, HEADS, 32])
        prob = [s.sb(f"prob{i}", [P, GH * T]) for i in range(2)]
        pv = s.sb("pv", [P, T])
        rsum = s.sb("rsum", [P, TPB, GH])
        o = s.sb("o", [P, TPB, D])
        oT = s.sb("oT", [P, T])
        y = s.sb("y", [P, TPB, D])
        stats = s.sb("y_stats", [P, TPB, 6])
        mv = s.sb("y_mean_var", [P, TPB, 2])
        yvar = s.sb("y_var", [P, TPB])
        yrstd = s.sb("y_rstd", [P, TPB])
        sc = [s.ps(f"scores{i}", (P, 2 * 512)) for i in range(2)]
        pvps = [s.ps(f"pv{i}") for i in range(2)]
        work = [s.ps(f"work{i}") for i in range(2)]

        names = ["filled", "v_padded", "zeroed", "c_fixed", "zT_ready", "k_projected", "v_projected", "q_projected",
                 "k_kept", "v_kept", "qp_ready", "k_squared", "q_squared", "k_clamped", "q_clamped",
                 "k_scale_next", "k_scale_ready", "q_norm_ready", "k_hi_ready", "k_lo_ready", "qn_ready", "q_hi_ready",
                 "q_lo_ready", "k_turned", "q_turned", "kS_ready", "qS_ready_dve", "qS_ready_act", "v_low_ready",
                 "v_high_ready", "scores_ready", "prob_ready", "pv_ready", "pv_kept", "pv_turned", "rsum_ready",
                 "o_ready", "o_turned", "oT_ready", "out_ready", "y_kept", "y_stats", "yvar_ready", "yrstd_ready", "y_ready",
                 "x_updated", "steps"]
        m = s.sems(names)
        block = s.block()

        @block.sync
        def _(sp):
            load_weights(g, sp)

        def stacked(ap, first, step):
            parts = ap.rearrange("p t (h k d) -> p (t h) k d", k=4, d=HD)
            return parts[:, :, first:first + step + 1:step, :]

        def repeated(ap):
            x = ap.rearrange("p t (h d) -> p (t h) d", d=HD)
            return bcast(x.unsqueeze(2), [P, x.shape[1], 2, HD])

        def turns(e, turn):
            turn(0)
            with e.Fori(1, B - 2) as b:
                turn(b)
            turn(B - 2)
            turn(B - 1)

        def parts(b):
            if isinstance(b, int):
                return b > 0, b + 1 < B, b + 2 < B
            return True, True, True

        @block.gpsimd
        def _(e):
            def fix_c(b):
                wait(e, m.v_projected, b)
                e.tensor_copy(cT[:, :], g.ctxT[:, bass.ds(b * S, S)]).then_inc(m.c_fixed, 1)

            def keep_v(b, low):
                done = 12 if low else 16
                wait(e, m.pv_ready, STEPS * (b - 1) + done)
                e.wait_ge(m.v_kept, b + 1)
                h = slice(0, 12) if low else slice(12, 16)
                rows = v_rows[:, :, :].rearrange("p t (h d) -> p t h d", d=HD)[:, :, h, :]
                ones = bcast(g.ones[:, 0:1].unsqueeze(2).unsqueeze(3), list(rows.shape))
                e.tensor_tensor(v[:, :, h, 0:HD], rows, ones, ALU.mult).then_inc(m.v_low_ready if low else m.v_high_ready, 1)

            def k_low(b):
                e.wait_ge(m.k_hi_ready, b + 1)
                e.tensor_tensor(stacked(kst[:, :, :], 1, 2), repeated(k_rows[:, :, :]), stacked(kst[:, :, :], 0, 2),
                                ALU.subtract).then_inc(m.k_lo_ready, 1)

            def k_scales(b):
                e.wait_ge(m.k_clamped, b + 1)
                e.tensor_tensor(kscale_next[:, :], kclamped[:, :], g.neg_half[:, 0:KT], ALU.pow).then_inc(m.k_scale_next, 1)

            def q_norms(b):
                e.wait_ge(m.q_clamped, b + 1)
                e.tensor_tensor(qnorm[:, :], qclamped[:, :], g.neg_half[:, 0:TPB], ALU.pow).then_inc(m.q_norm_ready, 1)

            def finish(b):
                e.wait_ge(m.yvar_ready, b + 1)
                e.tensor_tensor(yrstd[:, :], yvar[:, :], g.neg_half[:, 0:TPB], ALU.pow).then_inc(m.yrstd_ready, 1)

            def update(b):
                per_batch = lambda ap: bcast(ap.unsqueeze(1), [P, TPB, D])
                xs = g.x[:, bass.ds(TPB * b, TPB), :]
                e.wait_ge(m.y_ready, TPB * b + TPB)
                e.tensor_tensor(y[:, :, :], y[:, :, :], per_batch(g.l0_gamma[:, :]), ALU.mult).then_inc(m.x_updated, 1)
                e.wait_ge(m.x_updated, 3 * b + 1)
                e.tensor_tensor(y[:, :, :], y[:, :, :], per_batch(g.l0_beta[:, :]), ALU.add).then_inc(m.x_updated, 1)
                e.wait_ge(m.x_updated, 3 * b + 2)
                e.tensor_tensor(xs, xs, y[:, :, :], ALU.add).then_inc(m.x_updated, 1)

            def turn(b):
                before, after, after_that = parts(b)
                if before:
                    keep_v(b, False)
                if after:
                    front.gpsimd(e, b + 1)
                    if after_that:
                        fix_c(b + 2)
                    k_low(b + 1)
                if before:
                    finish(b - 1)
                if after:
                    k_scales(b + 1)
                if before:
                    update(b - 1)
                if after:
                    q_norms(b + 1)
                    keep_v(b + 1, True)

            e.memset(zero[:, :], 0.0).then_inc(m.filled, 1)
            e.memset(v[:, :, :, :], 0.0).then_inc(m.v_padded, 1)
            fix_c(0)
            front.gpsimd(e, 0)
            e.wait_ge(m.v_padded, 1)
            e.memset(v[:, :, :, HD:HD + 1], 1.0).then_inc(m.v_padded, 1)
            k_low(0)
            k_scales(0)
            q_norms(0)
            fix_c(1)
            keep_v(0, True)
            keep_v(0, False)
            turns(e, turn)
            finish(B - 1)
            update(B - 1)
            e.wait_ge(m.x_updated, 3 * B)

        @block.tensor
        def _(e):
            last_item = [None, None]

            def bank(n, kind, b, i=0):
                before = last_item[n % 2]
                if before is not None:
                    kept, c, j = before
                    for sem, count in {
                            "k": ((m.k_kept, c + 1),),
                            "v": ((m.v_kept, c + 1),),
                            "z": ((m.zT_ready, c + 1),),
                            "q": ((m.qp_ready, c + 1), (m.q_squared, TPB * c + TPB)),
                            "k_turned": ((m.kS_ready, GROUPS * c + j + 1),),
                            "q_turned": ((m.qS_ready_dve, 3 * (2 * c + j + 1)), (m.qS_ready_act, 2 * c + j + 1)),
                            "pv": ((m.o_ready, GROUPS * c + j + 1),),
                            "o": ((m.oT_ready, c + 1),),
                            "out": ((m.y_kept, c + 1),)}[kept]:
                        e.wait_ge(sem, count)
                last_item[n % 2] = (kind, b, i)
                return work[n % 2]

            def keys(n, b):
                w = bank(n, "k", b)
                e.wait_ge(m.c_fixed, b + 1)
                for t in range(KT):
                    last = e.matmul(w[:, t * P:(t + 1) * P], cT[:, t * P:(t + 1) * P], g.l0_wk[:, :], start=True, stop=True)
                last.then_inc(m.k_projected, 1)

            def values(n, b):
                w = bank(n, "v", b)
                for t in range(KT):
                    last = e.matmul(w[:, t * P:(t + 1) * P], cT[:, t * P:(t + 1) * P], g.l0_wv[:, :], start=True, stop=True)
                last.then_inc(m.v_projected, 1)

            def tokens(n, b):
                front.tensor(e, b, bank(n, "z", b))

            def queries(n, b):
                w = bank(n, "q", b)
                e.wait_ge(m.zT_ready, b + 1)
                for i in range(TPB):
                    e.matmul(w[:, i * P:(i + 1) * P], zT[:, i * P:(i + 1) * P], g.l0_wq[:, :], start=True, stop=False)
                    last = e.matmul(w[:, i * P:(i + 1) * P], g.ones[0:1, 0:P], g.l0_bq[:, :], start=False, stop=True)
                last.then_inc(m.q_projected, 1)

            def turn_keys(n, b, grp):
                w = bank(n, "k_turned", b, grp)
                if grp == 0:
                    e.wait_ge(m.k_lo_ready, b + 1)
                for t in range(KT):
                    last = e.transpose(w[:, t * P:(t + 1) * P].bitcast(F32R), kst[:, t, grp * P:(grp + 1) * P], ident[:, :])
                last.then_inc(m.k_turned, 1)

            def turn_queries(n, b, i):
                w = bank(n, "q_turned", b, i)
                if i == 0:
                    e.wait_ge(m.q_lo_ready, b + 1)
                for j in range(2):
                    for t in range(TPB):
                        last = e.transpose(w[:, j * T + t * P:j * T + (t + 1) * P].bitcast(F32R),
                                           qst[:, t, (2 * i + j) * P:(2 * i + j + 1) * P], ident[:, :])
                last.then_inc(m.q_turned, 1)

            def turn_pv(n, b, grp):
                w = bank(n, "pv", b, grp)
                e.wait_ge(m.pv_kept, GROUPS * b + grp + 1)
                for i in range(TPB):
                    last = e.transpose(w[:, i * P:(i + 1) * P], pv[:, i * P:(i + 1) * P], g.ident)
                last.then_inc(m.pv_turned, 1)

            def turn_o(n, b):
                w = bank(n, "o", b)
                e.wait_ge(m.o_ready, GROUPS * b + GROUPS)
                for i in range(TPB):
                    last = e.transpose(w[:, i * P:(i + 1) * P], o[:, i, :], g.ident)
                last.then_inc(m.o_turned, 1)

            def output(n, b):
                w = bank(n, "out", b)
                e.wait_ge(m.oT_ready, b + 1)
                for i in range(TPB):
                    e.matmul(w[:, i * P:(i + 1) * P], oT[:, i * P:(i + 1) * P], g.l0_wo[:, :], start=True, stop=False)
                    last = e.matmul(w[:, i * P:(i + 1) * P], g.ones[0:1, 0:P], g.l0_bo[:, :], start=False, stop=True)
                last.then_inc(m.out_ready, 1)

            def scores(b, n):
                grp, t = divmod(n, KT)
                wait(e, m.prob_ready, STEPS * b + n - 1)
                if t == 0:
                    e.wait_ge(m.kS_ready, GROUPS * b + grp + 1)
                    e.wait_ge(m.qS_ready_dve, 3 * (2 * b + grp // 2 + 1))
                    e.wait_ge(m.qS_ready_act, 2 * b + grp // 2 + 1)
                for half in range(2):
                    last = e.matmul(sc[n % 2][:, half * 512:half * 512 + 512], kS[:, grp, t * P:(t + 1) * P],
                                    qS[:, grp, 2 * half:2 * half + 2, :], start=True, stop=True)
                last.then_inc(m.scores_ready, 1)

            def weighted(b, n):
                grp, t = divmod(n % STEPS, KT)
                e.wait_ge(m.prob_ready, STEPS * b + n + 1)
                if n == 0:
                    e.wait_ge(m.v_low_ready, b + 1)
                if n == 12:
                    e.wait_ge(m.v_high_ready, b + 1)
                if t == 0:
                    wait(e, m.pv_kept, GROUPS * b + grp - 1)
                for j in range(GH):
                    last = e.matmul(pvps[grp % 2][32 * j:32 * j + 32, 0:T], v[:, t, GH * grp + j, :],
                                    prob[n % 2][:, j * T:(j + 1) * T], start=t == 0, stop=t == KT - 1,
                                    tile_position=(0, 32 * j))
                last.then_inc(m.pv_ready, 1)

            def turn(b):
                before, after, _ = parts(b)
                last_item[:] = [("k_turned", b, 3), ("q_turned", b, 1)]
                for n in range(STEPS):
                    if n + 1 < STEPS:
                        scores(b, n + 1)
                    elif after:
                        scores(b + 1, 0)
                    if n > 0 or before:
                        weighted(b, n - 1)
                    if before and n == 1:
                        turn_pv(n, b - 1, 3)
                    if before and n == 3:
                        turn_o(n, b - 1)
                    if before and n == 4:
                        output(n, b - 1)
                    if n in (6, 9, 13):
                        turn_pv(n, b, (6, 9, 13).index(n))
                    if after and n == 0:
                        keys(n, b + 1)
                    if after and n == 2:
                        values(n, b + 1)
                    if after and n == 5:
                        tokens(n, b + 1)
                    if after and n == 7:
                        queries(n, b + 1)
                    if after and n in (8, 10, 11, 14):
                        turn_keys(n, b + 1, (8, 10, 11, 14).index(n))
                    if after and n in (12, 15):
                        turn_queries(n, b + 1, (12, 15).index(n))

            e.wait_ge(m.zeroed, 1)
            e.wait_ge(m.v_padded, 2)
            keys(0, 0)
            tokens(1, 0)
            values(2, 0)
            queries(3, 0)
            turn_keys(4, 0, 0)
            turn_queries(5, 0, 0)
            turn_keys(6, 0, 1)
            turn_keys(7, 0, 2)
            turn_keys(8, 0, 3)
            turn_queries(9, 0, 1)
            scores(0, 0)
            turns(e, turn)
            weighted(B, -1)
            turn_pv(1, B - 1, 3)
            turn_o(3, B - 1)
            output(4, B - 1)

        @block.scalar
        def _(e):
            def keep_k(b):
                e.wait_ge(m.k_projected, b + 1)
                wait(e, m.k_lo_ready, b)
                e.activation(k_rows[:, :, :], work[0][:, :].rearrange("p (t d) -> p t d", d=D), ACT.Copy).then_inc(m.k_kept, 1)

            def square_k(b, t):
                if t == 0:
                    e.wait_ge(m.k_kept, b + 1)
                    wait(e, m.k_clamped, b)
                e.activation(square[:, t, :], k_rows[:, t, :], ACT.Square, accum_out=ksum[:, t:t + 1]).then_inc(m.k_squared, 1)

            def keep_v(b):
                e.wait_ge(m.v_projected, b + 1)
                wait(e, m.v_high_ready, b)
                e.activation(v_rows[:, :, :], work[0][:, :].rearrange("p (t d) -> p t d", d=D), ACT.Copy).then_inc(m.v_kept, 1)

            def keep_z(b):
                e.wait_ge(front.z_turned, b + 1)
                e.activation(zT[:, :], work[1][:, 0:T], ACT.Copy).then_inc(m.zT_ready, 1)

            def keep_q(b):
                e.wait_ge(m.q_projected, b + 1)
                e.activation(qp[:, bass.ds(TPB * b, TPB), :], work[1][:, 0:T].rearrange("p (i d) -> p i d", d=D),
                             ACT.Copy).then_inc(m.qp_ready, 1)
                wait(e, m.q_clamped, b)
                for i in range(TPB):
                    e.activation(square[:, KT + i, :], work[1][:, i * P:(i + 1) * P], ACT.Square,
                                 accum_out=qsum[:, i:i + 1]).then_inc(m.q_squared, 1)

            def keep_qS(b, i, w):
                e.wait_ge(m.q_turned, 2 * b + i + 1)
                wait(e, m.scores_ready, STEPS * (b - 1) + 8 * i + 8)
                e.activation(qS[96:128, 2 * i:2 * i + 2, 3, :], work[w][96:128, :].bitcast(F32R).rearrange("p (g q) -> p g q", q=T),
                             ACT.Copy).then_inc(m.qS_ready_act, 1)

            def keep_o(b):
                e.wait_ge(m.o_turned, b + 1)
                e.activation(oT[:, :], work[1][:, 0:T], ACT.Copy).then_inc(m.oT_ready, 1)

            def take_scales(b):
                wait(e, m.prob_ready, STEPS * b)
                e.wait_ge(m.k_scale_next, b + 1)
                e.activation(kscale[:, :], kscale_next[:, :], ACT.Copy).then_inc(m.k_scale_ready, 1)

            def exps(b, n):
                if n == 0:
                    e.wait_ge(m.k_scale_ready, b + 1)
                e.wait_ge(m.scores_ready, STEPS * b + n + 1)
                wait(e, m.pv_ready, STEPS * b + n - 1)
                e.activation(prob[n % 2][:, :], sc[n % 2][:, :], ACT.Exp, scale=kscale[:, n % KT:n % KT + 1]).then_inc(m.prob_ready, 1)

            def turn(b):
                before, after, _ = parts(b)
                for n in range(STEPS):
                    exps(b, n)
                    if n == 0 and before:
                        keep_qS(b, 1, 1)
                    if n == 1 and after:
                        keep_k(b + 1)
                    if n == 2 and after:
                        square_k(b + 1, 0)
                        square_k(b + 1, 1)
                    if n == 3 and after:
                        keep_v(b + 1)
                    if n == 4 and before:
                        keep_o(b - 1)
                    if n == 5 and after:
                        square_k(b + 1, 2)
                        square_k(b + 1, 3)
                    if n == 6 and after:
                        keep_z(b + 1)
                    if n == 8 and after:
                        keep_q(b + 1)
                    if n == 13 and after:
                        keep_qS(b + 1, 0, 0)
                    if n == 15 and after:
                        take_scales(b + 1)

            keep_k(0)
            for t in range(KT):
                square_k(0, t)
            keep_z(0)
            keep_v(0)
            keep_q(0)
            take_scales(0)
            e.wait_ge(m.zeroed, 1 + GROUPS)
            keep_qS(0, 0, 1)
            keep_qS(0, 1, 1)
            turns(e, turn)
            keep_o(B - 1)

        @block.vector
        def _(e):
            norm_steps = Steps(e, m.steps, front.steps)

            def norm(b):
                norm_steps.begin(b)
                front.vector(e, b, norm_steps)
                norm_steps.end()

            def k_high(b):
                e.wait_ge(m.k_kept, b + 1)
                wait(e, m.k_turned, GROUPS * b)
                e.tensor_copy(stacked(kst[:, :, :], 0, 2), repeated(k_rows[:, :, :])).then_inc(m.k_hi_ready, 1)

            def clamp_k(b):
                e.wait_ge(m.k_squared, KT * b + KT)
                wait(e, m.k_scale_ready, b)
                e.tensor_scalar(kclamped[:, :], ksum[:, :], 1e-24, float(HD), ALU.max, ALU.mult).then_inc(m.k_clamped, 1)

            def clamp_q(b):
                e.wait_ge(m.q_squared, TPB * b + TPB)
                e.tensor_scalar(qclamped[:, :], qsum[:, :], 1e-24, None, ALU.max).then_inc(m.q_clamped, 1)

            def split_q(b):
                e.wait_ge(m.q_norm_ready, b + 1)
                e.wait_ge(m.qp_ready, b + 1)
                wait(e, m.q_turned, 2 * b)
                for i in range(TPB):
                    e.tensor_scalar(qn[:, i, :], qp[:, TPB * b + i, :], qnorm[:, i:i + 1], None, ALU.mult).then_inc(m.qn_ready, 1)
                e.wait_ge(m.qn_ready, TPB * b + TPB)
                high = qst[:, :, :].rearrange("p t (h k d) -> p (t h) k d", k=4, d=HD)[:, :, 0:2, :]
                low = qst[:, :, :].rearrange("p t (h k d) -> p (t h) k d", k=4, d=HD)[:, :, 2:4, :]
                e.tensor_copy(high, repeated(qn[:, :, :])).then_inc(m.q_hi_ready, 1)
                e.wait_ge(m.q_hi_ready, b + 1)
                e.tensor_tensor(low, repeated(qn[:, :, :]), high, ALU.subtract).then_inc(m.q_lo_ready, 1)

            def keep_kS(b, grp, w):
                e.wait_ge(m.k_turned, GROUPS * b + grp + 1)
                wait(e, m.scores_ready, STEPS * (b - 1) + 4 * grp + 4)
                e.tensor_copy(kS[:, grp, :], work[w][:, :].bitcast(F32R)).then_inc(m.kS_ready, 1)

            def keep_qS(b, i, w):
                e.wait_ge(m.q_turned, 2 * b + i + 1)
                wait(e, m.scores_ready, STEPS * (b - 1) + 8 * i + 8)
                for j in range(3):
                    rows = slice(32 * j, 32 * j + 32)
                    e.tensor_copy(qS[rows, 2 * i:2 * i + 2, j, :],
                                  work[w][rows, :].bitcast(F32R).rearrange("p (g q) -> p g q", q=T)).then_inc(m.qS_ready_dve, 1)

            def keep_pv(b, grp):
                e.wait_ge(m.pv_ready, STEPS * b + KT * (grp + 1))
                wait(e, m.pv_turned, GROUPS * b + grp)
                e.tensor_copy(pv[:, :], pvps[grp % 2][:, 0:T]).then_inc(m.pv_kept, 1)

            def divide(b, grp, w):
                e.wait_ge(m.pv_turned, GROUPS * b + grp + 1)
                heads = work[w][:, 0:T].rearrange("p (i j d) -> p i j d", i=TPB, d=32)
                e.reciprocal(rsum[:, :, :], heads[:, :, :, HD]).then_inc(m.rsum_ready, 1)
                e.wait_ge(m.rsum_ready, GROUPS * b + grp + 1)
                if grp == 0:
                    wait(e, m.o_turned, b)
                e.tensor_tensor(o[:, :, 32 * grp:32 * grp + 32].rearrange("p i (j d) -> p i j d", d=HD),
                                heads[:, :, :, 0:HD], bcast(rsum[:, :, :].unsqueeze(3), [P, TPB, GH, HD]),
                                ALU.mult).then_inc(m.o_ready, 1)

            def add_qp(b):
                e.wait_ge(m.out_ready, b + 1)
                if isinstance(b, int):
                    wait(e, m.x_updated, 3 * b)
                e.tensor_tensor(y[:, :, :], work[0][:, 0:T].rearrange("p (i d) -> p i d", d=D),
                                qp[:, bass.ds(TPB * b, TPB), :], ALU.add).then_inc(m.y_kept, 1)
                e.wait_ge(m.y_kept, b + 1)
                for i in range(TPB):
                    e.bn_stats(stats[:, i, :], y[:, i, :]).then_inc(m.y_stats, 1)
                e.wait_ge(m.y_stats, 2 * TPB * b + TPB)
                e.memset(front.held[:, :], 0.0)
                for i in range(TPB):
                    e.bn_aggr(mv[:, i, :], stats[:, i, :]).then_inc(m.y_stats, 1)
                e.wait_ge(m.y_stats, 2 * TPB * b + 2 * TPB)
                e.tensor_scalar(yvar[:, :], mv[:, :, 1], EPS, None, ALU.add).then_inc(m.yvar_ready, 1)

            def norm_y(b):
                e.wait_ge(m.yrstd_ready, b + 1)
                for i in range(TPB):
                    e.tensor_scalar(y[:, i, :], y[:, i, :], mv[:, i, 0:1], yrstd[:, i:i + 1],
                                    ALU.subtract, ALU.mult).then_inc(m.y_ready, 1)

            def turn(b):
                before, after, _ = parts(b)
                for n in range(STEPS):
                    if n == 0 and before:
                        keep_qS(b, 1, 1)
                    if n == 1 and before:
                        keep_pv(b - 1, 3)
                    if n == 2 and before:
                        divide(b - 1, 3, 1)
                    if n == 3 and after:
                        k_high(b + 1)
                        norm(b + 1)
                    if n == 5:
                        keep_pv(b, 0)
                        if before:
                            add_qp(b - 1)
                    if n == 6:
                        if before:
                            norm_y(b - 1)
                        if after:
                            clamp_k(b + 1)
                    if n == 7:
                        divide(b, 0, 0)
                    if n == 9:
                        keep_pv(b, 1)
                        if after:
                            keep_kS(b + 1, 0, 0)
                            clamp_q(b + 1)
                    if n == 10:
                        divide(b, 1, 1)
                        if after:
                            split_q(b + 1)
                    if n == 11 and after:
                        keep_kS(b + 1, 1, 0)
                    if n == 12 and after:
                        keep_kS(b + 1, 2, 1)
                    if n == 13:
                        keep_pv(b, 2)
                        if after:
                            keep_qS(b + 1, 0, 0)
                    if n == 14:
                        divide(b, 2, 1)
                    if n == 15 and after:
                        keep_kS(b + 1, 3, 0)

            e.tensor_copy(ident[:, :], g.ident).then_inc(m.zeroed, 1)
            norm(0)
            k_high(0)
            clamp_k(0)
            e.wait_ge(m.filled, 1)
            for grp in range(GROUPS):
                e.tensor_copy(qS[:, grp, :, :].rearrange("p j q -> p (j q)"), zero[:, :]).then_inc(m.zeroed, 1)
            clamp_q(0)
            split_q(0)
            e.wait_ge(m.zeroed, 1 + GROUPS)
            keep_kS(0, 0, 0)
            keep_qS(0, 0, 1)
            keep_kS(0, 1, 0)
            keep_kS(0, 2, 1)
            keep_kS(0, 3, 0)
            keep_qS(0, 1, 1)
            turns(e, turn)
            keep_pv(B - 1, 3)
            divide(B - 1, 3, 1)
            add_qp(B - 1)
            norm_y(B - 1)



def l0_ffn(nc, g, a):
    HF = 256
    FT = HF // P
    CT = 4
    CHUNKS = TILES // CT
    with ExitStack() as outer:
        so = Scope(nc, outer, "l0f")
        logits = so.sb("logits", [P, TILES, E])
        gate = so.sb("gate", [P, TILES, E])
        gateT = so.sb("gateT", [E, N])
        z_hi, z_lo = so.sb("z_hi", [P, N], F32R), so.sb("z_lo", [P, N], F32R)
        w1_hi, w1_lo = so.sb("w1_hi", [P, E, HF], F32R), so.sb("w1_lo", [P, E, HF], F32R)

        with ExitStack() as ctx:
            s = Scope(nc, ctx, "l0f_norm")
            front = AllTiles(s, g, twice=True)
            turn = [s.ps(f"turn{n}") for n in range(front.BANKS)]
            lps = s.ps("logits")
            zT = s.sb("zT", [P, N])
            m = s.sems(["x_updated", "z_kept", "logits_ready", "logits_kept", "z_hi_ready", "z_lo_ready"])
            block = s.block()

            def router(e, n):
                e.wait_ge(m.z_kept, n + 1)
                for t in range(front.BANK * n, front.BANK * (n + 1)):
                    e.matmul(lps[:, t * E:(t + 1) * E], zT[:, t * P:(t + 1) * P], g.l0_rw[:, :], start=True, stop=False)
                    last = e.matmul(lps[:, t * E:(t + 1) * E], g.ones[0:1, 0:P], g.l0_rb[:, :], start=False, stop=True)
                last.then_inc(m.logits_ready, 1)

            @block.vector
            def _(e):
                front.vector(e)
                for n in range(front.BANKS):
                    tokens = slice(n * CT * P, (n + 1) * CT * P)
                    e.wait_ge(m.z_kept, n + 1)
                    e.tensor_copy(z_hi[:, tokens], zT[:, tokens]).then_inc(m.z_hi_ready, 1)
                    e.wait_ge(m.z_hi_ready, n + 1)
                    e.tensor_tensor(z_lo[:, tokens], zT[:, tokens], z_hi[:, tokens], ALU.subtract).then_inc(m.z_lo_ready, 1)
                e.wait_ge(m.z_lo_ready, front.BANKS)

            @block.gpsimd
            def _(e):
                front.gpsimd(e)
                e.wait_ge(front.outer_ready, TILES)
                e.tensor_tensor(g.x[:, :, :], g.x[:, :, :], front.outer[:, :, :], ALU.add).then_inc(m.x_updated, 1)

            @block.tensor
            def _(e):
                for n in range(front.BANKS):
                    front.tensor(e, n, turn[n])
                    if n == 0:
                        continue
                    router(e, n - 1)
                router(e, front.BANKS - 1)

            @block.scalar
            def _(e):
                for n in range(front.BANKS):
                    e.wait_ge(front.z_turned, n + 1)
                    e.activation(zT[:, n * CT * P:(n + 1) * CT * P], turn[n][:, :], ACT.Identity, scale=g.l0_lng[:, 0:1],
                                 bias=g.l0_lnb[:, 0:1]).then_inc(m.z_kept, 1)
                e.wait_ge(m.logits_ready, front.BANKS)
                e.activation(logits[:, :, :], lps[:, 0:TILES * E].rearrange("p (i e) -> p i e", e=E),
                             ACT.Copy).then_inc(m.logits_kept, 1)

        with ExitStack() as ctx:
            s = Scope(nc, ctx, "l0f_route")
            full = [P, TILES, E]
            red = s.sb("red", [P, 8, TILES])
            w = [s.sb(f"w{i}", full) for i in range(8)]
            turn = s.ps("turn", (P, 4 * 512))
            m = s.sems(["shifted", "exped", "gate_ready", "gate_turned", "steps", "gateT_ready",
                        "w_hi_ready", "w_lo_ready"])
            block = s.block()

            @block.gpsimd
            def _(e):
                e.tensor_copy(w1_hi[:, :, :], g.l0_w1[:, :, :]).then_inc(m.w_hi_ready, 1)
                e.wait_ge(m.w_hi_ready, 1)
                e.tensor_tensor(w1_lo[:, :, :], g.l0_w1[:, :, :], w1_hi[:, :, :], ALU.subtract).then_inc(m.w_lo_ready, 1)
                e.wait_ge(m.w_lo_ready, 1)

            @block.vector
            def _(e):
                steps = Steps(e, m.steps)

                def then(instruction):
                    steps.add(instruction)
                    steps.settle()

                def over(i):
                    return bcast(red[:, i, :].unsqueeze(2), full)

                rev = bcast(g.const[:, C_REV:C_REV + E].unsqueeze(1), full)
                then(e.tensor_reduce(red[:, 0, :], logits[:, :, :], AX.X, ALU.max))
                e.tensor_tensor(w[0][:, :, :], logits[:, :, :], over(0), ALU.subtract).then_inc(m.shifted, 1)
                e.wait_ge(m.exped, 1)
                then(e.tensor_reduce(red[:, 1, :], w[1][:, :, :], AX.X, ALU.add))
                then(e.reciprocal(red[:, 2, :], red[:, 1, :]))
                then(e.tensor_tensor(w[2][:, :, :], w[1][:, :, :], over(2), ALU.mult))
                then(e.tensor_reduce(red[:, 3, :], w[2][:, :, :], AX.X, ALU.max))
                then(e.tensor_tensor(w[3][:, :, :], w[2][:, :, :], over(3), ALU.is_equal))
                then(e.tensor_tensor(w[4][:, :, :], w[3][:, :, :], rev, ALU.mult))
                then(e.tensor_reduce(red[:, 4, :], w[4][:, :, :], AX.X, ALU.max))
                then(e.tensor_tensor(w[5][:, :, :], rev, over(4), ALU.is_equal))
                then(e.scalar_tensor_tensor(out=w[6][:, :, :].rearrange("p t e -> p (t e)"),
                                            in0=w[5][:, :, :].rearrange("p t e -> p (t e)"), scalar=-4.0,
                                            in1=w[2][:, :, :].rearrange("p t e -> p (t e)"), op0=ALU.mult, op1=ALU.add))
                then(e.tensor_reduce(red[:, 5, :], w[6][:, :, :], AX.X, ALU.max))
                then(e.tensor_tensor(w[3][:, :, :], w[6][:, :, :], over(5), ALU.is_equal))
                then(e.tensor_tensor(w[4][:, :, :], w[3][:, :, :], rev, ALU.mult))
                then(e.tensor_reduce(red[:, 6, :], w[4][:, :, :], AX.X, ALU.max))
                then(e.tensor_tensor(w[7][:, :, :], rev, over(6), ALU.is_equal))
                then(e.tensor_tensor(w[3][:, :, :], w[5][:, :, :], w[7][:, :, :], ALU.add))
                then(e.tensor_tensor(w[4][:, :, :], w[3][:, :, :], w[2][:, :, :], ALU.mult))
                then(e.tensor_reduce(red[:, 7, :], w[4][:, :, :], AX.X, ALU.add))
                then(e.tensor_scalar(red[:, 0, :], red[:, 7, :], 1e-8, None, ALU.max))
                then(e.reciprocal(red[:, 1, :], red[:, 0, :]))
                e.tensor_tensor(gate[:, :, :], w[4][:, :, :], over(1), ALU.mult).then_inc(m.gate_ready, 1)

            @block.scalar
            def _(e):
                e.wait_ge(m.shifted, 1)
                e.activation(w[1][:, :, :], w[0][:, :, :], ACT.Exp).then_inc(m.exped, 1)
                e.wait_ge(m.gate_turned, 1)
                e.activation(gateT[:, :], turn[0:E, :], ACT.Copy).then_inc(m.gateT_ready, 1)

            @block.tensor
            def _(e):
                e.wait_ge(m.gate_ready, 1)
                for t in range(TILES):
                    last = e.transpose(turn[0:E, t * P:(t + 1) * P], gate[:, t, :], g.ident)
                last.then_inc(m.gate_turned, 1)

        with ExitStack() as ctx:
            s = Scope(nc, ctx, "l0f_experts")
            gT = s.sb("gateT_chunk", [E, CT * P])
            gc = s.sb("gate_chunk", [P, CT, E])
            h = [s.sb(f"hidden{i}", [P, FT, CT * P]) for i in range(4)]
            acc = s.sb("acc", [P, CT, D])
            hps = [s.ps(f"hidden{i}") for i in range(2 * FT)]
            yps = [s.ps(f"y{i}") for i in range(2)]
            bps = s.ps("gated_bias")
            m = s.sems(["gates_fixed", "hidden_ready", "act_ready", "y_ready", "y_added",
                        "bias_ready", "bias_added", "x_updated"])
            block = s.block()

            def turns(e, turn):
                turn(0, True)
                with e.Fori(1, CHUNKS - 1) as c:
                    turn(c, True)
                turn(CHUNKS - 1, False)

            @block.gpsimd
            def _(e):
                def fix_gates(c):
                    wait(e, m.y_added, E * CT * c)
                    e.tensor_copy(gc[:, :, :], gate[:, bass.ds(c * CT, CT), :]).then_inc(m.gates_fixed, 1)
                    e.tensor_copy(gT[:, :], gateT[:, bass.ds(c * CT * P, CT * P)]).then_inc(m.gates_fixed, 1)

                def turn(c, more):
                    if more:
                        fix_gates(c + 1)

                fix_gates(0)
                turns(e, turn)

            @block.tensor
            def _(e):
                def hidden(c, x):
                    for f in range(FT):
                        n = FT * x + f
                        wait(e, m.act_ready, E * FT * c + n - 2 * FT + 1)
                        chunk = bass.ds((c + x // E) * CT * P, CT * P)
                        features = slice(f * P, (f + 1) * P)
                        out = hps[n % (2 * FT)][:, :]
                        e.matmul(out, w1_hi[:, x % E, features], z_hi[:, chunk], start=True, stop=False)
                        e.matmul(out, w1_lo[:, x % E, features], z_hi[:, chunk], start=False, stop=False)
                        e.matmul(out, w1_hi[:, x % E, features], z_lo[:, chunk], start=False, stop=True).then_inc(m.hidden_ready, 1)

                def gated_bias(c):
                    e.wait_ge(m.gates_fixed, 2 * c + 2)
                    wait(e, m.bias_added, c)
                    for t in range(CT):
                        last = e.matmul(bps[:, t * P:(t + 1) * P], gT[:, t * P:(t + 1) * P], g.l0_b2[:, :], start=True, stop=True)
                    last.then_inc(m.bias_ready, 1)

                def second(c, x):
                    e.wait_ge(m.act_ready, FT * (E * c + x + 1))
                    wait(e, m.y_added, CT * (E * c + x - 1))
                    for t in range(CT):
                        tokens = slice(t * P, (t + 1) * P)
                        out = yps[x % 2][:, tokens]
                        for f in range(FT):
                            last = e.matmul(out, h[x % 4][:, f, tokens], g.l0_w2[:, x, f, :], start=f == 0, stop=f == FT - 1)
                    last.then_inc(m.y_ready, 1)

                def turn(c, more):
                    for x in range(E):
                        if x + 2 < E or more:
                            hidden(c, x + 2)
                        if x == E // 2:
                            gated_bias(c)
                        second(c, x)

                hidden(0, 0)
                hidden(0, 1)
                turns(e, turn)

            @block.scalar
            def _(e):
                def gelus(c, x):
                    for f in range(FT):
                        e.wait_ge(m.hidden_ready, E * FT * c + FT * x + f + 1)
                        if f == 0:
                            wait(e, m.y_ready, E * c + x - 3)
                        n = FT * (x % E) + f
                        e.activation(h[x % 4][:, f, :], hps[n % (2 * FT)][:, :], ACT.Gelu, bias=g.l0_b1[:, n:n + 1]
                                     ).then_inc(m.act_ready, 1)

                def turn(c, more):
                    for x in range(E):
                        if x + 2 < E or more:
                            gelus(c, x + 2)

                gelus(0, 0)
                gelus(0, 1)
                turns(e, turn)

            @block.vector
            def _(e):
                def add(c, x):
                    e.wait_ge(m.y_ready, E * c + x + 1)
                    if x:
                        e.wait_ge(m.y_added, CT * (E * c + x))
                    else:
                        wait(e, m.x_updated, c)
                        e.wait_ge(m.gates_fixed, 2 * c + 1)
                    for t in range(CT):
                        y, factor = yps[x % 2][:, t * P:(t + 1) * P], gc[:, t, x:x + 1]
                        if x:
                            e.scalar_tensor_tensor(out=acc[:, t, :], in0=y, scalar=factor, in1=acc[:, t, :], op0=ALU.mult,
                                                   op1=ALU.add).then_inc(m.y_added, 1)
                        else:
                            e.tensor_scalar(acc[:, t, :], y, factor, None, ALU.mult).then_inc(m.y_added, 1)

                def turn(c, more):
                    for x in range(E):
                        add(c, x)
                    e.wait_ge(m.y_added, CT * E * (c + 1))
                    e.wait_ge(m.bias_ready, c + 1)
                    e.tensor_tensor(acc[:, :, :], acc[:, :, :], bps[:, :].rearrange("p (t d) -> p t d", d=D), ALU.add
                                    ).then_inc(m.bias_added, 1)
                    e.wait_ge(m.bias_added, c + 1)
                    xs = g.x[:, bass.ds(c * CT, CT), :]
                    e.tensor_tensor(xs, xs, acc[:, :, :], ALU.add).then_inc(m.x_updated, 1)

                turns(e, turn)



def prepare(nc, g, name, HEADS, wq, wk, wv, wo, A, G, z, ctx):
    (A_hi, A_lo), (z_hi, z_lo), (ctx_hi, ctx_lo) = A, z, ctx
    HD = 64
    SCALE = HD ** -0.5
    C = HEADS // 2
    with ExitStack() as scope:
        s = Scope(nc, scope, name)
        turned = s.sb("turned", [P, 3, C, P])
        stats = s.sb("ln_stats", [P, TILES, 6])
        mv = s.sb("ln_mean_var", [P, TILES, 2])
        var = s.sb("ln_var_eps", [P, TILES])
        rstd = s.sb("ln_rstd", [P, TILES])
        normed = s.sb("ln_z", [P, TILES, D])
        tps = [s.ps(f"turned{i}") for i in range(4)]
        pps = [s.ps(f"product{i}") for i in range(4)]
        m = s.sems(["turned", "turned_kept", "products", "A_hi_ready", "A_lo_ready", "G_kept", "stats_ready", "var_ready",
                    "rstd_ready", "z_ready", "z_turned", "z_hi_ready", "z_lo_ready", "ctx_hi_ready", "ctx_lo_ready"])
        jobs = [(i, c, w[:, c * P:(c + 1) * P]) for i, w in enumerate((wq, wk, wv)) for c in range(C)]
        block = s.block()

        @block.tensor
        def _(e):
            for n, (i, c, src) in enumerate(jobs):
                if n >= 4:
                    e.wait_ge(m.turned_kept, n - 3)
                rows = src.shape[0]
                e.transpose(tps[n % 4][:, 0:rows], src, g.ident[0:rows, 0:rows]).then_inc(m.turned, 1)
            e.wait_ge(m.turned_kept, len(jobs))
            for h in range(HEADS):
                c, lo = h // 2, 64 * (h % 2)
                half = slice(lo, lo + HD)
                if h >= 2:
                    e.wait_ge(m.A_lo_ready, h - 1)
                    e.wait_ge(m.G_kept, h - 1)
                e.matmul(pps[2 * (h % 2)][:, 0:DC], turned[half, 0, c, :], turned[half, 1, c, 0:DC], start=True,
                         stop=True, tile_position=(lo, 0)).then_inc(m.products, 1)
                e.matmul(pps[2 * (h % 2) + 1][0:DC, 0:D], turned[half, 2, c, 0:DC], wo[half, c, :], start=True,
                         stop=True, tile_position=(lo, 0)).then_inc(m.products, 1)
            e.wait_ge(m.z_ready, TILES)
            for n in range(TILES // 4):
                for i in range(4):
                    last = e.transpose(tps[n][:, i * P:(i + 1) * P], normed[:, 4 * n + i, :], g.ident)
                last.then_inc(m.z_turned, 1)

        @block.gpsimd
        def _(e):
            e.wait_ge(m.var_ready, 1)
            e.tensor_tensor(rstd[:, :], var[:, :], g.neg_half[:, 0:TILES], ALU.pow).then_inc(m.rstd_ready, 1)
            for b in range(B):
                e.wait_ge(m.ctx_hi_ready, b + 1)
                e.tensor_tensor(ctx_lo[:, b * S:(b + 1) * S], g.ctxT[0:DC, b * S:(b + 1) * S],
                                ctx_hi[:, b * S:(b + 1) * S], ALU.subtract).then_inc(m.ctx_lo_ready, 1)
            e.wait_ge(m.ctx_lo_ready, B)

        @block.scalar
        def _(e):
            for n, (i, c, src) in enumerate(jobs):
                rows = src.shape[0]
                e.wait_ge(m.turned, n + 1)
                e.activation(turned[:, i, c, 0:rows], tps[n % 4][:, 0:rows], ACT.Copy).then_inc(m.turned_kept, 1)
            for h in range(HEADS):
                e.wait_ge(m.products, 2 * h + 1)
                e.activation(A_hi[:, h, :], pps[2 * (h % 2)][:, 0:DC], ACT.Copy, scale=SCALE).then_inc(m.A_hi_ready, 1)
            for n in range(TILES // 4):
                e.wait_ge(m.z_turned, n + 1)
                e.activation(z_hi[:, 4 * n * P:4 * (n + 1) * P], tps[n][:, :], ACT.Copy).then_inc(m.z_hi_ready, 1)

        @block.vector
        def _(e):
            for i in range(TILES):
                e.bn_stats(stats[:, i, :], g.x[:, i, :]).then_inc(m.stats_ready, 1)
            for i in range(TILES):
                e.wait_ge(m.stats_ready, i + 1)
                e.bn_aggr(mv[:, i, :], stats[:, i, :]).then_inc(m.stats_ready, 1)
            e.wait_ge(m.stats_ready, 2 * TILES)
            e.tensor_scalar(var[:, :], mv[:, :, 1], EPS, None, ALU.add).then_inc(m.var_ready, 1)
            for b in range(B):
                e.tensor_copy(ctx_hi[:, b * S:(b + 1) * S], g.ctxT[0:DC, b * S:(b + 1) * S]).then_inc(m.ctx_hi_ready, 1)
            e.wait_ge(m.rstd_ready, 1)
            for i in range(TILES):
                e.tensor_scalar(normed[:, i, :], g.x[:, i, :], mv[:, i, 0:1], rstd[:, i:i + 1],
                                ALU.subtract, ALU.mult).then_inc(m.z_ready, 1)
            for h in range(HEADS):
                e.wait_ge(m.products, 2 * h + 2)
                e.tensor_copy(G[:, h, :], pps[2 * (h % 2) + 1][0:DC, 0:D]).then_inc(m.G_kept, 1)
                e.wait_ge(m.A_hi_ready, h + 1)
                e.scalar_tensor_tensor(out=A_lo[:, h, :], in0=pps[2 * (h % 2)][:, 0:DC], scalar=SCALE, in1=A_hi[:, h, :],
                                       op0=ALU.mult, op1=ALU.subtract).then_inc(m.A_lo_ready, 1)
            for n in range(TILES // 4):
                tokens = slice(4 * n * P, 4 * (n + 1) * P)
                e.wait_ge(m.z_hi_ready, n + 1)
                e.tensor_tensor(z_lo[:, tokens], tps[n][:, :], z_hi[:, tokens], ALU.subtract).then_inc(m.z_lo_ready, 1)
            e.wait_ge(m.z_lo_ready, TILES // 4)
            e.wait_ge(m.A_lo_ready, HEADS)
            e.wait_ge(m.G_kept, HEADS)


def wide_attention(nc, g, name, HEADS, A, G, z, ctx, bo):
    C = HEADS // 2
    UNITS = HEADS * TPB
    NS = NP_ = AHEAD = 4
    LAG = 3
    LEAD = 3
    RING = 4
    (A_hi, A_lo), (z_hi, z_lo), (ctx_hi, ctx_lo) = A, z, ctx
    with ExitStack() as scope:
        s = Scope(nc, scope, name)
        t_hi = s.sb("t_hi", [DC, 2 * RING, T], F32R)
        t_lo = s.sb("t_lo", [DC, 2 * RING, T], F32R)
        rows_hi = s.sb("ctx_rows_hi", [P, KT, DC], F32R)
        rows_lo = s.sb("ctx_rows_lo", [P, KT, DC], F32R)
        nmax = s.sb("nmax", [P, UNITS])
        rsum = s.sb("rsum", [P, UNITS])
        rinv = s.sb("rinv", [P, UNITS])
        prob = [s.sb(f"prob{i}", [P, S]) for i in range(NP_)]
        pT_hi = [s.sb(f"probT_hi{i}", [P, KT, 2, T], F32R) for i in range(2)]
        pT_lo = [s.sb(f"probT_lo{i}", [P, KT, 2, T], F32R) for i in range(2)]
        uT = s.sb("uT", [DC, 2, T])
        sps = [s.ps(f"scores{i}") for i in range(NS)]
        tps = [s.ps(f"turned{i}") for i in range(2)]
        jps = s.ps("u_and_t")
        yps = s.ps("y")
        m = s.sems(["rows_hi_ready", "rows_lo_ready", "t_projected", "t_hi_ready", "t_lo_ready", "scores_ready", "max_ready", "exp_ready",
                    "rinv_ready", "prob_ready", "prob_turned", "pT_hi_ready", "pT_lo_ready", "u_projected",
                    "u_kept", "u_used", "y_ready", "x_updated"])
        block = s.block()

        def turns(e, turn):
            turn(0, True)
            with e.Fori(1, B - 1) as b:
                turn(b, True)
            turn(B - 1, False)

        @block.gpsimd
        def _(e):
            def turn(b, more):
                for n in range(UNITS):
                    e.wait_ge(m.rinv_ready, UNITS * b + n + 1)
                    e.tensor_tensor(prob[n % NP_][:, :], prob[n % NP_][:, :], bcast(rinv[:, n:n + 1], [P, S]),
                                    ALU.mult).then_inc(m.prob_ready, 1)

            turns(e, turn)

        @block.tensor
        def _(e):
            def project(b, c):
                tokens = bass.ds(b * T, T)
                for j in range(2):
                    out, h = jps[0:DC, j * T:(j + 1) * T], 2 * c + j
                    e.matmul(out, A_hi[:, h, :], z_hi[:, tokens], start=True, stop=False)
                    e.matmul(out, A_lo[:, h, :], z_hi[:, tokens], start=False, stop=False)
                    last = e.matmul(out, A_hi[:, h, :], z_lo[:, tokens], start=False, stop=True)
                last.then_inc(m.t_projected, 1)

            def scores(b, n):
                h, i = divmod(n, TPB)
                wait(e, m.exp_ready, UNITS * b + n - NS + 1)
                if n % 4 == 0:
                    e.wait_ge(m.t_lo_ready, C * b + h // 2 + 1)
                queries = slice(i * P, (i + 1) * P)
                hi, lo = t_hi[:, h % (2 * RING), queries], t_lo[:, h % (2 * RING), queries]
                e.matmul(sps[n % NS][:, :], hi, ctx_hi[:, bass.ds(b * S, S)], start=True, stop=False)
                e.matmul(sps[n % NS][:, :], hi, ctx_lo[:, bass.ds(b * S, S)], start=False, stop=False)
                e.matmul(sps[n % NS][:, :], lo, ctx_hi[:, bass.ds(b * S, S)], start=False, stop=True).then_inc(m.scores_ready, 1)

            def turned(b, n):
                wait(e, m.pT_lo_ready, UNITS * b + n - 1)
                e.wait_ge(m.prob_ready, UNITS * b + n + 1)
                for t in range(KT):
                    last = e.transpose(tps[n % 2][:, t * P:(t + 1) * P], prob[n % NP_][:, t * P:(t + 1) * P], g.ident)
                last.then_inc(m.prob_turned, 1)

            def weighted(b, c):
                e.wait_ge(m.pT_lo_ready, UNITS * b + 4 * c + 4)
                if c == 0:
                    e.wait_ge(m.rows_lo_ready, b + 1)
                for t in range(KT):
                    hi, lo = pT_hi[c % 2][:, t, :, :], pT_lo[c % 2][:, t, :, :]
                    e.matmul(jps[0:DC, :], rows_hi[:, t, :], hi, start=t == 0, stop=False)
                    e.matmul(jps[0:DC, :], rows_lo[:, t, :], hi, start=False, stop=False)
                    last = e.matmul(jps[0:DC, :], rows_hi[:, t, :], lo, start=False, stop=t == KT - 1)
                last.then_inc(m.u_projected, 1)

            def joined(b, c):
                e.wait_ge(m.u_kept, C * b + c + 1)
                if c == 0:
                    wait(e, m.x_updated, b)
                for j in range(2):
                    for i in range(TPB):
                        last = e.matmul(yps[:, i * P:(i + 1) * P], uT[:, j, i * P:(i + 1) * P], G[:, (2 * c + j) % HEADS, :],
                                        start=c == 0 and j == 0 and i == 0, stop=False, skip_group_check=True)
                last.then_inc(m.u_used, 1)
                if c % C == C - 1:
                    for i in range(TPB):
                        last = e.matmul(yps[:, i * P:(i + 1) * P], g.ones[0:1, 0:P], bo[:, :], start=False, stop=True,
                                        skip_group_check=True)
                    last.then_inc(m.y_ready, 1)

            def turn(b, more):
                first = isinstance(b, int) and b == 0
                for n in range(UNITS):
                    turned(b, n)
                    if n + AHEAD < UNITS:
                        scores(b, n + AHEAD)
                    elif more:
                        scores(b + 1, n + AHEAD - UNITS)
                    ahead = n // 4 + LEAD
                    if n % 4 == 1 and (ahead < C or more):
                        wait(e, m.u_kept, C * b + n // 4 - 1)
                        e.wait_ge(m.t_lo_ready, C * b + ahead)
                        project(b + ahead // C, ahead % C)
                    if n % 4 == 3:
                        if ahead < C or more:
                            e.wait_ge(m.t_lo_ready, C * b + ahead + 1)
                        if n > 4 or not first:
                            weighted(b, n // 4 - 1)
                    if n % 4 == 2 and (n > 8 or not first):
                        joined(b, n // 4 - 2)

            for c in range(LEAD):
                if c:
                    e.wait_ge(m.t_lo_ready, c)
                project(0, c)
                if c == 0:
                    for n in range(AHEAD):
                        scores(0, n)
            turns(e, turn)
            joined(B, -2)
            weighted(B, -1)
            joined(B, -1)

        @block.scalar
        def _(e):
            def keep_t(b, c):
                e.wait_ge(m.t_projected, C * b + c + 1)
                wait(e, m.scores_ready, UNITS * b + 4 * (c - RING) + 4)
                at = 2 * (c % RING)
                e.activation(t_hi[:, at:at + 2, :], jps[0:DC, :].rearrange("p (h t) -> p h t", h=2),
                             ACT.Copy).then_inc(m.t_hi_ready, 1)

            def rows_high(b):
                wait(e, m.u_projected, C * b)
                e.activation(rows_hi[:, :, :], g.ctx_rows[:, bass.ds(b * KT, KT), :], ACT.Copy).then_inc(m.rows_hi_ready, 1)

            def exps(b, n):
                e.wait_ge(m.max_ready, UNITS * b + n + 1)
                wait(e, m.prob_turned, UNITS * b + n - NP_ + 1)
                e.activation(prob[n % NP_][:, :], sps[n % NS][:, :], ACT.Exp, bias=nmax[:, n:n + 1],
                             accum_out=rsum[:, n:n + 1]).then_inc(m.exp_ready, 1)

            def keep_high(b, k):
                e.wait_ge(m.prob_turned, UNITS * b + k + 1)
                wait(e, m.u_projected, C * b + k // 4 - 1)
                e.activation(pT_hi[k // 4 % 2][:, :, k // 2 % 2, k % 2 * P:k % 2 * P + P],
                             tps[k % 2][:, :].rearrange("p (t q) -> p t q", q=P), ACT.Copy).then_inc(m.pT_hi_ready, 1)

            def turn(b, more):
                first = isinstance(b, int) and b == 0
                for n in range(UNITS):
                    exps(b, n)
                    if n >= LAG or not first:
                        keep_high(b, n - LAG)
                    if n == 6:
                        rows_high(b)
                    ahead = n // 4 - 1 + LEAD
                    if n % 4 == 0 and (ahead < C or more):
                        keep_t(b + ahead // C, ahead % C)

            for c in range(LEAD - 1):
                keep_t(0, c)
            turns(e, turn)
            for k in range(-LAG, 0):
                keep_high(B, k)

        @block.vector
        def _(e):
            def maxima(b, n):
                e.wait_ge(m.scores_ready, UNITS * b + n + 1)
                e.tensor_reduce(nmax[:, n:n + 1], sps[n % NS][:, :], AX.X, ALU.max, negate=True).then_inc(m.max_ready, 1)

            def invert(b, k):
                e.wait_ge(m.exp_ready, UNITS * b + k + 1)
                k %= UNITS
                e.reciprocal(rinv[:, k:k + 1], rsum[:, k:k + 1]).then_inc(m.rinv_ready, 1)

            def t_low(b, c):
                e.wait_ge(m.t_hi_ready, C * b + c + 1)
                wait(e, m.scores_ready, UNITS * b + 4 * (c - RING) + 4)
                at = 2 * (c % RING)
                e.tensor_tensor(t_lo[:, at:at + 2, :], jps[0:DC, :].rearrange("p (h t) -> p h t", h=2),
                                t_hi[:, at:at + 2, :], ALU.subtract).then_inc(m.t_lo_ready, 1)

            def rows_low(b):
                e.wait_ge(m.rows_hi_ready, b + 1)
                e.tensor_tensor(rows_lo[:, :, :], g.ctx_rows[:, bass.ds(b * KT, KT), :], rows_hi[:, :, :],
                                ALU.subtract).then_inc(m.rows_lo_ready, 1)

            def keep_low(b, k):
                e.wait_ge(m.pT_hi_ready, UNITS * b + k + 1)
                wait(e, m.u_projected, C * b + k // 4 - 1)
                place = (slice(None), slice(None), k // 2 % 2, slice(k % 2 * P, k % 2 * P + P))
                e.tensor_tensor(pT_lo[k // 4 % 2][place], tps[k % 2][:, :].rearrange("p (t q) -> p t q", q=P),
                                pT_hi[k // 4 % 2][place], ALU.subtract).then_inc(m.pT_lo_ready, 1)

            def keep_u(b, c):
                e.wait_ge(m.u_projected, C * b + c + 1)
                wait(e, m.u_used, C * b + c)
                e.tensor_copy(uT[:, :, :], jps[0:DC, :].rearrange("p (h t) -> p h t", h=2)).then_inc(m.u_kept, 1)

            def update(b):
                e.wait_ge(m.y_ready, b)
                xs = g.x[:, bass.ds(TPB * (b - 1), TPB), :]
                e.tensor_tensor(xs, yps[:, 0:T].rearrange("p (i d) -> p i d", d=D), xs, ALU.add).then_inc(m.x_updated, 1)

            def turn(b, more):
                first = isinstance(b, int) and b == 0
                for n in range(UNITS):
                    if n > 0 or not first:
                        invert(b, n - 1)
                    maxima(b, n)
                    if n > LAG or not first:
                        keep_low(b, n - LAG - 1)
                    ahead = n // 4 - 1 + LEAD
                    if n % 4 == 1 and (ahead < C or more):
                        t_low(b + ahead // C, ahead % C)
                    if n == 7:
                        rows_low(b)
                    if n % 4 == 3 and (n > 8 or not first):
                        keep_u(b, n // 4 - 2)
                    if n == 9 and not first:
                        update(b)

            for c in range(LEAD - 1):
                t_low(0, c)
            turns(e, turn)
            invert(B, -1)
            for k in range(-LAG - 1, 0):
                keep_low(B, k)
            keep_u(B, -2)
            keep_u(B, -1)
            update(B)



def l2_attention(nc, g, a):
    HEADS = 8
    with ExitStack() as ctx:
        s = Scope(nc, ctx, "l2h")
        G = s.sb("G", [DC, HEADS, D])
        A = [s.sb(f"A_{part}", [P, HEADS, DC], F32R) for part in ("hi", "lo")]
        z = [s.sb(f"z_{part}", [P, N], F32R) for part in ("hi", "lo")]
        split_ctx = [s.sb(f"ctx_{part}", [DC, B * S], F32R) for part in ("hi", "lo")]
        prepare(nc, g, "l2w", HEADS, g.l2_wq, g.l2_wk, g.l2_wv, g.l2_wo, A, G, z, split_ctx)
        wide_attention(nc, g, "l2a", HEADS, A, G, z, split_ctx, g.l2_bo)


def l3_attention(nc, g, a):
    HEADS = 16
    with ExitStack() as ctx:
        s = Scope(nc, ctx, "l3h")
        G = s.sb("G", [DC, HEADS, D])
        A = [s.sb(f"A_{part}", [P, HEADS, DC], F32R) for part in ("hi", "lo")]
        z = [s.sb(f"z_{part}", [P, N], F32R) for part in ("hi", "lo")]
        split_ctx = [s.sb(f"ctx_{part}", [DC, B * S], F32R) for part in ("hi", "lo")]
        prepare(nc, g, "l3w", HEADS, g.l3_wq, g.l3_wk, g.l3_wv, g.l3_wo, A, G, z, split_ctx)
        wide_attention(nc, g, "l3a", HEADS, A, G, z, split_ctx, g.l3_bo)




def l1_ffn(nc, g, a):
    FF = 512
    FT = FF // P
    MB = TILES // E
    PAIR = 2
    NT = PAIR * MB
    TURNS = E // PAIR
    W = MB * P
    with ExitStack() as outer:
        so = Scope(nc, outer, "l1f")
        xaT = so.sb("xaT", [P, N])
        w1 = so.sb("w1", [P, PAIR, FF])
        w2 = so.sb("w2", [P, PAIR, FT, D])
        w1_loaded = [so.sem(f"w1_loaded{j}") for j in range(PAIR)]
        w2_loaded = [so.sem(f"w2_loaded{j}") for j in range(PAIR)]

        def load(sp, u, j, first):
            src, dst, loaded = ((a["L1_ffn_w1"].rearrange("e d f -> d e f"), w1, w1_loaded) if first else
                                (a["L1_ffn_w2"].rearrange("e (f p) d -> p e f d", p=P), w2, w2_loaded))
            expert = (slice(None), bass.ds(PAIR * u + j, 1))
            sp.dma_start(dst[:, j:j + 1], src[expert]).then_inc(loaded[j], 16)

        with ExitStack() as ctx:
            s = Scope(nc, ctx, "l1f_front")
            front = AllTiles(s, g, order=[m * E + x for x in range(E) for m in range(MB)], twice=True)
            zT = [s.sb(f"zT{i}", [P, NT * P]) for i in range(2)]
            zps = [s.ps(f"z{i}") for i in range(2)]
            xps = [s.ps(f"xa{i}") for i in range(2)]
            m = s.sems(["zT_ready", "xa_ready", "xaT_ready"])
            block = s.block()

            def keep_xa(e, n):
                e.wait_ge(m.xa_ready, n + 1)
                e.activation(xaT[:, n * NT * P:(n + 1) * NT * P], xps[n % 2][:, :], ACT.Identity,
                             bias=g.l1_attn_b[:, 0:1]).then_inc(m.xaT_ready, 1)

            @block.sync
            def _(sp):
                for j in range(PAIR):
                    load(sp, 0, j, True)
                    load(sp, 0, j, False)

            @block.gpsimd
            def _(e):
                front.gpsimd(e)

            @block.vector
            def _(e):
                front.vector(e)

            @block.tensor
            def _(e):
                for n in range(front.BANKS + 1):
                    if n < front.BANKS:
                        if n >= 2:
                            e.wait_ge(m.zT_ready, n - 1)
                        front.tensor(e, n, zps[n % 2])
                    if n > 0:
                        c = n - 1
                        e.wait_ge(m.zT_ready, c + 1)
                        if c >= 2:
                            e.wait_ge(m.xaT_ready, c - 1)
                        e.matmul(xps[c % 2][:, :], g.l1_attn_w[:, :], zT[c % 2][:, :], start=True, stop=False)
                        for i in range(NT):
                            last = e.matmul(xps[c % 2][:, i * P:(i + 1) * P], front.outer[:, NT * c + i, :], g.ident,
                                            start=False, stop=i == NT - 1)
                        last.then_inc(m.xa_ready, 1)

            @block.scalar
            def _(e):
                for n in range(front.BANKS):
                    e.wait_ge(front.z_turned, n + 1)
                    if n >= 2:
                        e.wait_ge(m.xa_ready, n - 1)
                    e.activation(zT[n % 2][:, :], zps[n % 2][:, :], ACT.Identity, scale=g.l1_lng[:, 0:1],
                                 bias=g.l1_lnb[:, 0:1]).then_inc(m.zT_ready, 1)
                    if n > 0:
                        keep_xa(e, n - 1)
                keep_xa(e, front.BANKS - 1)
                e.wait_ge(m.xaT_ready, front.BANKS)

        with ExitStack() as ctx:
            s = Scope(nc, ctx, "l1f_experts")
            h = s.sb("h", [P, PAIR, FT, W])
            yT = s.sb("yT", [P, NT * P])
            og = s.sb("og", [P, NT, D])
            hps = [s.ps(f"h{i}") for i in range(4)]
            yps = [s.ps(f"y{i}") for i in range(PAIR)]
            ops = s.ps("o")
            m = s.sems(["h_ready", "h_kept", "y_ready", "yT_ready", "o_ready", "og_ready", "x_updated"])
            x_e = g.x[:, :, :].rearrange("p (m e) d -> p e m d", e=E)
            HB = PAIR * FT // 2
            block = s.block()

            def turns(e, turn):
                turn(0, False, True)
                with e.Fori(1, TURNS - 1) as u:
                    turn(u, True, True)
                turn(TURNS - 1, True, False)

            @block.sync
            def _(sp):
                with sp.Fori(1, TURNS) as u:
                    for j in range(PAIR):
                        sp.wait_ge(m.h_ready, HB * (u - 1) + FT // 2 * (j + 1))
                        load(sp, u, j, True)
                    for j in range(PAIR):
                        sp.wait_ge(m.y_ready, PAIR * (u - 1) + j + 1)
                        load(sp, u, j, False)

            @block.tensor
            def _(e):
                def hidden(u, j):
                    e.wait_ge(w1_loaded[j], 16 * u + 16)
                    for f in range(0, FT, 2):
                        n = (j * FT + f) // 2
                        wait(e, m.h_kept, PAIR * FT * (u - 1) + 2 * n + 2)
                        for k in range(2):
                            last = e.matmul(hps[n][:, k * W:(k + 1) * W], w1[:, j, (f + k) * P:(f + k + 1) * P],
                                            xaT[:, bass.ds(u * NT * P + j * W, W)], start=True, stop=True)
                        last.then_inc(m.h_ready, 1)

                def second(u, j):
                    e.wait_ge(w2_loaded[j], 16 * u + 16)
                    e.wait_ge(m.h_kept, PAIR * FT * u + FT * (j + 1))
                    wait(e, m.yT_ready, PAIR * (u - 1) + j + 1)
                    for f in range(FT):
                        last = e.matmul(yps[j][:, 0:W], w2[:, j, f, :], h[:, j, f, :], start=f == 0, stop=f == FT - 1)
                    last.then_inc(m.y_ready, 1)

                def next_layer(u):
                    e.wait_ge(m.yT_ready, PAIR * u + PAIR)
                    if isinstance(u, int):
                        wait(e, m.og_ready, u)
                    for i in range(NT):
                        e.matmul(ops[:, i * P:(i + 1) * P], yT[:, i * P:(i + 1) * P], g.l1_next_w[:, :], start=True, stop=False)
                        last = e.matmul(ops[:, i * P:(i + 1) * P], g.ones[0:1, 0:P], g.l1_next_b[:, :], start=False, stop=True)
                    last.then_inc(m.o_ready, 1)

                def turn(u, before, after):
                    second(u, 0)
                    if before:
                        next_layer(u - 1)
                    second(u, 1)
                    if after:
                        hidden(u + 1, 0)
                        hidden(u + 1, 1)

                hidden(0, 0)
                hidden(0, 1)
                turns(e, turn)
                next_layer(TURNS - 1)

            @block.scalar
            def _(e):
                def gelus(u, j):
                    for f in range(FT):
                        n = j * FT + f
                        e.wait_ge(m.h_ready, HB * u + n // 2 + 1)
                        wait(e, m.y_ready, PAIR * (u - 1) + j + 1)
                        e.activation(h[:, j, f, :], hps[n // 2][:, (n % 2) * W:(n % 2 + 1) * W], ACT.Gelu,
                                     bias=g.l1_b1[:, bass.ds((PAIR * u + j) * FT + f, 1)]).then_inc(m.h_kept, 1)

                def gelu_out(u):
                    e.wait_ge(m.o_ready, u + 1)
                    e.activation(og[:, :, :], ops[:, :].rearrange("p (i d) -> p i d", d=D), ACT.Gelu).then_inc(m.og_ready, 1)

                def turn(u, before, after):
                    if before:
                        gelu_out(u - 1)
                    if after:
                        gelus(u + 1, 0)
                        gelus(u + 1, 1)

                gelus(0, 0)
                gelus(0, 1)
                turns(e, turn)
                gelu_out(TURNS - 1)

            @block.vector
            def _(e):
                def keep_y(u, j):
                    e.wait_ge(m.y_ready, PAIR * u + j + 1)
                    wait(e, m.o_ready, u)
                    e.tensor_scalar(yT[:, j * W:(j + 1) * W], yps[j][:, 0:W], g.l1_b2[:, bass.ds(PAIR * u + j, 1)], None,
                                    ALU.add).then_inc(m.yT_ready, 1)

                def update(u):
                    e.wait_ge(m.og_ready, u + 1)
                    for j in range(PAIR):
                        xs = x_e[:, bass.ds(PAIR * u + j, 1), :, :].squeeze(1)
                        e.tensor_tensor(xs, xs, og[:, j * MB:(j + 1) * MB, :], ALU.add).then_inc(m.x_updated, 1)

                def turn(u, before, after):
                    keep_y(u, 0)
                    if before:
                        update(u - 1)
                    keep_y(u, 1)

                turns(e, turn)
                update(TURNS - 1)



def l2_ffn(nc, g, a):
    C = 4
    CT = 4
    W = CT * P
    TURNS = TILES // CT
    LO = 32
    with ExitStack() as outer:
        so = Scope(nc, outer, "l2f")
        qT = [so.sb(f"qT{r}", [P, N]) for r in range(2)]
        cum = [so.sb(f"cum{r}", [P, N]) for r in range(2)]
        wT = so.sb("wT", [P, 2, N], F32R)
        sel = so.sb("sel", [P, C * P], F32R)
        v_hi = [so.sb(f"v_hi{r}", [P, E * 64], F32R) for r in range(2)]
        v_lo = [so.sb(f"v_lo{r}", [P, E * 64], F32R) for r in range(2)]
        w_hi = [so.sb(f"w_hi{r}", [P, E * 64], F32R) for r in range(2)]
        w_lo = [so.sb(f"w_lo{r}", [P, E * 64], F32R) for r in range(2)]
        b_hi = [so.sb(f"b_hi{r}", [P, D], F32R) for r in range(2)]
        b_lo = [so.sb(f"b_lo{r}", [P, D], F32R) for r in range(2)]

        with ExitStack() as ctx:
            s = Scope(nc, ctx, "l2f_front")
            front = AllTiles(s, g)
            zT = [s.sb(f"zT{i}", [P, W]) for i in range(2)]
            hT = [[s.sb(f"hT{r}{i}", [P, W]) for i in range(2)] for r in range(2)]
            ones = s.sb("ones", [P, T])
            zero = s.sb("zero", [P, D])
            ident = s.sb("ident", [P, P], F32R)
            G = 2 * TILES
            scale = s.sb("scale", [P, G])
            red = s.sb("red", [P, 4, G])
            bias = s.sb("bias", [P, E])
            biased = s.sb("biased", [P, G, E])
            shifted = s.sb("shifted", [P, G, E])
            ex = s.sb("ex", [P, G, E])
            w = s.sb("w", [P, G, E])
            w_st = s.sb("w_stacked", [P, G, P], F32R)
            zps = [s.ps(f"z{i}") for i in range(2)]
            ring = [s.ps(f"ring{i}") for i in range(5)]
            lps = s.ps("logits")
            m = s.sems(["zT_ready", "q_ready", "q_kept", "k_ready", "cum_kept", "iq_ready", "iq_kept", "h_ready",
                        "h_kept", "ic_ready", "ic_kept", "logits_ready", "shifted_ready", "ex_ready", "steps",
                        "scale_ready", "filled", "zeroed", "w_hi_ready", "w_st_ready", "w_turned", "wT_kept_act",
                        "wT_kept_dve", "ident_ready", "split_hi", "split_lo", "b_ready"])
            order = []
            for step in range(TURNS + 3):
                order += [(step - 1, kind) for kind in ("q", "k") if 0 <= step - 1 < TURNS]
                order += [(step - 2, kind) for kind in ("iq", "h0", "ic", "h1") if 0 <= step - 2 < TURNS]
            order += [(n, "w") for n in range(2 * TURNS)]
            place = {item: n % len(ring) for n, item in enumerate(order)}

            def keep_weights(e, n, kept):
                r, c = divmod(n, TURNS)
                e.wait_ge(m.w_turned, n + 1)
                dst, src = wT[:, r, c * W:(c + 1) * W], ring[place[n, "w"]][:, :].bitcast(F32R)
                if kept is m.wT_kept_act:
                    e.activation(dst, src, ACT.Copy).then_inc(kept, 1)
                else:
                    e.tensor_copy(dst, src).then_inc(kept, 1)

            block = s.block()

            @block.gpsimd
            def _(e):
                e.memset(ones[:, :], 1.0).then_inc(m.filled, 1)
                e.memset(zero[:, :], 0.0).then_inc(m.filled, 1)
                front.gpsimd(e)
                e.wait_ge(m.filled, 2)
                for rows in (slice(E, LO), slice(LO + E, P)):
                    e.tensor_copy(w_st[:, :, rows], bcast(zero[:, 0:1].unsqueeze(2), [P, G, rows.stop - rows.start])
                                  ).then_inc(m.zeroed, 1)
                pairs = [(src[r], hi[r], lo[r]) for r in range(2)
                         for src, hi, lo in ((g.l2_v, v_hi, v_lo), (g.l2_w, w_hi, w_lo))]
                for src, hi, lo in pairs:
                    e.tensor_copy(hi[:, :], src[:, :, :].rearrange("p k r -> p (k r)")).then_inc(m.split_hi, 1)
                for n, (src, hi, lo) in enumerate(pairs):
                    e.wait_ge(m.split_hi, n + 1)
                    e.tensor_tensor(lo[:, :], src[:, :, :].rearrange("p k r -> p (k r)"), hi[:, :],
                                    ALU.subtract).then_inc(m.split_lo, 1)
                e.wait_ge(m.split_lo, len(pairs))
                e.wait_ge(m.zeroed, 2)

            @block.tensor
            def _(e):
                used = [None] * len(ring)
                turn = 0

                def bank(sem, count):
                    nonlocal turn
                    i = turn % len(ring)
                    if used[i]:
                        e.wait_ge(*used[i])
                    used[i] = (sem, count)
                    turn += 1
                    return ring[i]

                def product(lhsT, rhs, kept, ready):
                    e.matmul(bank(*kept)[:, :], lhsT[:, :], rhs, start=True, stop=True).then_inc(ready, 1)

                def logits(c, r):
                    e.wait_ge(m.h_kept, 2 * c + r + 1)
                    for i in range(CT):
                        at = (r * TILES + CT * c + i) * E
                        last = e.matmul(lps[:, at:at + E], hT[r][c % 2][:, i * P:(i + 1) * P], g.l2_rw2T[:, :],
                                        start=True, stop=True)
                    last.then_inc(m.logits_ready, 1)

                for step in range(TURNS + 3):
                    if step < TURNS:
                        if step >= 2:
                            e.wait_ge(m.zT_ready, step - 1)
                        front.tensor(e, step, zps[step % 2])
                    c = step - 1
                    if 0 <= c < TURNS:
                        e.wait_ge(m.zT_ready, c + 1)
                        product(g.l2_wqT, zT[c % 2][:, :], (m.q_kept, c + 1), m.q_ready)
                        product(g.l2_wkT, zT[c % 2][:, :], (m.cum_kept, 2 * c + 2), m.k_ready)
                    c = step - 2
                    if 0 <= c < TURNS:
                        at = slice(c * W, (c + 1) * W)
                        e.wait_ge(m.q_kept, c + 1)
                        product(g.l2_winvT, qT[0][:, at], (m.iq_kept, c + 1), m.iq_ready)
                        product(g.l2_rw1T, qT[0][:, at], (m.h_kept, 2 * c + 1), m.h_ready)
                        e.wait_ge(m.cum_kept, 2 * c + 2)
                        product(g.l2_winvT, cum[0][:, at], (m.ic_kept, c + 1), m.ic_ready)
                        e.wait_ge(m.iq_kept, c + 1)
                        product(g.l2_rw1T, qT[1][:, at], (m.h_kept, 2 * c + 2), m.h_ready)
                    c = step - 3
                    if 0 <= c < TURNS:
                        for r in range(2):
                            logits(c, r)
                e.wait_ge(m.w_st_ready, 2)
                e.wait_ge(m.zeroed, 2)
                e.wait_ge(m.ident_ready, 1)
                for n in range(2 * TURNS):
                    b = bank(*((m.wT_kept_dve, n // 2 + 1) if n % 2 else (m.wT_kept_act, n // 2 + 1)))
                    for i in range(CT):
                        last = e.transpose(b[:, i * P:(i + 1) * P].bitcast(F32R), w_st[:, CT * n + i, :], ident[:, :])
                    last.then_inc(m.w_turned, 1)

            @block.scalar
            def _(e):
                for step in range(TURNS + 2):
                    if step < TURNS:
                        e.wait_ge(front.z_turned, step + 1)
                        if step >= 2:
                            e.wait_ge(m.k_ready, step - 1)
                        e.activation(zT[step % 2][:, :], zps[step % 2][:, :], ACT.Copy).then_inc(m.zT_ready, 1)
                    c = step - 1
                    if 0 <= c < TURNS:
                        e.wait_ge(m.q_ready, c + 1)
                        e.activation(qT[0][:, c * W:(c + 1) * W], ring[place[c, "q"]][:, :], ACT.Copy).then_inc(m.q_kept, 1)
                    c = step - 2
                    if 0 <= c < TURNS:
                        e.wait_ge(m.iq_ready, c + 1)
                        e.activation(qT[1][:, c * W:(c + 1) * W], ring[place[c, "iq"]][:, :], ACT.Copy).then_inc(m.iq_kept, 1)
                        for r in range(2):
                            if c >= 2:
                                e.wait_ge(m.logits_ready, 2 * (c - 2) + r + 1)
                            e.wait_ge(m.h_ready, 2 * c + r + 1)
                            e.activation(hT[r][c % 2][:, :], ring[place[c, f"h{r}"]][:, :], ACT.Gelu,
                                         bias=g.l2_rb1[:, 0:1]).then_inc(m.h_kept, 1)
                e.wait_ge(m.shifted_ready, 1)
                e.activation(ex[:, :, :], shifted[:, :, :], ACT.Exp).then_inc(m.ex_ready, 1)
                for n in range(0, 2 * TURNS, 2):
                    keep_weights(e, n, m.wT_kept_act)
                e.wait_ge(m.wT_kept_act, TURNS)

            @block.vector
            def _(e):
                steps = Steps(e, m.steps)

                def then(instruction):
                    steps.add(instruction)
                    steps.settle()

                e.tensor_copy(ident[:, :], g.ident).then_inc(m.ident_ready, 1)
                e.wait_ge(m.filled, 2)
                then(e.tensor_tensor(bias[:, :], g.l2_rb2[:, :], g.l2_eb[:, :], ALU.add))
                places = scale[:, :].rearrange("p (r b i) -> p r b i", r=2, i=TPB)
                by_place = bcast(g.const[:, C_INVN:C_INVN + TPB].unsqueeze(1), [P, B, TPB])
                e.tensor_copy(places[:, 0], by_place).then_inc(m.scale_ready, 1)
                e.tensor_scalar(places[:, 1], by_place, g.l2_alpha[:, 0:1], None, ALU.mult).then_inc(m.scale_ready, 1)
                front.vector(e)
                for step in range(1, TURNS + 2):
                    c = step - 1
                    if 0 <= c < TURNS:
                        e.wait_ge(m.k_ready, c + 1)
                        for n in range(CT // TPB):
                            e.tensor_tensor_scan(cum[0][:, c * W + n * T:c * W + (n + 1) * T], ones[:, :],
                                                 ring[place[c, "k"]][:, n * T:(n + 1) * T], 0.0, ALU.mult,
                                                 ALU.add).then_inc(m.cum_kept, 1)
                    c = step - 2
                    if 0 <= c < TURNS:
                        e.wait_ge(m.ic_ready, c + 1)
                        e.tensor_copy(cum[1][:, c * W:(c + 1) * W], ring[place[c, "ic"]][:, :]).then_inc(m.ic_kept, 1)
                e.tensor_copy(sel[:, :], g.const[:, C_SEL:C_SEL + C * P]).then_inc(m.b_ready, 1)
                done = 1
                for r in range(2):
                    for part in (b_hi, b_lo):
                        e.tensor_copy(part[r][:, :], zero[:, :]).then_inc(m.b_ready, 1)
                done += 4
                e.wait_ge(m.b_ready, done)
                for r in range(2):
                    for at in (0, LO):
                        e.tensor_copy(b_hi[r][at:at + E, :], g.l2_b[r][at:at + E, :]).then_inc(m.b_ready, 1)
                done += 4
                e.wait_ge(m.b_ready, done)
                for r in range(2):
                    for at in (0, LO):
                        e.tensor_tensor(b_lo[r][at:at + E, :], g.l2_b[r][at:at + E, :], b_hi[r][at:at + E, :],
                                        ALU.subtract).then_inc(m.b_ready, 1)
                e.wait_ge(m.logits_ready, 2 * TURNS)
                full = [P, G, E]
                then(e.tensor_tensor(biased[:, :, :], lps[:, 0:G * E].rearrange("p (i e) -> p i e", e=E),
                                     bcast(bias[:, :].unsqueeze(1), full), ALU.add))
                logits = biased[:, :, :]
                then(e.tensor_reduce(red[:, 0, :], logits, AX.X, ALU.max))
                e.tensor_tensor(shifted[:, :, :], logits, bcast(red[:, 0, :].unsqueeze(2), full),
                                ALU.subtract).then_inc(m.shifted_ready, 1)
                e.wait_ge(m.ex_ready, 1)
                e.wait_ge(m.scale_ready, 2)
                then(e.tensor_reduce(red[:, 1, :], ex[:, :, :], AX.X, ALU.add))
                then(e.reciprocal(red[:, 2, :], red[:, 1, :]))
                then(e.tensor_tensor(red[:, 3, :], red[:, 2, :], scale[:, :], ALU.mult))
                then(e.tensor_tensor(w[:, :, :], ex[:, :, :], bcast(red[:, 3, :].unsqueeze(2), full), ALU.mult))
                e.tensor_copy(w_st[:, :, 0:E], w[:, :, :]).then_inc(m.w_st_ready, 1)
                e.wait_ge(m.w_st_ready, 1)
                e.tensor_tensor(w_st[:, :, LO:LO + E], w[:, :, :], w_st[:, :, 0:E], ALU.subtract).then_inc(m.w_st_ready, 1)
                for n in range(1, 2 * TURNS, 2):
                    keep_weights(e, n, m.wT_kept_dve)
                e.wait_ge(m.wT_kept_dve, TURNS)
                e.wait_ge(m.b_ready, 13)

        with ExitStack() as ctx:
            s = Scope(nc, ctx, "l2f_experts")
            q_hi = [s.sb(f"q_hi{r}", [P, W], F32R) for r in range(2)]
            q_lo = [s.sb(f"q_lo{r}", [P, W], F32R) for r in range(2)]
            c_hi = [s.sb(f"c_hi{r}", [P, W], F32R) for r in range(2)]
            c_lo = [s.sb(f"c_lo{r}", [P, W], F32R) for r in range(2)]
            xv = [s.sb(f"xv{i}", [P, W]) for i in range(2)]
            xy = [s.sb(f"xy{i}", [P, W]) for i in range(2)]
            prod = [s.sb(f"prod{i}", [P, W]) for i in range(2)]
            oT = s.sb("oT", [P, W])
            xps = [s.ps(f"xv{i}") for i in range(2)]
            yps = [s.ps(f"yw{i}") for i in range(2)]
            wps = [s.ps(f"weights{i}") for i in range(2)]
            ops = s.ps("out")
            ups = s.ps("update")
            m = s.sems(["hi_ready", "lo_ready", "xv_ready", "xv_kept", "yw_ready", "xy_kept", "wb_ready", "prod_ready",
                        "prod_used", "o_ready", "oT_kept", "y_ready", "x_updated"])
            STEPS = 2 * C
            block = s.block()

            def turns(e, turn):
                turn(0, False, True)
                with e.Fori(1, TURNS - 1) as u:
                    turn(u, True, True)
                turn(TURNS - 1, True, False)

            @block.tensor
            def _(e):
                def products(u, n):
                    r, c = divmod(n, C)
                    if c == 0:
                        e.wait_ge(m.lo_ready, 4 * u + 2 * r + 2)
                    pair = slice(c * P, (c + 1) * P)
                    wait(e, m.xv_kept, STEPS * u + n - 1)
                    for k, (x, y) in enumerate(((v_hi, q_hi), (v_lo, q_hi), (v_hi, q_lo))):
                        last = e.matmul(xps[n % 2][:, :], x[r][:, pair], y[r][:, :], start=k == 0, stop=k == 2)
                    last.then_inc(m.xv_ready, 1)
                    wait(e, m.xy_kept, STEPS * u + n - 1)
                    for k, (x, y) in enumerate(((w_hi, c_hi), (w_lo, c_hi), (w_hi, c_lo))):
                        last = e.matmul(yps[n % 2][:, :], x[r][:, pair], y[r][:, :], start=k == 0, stop=k == 2)
                    last.then_inc(m.yw_ready, 1)
                    wait(e, m.prod_ready, STEPS * u + n - 1)
                    e.matmul(wps[n % 2][:, :], sel[:, pair], wT[:, r, bass.ds(u * W, W)], start=True, stop=True).then_inc(m.wb_ready, 1)

                def out(u, n):
                    r, c = divmod(n, C)
                    if n == 0:
                        wait(e, m.oT_kept, u)
                    e.wait_ge(m.prod_ready, STEPS * u + n + 1)
                    e.matmul(ops[:, :], g.l2_uT[r][:, c, :], prod[n % 2][:, :], start=n == 0, stop=False).then_inc(m.prod_used, 1)
                    if n == STEPS - 1:
                        for r in range(2):
                            for part in (b_hi, b_lo):
                                last = e.matmul(ops[:, :], part[r][:, :], wT[:, r, bass.ds(u * W, W)], start=False,
                                                stop=r == 1 and part is b_lo)
                        last.then_inc(m.o_ready, 1)

                def output(u):
                    e.wait_ge(m.oT_kept, u + 1)
                    for i in range(CT):
                        last = e.matmul(ups[:, i * P:(i + 1) * P], oT[:, i * P:(i + 1) * P], g.l2_woT[:, :], start=True, stop=True)
                    last.then_inc(m.y_ready, 1)

                def turn(u, before, after):
                    for n in range(STEPS):
                        if n + 1 < STEPS:
                            products(u, n + 1)
                        elif after:
                            products(u + 1, 0)
                        out(u, n)
                        if n == 1 and before:
                            output(u - 1)

                products(0, 0)
                turns(e, turn)
                output(TURNS - 1)

            @block.scalar
            def _(e):
                def split(u, r):
                    wait(e, m.yw_ready, STEPS * (u - 1) + 4 * r + 4)
                    e.activation(q_hi[r][:, :], qT[r][:, bass.ds(u * W, W)], ACT.Copy).then_inc(m.hi_ready, 1)
                    e.activation(c_hi[r][:, :], cum[r][:, bass.ds(u * W, W)], ACT.Copy).then_inc(m.hi_ready, 1)

                def keep_xv(u, n):
                    e.wait_ge(m.xv_ready, STEPS * u + n + 1)
                    wait(e, m.xy_kept, STEPS * u + n - 1)
                    e.activation(xv[n % 2][:, :], xps[n % 2][:, :], ACT.Copy).then_inc(m.xv_kept, 1)

                def keep_o(u):
                    e.wait_ge(m.o_ready, u + 1)
                    e.activation(oT[:, :], ops[:, :], ACT.Copy).then_inc(m.oT_kept, 1)

                def turn(u, before, after):
                    for n in range(STEPS):
                        keep_xv(u, n)
                        if n == 0:
                            if before:
                                keep_o(u - 1)
                            split(u, 1)
                        if n == 4 and after:
                            split(u + 1, 0)

                split(0, 0)
                turns(e, turn)
                keep_o(TURNS - 1)

            @block.vector
            def _(e):
                def split(u, r):
                    e.wait_ge(m.hi_ready, 4 * u + 2 * r + 2)
                    e.tensor_tensor(q_lo[r][:, :], qT[r][:, bass.ds(u * W, W)], q_hi[r][:, :], ALU.subtract).then_inc(m.lo_ready, 1)
                    e.tensor_tensor(c_lo[r][:, :], cum[r][:, bass.ds(u * W, W)], c_hi[r][:, :], ALU.subtract).then_inc(m.lo_ready, 1)

                def multiply(u, n):
                    e.wait_ge(m.xv_kept, STEPS * u + n + 1)
                    e.wait_ge(m.yw_ready, STEPS * u + n + 1)
                    e.tensor_tensor(xy[n % 2][:, :], xv[n % 2][:, :], yps[n % 2][:, :], ALU.mult).then_inc(m.xy_kept, 1)
                    e.wait_ge(m.wb_ready, STEPS * u + n + 1)
                    e.wait_ge(m.xy_kept, STEPS * u + n + 1)
                    wait(e, m.prod_used, STEPS * u + n - 1)
                    e.tensor_tensor(prod[n % 2][:, :], xy[n % 2][:, :], wps[n % 2][:, :], ALU.mult).then_inc(m.prod_ready, 1)

                def update(u):
                    e.wait_ge(m.y_ready, u + 1)
                    xs = g.x[:, bass.ds(CT * u, CT), :]
                    e.tensor_tensor(xs, ups[:, :].rearrange("p (i d) -> p i d", d=D), xs, ALU.add).then_inc(m.x_updated, 1)

                def turn(u, before, after):
                    for n in range(STEPS):
                        multiply(u, n)
                        if n == 1:
                            split(u, 1)
                        if n == 3 and before:
                            update(u - 1)
                        if n == 5 and after:
                            split(u + 1, 0)

                split(0, 0)
                turns(e, turn)
                update(TURNS - 1)



def l3_ffn(nc, g, a):
    K = 2
    with ExitStack() as outer:
        so = Scope(nc, outer, "l3f")
        zT = so.sb("zT", [P, N])
        zT0 = so.sb("zT_first", [P, B])
        index = so.sb("index", [K, B], I32)

        with ExitStack() as ctx:
            s = Scope(nc, ctx, "l3f_norm")
            front = AllTiles(s, g)
            red = s.sb("red", [B, 4])
            w = [s.sb(f"w{i}", [B, E]) for i in range(6)]
            pick = s.sb("pick", [B, K])
            turns = [s.ps(f"turn{n}") for n in range(front.BANKS)]
            turn = s.ps("turn")
            sps = s.ps("scores")
            m = s.sems(["zT_kept", "scores_ready", "pick_ready", "pick_turned", "index_ready", "steps"])
            block = s.block()

            @block.gpsimd
            def _(e):
                front.gpsimd(e)

            @block.tensor
            def _(e):
                for n in range(front.BANKS):
                    front.tensor(e, n, turns[n])
                e.wait_ge(m.zT_kept, 2 * front.BANKS)
                e.matmul(sps[0:B, 0:E], zT0[:, :], g.l3_wr[:, :], start=True, stop=False)
                e.matmul(sps[0:B, 0:E], g.ones[0:1, 0:B], g.l3_br[:, :], start=False, stop=True).then_inc(m.scores_ready, 1)
                e.wait_ge(m.pick_ready, K)
                e.transpose(turn[0:K, 0:B], pick[:, :], g.ident[0:B, 0:B]).then_inc(m.pick_turned, 1)

            @block.scalar
            def _(e):
                for n in range(front.BANKS):
                    e.wait_ge(front.z_turned, n + 1)
                    e.activation(zT0[:, 2 * n:2 * n + 2], turns[n][:, 0:T + 1:T], ACT.Copy).then_inc(m.zT_kept, 1)
                    e.activation(zT[:, n * 2 * T:(n + 1) * 2 * T], turns[n][:, :], ACT.Copy).then_inc(m.zT_kept, 1)

            @block.vector
            def _(e):
                front.vector(e)
                steps = Steps(e, m.steps)

                def then(instruction):
                    steps.add(instruction)
                    steps.settle()

                rev = g.const[0:B, C_REV:C_REV + E]

                def first_of_largest(source, at, k):
                    then(e.tensor_reduce(red[:, at:at + 1], source, AX.X, ALU.max))
                    then(e.tensor_scalar(w[0][:, :], source, red[:, at:at + 1], None, ALU.is_equal))
                    then(e.tensor_tensor(w[1][:, :], w[0][:, :], rev, ALU.mult))
                    then(e.tensor_reduce(red[:, at + 1:at + 2], w[1][:, :], AX.X, ALU.max))
                    e.tensor_scalar(pick[:, k:k + 1], red[:, at + 1:at + 2], -1.0, float(E), ALU.mult,
                                    ALU.add).then_inc(m.pick_ready, 1)

                e.wait_ge(m.scores_ready, 1)
                then(e.tensor_copy(w[2][:, :], sps[0:B, 0:E]))
                first_of_largest(w[2][:, :], 0, 0)
                then(e.tensor_scalar(w[3][:, :], rev, red[:, 1:2], None, ALU.is_equal))
                then(e.tensor_scalar(w[4][:, :], w[3][:, :], -3.0e38, None, ALU.mult))
                then(e.tensor_tensor(w[5][:, :], w[2][:, :], w[4][:, :], ALU.add))
                first_of_largest(w[5][:, :], 2, 1)
                e.wait_ge(m.pick_turned, 1)
                e.tensor_copy(index[:, :], turn[0:K, 0:B]).then_inc(m.index_ready, 1)
                e.wait_ge(m.index_ready, 1)

        with ExitStack() as ctx:
            s = Scope(nc, ctx, "l3f_experts")
            w1 = s.sb("w1", [P, B, K, D])
            w2 = s.sb("w2", [P, B, K, D])
            h = [s.sb(f"h{p}", [P, K, T]) for p in range(2)]
            hps = [s.ps(f"h{p}") for p in range(2)]
            ops = [s.ps(f"o{p}") for p in range(2)]
            m = s.sems(["h_projected", "h_kept", "o_ready", "x_updated"])
            loaded = [s.sem(f"loaded{b}") for b in range(B)]
            second_loaded = [s.sem(f"second_loaded{b}") for b in range(B)]
            block = s.block()

            @block.sync
            def _(sp):
                for b in range(B):
                    for k in range(K):
                        x = sp.value_load(index[k:k + 1, b:b + 1], min_val=0, max_val=E - 1)
                        sp.dma_start(w1[:, b, k, :], a["L3_ffn_W1"][bass.ds(x, 1), :, :].squeeze(0)).then_inc(loaded[b], 16)

            @block.tensor
            def _(e):
                def hidden(b):
                    e.wait_ge(loaded[b], 16 * K)
                    if b >= 2:
                        e.wait_ge(m.h_kept, K * (b - 1))
                    for k in range(K):
                        last = e.matmul(hps[b % 2][:, k * T:(k + 1) * T], w1[:, b, k, :], zT[:, b * T:(b + 1) * T],
                                        start=True, stop=True)
                    last.then_inc(m.h_projected, 1)

                hidden(0)
                for b in range(B):
                    if b + 1 < B:
                        hidden(b + 1)
                    e.wait_ge(m.h_kept, K * (b + 1))
                    e.wait_ge(second_loaded[b], 16 * K)
                    if b >= 2:
                        e.wait_ge(m.x_updated, b - 1)
                    experts = [e.value_load(index[k:k + 1, b:b + 1], min_val=0, max_val=E - 1) for k in range(K)]
                    for i in range(TPB):
                        out = ops[b % 2][:, i * P:(i + 1) * P]
                        for k in range(K):
                            e.matmul(out, h[b % 2][:, k, i * P:(i + 1) * P], w2[:, b, k, :], start=k == 0, stop=False)
                            last = e.matmul(out, g.ones[0:1, 0:P], g.l3_b2[:, bass.ds(experts[k] * D, D)], start=False,
                                            stop=k == K - 1)
                    last.then_inc(m.o_ready, 1)

            @block.scalar
            def _(e):
                experts = [[e.value_load(index[k:k + 1, b:b + 1], min_val=0, max_val=E - 1) for k in range(K)]
                           for b in range(2)]

                def load_second(b):
                    if b >= 2:
                        experts.append([e.value_load(index[k:k + 1, b:b + 1], min_val=0, max_val=E - 1) for k in range(K)])
                    for k, x in enumerate(experts[b]):
                        e.dma_start(w2[:, b, k, :], a["L3_ffn_W2"][bass.ds(x, 1), :, :].squeeze(0)).then_inc(second_loaded[b], 16)

                load_second(0)
                load_second(1)
                for b in range(B):
                    if b + 2 < B:
                        load_second(b + 2)
                    e.wait_ge(m.h_projected, b + 1)
                    if b >= 2:
                        e.wait_ge(m.o_ready, b - 1)
                    for k, x in enumerate(experts[b]):
                        e.activation(h[b % 2][:, k, :], hps[b % 2][:, k * T:(k + 1) * T], ACT.Gelu,
                                     bias=g.l3_b1[:, bass.ds(x, 1)]).then_inc(m.h_kept, 1)

            @block.vector
            def _(e):
                for b in range(B):
                    e.wait_ge(m.o_ready, b + 1)
                    xs = g.x[:, TPB * b:TPB * (b + 1), :]
                    e.scalar_tensor_tensor(out=xs, in0=ops[b % 2][:, 0:T].rearrange("p (i d) -> p i d", d=D), scalar=1.0 / K,
                                           in1=xs, op0=ALU.mult, op1=ALU.add).then_inc(m.x_updated, 1)



QW = ["d2v", "img", "txt", "att0", "att1", "f1", "f2"]


def raw_weights(s):
    shape = {"d2v": (P, DC), "img": (P, D), "txt": (P, D), "att0": (D // 2, D), "att1": (D // 2, D),
             "f1": (P, 4, 2 * D), "f2": (P, 4, D)}
    return {n: s.sb("raw_" + n, list(shape[n])) for n in QW}


def load_raw_weights(sp, a, raw, loaded):
    for n in ("d2v", "img", "txt", "att0", "att1"):
        sp.dma_start(raw[n][:, :], a["L1_xattn_W_" + n]).then_inc(loaded, 16)
    sp.dma_start(raw["f1"][:, :, :], a["L1_xattn_W_f1"].rearrange("(f p) i -> p f i", p=P)).then_inc(loaded, 16)
    sp.dma_start(raw["f2"][:, :, :], a["L1_xattn_W_f2"].rearrange("o (f i) -> o f i", i=D)).then_inc(loaded, 16)


def quantise_weights(nc, g, raw, loaded, q, wscale):
    FT = 4
    with ExitStack() as ctx:
        s = Scope(nc, ctx, "l1q")
        low = {n: s.sb("low_" + n, list(raw[n].shape)) for n in QW}
        absum = s.sb("absum", [P, len(QW)])
        thr = s.sb("threshold", [P, len(QW)])
        nthr = s.sb("neg_threshold", [P, len(QW)])
        total = s.ps("total")
        turned = [s.ps(f"turned{i}") for i in range(4)]
        m = s.sems(["zeroed", "summed", "total_ready", "scale_ready", "thr_ready", "low_ready", "q_ready",
                    "turned", "kept"])
        moves = [(raw["d2v"][:, :], [q["d2v"][:, :]]), (raw["img"][:, :], [q["img"][:, :]]),
                 (raw["txt"][:, :], [q["txt"][:, :]])]
        for n in ("att0", "att1"):
            moves.append((raw[n][:, :], [q[n][:, 0:D // 2], q[n][:, D // 2:D]]))
        for f in range(FT):
            for half in range(2):
                moves.append((raw["f1"][:, f, half * D:(half + 1) * D], [q["f1"][:, half, f * P:(f + 1) * P]]))
        for f in range(FT):
            moves.append((raw["f2"][:, f, :], [q["f2"][:, f, :]]))
        block = s.block()

        @block.vector
        def _(e):
            e.memset(absum[:, :], 0.0).then_inc(m.zeroed, 1)
            e.wait_ge(m.zeroed, 1)
            e.wait_ge(loaded, 16 * len(QW))
            size = {}
            for i, n in enumerate(QW):
                t = raw[n]
                rows = t.shape[0]
                size[n] = int(np.prod(t.shape))
                flat = t[:, :, :].rearrange("p f i -> p (f i)") if len(t.shape) == 3 else t[:, :]
                e.tensor_reduce(absum[0:rows, i:i + 1], flat, AX.X, ALU.add, apply_absolute_value=True).then_inc(m.summed, 1)
            e.wait_ge(m.total_ready, 1)
            for i, n in enumerate(QW):
                e.tensor_scalar(wscale[:, i:i + 1], total[:, i:i + 1], 1.0 / size[n], 1e-5, ALU.mult, ALU.max
                                ).then_inc(m.scale_ready, 1)
            e.wait_ge(m.scale_ready, len(QW))
            e.tensor_scalar(thr[:, :], wscale[:, :], 0.5, None, ALU.mult).then_inc(m.thr_ready, 1)
            e.tensor_scalar(nthr[:, :], wscale[:, :], -0.5, None, ALU.mult).then_inc(m.thr_ready, 1)
            e.wait_ge(m.thr_ready, 2)
            for i, n in enumerate(QW):
                rows = raw[n].shape[0]
                whole = tuple(slice(None) for _ in raw[n].shape)
                e.tensor_scalar(low[n][whole], raw[n][whole], nthr[0:rows, i:i + 1], None, ALU.is_lt).then_inc(m.low_ready, 1)
            for i, n in enumerate(QW):
                rows = raw[n].shape[0]
                whole = tuple(slice(None) for _ in raw[n].shape)
                e.wait_ge(m.low_ready, i + 1)
                e.scalar_tensor_tensor(out=raw[n][whole], in0=raw[n][whole], scalar=thr[0:rows, i:i + 1],
                                       in1=low[n][whole], op0=ALU.is_gt, op1=ALU.subtract).then_inc(m.q_ready, 1)

        @block.tensor
        def _(e):
            e.wait_ge(m.summed, len(QW))
            e.matmul(total[:, 0:len(QW)], g.ones[:, 0:P], absum[:, :], start=True, stop=True).then_inc(m.total_ready, 1)
            e.wait_ge(m.q_ready, len(QW))
            for n, (src, _dst) in enumerate(moves):
                if n >= 4:
                    e.wait_ge(m.kept, n - 3)
                rows, cols = src.shape
                e.transpose(turned[n % 4][0:cols, 0:rows], src, g.ident[0:rows, 0:rows]).then_inc(m.turned, 1)

        @block.scalar
        def _(e):
            for n, (src, dsts) in enumerate(moves):
                rows, cols = src.shape
                e.wait_ge(m.turned, n + 1)
                for k, dst in enumerate(dsts):
                    last = e.activation(dst, turned[n % 4][0:cols, 0:rows], ACT.Copy)
                last.then_inc(m.kept, 1)
            e.wait_ge(m.kept, len(moves))


def activation_scales(nc, g, name, groups, scales):
    G = len(groups)
    with ExitStack() as ctx:
        s = Scope(nc, ctx, name)
        part = s.sb("part", [P, G])
        top = s.sb("top", [1, G])
        step = s.sb("step", [1, G])
        turned = s.ps("turned")
        spread = s.ps("spread")
        m = s.sems(["zeroed", "part_ready", "turned", "top_ready", "step_ready", "spread", "scale_ready"])
        block = s.block()

        @block.vector
        def _(e):
            e.memset(part[:, :], 0.0).then_inc(m.zeroed, 1)
            e.wait_ge(m.zeroed, 1)
            for i, x in enumerate(groups):
                e.tensor_reduce(part[0:x.shape[0], i:i + 1], x, AX.X, ALU.max).then_inc(m.part_ready, 1)
            e.wait_ge(m.turned, 1)
            e.tensor_reduce(top[:, :], turned[0:1, 0:G * P].rearrange("p (g n) -> p g n", n=P), AX.X, ALU.max).then_inc(m.top_ready, 1)
            e.wait_ge(m.top_ready, 1)
            e.tensor_scalar(step[:, :], top[:, :], 1e-8, 1.0 / 127.0, ALU.max, ALU.mult).then_inc(m.step_ready, 1)
            e.wait_ge(m.spread, 1)
            for i, (step_all, inverse) in enumerate(scales):
                e.tensor_copy(step_all, spread[:, i:i + 1]).then_inc(m.scale_ready, 1)
                e.reciprocal(inverse, spread[:, i:i + 1]).then_inc(m.scale_ready, 1)
            e.wait_ge(m.scale_ready, 2 * G)

        @block.tensor
        def _(e):
            e.wait_ge(m.part_ready, G)
            for i in range(G):
                last = e.transpose(turned[0:1, i * P:(i + 1) * P], part[:, i:i + 1], g.ident)
            last.then_inc(m.turned, 1)
            e.wait_ge(m.step_ready, 1)
            e.matmul(spread[:, 0:G], g.ones[0:1, 0:P], step[:, :], start=True, stop=True).then_inc(m.spread, 1)


def quantised_projection(nc, g, name, src, rows, weight, dst, top, step, inverse, wstep, bias, mean=None):
    with ExitStack() as ctx:
        s = Scope(nc, ctx, name)
        out_scale = s.sb("out_scale", [P, 1])
        shifted = [s.sb(f"shifted{i}", [rows, S]) for i in range(2)]
        qx = [s.sb(f"qx{i}", [rows, S], BF16) for i in range(2)]
        ps = [s.ps(f"y{i}") for i in range(2)]
        m = s.sems(["scale_ready", "shifted_ready", "qx_ready", "y_ready", "y_kept", "top_ready", "mean_ready"])
        U = 2
        block = s.block()

        @block.vector
        def _(e):
            e.tensor_tensor(out_scale[:, :], step, wstep, ALU.mult).then_inc(m.scale_ready, 1)
            def turn(u):
                for p in range(U):
                    wait(e, m.shifted_ready, U * u + p + 1)
                    wait(e, m.y_ready, U * u)
                    e.tensor_scalar(qx[p][:, :], shifted[p][:, :], MAGIC, None, ALU.subtract).then_inc(m.qx_ready, 1)
                for p in range(U):
                    wait(e, m.y_kept, U * u + p + 1)
                    at = U * u + p
                    e.tensor_reduce(top[:, bass.ds(at, 1)], dst[:, bass.ds(at * S, S)], AX.X, ALU.max,
                                    apply_absolute_value=True).then_inc(m.top_ready, 1)
                    if mean is not None:
                        e.tensor_reduce(mean[:, bass.ds(at, 1)], dst[:, bass.ds(at * S, S)], AX.X, ALU.add).then_inc(m.mean_ready, 1)

            first_and_rest(e, B // U, turn)

        @block.scalar
        def _(e):
            e.wait_ge(m.scale_ready, 1)
            def turn(u):
                for p in range(U):
                    wait(e, m.qx_ready, U * u)
                    e.activation(shifted[p][:, :], src[0:rows, bass.ds((U * u + p) * S, S)], ACT.Identity,
                                 scale=inverse[0:rows, :], bias=g.magic[0:rows, :]).then_inc(m.shifted_ready, 1)
                for p in range(U):
                    wait(e, m.y_ready, U * u + p + 1)
                    e.activation(dst[:, bass.ds((U * u + p) * S, S)], ps[p][:, :], ACT.Identity, scale=out_scale[:, :],
                                 bias=bias).then_inc(m.y_kept, 1)

            first_and_rest(e, B // U, turn)

        @block.tensor
        def _(e):
            def turn(u):
                for p in range(U):
                    wait(e, m.y_kept, U * u)
                    wait(e, m.qx_ready, U * u + p + 1)
                    e.matmul(ps[p][:, :], weight, qx[p][:, :], start=True, stop=True).then_inc(m.y_ready, 1)

            first_and_rest(e, B // U, turn)


def l1_attention(nc, g, a):
    FT = 4
    INV_SQRT = 1.0 / np.sqrt(D)
    with ExitStack() as outer:
        so = Scope(nc, outer, "l1a")
        q = {"d2v": so.sb("q_d2v", [DC, D], BF16), "img": so.sb("q_img", [D, D], BF16), "txt": so.sb("q_txt", [D, D], BF16),
             "att0": so.sb("q_att0", [D, D], BF16), "att1": so.sb("q_att1", [D, D], BF16),
             "f1": so.sb("q_f1", [D, 2, FT * P], BF16), "f2": so.sb("q_f2", [P, FT, D], BF16)}
        wscale = so.sb("wscale", [P, len(QW)])
        step = so.sb("step", [P, 8])
        inverse = so.sb("inverse", [P, 8])
        CTX, Z, VIS, IMG, FUSED, HID = range(6)
        big = so.sb("big", [P, 2 * B * S])
        vis, img = big[:, 0:B * S], big[:, B * S:2 * B * S]
        hid = big[:, :].rearrange("p (f n) -> p f n", f=FT)
        zT = so.sb("zT", [P, N])
        top = so.sb("top", [P, 2 * B])
        ctx_top = so.sb("ctx_top", [DC, 1])
        avg = so.sb("avg", [P, B])
        f1_bias = so.sb("f1_bias", [P, FT, B])

        def scales(i):
            return step[:, i:i + 1], inverse[:, i:i + 1]

        def w(n):
            return wscale[:, QW.index(n):QW.index(n) + 1]

        raw = raw_weights(so)
        loaded = so.sem("raw_loaded")

        with ExitStack() as ctx:
            s = Scope(nc, ctx, "l1a_norm")
            front = AllTiles(s, g)
            turn = [s.ps(f"turn{n}") for n in range(front.BANKS)]
            m = s.sems(["z_kept", "top_ready", "ctx_top_ready"])
            block = s.block()

            @block.sync
            def _(sp):
                load_raw_weights(sp, a, raw, loaded)

            @block.gpsimd
            def _(e):
                front.gpsimd(e)

            @block.tensor
            def _(e):
                for n in range(front.BANKS):
                    front.tensor(e, n, turn[n])

            @block.scalar
            def _(e):
                for n in range(front.BANKS):
                    e.wait_ge(front.z_turned, n + 1)
                    e.activation(zT[:, n * S:(n + 1) * S], turn[n][:, :], ACT.Copy).then_inc(m.z_kept, 1)

            @block.vector
            def _(e):
                front.vector(e)
                e.tensor_reduce(ctx_top[:, :], g.ctxT[0:DC, :], AX.X, ALU.max, apply_absolute_value=True).then_inc(m.ctx_top_ready, 1)
                for n in range(front.BANKS):
                    e.wait_ge(m.z_kept, n + 1)
                    e.tensor_reduce(top[:, n:n + 1], zT[:, n * S:(n + 1) * S], AX.X, ALU.max,
                                    apply_absolute_value=True).then_inc(m.top_ready, 1)

        quantise_weights(nc, g, raw, loaded, q, wscale)
        activation_scales(nc, g, "l1s_in", [ctx_top[:, :], top[:, 0:AllTiles.BANKS]], [scales(CTX), scales(Z)])
        quantised_projection(nc, g, "l1p_vis", g.ctxT, DC, q["d2v"][:, :], vis, top, step[:, CTX:CTX + 1],
                             inverse[:, CTX:CTX + 1], w("d2v"), g.l1_bd2v[:, 0:1])
        activation_scales(nc, g, "l1s_vis", [top[:, 0:B]], [scales(VIS)])
        quantised_projection(nc, g, "l1p_img", vis, P, q["img"][:, :], img, top, step[:, VIS:VIS + 1],
                             inverse[:, VIS:VIS + 1], w("img"), g.l1_bimg[:, 0:1], mean=avg)
        activation_scales(nc, g, "l1s_img", [top[:, 0:B]], [scales(IMG)])

        with ExitStack() as ctx:
            s = Scope(nc, ctx, "l1a_att")
            R, U = 2, 2
            TURNS = B // U
            UNITS = U * TPB
            sc = s.sb("out_scales", [P, 3])
            shift_i = s.sb("shifted_img", [P, U * S])
            shift_z = s.sb("shifted_z", [P, U * T])
            qi = s.sb("q_img_chunk", [P, U * S], BF16)
            qz = s.sb("q_z_chunk", [P, U * T], BF16)
            kT = [[s.sb(f"kT{r}{p}", [P, S]) for p in range(U)] for r in range(R)]
            kt = [[s.sb(f"k_rows{r}{p}", [P, KT, D]) for p in range(U)] for r in range(R)]
            f0 = s.sb("fused0", [P, U, T])
            f1 = s.sb("fused1", [P, U, T])
            rmax = s.sb("rmax", [P, R * UNITS])
            nmax = s.sb("nmax", [P, R * UNITS])
            rsum = s.sb("rsum", [P, R * UNITS])
            rinv = s.sb("rinv", [P, R * UNITS])
            prob = [s.sb(f"prob{k}", [P, S]) for k in range(UNITS)]
            pT = [s.sb(f"probT{p}", [P, KT, T]) for p in range(U)]
            kT_ps, kr_ps = s.ps("kT_and_f"), s.ps("k_rows")
            sps = [s.ps(f"scores{i}") for i in range(TPB)]
            tps = [s.ps(f"turned{i}") for i in range(TPB)]
            ops = [s.ps(f"o{p}") for p in range(U)]
            m = s.sems(["scales_ready", "shifted", "quantised_i", "quantised_z", "kT_projected", "kT_kept", "kr_projected",
                        "kr_kept", "f_projected", "f0_ready", "scores_ready", "max_ready", "nmax_ready", "exp_ready",
                        "rinv_ready", "prob_ready", "turned", "pT_kept", "o_ready", "f_updated", "top_ready",
                        "avg_scaled"])
            block = s.block()

            def unit(u, r, k):
                return R * UNITS * u + UNITS * r + k

            def pair(u, r, p):
                return R * U * u + U * r + p

            def turns(e, turn):
                turn(0, True)
                with e.Fori(1, TURNS - 1) as u:
                    turn(u, True)
                turn(TURNS - 1, False)

            @block.vector
            def _(e):
                def quantise(u):
                    e.wait_ge(m.shifted, 2 * u + 1)
                    wait(e, m.kr_projected, pair(u, 0, 0))
                    e.tensor_scalar(qi[:, :], shift_i[:, :], MAGIC, None, ALU.subtract).then_inc(m.quantised_i, 1)
                    e.wait_ge(m.shifted, 2 * u + 2)
                    wait(e, m.f_projected, u)
                    e.tensor_scalar(qz[:, :], shift_z[:, :], MAGIC, None, ALU.subtract).then_inc(m.quantised_z, 1)

                def keep_rows(u, r, p):
                    e.wait_ge(m.kr_projected, pair(u, r, p) + 1)
                    wait(e, m.o_ready, pair(u, r, p) - R * U + 1)
                    e.scalar_tensor_tensor(out=kt[r][p][:, :, :], in0=kr_ps[:, :].rearrange("p (t d) -> p t d", d=D),
                                           scalar=sc[:, r:r + 1], in1=bcast(g.l1_batt_rows[r][:, :].unsqueeze(1), [P, KT, D]),
                                           op0=ALU.mult, op1=ALU.add).then_inc(m.kr_kept, 1)

                def maximum(u, r, k):
                    n = UNITS * r + k
                    e.wait_ge(m.scores_ready, unit(u, r, k) + 1)
                    e.tensor_reduce(rmax[:, n:n + 1], sps[k % TPB][:, :], AX.X, ALU.max, negate=True).then_inc(m.max_ready, 1)
                    e.wait_ge(m.max_ready, unit(u, r, k) + 1)
                    e.tensor_scalar(nmax[:, n:n + 1], rmax[:, n:n + 1], INV_SQRT, None, ALU.mult).then_inc(m.nmax_ready, 1)

                def divide(u, r, k):
                    n = UNITS * r + k
                    e.wait_ge(m.exp_ready, unit(u, r, k) + 1)
                    e.reciprocal(rinv[:, n:n + 1], rsum[:, n:n + 1]).then_inc(m.rinv_ready, 1)
                    e.wait_ge(m.rinv_ready, unit(u, r, k) + 1)
                    e.tensor_scalar(prob[k][:, :], prob[k][:, :], rinv[:, n:n + 1], None, ALU.mult).then_inc(m.prob_ready, 1)

                def update(u, r, p):
                    e.wait_ge(m.o_ready, pair(u, r, p) + 1)
                    if r == 0:
                        e.wait_ge(m.f0_ready, u + 1)
                        e.scalar_tensor_tensor(out=f1[:, p, :], in0=ops[p][:, 0:T], scalar=0.1, in1=f0[:, p, :],
                                               op0=ALU.mult, op1=ALU.add).then_inc(m.f_updated, 1)
                    else:
                        e.wait_ge(m.f_updated, pair(u, 0, p) + 1)
                        b = U * u + p
                        e.scalar_tensor_tensor(out=zT[:, bass.ds(b * T, T)], in0=ops[p][:, 0:T], scalar=0.1, in1=f1[:, p, :],
                                               op0=ALU.mult, op1=ALU.add).then_inc(m.f_updated, 1)
                        e.wait_ge(m.f_updated, pair(u, 1, p) + 1)
                        e.tensor_reduce(top[:, bass.ds(b, 1)], zT[:, bass.ds(b * T, T)], AX.X, ALU.max,
                                        apply_absolute_value=True).then_inc(m.top_ready, 1)

                def turn(u, more):
                    for r in range(R):
                        prepare_rows = r == 0 or more
                        maximum(u, r, 0)
                        maximum(u, r, 1)
                        divide(u, r, 0)
                        divide(u, r, 1)
                        if prepare_rows:
                            keep_rows(u + r, 1 - r, 0)
                        maximum(u, r, 2)
                        maximum(u, r, 3)
                        divide(u, r, 2)
                        divide(u, r, 3)
                        if prepare_rows:
                            keep_rows(u + r, 1 - r, 1)
                        update(u, r, 0)
                        if r == 0 and more:
                            quantise(u + 1)
                        update(u, r, 1)

                e.tensor_tensor(sc[:, 0:1], step[:, IMG:IMG + 1], w("att0"), ALU.mult).then_inc(m.scales_ready, 1)
                e.tensor_tensor(sc[:, 1:2], step[:, IMG:IMG + 1], w("att1"), ALU.mult).then_inc(m.scales_ready, 1)
                e.tensor_tensor(sc[:, 2:3], step[:, Z:Z + 1], w("txt"), ALU.mult).then_inc(m.scales_ready, 1)
                e.tensor_scalar(avg[:, :], avg[:, :], 1.0 / S, None, ALU.mult).then_inc(m.avg_scaled, 1)
                e.wait_ge(m.scales_ready, 3)
                quantise(0)
                keep_rows(0, 0, 0)
                keep_rows(0, 0, 1)
                turns(e, turn)
                e.wait_ge(m.avg_scaled, 1)
                e.tensor_reduce(top[:, B:B + 1], avg[:, :], AX.X, ALU.max, apply_absolute_value=True).then_inc(m.top_ready, 1)

            @block.scalar
            def _(e):
                def shift(u):
                    wait(e, m.quantised_z, u)
                    e.activation(shift_i[:, :], img[:, bass.ds(u * U * S, U * S)], ACT.Identity, scale=inverse[:, IMG:IMG + 1],
                                 bias=g.magic[:, :]).then_inc(m.shifted, 1)
                    e.activation(shift_z[:, :], zT[:, bass.ds(u * U * T, U * T)], ACT.Identity, scale=inverse[:, Z:Z + 1],
                                 bias=g.magic[:, :]).then_inc(m.shifted, 1)

                def keep_k(u, r, p):
                    e.wait_ge(m.kT_projected, pair(u, r, p) + 1)
                    wait(e, m.scores_ready, unit(u, r, TPB * p) - R * UNITS + TPB)
                    e.activation(kT[r][p][:, :], kT_ps[:, :], ACT.Identity, scale=sc[:, r:r + 1],
                                 bias=g.l1_batt[r][:, 0:1]).then_inc(m.kT_kept, 1)

                def keep_f(u):
                    e.wait_ge(m.f_projected, u + 1)
                    wait(e, m.f_updated, pair(u, 0, 0) - R * U + U)
                    e.activation(f0[:, :, :], kT_ps[:, :].rearrange("p (b t) -> p b t", t=T), ACT.Identity, scale=sc[:, 2:3],
                                 bias=g.l1_btxt[:, 0:1]).then_inc(m.f0_ready, 1)

                def exps(u, r, k):
                    n = UNITS * r + k
                    e.wait_ge(m.nmax_ready, unit(u, r, k) + 1)
                    wait(e, m.turned, unit(u, r, k) - UNITS + 1)
                    e.activation(prob[k][:, :], sps[k % TPB][:, :], ACT.Exp, scale=INV_SQRT, bias=nmax[:, n:n + 1],
                                 accum_out=rsum[:, n:n + 1]).then_inc(m.exp_ready, 1)

                def keep_turned(u, r, k):
                    p, i = divmod(k, TPB)
                    e.wait_ge(m.turned, unit(u, r, k) + 1)
                    wait(e, m.o_ready, pair(u, r, p) - U + 1)
                    e.activation(pT[p][:, :, i * P:(i + 1) * P], tps[i][:, :].rearrange("p (t q) -> p t q", q=P),
                                 ACT.Copy).then_inc(m.pT_kept, 1)

                def turn(u, more):
                    for r in range(R):
                        prepare_k = r == 0 or more
                        exps(u, r, 0)
                        exps(u, r, 1)
                        if prepare_k:
                            keep_k(u + r, 1 - r, 0)
                        keep_turned(u, r, 0)
                        exps(u, r, 2)
                        keep_turned(u, r, 1)
                        exps(u, r, 3)
                        if prepare_k:
                            keep_k(u + r, 1 - r, 1)
                        keep_turned(u, r, 2)
                        keep_turned(u, r, 3)
                        if r == 0 and more:
                            shift(u + 1)
                        if r == 1 and more:
                            keep_f(u + 1)

                shift(0)
                e.wait_ge(m.scales_ready, 3)
                keep_k(0, 0, 0)
                keep_k(0, 0, 1)
                keep_f(0)
                turns(e, turn)

            @block.tensor
            def _(e):
                weights = ("att0", "att1")

                def project(u, r, p):
                    if r == 0 and p == 0:
                        e.wait_ge(m.quantised_i, u + 1)
                    wait(e, m.kT_kept, pair(u, r, p))
                    if r == 1 and p == 0:
                        e.wait_ge(m.f0_ready, u + 1)
                    chunk = p * S
                    e.matmul(kT_ps[:, :], q[weights[r]][:, :], qi[:, chunk:chunk + S], start=True, stop=True).then_inc(m.kT_projected, 1)
                    wait(e, m.kr_kept, pair(u, r, p))
                    for t in range(KT):
                        last = e.matmul(kr_ps[:, t * P:(t + 1) * P], qi[:, chunk + t * P:chunk + (t + 1) * P],
                                        q[weights[r]][:, :], start=True, stop=True)
                    last.then_inc(m.kr_projected, 1)

                def project_f(u):
                    e.wait_ge(m.quantised_z, u + 1)
                    e.wait_ge(m.kT_kept, pair(u, 0, U))
                    e.matmul(kT_ps[:, :], q["txt"][:, :], qz[:, :], start=True, stop=True).then_inc(m.f_projected, 1)

                def scores(u, r, k):
                    p, i = divmod(k, TPB)
                    wait(e, m.exp_ready, unit(u, r, k) - TPB + 1)
                    if i == 0:
                        e.wait_ge(m.kT_kept, pair(u, r, p) + 1)
                        if r == 0:
                            e.wait_ge(m.f0_ready, u + 1)
                        else:
                            e.wait_ge(m.f_updated, pair(u, 0, p) + 1)
                    f = f1 if r else f0
                    e.matmul(sps[i][:, :], f[:, p, i * P:(i + 1) * P], kT[r][p][:, :], start=True, stop=True).then_inc(m.scores_ready, 1)

                def turned(u, r, k):
                    e.wait_ge(m.prob_ready, unit(u, r, k) + 1)
                    wait(e, m.pT_kept, unit(u, r, k) - TPB + 1)
                    for t in range(KT):
                        last = e.transpose(tps[k % TPB][:, t * P:(t + 1) * P], prob[k][:, t * P:(t + 1) * P], g.ident)
                    last.then_inc(m.turned, 1)

                def attended(u, r, p):
                    e.wait_ge(m.pT_kept, unit(u, r, TPB * p) + TPB)
                    e.wait_ge(m.kr_kept, pair(u, r, p) + 1)
                    wait(e, m.f_updated, pair(u, r, p) - U + 1)
                    for t in range(KT):
                        last = e.matmul(ops[p][:, 0:T], kt[r][p][:, t, :], pT[p][:, t, :], start=t == 0, stop=t == KT - 1)
                    last.then_inc(m.o_ready, 1)

                def turn(u, more):
                    for r in range(R):
                        prepare = r == 0 or more
                        scores(u, r, 0)
                        scores(u, r, 1)
                        if prepare:
                            project(u + r, 1 - r, 0)
                        scores(u, r, 2)
                        scores(u, r, 3)
                        turned(u, r, 0)
                        turned(u, r, 1)
                        if prepare:
                            project(u + r, 1 - r, 1)
                        attended(u, r, 0)
                        turned(u, r, 2)
                        turned(u, r, 3)
                        if r == 1 and more:
                            project_f(u + 1)
                        attended(u, r, 1)

                project(0, 0, 0)
                project(0, 0, 1)
                project_f(0)
                turns(e, turn)

        activation_scales(nc, g, "l1s_fused", [top[:, 0:B + 1]], [scales(FUSED)])

        with ExitStack() as ctx:
            s = Scope(nc, ctx, "l1a_f1")
            sc = s.sb("out_scale", [P, 1])
            shift_a = s.sb("shifted_avg", [P, B])
            qa = s.sb("q_avg", [P, B], BF16)
            shift = [s.sb(f"shifted{i}", [P, T]) for i in range(2)]
            qx = [s.sb(f"qx{i}", [P, T], BF16) for i in range(2)]
            aps = s.ps("avg")
            hps = [s.ps(f"h{i}", (P, 2 * 512)) for i in range(2)]
            U = 2
            m = s.sems(["scale_ready", "avg_shifted", "avg_quantised", "avg_projected", "bias_ready", "shifted",
                        "quantised", "h_ready", "h_kept", "top_ready"])
            block = s.block()

            @block.scalar
            def _(e):
                e.activation(shift_a[:, :], avg[:, :], ACT.Identity, scale=inverse[:, FUSED:FUSED + 1], bias=g.magic[:, :]).then_inc(m.avg_shifted, 1)
                e.wait_ge(m.bias_ready, FT)
                def turn(u):
                    for p in range(U):
                        wait(e, m.quantised, U * u)
                        e.activation(shift[p][:, :], zT[:, bass.ds((U * u + p) * T, T)], ACT.Identity,
                                     scale=inverse[:, FUSED:FUSED + 1], bias=g.magic[:, :]).then_inc(m.shifted, 1)
                    for p in range(U):
                        for k in range(FT):
                            wait(e, m.h_ready, U * u + p + 1)
                            e.activation(hid[:, k, bass.ds((U * u + p) * T, T)], hps[p][:, k * T:(k + 1) * T], ACT.Relu,
                                         scale=sc[:, :], bias=f1_bias[:, k, bass.ds(U * u + p, 1)]).then_inc(m.h_kept, 1)

                first_and_rest(e, B // U, turn)

            @block.vector
            def _(e):
                e.tensor_tensor(sc[:, :], step[:, FUSED:FUSED + 1], w("f1"), ALU.mult).then_inc(m.scale_ready, 1)
                e.wait_ge(m.avg_shifted, 1)
                e.tensor_scalar(qa[:, :], shift_a[:, :], MAGIC, None, ALU.subtract).then_inc(m.avg_quantised, 1)
                e.wait_ge(m.avg_projected, 1)
                e.wait_ge(m.scale_ready, 1)
                for k in range(FT):
                    e.tensor_scalar(f1_bias[:, k, :], aps[:, k * B:(k + 1) * B], sc[:, :], g.l1_bf1[:, k:k + 1], ALU.mult,
                                    ALU.add).then_inc(m.bias_ready, 1)
                def turn(u):
                    for p in range(U):
                        wait(e, m.shifted, U * u + p + 1)
                        wait(e, m.h_ready, U * u)
                        e.tensor_scalar(qx[p][:, :], shift[p][:, :], MAGIC, None, ALU.subtract).then_inc(m.quantised, 1)
                    for p in range(U):
                        wait(e, m.h_kept, FT * (U * u + p + 1))
                        e.tensor_reduce(top[:, bass.ds(U * u + p, 1)], hid[:, :, bass.ds((U * u + p) * T, T)], AX.XY,
                                        ALU.max).then_inc(m.top_ready, 1)

                first_and_rest(e, B // U, turn)

            @block.tensor
            def _(e):
                e.wait_ge(m.avg_quantised, 1)
                for k in range(FT):
                    last = e.matmul(aps[:, k * B:(k + 1) * B], q["f1"][:, 1, k * P:(k + 1) * P], qa[:, :], start=True, stop=True)
                last.then_inc(m.avg_projected, 1)
                def turn(u):
                    for p in range(U):
                        wait(e, m.quantised, U * u + p + 1)
                        wait(e, m.h_kept, FT * U * u)
                        for k in range(FT):
                            last = e.matmul(hps[p][:, k * T:(k + 1) * T], q["f1"][:, 0, k * P:(k + 1) * P], qx[p][:, :], start=True, stop=True)
                        last.then_inc(m.h_ready, 1)

                first_and_rest(e, B // U, turn)

        activation_scales(nc, g, "l1s_hid", [top[:, 0:B]], [scales(HID)])

        with ExitStack() as ctx:
            s = Scope(nc, ctx, "l1a_f2")
            sc = s.sb("out_scale", [P, 1])
            shift = [s.sb(f"shifted{i}", [P, FT, T]) for i in range(2)]
            qx = [s.sb(f"qx{i}", [P, FT, T], BF16) for i in range(2)]
            yps = [s.ps(f"y{i}") for i in range(2)]
            U = 2
            m = s.sems(["scale_ready", "shifted", "quantised", "y_ready", "x_biased", "x_updated"])
            block = s.block()

            @block.scalar
            def _(e):
                def turn(u):
                    for p in range(U):
                        wait(e, m.quantised, U * u)
                        e.activation(shift[p][:, :, :], hid[:, :, bass.ds((U * u + p) * T, T)], ACT.Identity,
                                     scale=inverse[:, HID:HID + 1], bias=g.magic[:, :]).then_inc(m.shifted, 1)

                first_and_rest(e, B // U, turn)

            @block.vector
            def _(e):
                e.tensor_tensor(sc[:, :], step[:, HID:HID + 1], w("f2"), ALU.mult).then_inc(m.scale_ready, 1)
                e.wait_ge(m.scale_ready, 1)
                def turn(u):
                    for p in range(U):
                        wait(e, m.shifted, U * u + p + 1)
                        wait(e, m.y_ready, U * u)
                        e.tensor_scalar(qx[p][:, :, :], shift[p][:, :, :], MAGIC, None, ALU.subtract).then_inc(m.quantised, 1)
                        xs = g.x[:, bass.ds(TPB * (U * u + p), TPB), :]
                        e.tensor_tensor(xs, xs, bcast(g.l1_bf2[:, :].unsqueeze(1), [P, TPB, D]), ALU.add).then_inc(m.x_biased, 1)
                    for p in range(U):
                        wait(e, m.y_ready, U * u + p + 1)
                        wait(e, m.x_biased, U * u + p + 1)
                        xs = g.x[:, bass.ds(TPB * (U * u + p), TPB), :]
                        e.scalar_tensor_tensor(out=xs, in0=yps[p][:, 0:T].rearrange("p (i d) -> p i d", d=D), scalar=sc[:, :],
                                               in1=xs, op0=ALU.mult, op1=ALU.add).then_inc(m.x_updated, 1)

                first_and_rest(e, B // U, turn)

            @block.tensor
            def _(e):
                def turn(u):
                    for p in range(U):
                        wait(e, m.quantised, U * u + p + 1)
                        wait(e, m.x_updated, U * u)
                        for i in range(TPB):
                            for k in range(FT):
                                last = e.matmul(yps[p][:, i * P:(i + 1) * P], qx[p][:, k, i * P:(i + 1) * P], q["f2"][:, k, :],
                                                start=k == 0, stop=k == FT - 1)
                        last.then_inc(m.y_ready, 1)

                first_and_rest(e, B // U, turn)



def load_weights(g, sp):
    for dst, src in g.loads:
        sp.dma_start(dst, src).then_inc(g.weights_loaded, 16)


def weights_stage(nc, g, a, load=False):
    with ExitStack() as ctx:
        s = Scope(nc, ctx, "weights")
        ps = [s.ps(f"turned{i}") for i in range(2)]
        turned = s.sem("turned")
        kept = s.sem("kept")
        block = s.block()

        if load:
            @block.sync
            def _(sp):
                load_weights(g, sp)

        @block.tensor
        def _(e):
            e.wait_ge(g.weights_loaded, 16 * len(g.loads))
            for n, (dst, src) in enumerate(g.to_turn):
                if n >= 2:
                    e.wait_ge(kept, n - 1)
                rows, cols = src.shape
                e.transpose(ps[n % 2][0:cols, 0:rows], src, g.ident[0:rows, 0:rows]).then_inc(turned, 1)

        @block.scalar
        def _(e):
            for n, (dst, src) in enumerate(g.to_turn):
                rows, cols = src.shape
                e.wait_ge(turned, n + 1)
                e.activation(dst, ps[n % 2][0:cols, 0:rows], ACT.Copy).then_inc(kept, 1)
            e.wait_ge(kept, len(g.to_turn))


def store_stage(nc, g, a):
    with ExitStack() as ctx:
        s = Scope(nc, ctx, "store")
        stored = s.sem("stored")
        block = s.block()

        @block.sync
        def _(sp):
            sp.dma_start(a["out"].rearrange("b (i p) d -> p (b i) d", p=P), g.x[:, :, :]).then_inc(stored, 16)
            sp.wait_ge(stored, 16)


STAGES = [l0_attention, l0_ffn, l1_attention, l1_ffn, l2_attention, l2_ffn, l3_attention, l3_ffn]


def build(nc, a, stages=None):
    with ExitStack() as ctx, ExitStack() as for_l3, ExitStack() as for_l2, ExitStack() as for_l0, ExitStack() as for_turning:
        g = Shared()
        life = [ctx]
        raws = []

        def keep(name, shape, dtype=F32):
            return life[-1].enter_context(nc.sbuf_tensor(name, shape, dtype))

        def loaded(name, shape, src, first=False):
            t = keep("w_" + name, shape)
            (g.loads_first if first else g.loads).append((t[tuple(slice(None) for _ in shape)], src))
            return t

        g.loads_first, g.loads, g.to_turn = [], [], []
        g.const = keep("const", [P, C_ALL])
        g.x = keep("x_tokens", [P, TILES, D])
        g.ctxT = keep("ctxT", [DC + 1, B * S])
        g.ctx_rows = keep("ctx_rows", [P, B * KT, DC])
        g.ones = keep("ones", [P, P])
        g.neg_half = keep("neg_half", [P, TILES])
        g.magic = keep("magic", [P, 1])
        g.ident = g.const[:, C_ID:C_ID + P]
        g.vector_rows = keep("vector_rows", [P, P])
        g.vectors = keep("vectors", [P, P])
        g.vectors_used = 0
        g.weights_loaded = ctx.enter_context(nc.semaphore("weights_loaded"))

        def row(v):
            return a[v].unsqueeze(0)

        def rows(v):
            return a[v].unsqueeze(0).to_broadcast([P, a[v].shape[0]])

        def columns(*sources):
            first = g.vectors_used
            for src, at in sources:
                n, width = src.shape
                g.loads_first.append((g.vector_rows[first:first + n, at:at + width], src))
            g.vectors_used = first + n
            return g.vectors[:, first:first + n]

        def transposed(name, w):
            rows, cols = a[w].shape
            t = keep("w_" + name, [cols, rows])
            raws.append((name, [rows, cols], a[w], [(t[:, :], lambda raw: raw[:, :])]))
            return t

        def biased(name, w, bias, width):
            t = keep("w_" + name, [DC + 1, width])
            g.loads_first.append((t[0:DC, :], a[w]))
            if bias is not None:
                g.loads_first.append((t[DC:DC + 1, :], row(bias)))
            return t

        g.l1_lng = columns((row("L1_ffn_ln_g"), 0))
        g.l1_lnb = columns((row("L1_ffn_ln_b"), 0))
        g.l1_attn_b = columns((row("L1_ffn_attn_b"), 0))
        g.l1_b1 = columns((a["L1_ffn_b1"].rearrange("e (f p) -> (e f) p", p=P), 0))
        g.l1_b2 = columns((a["L1_ffn_b2"], 0))
        g.l1_attn_w = loaded("l1_attn_w", [D, D], a["L1_ffn_attn_w"])
        g.l1_next_w = loaded("l1_next_w", [D, D], a["L1_ffn_next_w"])
        g.l1_next_b = loaded("l1_next_b", [1, D], row("L1_ffn_next_b"))

        g.l3_b1 = columns((a["L3_ffn_b1"], 0))
        g.l1_bd2v = columns((row("L1_xattn_b_d2v"), 0))
        g.l1_bimg = columns((row("L1_xattn_b_img"), 0))
        g.l1_btxt = columns((row("L1_xattn_b_txt"), 0))
        g.l1_batt = [columns((row(f"L1_xattn_b_att{i}"), 0), (row(f"L1_xattn_b_att{i}"), D // 2)) for i in range(2)]
        g.l1_batt_rows = []
        for i in range(2):
            t = keep(f"w_l1_batt_rows{i}", [P, D])
            for half in range(2):
                g.loads.append((t[:, half * D // 2:(half + 1) * D // 2], rows(f"L1_xattn_b_att{i}")))
            g.l1_batt_rows.append(t)
        g.l1_bf1 = columns((a["L1_xattn_b_f1"].rearrange("(f p) -> f p", p=P), 0))
        g.l1_bf2 = loaded("l1_bf2", [P, D], rows("L1_xattn_b_f2"))
        def wide_weights(l, heads):
            w = heads * 64
            wq = loaded(f"l{l}_wq", [D, w], a[f"L{l}_xattn_Wq"])
            wk = loaded(f"l{l}_wk", [DC, w], a[f"L{l}_xattn_Wk"])
            wv = loaded(f"l{l}_wv", [DC, w], a[f"L{l}_xattn_Wv"])
            wo = loaded(f"l{l}_wo", [P, heads // 2, D], a[f"L{l}_xattn_Wo"].rearrange("(c p) d -> p c d", p=P))
            bo = loaded(f"l{l}_bo", [1, D], row(f"L{l}_xattn_bo"))
            return wq, wk, wv, wo, bo

        life.append(for_l3)
        g.l3_wq, g.l3_wk, g.l3_wv, g.l3_wo, g.l3_bo = wide_weights("3", 16)
        g.l3_wr = loaded("l3_wr", [D, E], a["L3_ffn_Wr"])
        g.l3_b2 = loaded("l3_b2", [1, E * D], a["L3_ffn_b2"].rearrange("e d -> (e d)").unsqueeze(0))
        g.l3_br = loaded("l3_br", [1, E], row("L3_ffn_br"))

        life.append(for_l2)
        g.l2_wq, g.l2_wk, g.l2_wv, g.l2_wo, g.l2_bo = wide_weights("2", 8)
        g.l2_wqT = transposed("l2_wqT", "L2_ffn_W_Q")
        g.l2_wkT = transposed("l2_wkT", "L2_ffn_W_K")
        g.l2_woT = transposed("l2_woT", "L2_ffn_W_O")
        g.l2_winvT = transposed("l2_winvT", "L2_ffn_W_inv")
        g.l2_rw1T = transposed("l2_rw1T", "L2_ffn_router_w1")
        g.l2_rw2T = transposed("l2_rw2T", "L2_ffn_router_w2")
        g.l2_rb1 = columns((row("L2_ffn_router_b1"), 0))
        g.l2_rb2 = loaded("l2_rb2", [P, E], rows("L2_ffn_router_b2"))
        g.l2_eb = loaded("l2_eb", [P, E], rows("L2_ffn_expert_bias"))
        g.l2_alpha = loaded("l2_alpha", [P, 1], a["L2_ffn_alpha_bi"].unsqueeze(0).to_broadcast([P, 1]))
        g.l2_v = [loaded(f"l2_v{i}", [D, E, 64], a[w].rearrange("k d r -> d k r")) for i, w in
                  enumerate(("L2_ffn_V_fwd", "L2_ffn_W_inv_exp"))]
        g.l2_w = [loaded(f"l2_w{i}", [D, E, 64], a[w].rearrange("k d r -> d k r")) for i, w in
                  enumerate(("L2_ffn_W_fwd", "L2_ffn_V_inv"))]
        g.l2_uT = []
        for i, w in enumerate(("L2_ffn_U_fwd", "L2_ffn_U_inv")):
            uT = keep(f"l2_uT{i}", [P, 4, D])
            raws.append((f"l2_u{i}", [D, E, 64], a[w].rearrange("k d r -> d k r"),
                         [(uT[:, c, :], lambda raw, c=c: raw[:, 2 * c:2 * c + 2, :].rearrange("p k r -> p (k r)"))
                          for c in range(4)]))
            g.l2_uT.append(uT)
        g.l2_b = []
        for i, w in enumerate(("L2_ffn_b_fwd", "L2_ffn_b_inv")):
            t = keep(f"w_l2_b{i}", [32 + E, D])
            for at in (0, 32):
                g.loads.append((t[at:at + E, :], a[w]))
            g.l2_b.append(t)

        life.append(for_l0)
        g.l0_wk = biased("l0_wk", "L0_xattn_Wk", "L0_xattn_bk", D)
        g.l0_wv = biased("l0_wv", "L0_xattn_Wv", "L0_xattn_bv", D)
        g.l0_wq = loaded("l0_wq", [D, D], a["L0_xattn_Wq"], True)
        g.l0_bq = loaded("l0_bq", [1, D], row("L0_xattn_bq"), True)
        g.l0_wo = loaded("l0_wo", [D, D], a["L0_xattn_Wo"], True)
        g.l0_bo = loaded("l0_bo", [1, D], row("L0_xattn_bo"), True)
        g.l0_gamma = loaded("l0_gamma", [P, D], rows("L0_xattn_ln_gamma"), True)
        g.l0_beta = loaded("l0_beta", [P, D], rows("L0_xattn_ln_beta"), True)

        g.l0_lng = columns((row("L0_ffn_ln_g"), 0))
        g.l0_lnb = columns((row("L0_ffn_ln_b"), 0))
        g.l0_rw = loaded("l0_rw", [D, E], a["L0_ffn_rW"])
        g.l0_rb = loaded("l0_rb", [1, E], row("L0_ffn_rb"))
        g.l0_w1 = loaded("l0_w1", [D, E, 256], a["L0_ffn_W1"].rearrange("e d f -> d e f"))
        g.l0_b1 = columns((a["L0_ffn_b1"].rearrange("e (f p) -> (e f) p", p=P), 0))
        g.l0_w2 = loaded("l0_w2", [P, E, 2, D], a["L0_ffn_W2"].rearrange("e (f p) d -> p e f d", p=P))
        g.l0_b2 = loaded("l0_b2", [E, D], a["L0_ffn_b2"])

        life.append(for_turning)
        for name, shape, src, moves in raws:
            raw = loaded(name + "_raw", shape, src)
            for dst, part in moves:
                g.to_turn.append((dst, part(raw)))

        load_stage(nc, g, a)
        for stage in STAGES:
            if stages is None or stage in stages:
                stage(nc, g, a)
                clear_semaphores(nc)
            if stage is l0_attention:
                weights_stage(nc, g, a, load=stages is not None and l0_attention not in stages)
                for_turning.close()
            if stage is l0_ffn:
                for_l0.close()
            if stage is l2_ffn:
                for_l2.close()
        store_stage(nc, g, a)


def kernel(**inputs):
    import concourse.bacc as bacc
    from concourse.bass_utils import run_bass_kernel_spmd

    nc = bacc.Bacc("TRN2", target_bir_lowering=False, num_devices=1)
    arrays, args = {}, {}
    for name, value in {**inputs, "constants": shape_constants()}.items():
        v = np.ascontiguousarray(value)
        v = v.reshape(v.shape or (1,))
        arrays["in_" + name] = v
        args[name] = nc.dram_tensor("in_" + name, v.shape, mybir.dt.from_np(v.dtype), kind="ExternalInput").ap()
    args["out"] = nc.dram_tensor("out_x", (B, T, D), F32, kind="ExternalOutput").ap()
    build(nc, args)
    return run_bass_kernel_spmd(nc, [arrays], core_ids=[0]).results[0]["out_x"]
```
